# Optimizing a Trainium2 kernel written in Bass

```python
import numpy as np
import jax
import jax.numpy as jnp

def _softmax(x, axis=-1):
    return jax.nn.softmax(x, axis=axis)

def _gelu(x):
    return jax.nn.gelu(x, approximate=True)

def _silu(x):
    return jax.nn.silu(x)

def _sigmoid(x):
    return jax.nn.sigmoid(x)

def _layernorm(x, axis=-1, eps=1e-05):
    m = jnp.mean(x, axis=axis, keepdims=True)
    v = jnp.var(x, axis=axis, keepdims=True)
    return (x - m) / jnp.sqrt(v + eps)

def _scatter_add(tgt, idx, src, axis=0):
    return tgt.at[idx].add(src)

def _segment_sum(src, seg, n):
    return jax.ops.segment_sum(src, seg, n)
kernel_name = 'mk_decoder_postln_d4_seqx_r8_695a0c'

def setup_inputs(seed: int=0):
    np.random.seed(seed)
    _w = jnp.asarray

    def _rec_inputs():
        import jax
        import jax.numpy as jnp
        _rk = jax.random.key(seed)
        x = -0.0003929 + 0.9999 * jax.random.normal(jax.random.fold_in(_rk, 1), (64, 128, 128), jnp.float32)
        _lenS = 128 - jax.random.randint(jax.random.fold_in(_rk, 7), (64,), 0, max(1, 128 // 4) + 1, jnp.int32)
        _lenS2 = 77 - jax.random.randint(jax.random.fold_in(_rk, 8), (64,), 0, max(1, 77 // 4) + 1, jnp.int32)
        _ctx_512P = jax.random.normal(jax.random.fold_in(_rk, 11), (64, 16, 64), jnp.float32)
        _ctx_512c = jax.random.dirichlet(jax.random.fold_in(_rk, 511), 0.3 * jnp.ones((16,), jnp.float32), (64, 77))
        _ctx_512t = jnp.einsum('bsk,bkd->bsd', _ctx_512c, _ctx_512P)
        _ctx_512t = _ctx_512t * jax.lax.rsqrt(jnp.mean(jnp.square(_ctx_512t)) + 1e-12) * 0.953939
        ctx_512 = -1.39393e-06 + 0.999914 * (_ctx_512t + 0.3 * jax.random.normal(jax.random.fold_in(_rk, 611), (64, 77, 64), jnp.float32))
        return (x, ctx_512)
    x, ctx_512 = _rec_inputs()

    def _L0_attn_setup():
        import jax, jax.numpy as jnp
        import numpy as np
        EMBED_DIM = 128
        NUM_HEADS = 16
        HEAD_DIM = EMBED_DIM // NUM_HEADS
        L, B = (256, 2)
        EPS = 1e-08

        def gated_rms_norm(x, weight, gate):
            rms = jnp.linalg.norm(x, axis=-1, keepdims=True) * EMBED_DIM ** (-0.5)
            x_normed = x / (rms + EPS)
            return weight * x_normed * jax.nn.sigmoid(gate * x)
        key = jax.random.key(seed)
        ks = jax.random.split(key, 12)
        s = EMBED_DIM ** (-0.5)
        return {'query': jax.random.normal(ks[0], (L, B, EMBED_DIM), jnp.float32), 'key': jax.random.normal(ks[1], (L, B, EMBED_DIM), jnp.float32), 'value': jax.random.normal(ks[2], (L, B, EMBED_DIM), jnp.float32), 'Wq': jax.random.normal(ks[3], (EMBED_DIM, EMBED_DIM), jnp.float32) * s, 'bq': jnp.zeros((EMBED_DIM,), jnp.float32), 'Wk': jax.random.normal(ks[4], (EMBED_DIM, EMBED_DIM), jnp.float32) * s, 'bk': jnp.zeros((EMBED_DIM,), jnp.float32), 'Wv': jax.random.normal(ks[5], (EMBED_DIM, EMBED_DIM), jnp.float32) * s, 'bv': jnp.zeros((EMBED_DIM,), jnp.float32), 'Wo': jax.random.normal(ks[6], (EMBED_DIM, EMBED_DIM), jnp.float32) * s, 'bo': jnp.zeros((EMBED_DIM,), jnp.float32), 'norm_weight': jnp.ones((EMBED_DIM,), jnp.float32), 'norm_gate': jnp.ones((EMBED_DIM,), jnp.float32)}
    _L0_attn_all = _L0_attn_setup()
    _L0_attn_in = {k: v for k, v in _L0_attn_all.items() if k in ('key', 'value', 'Wq', 'bq', 'Wk', 'bk', 'Wv', 'bv', 'Wo', 'bo', 'norm_weight', 'norm_gate')}
    del _L0_attn_all

    def _L0_xattn_setup():
        import jax, jax.numpy as jnp
        import numpy as np
        HEADS = 16
        D_MODEL = 128
        IMG_MODEL = 64
        D_K = D_MODEL // HEADS
        key = jax.random.key(seed)
        ks = jax.random.split(key, 12)
        B, LQ, LKV = (8, 256, 128)
        s_dm = 1.0 / np.sqrt(D_MODEL)
        s_im = 1.0 / np.sqrt(IMG_MODEL)
        return {'q': jax.random.normal(ks[0], (B, LQ, D_MODEL), jnp.float32), 'k': jax.random.normal(ks[1], (B, LKV, IMG_MODEL), jnp.float32), 'v': jax.random.normal(ks[2], (B, LKV, IMG_MODEL), jnp.float32), 'Wq': jax.random.normal(ks[3], (D_MODEL, D_MODEL), jnp.float32) * s_dm, 'bq': jnp.zeros((D_MODEL,), jnp.float32), 'Wk': jax.random.normal(ks[4], (IMG_MODEL, D_MODEL), jnp.float32) * s_im, 'bk': jnp.zeros((D_MODEL,), jnp.float32), 'Wv': jax.random.normal(ks[5], (IMG_MODEL, D_MODEL), jnp.float32) * s_im, 'bv': jnp.zeros((D_MODEL,), jnp.float32), 'Wo': jax.random.normal(ks[6], (D_MODEL, D_MODEL), jnp.float32) * s_dm, 'bo': jnp.zeros((D_MODEL,), jnp.float32)}
    _L0_xattn_all = _L0_xattn_setup()
    _L0_xattn_in = {k: v for k, v in _L0_xattn_all.items() if k in ('Wq', 'bq', 'Wk', 'bk', 'Wv', 'bv', 'Wo', 'bo')}
    del _L0_xattn_all

    def _L0_ffn_setup():
        import jax, jax.numpy as jnp
        import numpy as np
        DIM = 128
        HIDDEN = 384
        SCALE = 1.0 / 127.0

        def _dequant(w_int, dtype):
            return w_int.astype(dtype) * jnp.asarray(SCALE, dtype)
        key = jax.random.key(seed)
        k_x, k_g, k_u, k_d = jax.random.split(key, 4)
        x = jax.random.normal(k_x, (4, 256, DIM), dtype=jnp.float32)
        w_gate = jax.random.randint(k_g, (HIDDEN, DIM), -127, 128, dtype=jnp.int32)
        w_up = jax.random.randint(k_u, (HIDDEN, DIM), -127, 128, dtype=jnp.int32)
        w_down = jax.random.randint(k_d, (DIM, HIDDEN), -127, 128, dtype=jnp.int32)
        return {'x': x, 'w_gate': w_gate, 'w_up': w_up, 'w_down': w_down}
    _L0_ffn_all = _L0_ffn_setup()
    _L0_ffn_in = {k: v for k, v in _L0_ffn_all.items() if k in ('w_gate', 'w_up', 'w_down')}
    del _L0_ffn_all

    def _L1_attn_setup():
        import jax, jax.numpy as jnp
        import numpy as np
        B, N, C, H = (2, 256, 128, 16)
        R1, R2 = (4, 8)
        HEAD_DIM = C // H
        SCALE = float((R1 * R2) ** (-0.5))
        key = jax.random.key(seed)
        ks = jax.random.split(key, 8)
        g = lambda k, shape, s: jax.random.normal(k, shape, jnp.float32) * s
        return {'x': g(ks[0], (B, N, C), 1.0), 'Wq1': g(ks[1], (H * R1, C), C ** (-0.5)), 'Wk1': g(ks[2], (H * R1, C), C ** (-0.5)), 'Wq2': g(ks[3], (H * R2, C), C ** (-0.5)), 'Wk2': g(ks[4], (H * R2, C), C ** (-0.5)), 'Wv': g(ks[5], (C, C), C ** (-0.5)), 'Wo': g(ks[6], (C, C), C ** (-0.5)), 'bo': jnp.zeros((C,), jnp.float32)}
    _L1_attn_all = _L1_attn_setup()
    _L1_attn_in = {k: v for k, v in _L1_attn_all.items() if k in ('Wq1', 'Wk1', 'Wq2', 'Wk2', 'Wv', 'Wo', 'bo')}
    del _L1_attn_all

    def _L1_xattn_setup():
        import jax, jax.numpy as jnp
        import numpy as np
        B, LQ, LK = (8, 256, 256)
        QD, KD, VD = (128, 64, 64)
        key = jax.random.key(seed)
        ks = jax.random.split(key, 9)
        s = 0.02
        return {'query': jax.random.normal(ks[0], (B, LQ, QD), jnp.float32), 'key': jax.random.normal(ks[1], (B, LK, KD), jnp.float32), 'value': jax.random.normal(ks[2], (B, LK, VD), jnp.float32), 'Wq': jax.random.normal(ks[3], (QD, QD), jnp.float32) * s, 'bq': jnp.zeros((QD,), jnp.float32), 'Wk': jax.random.normal(ks[4], (KD, QD), jnp.float32) * s, 'bk': jnp.zeros((QD,), jnp.float32), 'Wv': jax.random.normal(ks[5], (VD, QD), jnp.float32) * s, 'bv': jnp.zeros((QD,), jnp.float32)}
    _L1_xattn_all = _L1_xattn_setup()
    _L1_xattn_in = {k: v for k, v in _L1_xattn_all.items() if k in ('Wq', 'bq', 'Wk', 'bk', 'Wv', 'bv')}
    del _L1_xattn_all

    def _L1_ffn_setup():
        import jax, jax.numpy as jnp
        import numpy as np
        import math
        N_EMBD = 128
        HIDDEN = 4 * N_EMBD
        N_EXPERTS = 8
        TOP_K = 2
        B, T = (4, 256)

        def new_gelu(x):
            c = math.sqrt(2.0 / math.pi)
            return 0.5 * x * (1.0 + jnp.tanh(c * (x + 0.044715 * x * x * x)))

        def _moe_forward(x, Wfc_s, bfc_s, Wproj_s, bproj_s, Wr, Wfc, bfc, Wproj, bproj):
            Bb, Tt, C = x.shape
            xf = x.reshape(Bb * Tt, C)
            N = Bb * Tt
            shared = new_gelu(xf @ Wfc_s + bfc_s) @ Wproj_s + bproj_s
            logits = xf @ Wr
            probs = jax.nn.softmax(logits, axis=-1)
            topk_p, topk_i = jax.lax.top_k(probs, TOP_K)
            topk_p = topk_p / jnp.sum(topk_p, axis=-1, keepdims=True)
            gate = jnp.zeros((N, N_EXPERTS), dtype=xf.dtype)
            gate = gate.at[jnp.arange(N)[:, None], topk_i].add(topk_p)
            routed = jnp.zeros_like(xf)
            for e in range(N_EXPERTS):
                h = new_gelu(xf @ Wfc[e] + bfc[e]) @ Wproj[e] + bproj[e]
                routed = routed + h * gate[:, e:e + 1]
            return (shared + routed).reshape(Bb, Tt, C)
        key = jax.random.key(seed)
        ks = jax.random.split(key, 10)
        s = 0.02
        return {'x': jax.random.normal(ks[0], (B, T, N_EMBD), dtype=jnp.float32), 'Wfc_s': jax.random.normal(ks[1], (N_EMBD, HIDDEN), dtype=jnp.float32) * s, 'bfc_s': jnp.zeros((HIDDEN,), dtype=jnp.float32), 'Wproj_s': jax.random.normal(ks[2], (HIDDEN, N_EMBD), dtype=jnp.float32) * s, 'bproj_s': jnp.zeros((N_EMBD,), dtype=jnp.float32), 'Wr': jax.random.normal(ks[3], (N_EMBD, N_EXPERTS), dtype=jnp.float32) * s, 'Wfc': jax.random.normal(ks[4], (N_EXPERTS, N_EMBD, HIDDEN), dtype=jnp.float32) * s, 'bfc': jnp.zeros((N_EXPERTS, HIDDEN), dtype=jnp.float32), 'Wproj': jax.random.normal(ks[5], (N_EXPERTS, HIDDEN, N_EMBD), dtype=jnp.float32) * s, 'bproj': jnp.zeros((N_EXPERTS, N_EMBD), dtype=jnp.float32)}
    _L1_ffn_all = _L1_ffn_setup()
    _L1_ffn_in = {k: v for k, v in _L1_ffn_all.items() if k in ('Wfc_s', 'bfc_s', 'Wproj_s', 'bproj_s', 'Wr', 'Wfc', 'bfc', 'Wproj', 'bproj')}
    del _L1_ffn_all

    def _L2_attn_setup():
        import jax, jax.numpy as jnp
        import numpy as np
        import math
        B, T, C, NH = (4, 256, 128, 16)
        HS = C // NH

        def rope_cache(dim, max_pos):
            half = dim // 2
            inv_freq = 1.0 / 10000.0 ** (jnp.arange(half, dtype=jnp.float32) * 2.0 / dim)
            ang = jnp.arange(max_pos, dtype=jnp.float32)[:, None] * inv_freq[None, :]
            return (jnp.cos(ang), jnp.sin(ang))

        def apply_rope(x, cos, sin):
            x0 = x[..., 0::2]
            x1 = x[..., 1::2]
            c = cos[None, None, :, :]
            s = sin[None, None, :, :]
            r0 = x0 * c - x1 * s
            r1 = x0 * s + x1 * c
            return jnp.stack([r0, r1], axis=-1).reshape(x.shape)
        key = jax.random.key(seed)
        ks = jax.random.split(key, 5)
        sc = 1.0 / math.sqrt(C)
        return {'x': jax.random.normal(ks[0], (B, T, C), jnp.float32), 'Wq': jax.random.normal(ks[1], (C, C), jnp.float32) * sc, 'bq': jnp.zeros((C,), jnp.float32), 'Wk': jax.random.normal(ks[2], (C, C), jnp.float32) * sc, 'bk': jnp.zeros((C,), jnp.float32), 'Wv': jax.random.normal(ks[3], (C, C), jnp.float32) * sc, 'bv': jnp.zeros((C,), jnp.float32), 'Wp': jax.random.normal(ks[4], (C, C), jnp.float32) * sc, 'bp': jnp.zeros((C,), jnp.float32)}
    _L2_attn_all = _L2_attn_setup()
    _L2_attn_in = {k: v for k, v in _L2_attn_all.items() if k in ('Wq', 'bq', 'Wk', 'bk', 'Wv', 'bv', 'Wp', 'bp')}
    del _L2_attn_all

    def _L2_xattn_setup():
        import jax, jax.numpy as jnp
        import numpy as np
        H, D, C1, C2, S, M, B, W = (16, 32, 128, 64, 256, 64, 2, 4)

        def _ln(x, g, b):
            m = jnp.mean(x, -1, keepdims=True)
            v = jnp.var(x, -1, keepdims=True)
            return (x - m) * jax.lax.rsqrt(v + 1e-05) * g + b

        def _mha(x, y, wq, wk, wv, li1_w, li1_b, lnx_g, lnx_b, lny_g, lny_b, ln3_g, ln3_b, li2_w, li2_b, li3_w, li3_b, causal):
            xn = _ln(x, lnx_g, lnx_b)
            yn = _ln(y, lny_g, lny_b)
            q = jnp.einsum('bsc,hcd->bhsd', xn, wq)
            k = jnp.einsum('btc,hcd->bhtd', yn, wk)
            v = jnp.einsum('btc,hcd->bhtd', yn, wv)
            a = jax.nn.softmax(jnp.einsum('bhsd,bhtd->bhst', q, k) * D ** (-0.5), axis=-1)
            if causal:
                s, t = (a.shape[-2], a.shape[-1])
                mask = (jnp.arange(t)[None, :] > jnp.arange(s)[:, None]).astype(a.dtype)
                a = a * mask
            o = jnp.einsum('bhst,bhtd->bhsd', a, v)
            o = o.transpose(0, 2, 1, 3).reshape(x.shape[0], x.shape[1], H * D)
            x_out = x + o @ li1_w + li1_b
            h = jax.nn.gelu(_ln(x_out, ln3_g, ln3_b) @ li2_w + li2_b, approximate=False)
            return x_out + h @ li3_w + li3_b
        key = jax.random.key(seed)
        ks = iter(jax.random.split(key, 64))

        def w(shape, scale=0.02):
            return jax.random.normal(next(ks), shape, jnp.float32) * scale
        inp = {'xx': jax.random.normal(next(ks), (B, S, C1), jnp.float32), 'ee': jax.random.normal(next(ks), (B, M, C2), jnp.float32), 'ln1_g': jnp.ones(C1, jnp.float32), 'ln1_b': jnp.zeros(C1, jnp.float32), 'ln2_g': jnp.ones(C1, jnp.float32), 'ln2_b': jnp.zeros(C1, jnp.float32)}
        for pfx, cy in (('a1', C1), ('a2', C2)):
            inp[pfx + '_wq'] = w((H, C1, D))
            inp[pfx + '_wk'] = w((H, cy, D))
            inp[pfx + '_wv'] = w((H, cy, D))
            inp[pfx + '_li1_w'] = w((H * D, C1))
            inp[pfx + '_li1_b'] = jnp.zeros(C1, jnp.float32)
            inp[pfx + '_lnx_g'] = jnp.ones(C1, jnp.float32)
            inp[pfx + '_lnx_b'] = jnp.zeros(C1, jnp.float32)
            inp[pfx + '_lny_g'] = jnp.ones(cy, jnp.float32)
            inp[pfx + '_lny_b'] = jnp.zeros(cy, jnp.float32)
            inp[pfx + '_ln3_g'] = jnp.ones(C1, jnp.float32)
            inp[pfx + '_ln3_b'] = jnp.zeros(C1, jnp.float32)
            inp[pfx + '_li2_w'] = w((C1, C1 * W))
            inp[pfx + '_li2_b'] = jnp.zeros(C1 * W, jnp.float32)
            inp[pfx + '_li3_w'] = w((C1 * W, C1))
            inp[pfx + '_li3_b'] = jnp.zeros(C1, jnp.float32)
        inp['training'] = 0
        return inp
    _L2_xattn_all = _L2_xattn_setup()
    _L2_xattn_in = {k: v for k, v in _L2_xattn_all.items() if k in ('ln1_g', 'ln1_b', 'ln2_g', 'ln2_b', 'a1_wq', 'a1_wk', 'a1_wv', 'a1_li1_w', 'a1_li1_b', 'a1_lnx_g', 'a1_lnx_b', 'a1_lny_g', 'a1_lny_b', 'a1_ln3_g', 'a1_ln3_b', 'a1_li2_w', 'a1_li2_b', 'a1_li3_w', 'a1_li3_b', 'a2_wq', 'a2_wk', 'a2_wv', 'a2_li1_w', 'a2_li1_b', 'a2_lnx_g', 'a2_lnx_b', 'a2_lny_g', 'a2_lny_b', 'a2_ln3_g', 'a2_ln3_b', 'a2_li2_w', 'a2_li2_b', 'a2_li3_w', 'a2_li3_b')}
    del _L2_xattn_all

    def _L2_ffn_setup():
        import jax, jax.numpy as jnp
        import numpy as np
        DIM = 128
        MOE_HID = 64
        SHARED_HID = 256
        N_EXPERTS = 16
        TOP_K = 2
        NORM_TOPK_PROB = True
        key = jax.random.key(seed)
        ks = jax.random.split(key, 9)
        s = 0.02
        x = jax.random.normal(ks[0], (2, 128, DIM), dtype=jnp.float32)
        Wg = jax.random.normal(ks[1], (N_EXPERTS, DIM), dtype=jnp.float32) * s
        We_gate = jax.random.normal(ks[2], (N_EXPERTS, MOE_HID, DIM), dtype=jnp.float32) * s
        We_up = jax.random.normal(ks[3], (N_EXPERTS, MOE_HID, DIM), dtype=jnp.float32) * s
        We_down = jax.random.normal(ks[4], (N_EXPERTS, DIM, MOE_HID), dtype=jnp.float32) * s
        Ws_gate = jax.random.normal(ks[5], (SHARED_HID, DIM), dtype=jnp.float32) * s
        Ws_up = jax.random.normal(ks[6], (SHARED_HID, DIM), dtype=jnp.float32) * s
        Ws_down = jax.random.normal(ks[7], (DIM, SHARED_HID), dtype=jnp.float32) * s
        Wsg = jax.random.normal(ks[8], (1, DIM), dtype=jnp.float32) * s
        return {'x': x, 'Wg': Wg, 'We_gate': We_gate, 'We_up': We_up, 'We_down': We_down, 'Ws_gate': Ws_gate, 'Ws_up': Ws_up, 'Ws_down': Ws_down, 'Wsg': Wsg}
    _L2_ffn_all = _L2_ffn_setup()
    _L2_ffn_in = {k: v for k, v in _L2_ffn_all.items() if k in ('Wg', 'We_gate', 'We_up', 'We_down', 'Ws_gate', 'Ws_up', 'Ws_down', 'Wsg')}
    del _L2_ffn_all

    def _L3_attn_setup():
        import jax, jax.numpy as jnp
        import numpy as np
        H = 16
        G = 16
        R = 4
        WIN = 64
        NEG = -1000000000.0
        key = jax.random.key(seed)
        ks = jax.random.split(key, 9)
        dm, D = (128, 128 // H)
        s = 0.02
        return {'x': jax.random.normal(ks[0], (1, 256, dm), dtype=jnp.float32), 'Wq': jax.random.normal(ks[1], (dm, dm), dtype=jnp.float32) * s, 'Wk': jax.random.normal(ks[2], (dm, dm), dtype=jnp.float32) * s, 'Wv': jax.random.normal(ks[3], (dm, dm), dtype=jnp.float32) * s, 'Wo': jax.random.normal(ks[4], (dm, dm), dtype=jnp.float32) * s, 'Wck': jax.random.normal(ks[5], (G * D, D), dtype=jnp.float32) * s, 'Wcv': jax.random.normal(ks[6], (G * D, D), dtype=jnp.float32) * s, 'Wg': jax.random.normal(ks[7], (D, 3), dtype=jnp.float32) * s, 'bg': jnp.zeros((3,), dtype=jnp.float32)}
    _L3_attn_all = _L3_attn_setup()
    _L3_attn_in = {k: v for k, v in _L3_attn_all.items() if k in ('Wq', 'Wk', 'Wv', 'Wo', 'Wck', 'Wcv', 'Wg', 'bg')}
    del _L3_attn_all

    def _L3_xattn_setup():
        import jax, jax.numpy as jnp
        import numpy as np
        DIM = 128
        LATENT_DIM = 64
        NUM_HEADS = 16
        HEAD_DIM = DIM // NUM_HEADS
        SCALE = HEAD_DIM ** (-0.5)
        key = jax.random.key(seed)
        k1, k2, k3, k4, k5 = jax.random.split(key, 5)
        B, xN, zN = (2, 256, 256)
        x = jax.random.normal(k1, (B, xN, DIM), dtype=jnp.float32)
        z = jax.random.normal(k2, (B, zN, LATENT_DIM), dtype=jnp.float32)
        Wq = jax.random.normal(k3, (DIM, DIM), dtype=jnp.float32) * DIM ** (-0.5)
        Wkv = jax.random.normal(k4, (2 * DIM, LATENT_DIM), dtype=jnp.float32) * LATENT_DIM ** (-0.5)
        Wo = jax.random.normal(k5, (DIM, DIM), dtype=jnp.float32) * DIM ** (-0.5)
        return {'x': x, 'z': z, 'Wq': Wq, 'Wkv': Wkv, 'Wo': Wo}
    _L3_xattn_all = _L3_xattn_setup()
    _L3_xattn_in = {k: v for k, v in _L3_xattn_all.items() if k in ('Wq', 'Wkv', 'Wo')}
    del _L3_xattn_all

    def _L3_ffn_setup():
        import jax, jax.numpy as jnp
        import numpy as np
        B, S, K, N = (8, 1024, 128, 128)
        key = jax.random.key(seed)
        k1, k2, k3, k4 = jax.random.split(key, 4)
        x = jax.random.normal(k1, (B, S, K), dtype=jnp.float32)
        CB = jnp.clip(jnp.round(jax.random.normal(k2, (N, K), dtype=jnp.float32) * 42.0), -127.0, 127.0)
        SCB = jax.random.uniform(k3, (N,), dtype=jnp.float32, minval=0.5, maxval=2.0)
        bias = jax.random.normal(k4, (N,), dtype=jnp.float32) * 0.02
        return {'x': x, 'CB': CB, 'SCB': SCB, 'bias': bias}
    _L3_ffn_all = _L3_ffn_setup()
    _L3_ffn_in = {k: v for k, v in _L3_ffn_all.items() if k in ('CB', 'SCB', 'bias')}
    del _L3_ffn_all
    return {'x': x, 'ctx_512': ctx_512, 'L0_attn_key': _L0_attn_in['key'], 'L0_attn_value': _L0_attn_in['value'], 'L0_attn_Wq': _L0_attn_in['Wq'], 'L0_attn_bq': _L0_attn_in['bq'], 'L0_attn_Wk': _L0_attn_in['Wk'], 'L0_attn_bk': _L0_attn_in['bk'], 'L0_attn_Wv': _L0_attn_in['Wv'], 'L0_attn_bv': _L0_attn_in['bv'], 'L0_attn_Wo': _L0_attn_in['Wo'], 'L0_attn_bo': _L0_attn_in['bo'], 'L0_attn_norm_weight': _L0_attn_in['norm_weight'], 'L0_attn_norm_gate': _L0_attn_in['norm_gate'], 'L0_xattn_Wq': _L0_xattn_in['Wq'], 'L0_xattn_bq': _L0_xattn_in['bq'], 'L0_xattn_Wk': _L0_xattn_in['Wk'], 'L0_xattn_bk': _L0_xattn_in['bk'], 'L0_xattn_Wv': _L0_xattn_in['Wv'], 'L0_xattn_bv': _L0_xattn_in['bv'], 'L0_xattn_Wo': _L0_xattn_in['Wo'], 'L0_xattn_bo': _L0_xattn_in['bo'], 'L0_ffn_w_gate': _L0_ffn_in['w_gate'], 'L0_ffn_w_up': _L0_ffn_in['w_up'], 'L0_ffn_w_down': _L0_ffn_in['w_down'], 'L1_attn_Wq1': _L1_attn_in['Wq1'], 'L1_attn_Wk1': _L1_attn_in['Wk1'], 'L1_attn_Wq2': _L1_attn_in['Wq2'], 'L1_attn_Wk2': _L1_attn_in['Wk2'], 'L1_attn_Wv': _L1_attn_in['Wv'], 'L1_attn_Wo': _L1_attn_in['Wo'], 'L1_attn_bo': _L1_attn_in['bo'], 'L1_xattn_Wq': _L1_xattn_in['Wq'], 'L1_xattn_bq': _L1_xattn_in['bq'], 'L1_xattn_Wk': _L1_xattn_in['Wk'], 'L1_xattn_bk': _L1_xattn_in['bk'], 'L1_xattn_Wv': _L1_xattn_in['Wv'], 'L1_xattn_bv': _L1_xattn_in['bv'], 'L1_ffn_Wfc_s': _L1_ffn_in['Wfc_s'], 'L1_ffn_bfc_s': _L1_ffn_in['bfc_s'], 'L1_ffn_Wproj_s': _L1_ffn_in['Wproj_s'], 'L1_ffn_bproj_s': _L1_ffn_in['bproj_s'], 'L1_ffn_Wr': _L1_ffn_in['Wr'], 'L1_ffn_Wfc': _L1_ffn_in['Wfc'], 'L1_ffn_bfc': _L1_ffn_in['bfc'], 'L1_ffn_Wproj': _L1_ffn_in['Wproj'], 'L1_ffn_bproj': _L1_ffn_in['bproj'], 'L2_attn_Wq': _L2_attn_in['Wq'], 'L2_attn_bq': _L2_attn_in['bq'], 'L2_attn_Wk': _L2_attn_in['Wk'], 'L2_attn_bk': _L2_attn_in['bk'], 'L2_attn_Wv': _L2_attn_in['Wv'], 'L2_attn_bv': _L2_attn_in['bv'], 'L2_attn_Wp': _L2_attn_in['Wp'], 'L2_attn_bp': _L2_attn_in['bp'], 'L2_xattn_ln1_g': _L2_xattn_in['ln1_g'], 'L2_xattn_ln1_b': _L2_xattn_in['ln1_b'], 'L2_xattn_ln2_g': _L2_xattn_in['ln2_g'], 'L2_xattn_ln2_b': _L2_xattn_in['ln2_b'], 'L2_xattn_a1_wq': _L2_xattn_in['a1_wq'], 'L2_xattn_a1_wk': _L2_xattn_in['a1_wk'], 'L2_xattn_a1_wv': _L2_xattn_in['a1_wv'], 'L2_xattn_a1_li1_w': _L2_xattn_in['a1_li1_w'], 'L2_xattn_a1_li1_b': _L2_xattn_in['a1_li1_b'], 'L2_xattn_a1_lnx_g': _L2_xattn_in['a1_lnx_g'], 'L2_xattn_a1_lnx_b': _L2_xattn_in['a1_lnx_b'], 'L2_xattn_a1_lny_g': _L2_xattn_in['a1_lny_g'], 'L2_xattn_a1_lny_b': _L2_xattn_in['a1_lny_b'], 'L2_xattn_a1_ln3_g': _L2_xattn_in['a1_ln3_g'], 'L2_xattn_a1_ln3_b': _L2_xattn_in['a1_ln3_b'], 'L2_xattn_a1_li2_w': _L2_xattn_in['a1_li2_w'], 'L2_xattn_a1_li2_b': _L2_xattn_in['a1_li2_b'], 'L2_xattn_a1_li3_w': _L2_xattn_in['a1_li3_w'], 'L2_xattn_a1_li3_b': _L2_xattn_in['a1_li3_b'], 'L2_xattn_a2_wq': _L2_xattn_in['a2_wq'], 'L2_xattn_a2_wk': _L2_xattn_in['a2_wk'], 'L2_xattn_a2_wv': _L2_xattn_in['a2_wv'], 'L2_xattn_a2_li1_w': _L2_xattn_in['a2_li1_w'], 'L2_xattn_a2_li1_b': _L2_xattn_in['a2_li1_b'], 'L2_xattn_a2_lnx_g': _L2_xattn_in['a2_lnx_g'], 'L2_xattn_a2_lnx_b': _L2_xattn_in['a2_lnx_b'], 'L2_xattn_a2_lny_g': _L2_xattn_in['a2_lny_g'], 'L2_xattn_a2_lny_b': _L2_xattn_in['a2_lny_b'], 'L2_xattn_a2_ln3_g': _L2_xattn_in['a2_ln3_g'], 'L2_xattn_a2_ln3_b': _L2_xattn_in['a2_ln3_b'], 'L2_xattn_a2_li2_w': _L2_xattn_in['a2_li2_w'], 'L2_xattn_a2_li2_b': _L2_xattn_in['a2_li2_b'], 'L2_xattn_a2_li3_w': _L2_xattn_in['a2_li3_w'], 'L2_xattn_a2_li3_b': _L2_xattn_in['a2_li3_b'], 'L2_ffn_Wg': _L2_ffn_in['Wg'], 'L2_ffn_We_gate': _L2_ffn_in['We_gate'], 'L2_ffn_We_up': _L2_ffn_in['We_up'], 'L2_ffn_We_down': _L2_ffn_in['We_down'], 'L2_ffn_Ws_gate': _L2_ffn_in['Ws_gate'], 'L2_ffn_Ws_up': _L2_ffn_in['Ws_up'], 'L2_ffn_Ws_down': _L2_ffn_in['Ws_down'], 'L2_ffn_Wsg': _L2_ffn_in['Wsg'], 'L3_attn_Wq': _L3_attn_in['Wq'], 'L3_attn_Wk': _L3_attn_in['Wk'], 'L3_attn_Wv': _L3_attn_in['Wv'], 'L3_attn_Wo': _L3_attn_in['Wo'], 'L3_attn_Wck': _L3_attn_in['Wck'], 'L3_attn_Wcv': _L3_attn_in['Wcv'], 'L3_attn_Wg': _L3_attn_in['Wg'], 'L3_attn_bg': _L3_attn_in['bg'], 'L3_xattn_Wq': _L3_xattn_in['Wq'], 'L3_xattn_Wkv': _L3_xattn_in['Wkv'], 'L3_xattn_Wo': _L3_xattn_in['Wo'], 'L3_ffn_CB': _L3_ffn_in['CB'], 'L3_ffn_SCB': _L3_ffn_in['SCB'], 'L3_ffn_bias': _L3_ffn_in['bias']}

def reference(x, ctx_512, L0_attn_key, L0_attn_value, L0_attn_Wq, L0_attn_bq, L0_attn_Wk, L0_attn_bk, L0_attn_Wv, L0_attn_bv, L0_attn_Wo, L0_attn_bo, L0_attn_norm_weight, L0_attn_norm_gate, L0_xattn_Wq, L0_xattn_bq, L0_xattn_Wk, L0_xattn_bk, L0_xattn_Wv, L0_xattn_bv, L0_xattn_Wo, L0_xattn_bo, L0_ffn_w_gate, L0_ffn_w_up, L0_ffn_w_down, L1_attn_Wq1, L1_attn_Wk1, L1_attn_Wq2, L1_attn_Wk2, L1_attn_Wv, L1_attn_Wo, L1_attn_bo, L1_xattn_Wq, L1_xattn_bq, L1_xattn_Wk, L1_xattn_bk, L1_xattn_Wv, L1_xattn_bv, L1_ffn_Wfc_s, L1_ffn_bfc_s, L1_ffn_Wproj_s, L1_ffn_bproj_s, L1_ffn_Wr, L1_ffn_Wfc, L1_ffn_bfc, L1_ffn_Wproj, L1_ffn_bproj, L2_attn_Wq, L2_attn_bq, L2_attn_Wk, L2_attn_bk, L2_attn_Wv, L2_attn_bv, L2_attn_Wp, L2_attn_bp, L2_xattn_ln1_g, L2_xattn_ln1_b, L2_xattn_ln2_g, L2_xattn_ln2_b, L2_xattn_a1_wq, L2_xattn_a1_wk, L2_xattn_a1_wv, L2_xattn_a1_li1_w, L2_xattn_a1_li1_b, L2_xattn_a1_lnx_g, L2_xattn_a1_lnx_b, L2_xattn_a1_lny_g, L2_xattn_a1_lny_b, L2_xattn_a1_ln3_g, L2_xattn_a1_ln3_b, L2_xattn_a1_li2_w, L2_xattn_a1_li2_b, L2_xattn_a1_li3_w, L2_xattn_a1_li3_b, L2_xattn_a2_wq, L2_xattn_a2_wk, L2_xattn_a2_wv, L2_xattn_a2_li1_w, L2_xattn_a2_li1_b, L2_xattn_a2_lnx_g, L2_xattn_a2_lnx_b, L2_xattn_a2_lny_g, L2_xattn_a2_lny_b, L2_xattn_a2_ln3_g, L2_xattn_a2_ln3_b, L2_xattn_a2_li2_w, L2_xattn_a2_li2_b, L2_xattn_a2_li3_w, L2_xattn_a2_li3_b, L2_ffn_Wg, L2_ffn_We_gate, L2_ffn_We_up, L2_ffn_We_down, L2_ffn_Ws_gate, L2_ffn_Ws_up, L2_ffn_Ws_down, L2_ffn_Wsg, L3_attn_Wq, L3_attn_Wk, L3_attn_Wv, L3_attn_Wo, L3_attn_Wck, L3_attn_Wcv, L3_attn_Wg, L3_attn_bg, L3_xattn_Wq, L3_xattn_Wkv, L3_xattn_Wo, L3_ffn_CB, L3_ffn_SCB, L3_ffn_bias):
    import jax
    import jax.numpy as jnp

    def _L0_attn_ref(query, key, value, Wq, bq, Wk, bk, Wv, bv, Wo, bo, norm_weight, norm_gate):
        import jax, jax.numpy as jnp
        import numpy as np
        EMBED_DIM = 128
        NUM_HEADS = 16
        HEAD_DIM = EMBED_DIM // NUM_HEADS
        L, B = (256, 2)
        EPS = 1e-08

        def gated_rms_norm(x, weight, gate):
            rms = jnp.linalg.norm(x, axis=-1, keepdims=True) * EMBED_DIM ** (-0.5)
            x_normed = x / (rms + EPS)
            return weight * x_normed * jax.nn.sigmoid(gate * x)
        Lq, Bq, E = query.shape
        H, hd = (NUM_HEADS, HEAD_DIM)
        scaling = hd ** (-0.5)
        q = (query @ Wq.T + bq) * scaling
        k = key @ Wk.T + bk
        v = value @ Wv.T + bv
        q = q.reshape(Lq, Bq, H, hd).transpose(1, 2, 0, 3)
        k = k.reshape(-1, Bq, H, hd).transpose(1, 2, 0, 3)
        v = v.reshape(-1, Bq, H, hd).transpose(1, 2, 0, 3)
        logits = jnp.einsum('bhld,bhsd->bhls', q, k)
        prob = jax.nn.relu(logits)
        out = jnp.einsum('bhls,bhsd->bhld', prob, v)
        out = out.transpose(2, 0, 1, 3).reshape(Lq, Bq, E)
        out = gated_rms_norm(out, norm_weight, norm_gate)
        out = out @ Wo.T + bo
        return out

    def _L0_xattn_ref(q, k, v, Wq, bq, Wk, bk, Wv, bv, Wo, bo):
        import jax, jax.numpy as jnp
        import numpy as np
        HEADS = 16
        D_MODEL = 128
        IMG_MODEL = 64
        D_K = D_MODEL // HEADS
        B, LQ, _ = q.shape
        LKV = k.shape[1]
        qh = (q @ Wq + bq).reshape(B, LQ, HEADS, D_K).transpose(0, 2, 1, 3)
        kh = (k @ Wk + bk).reshape(B, LKV, HEADS, D_K).transpose(0, 2, 1, 3)
        vh = (v @ Wv + bv).reshape(B, LKV, HEADS, D_K).transpose(0, 2, 1, 3)
        scale = 1.0 / np.sqrt(D_K)
        scores = jnp.einsum('bhqd,bhkd->bhqk', qh, kh) * scale
        attn = jax.nn.softmax(scores, axis=-1)
        out = jnp.einsum('bhqk,bhkd->bhqd', attn, vh)
        concat = out.transpose(0, 2, 1, 3).reshape(B, LQ, D_MODEL)
        return concat @ Wo + bo

    def _L0_ffn_ref(x, w_gate, w_up, w_down):
        import jax, jax.numpy as jnp
        import numpy as np
        DIM = 128
        HIDDEN = 384
        SCALE = 1.0 / 127.0

        def _dequant(w_int, dtype):
            return w_int.astype(dtype) * jnp.asarray(SCALE, dtype)
        wg = _dequant(w_gate, x.dtype)
        wu = _dequant(w_up, x.dtype)
        wd = _dequant(w_down, x.dtype)
        gate = jnp.einsum('bsd,hd->bsh', x, wg)
        up = jnp.einsum('bsd,hd->bsh', x, wu)
        h = jax.nn.silu(gate) * up
        return jnp.einsum('bsh,dh->bsd', h, wd)

    def _L1_attn_ref(x, Wq1, Wk1, Wq2, Wk2, Wv, Wo, bo):
        import jax, jax.numpy as jnp
        import numpy as np
        B, N, C, H = (2, 256, 128, 16)
        R1, R2 = (4, 8)
        HEAD_DIM = C // H
        SCALE = float((R1 * R2) ** (-0.5))
        b, n, c = x.shape
        q1 = (x @ Wq1.T).reshape(b, n, H, R1)
        k1 = (x @ Wk1.T).reshape(b, n, H, R1)
        q2 = (x @ Wq2.T).reshape(b, n, H, R2)
        k2 = (x @ Wk2.T).reshape(b, n, H, R2)
        v = (x @ Wv.T).reshape(b, n, H, HEAD_DIM)
        A1 = jnp.einsum('bnhr,bmhr->bhnm', q1, k1)
        A2 = jnp.einsum('bnhr,bmhr->bhnm', q2, k2)
        logits = A1 * A2 * SCALE
        causal = jnp.triu(jnp.ones((n, n), dtype=bool), 1)
        logits = jnp.where(causal[None, None], -jnp.inf, logits)
        attn = jax.nn.softmax(logits, axis=-1)
        out = jnp.einsum('bhnm,bmhd->bnhd', attn, v).reshape(b, n, c)
        return out @ Wo.T + bo

    def _L1_xattn_ref(query, key, value, Wq, bq, Wk, bk, Wv, bv):
        import jax, jax.numpy as jnp
        import numpy as np
        B, LQ, LK = (8, 256, 256)
        QD, KD, VD = (128, 64, 64)
        q = jnp.einsum('bld,de->ble', query, Wq) + bq
        k = jnp.einsum('bld,de->ble', key, Wk) + bk
        v = jnp.einsum('bld,de->ble', value, Wv) + bv
        scores = jnp.einsum('bqe,bke->bqk', q, k)
        attn = jax.nn.softmax(scores, axis=-1)
        out = jnp.einsum('bqk,bke->bqe', attn, v)
        return out

    def _L1_ffn_ref(x, Wfc_s, bfc_s, Wproj_s, bproj_s, Wr, Wfc, bfc, Wproj, bproj):
        import jax, jax.numpy as jnp
        import numpy as np
        import math
        N_EMBD = 128
        HIDDEN = 4 * N_EMBD
        N_EXPERTS = 8
        TOP_K = 2
        B, T = (4, 256)

        def new_gelu(x):
            c = math.sqrt(2.0 / math.pi)
            return 0.5 * x * (1.0 + jnp.tanh(c * (x + 0.044715 * x * x * x)))

        def _moe_forward(x, Wfc_s, bfc_s, Wproj_s, bproj_s, Wr, Wfc, bfc, Wproj, bproj):
            Bb, Tt, C = x.shape
            xf = x.reshape(Bb * Tt, C)
            N = Bb * Tt
            shared = new_gelu(xf @ Wfc_s + bfc_s) @ Wproj_s + bproj_s
            logits = xf @ Wr
            probs = jax.nn.softmax(logits, axis=-1)
            topk_p, topk_i = jax.lax.top_k(probs, TOP_K)
            topk_p = topk_p / jnp.sum(topk_p, axis=-1, keepdims=True)
            gate = jnp.zeros((N, N_EXPERTS), dtype=xf.dtype)
            gate = gate.at[jnp.arange(N)[:, None], topk_i].add(topk_p)
            routed = jnp.zeros_like(xf)
            for e in range(N_EXPERTS):
                h = new_gelu(xf @ Wfc[e] + bfc[e]) @ Wproj[e] + bproj[e]
                routed = routed + h * gate[:, e:e + 1]
            return (shared + routed).reshape(Bb, Tt, C)
        return _moe_forward(x, Wfc_s, bfc_s, Wproj_s, bproj_s, Wr, Wfc, bfc, Wproj, bproj)

    def _L2_attn_ref(x, Wq, bq, Wk, bk, Wv, bv, Wp, bp):
        import jax, jax.numpy as jnp
        import numpy as np
        import math
        B, T, C, NH = (4, 256, 128, 16)
        HS = C // NH

        def rope_cache(dim, max_pos):
            half = dim // 2
            inv_freq = 1.0 / 10000.0 ** (jnp.arange(half, dtype=jnp.float32) * 2.0 / dim)
            ang = jnp.arange(max_pos, dtype=jnp.float32)[:, None] * inv_freq[None, :]
            return (jnp.cos(ang), jnp.sin(ang))

        def apply_rope(x, cos, sin):
            x0 = x[..., 0::2]
            x1 = x[..., 1::2]
            c = cos[None, None, :, :]
            s = sin[None, None, :, :]
            r0 = x0 * c - x1 * s
            r1 = x0 * s + x1 * c
            return jnp.stack([r0, r1], axis=-1).reshape(x.shape)
        Bx, Tx, Cx = x.shape

        def split_heads(y):
            return y.reshape(Bx, Tx, NH, HS).transpose(0, 2, 1, 3)
        q = split_heads(x @ Wq + bq)
        k = split_heads(x @ Wk + bk)
        v = split_heads(x @ Wv + bv)
        cos, sin = rope_cache(HS, Tx)
        q = apply_rope(q, cos, sin)
        k = apply_rope(k, cos, sin)
        att = jnp.einsum('bhqd,bhkd->bhqk', q, k) * (1.0 / math.sqrt(HS))
        causal = jnp.tril(jnp.ones((Tx, Tx), bool))
        att = jnp.where(causal[None, None, :, :], att, jnp.float32(-10000000000.0))
        att = jax.nn.softmax(att, axis=-1)
        y = jnp.einsum('bhqk,bhkd->bhqd', att, v)
        y = y.transpose(0, 2, 1, 3).reshape(Bx, Tx, Cx)
        return y @ Wp + bp

    def _L2_xattn_ref(xx, ee, ln1_g, ln1_b, ln2_g, ln2_b, a1_wq, a1_wk, a1_wv, a1_li1_w, a1_li1_b, a1_lnx_g, a1_lnx_b, a1_lny_g, a1_lny_b, a1_ln3_g, a1_ln3_b, a1_li2_w, a1_li2_b, a1_li3_w, a1_li3_b, a2_wq, a2_wk, a2_wv, a2_li1_w, a2_li1_b, a2_lnx_g, a2_lnx_b, a2_lny_g, a2_lny_b, a2_ln3_g, a2_ln3_b, a2_li2_w, a2_li2_b, a2_li3_w, a2_li3_b, training):
        import jax, jax.numpy as jnp
        import numpy as np
        H, D, C1, C2, S, M, B, W = (16, 32, 128, 64, 256, 64, 2, 4)

        def _ln(x, g, b):
            m = jnp.mean(x, -1, keepdims=True)
            v = jnp.var(x, -1, keepdims=True)
            return (x - m) * jax.lax.rsqrt(v + 1e-05) * g + b

        def _mha(x, y, wq, wk, wv, li1_w, li1_b, lnx_g, lnx_b, lny_g, lny_b, ln3_g, ln3_b, li2_w, li2_b, li3_w, li3_b, causal):
            xn = _ln(x, lnx_g, lnx_b)
            yn = _ln(y, lny_g, lny_b)
            q = jnp.einsum('bsc,hcd->bhsd', xn, wq)
            k = jnp.einsum('btc,hcd->bhtd', yn, wk)
            v = jnp.einsum('btc,hcd->bhtd', yn, wv)
            a = jax.nn.softmax(jnp.einsum('bhsd,bhtd->bhst', q, k) * D ** (-0.5), axis=-1)
            if causal:
                s, t = (a.shape[-2], a.shape[-1])
                mask = (jnp.arange(t)[None, :] > jnp.arange(s)[:, None]).astype(a.dtype)
                a = a * mask
            o = jnp.einsum('bhst,bhtd->bhsd', a, v)
            o = o.transpose(0, 2, 1, 3).reshape(x.shape[0], x.shape[1], H * D)
            x_out = x + o @ li1_w + li1_b
            h = jax.nn.gelu(_ln(x_out, ln3_g, ln3_b) @ li2_w + li2_b, approximate=False)
            return x_out + h @ li3_w + li3_b
        x = _ln(xx, ln1_g, ln1_b)
        x = x + _mha(x, x, a1_wq, a1_wk, a1_wv, a1_li1_w, a1_li1_b, a1_lnx_g, a1_lnx_b, a1_lny_g, a1_lny_b, a1_ln3_g, a1_ln3_b, a1_li2_w, a1_li2_b, a1_li3_w, a1_li3_b, causal=True)
        x = _ln(x, ln2_g, ln2_b)
        return x + _mha(x, ee, a2_wq, a2_wk, a2_wv, a2_li1_w, a2_li1_b, a2_lnx_g, a2_lnx_b, a2_lny_g, a2_lny_b, a2_ln3_g, a2_ln3_b, a2_li2_w, a2_li2_b, a2_li3_w, a2_li3_b, causal=False)

    def _L2_ffn_ref(x, Wg, We_gate, We_up, We_down, Ws_gate, Ws_up, Ws_down, Wsg):
        import jax, jax.numpy as jnp
        import numpy as np
        DIM = 128
        MOE_HID = 64
        SHARED_HID = 256
        N_EXPERTS = 16
        TOP_K = 2
        NORM_TOPK_PROB = True
        B, S, D = x.shape
        xt = x.reshape(-1, D)
        gates = jax.nn.softmax(xt @ Wg.T, axis=-1)
        scores, inds = jax.lax.top_k(gates, TOP_K)
        if NORM_TOPK_PROB:
            scores = scores / jnp.sum(scores, axis=-1, keepdims=True)
        g = jnp.einsum('td,ehd->teh', xt, We_gate)
        u = jnp.einsum('td,ehd->teh', xt, We_up)
        h = jax.nn.silu(g) * u
        y_all = jnp.einsum('teh,edh->ted', h, We_down)
        y_sel = jnp.take_along_axis(y_all, inds[:, :, None], axis=1)
        y = jnp.sum(y_sel * scores[:, :, None], axis=1)
        shared = jax.nn.silu(xt @ Ws_gate.T) * (xt @ Ws_up.T) @ Ws_down.T
        y = y + jax.nn.sigmoid(xt @ Wsg.T) * shared
        return y.reshape(B, S, D)

    def _L3_attn_ref(x, Wq, Wk, Wv, Wo, Wck, Wcv, Wg, bg):
        import jax, jax.numpy as jnp
        import numpy as np
        H = 16
        G = 16
        R = 4
        WIN = 64
        NEG = -1000000000.0
        B, T, dm = x.shape
        D = dm // H
        scale = float(np.sqrt(D))

        def split_heads(y):
            return y.reshape(B, T, H, D).transpose(0, 2, 1, 3)
        q = split_heads(x @ Wq)
        k = split_heads(x @ Wk)
        v = split_heads(x @ Wv)
        pad = -T % G
        T_pad = T + pad
        k_pad = jnp.pad(k, ((0, 0), (0, 0), (0, pad), (0, 0)))
        v_pad = jnp.pad(v, ((0, 0), (0, 0), (0, pad), (0, 0)))
        nb = T_pad // G
        k_c = k_pad.reshape(B, H, nb, G * D) @ Wck
        v_c = v_pad.reshape(B, H, nb, G * D) @ Wcv
        pos = jnp.arange(T)
        blk_end = (jnp.arange(nb) + 1) * G
        c_ok = pos[:, None] >= blk_end[None, :]
        s_b = jnp.einsum('bhtd,bhnd->bhtn', q, k_c) / scale
        logits_c = jnp.where(c_ok, s_b, NEG)
        out_c = jnp.einsum('bhtn,bhnd->bhtd', jax.nn.softmax(logits_c, axis=-1), v_c)
        out_c = out_c * jnp.any(c_ok, axis=-1)[:, None].astype(out_c.dtype)
        r_eff = min(R, nb)
        _, top_idx = jax.lax.top_k(logits_c, r_eff)
        tok = (top_idx[..., None] * G + jnp.arange(G)).reshape(B, H, T, r_eff * G)
        tok = jnp.clip(tok, 0, T_pad - 1)
        bi = jnp.arange(B)[:, None, None, None]
        hi = jnp.arange(H)[None, :, None, None]
        k_s = k_pad[bi, hi, tok]
        v_s = v_pad[bi, hi, tok]
        allowed = tok <= pos[None, None, :, None]
        logits_s = jnp.where(allowed, jnp.einsum('bhtd,bhtnd->bhtn', q, k_s) / scale, NEG)
        out_s = jnp.einsum('bhtn,bhtnd->bhtd', jax.nn.softmax(logits_s, axis=-1), v_s)
        out_s = out_s * jnp.any(allowed, axis=-1)[..., None].astype(out_s.dtype)
        wmask = (jnp.abs(pos[:, None] - pos[None, :]) <= WIN // 2) & (pos[:, None] >= pos[None, :])
        logits_l = jnp.where(wmask, jnp.einsum('bhtd,bhsd->bhts', q, k) / scale, NEG)
        out_l = jnp.einsum('bhts,bhsd->bhtd', jax.nn.softmax(logits_l, axis=-1), v)
        gates = jax.nn.softmax(q.mean(axis=1) @ Wg + bg, axis=-1)

        def merge(o):
            return o.transpose(0, 2, 1, 3).reshape(B, T, dm)
        out = gates[..., 0:1] * merge(out_c) + gates[..., 1:2] * merge(out_s) + gates[..., 2:3] * merge(out_l)
        return out @ Wo

    def _L3_xattn_ref(x, z, Wq, Wkv, Wo):
        import jax, jax.numpy as jnp
        import numpy as np
        DIM = 128
        LATENT_DIM = 64
        NUM_HEADS = 16
        HEAD_DIM = DIM // NUM_HEADS
        SCALE = HEAD_DIM ** (-0.5)
        B, xN, _ = x.shape
        _, zN, _ = z.shape
        Q = (x @ Wq.T).reshape(B, xN, NUM_HEADS, HEAD_DIM)
        KV = (z @ Wkv.T).reshape(B, zN, 2, NUM_HEADS, HEAD_DIM)
        K = KV[:, :, 0]
        V = KV[:, :, 1]
        attn = jnp.einsum('bqhd,bkhd->bhqk', Q, K) * SCALE
        attn = jax.nn.softmax(attn, axis=-1)
        O = jnp.einsum('bhqk,bkhd->bqhd', attn, V).reshape(B, xN, DIM)
        return O @ Wo.T

    def _L3_ffn_ref(x, CB, SCB, bias):
        import jax, jax.numpy as jnp
        import numpy as np
        B, S, K, N = (8, 1024, 128, 128)
        out = jnp.einsum('bsk,nk->bsn', x, CB)
        out = out * (SCB * (1.0 / 127.0)) + bias
        return out
    x = _layernorm(x + _L0_attn_ref(x, L0_attn_key, L0_attn_value, L0_attn_Wq, L0_attn_bq, L0_attn_Wk, L0_attn_bk, L0_attn_Wv, L0_attn_bv, L0_attn_Wo, L0_attn_bo, L0_attn_norm_weight, L0_attn_norm_gate), axis=-1)
    x = _layernorm(x + _L0_xattn_ref(x, ctx_512, ctx_512, L0_xattn_Wq, L0_xattn_bq, L0_xattn_Wk, L0_xattn_bk, L0_xattn_Wv, L0_xattn_bv, L0_xattn_Wo, L0_xattn_bo), axis=-1)
    x = _layernorm(x + _L0_ffn_ref(x, L0_ffn_w_gate, L0_ffn_w_up, L0_ffn_w_down), axis=-1)
    x = _layernorm(x + _L1_attn_ref(x, L1_attn_Wq1, L1_attn_Wk1, L1_attn_Wq2, L1_attn_Wk2, L1_attn_Wv, L1_attn_Wo, L1_attn_bo), axis=-1)
    x = _layernorm(x + _L1_xattn_ref(x, ctx_512, ctx_512, L1_xattn_Wq, L1_xattn_bq, L1_xattn_Wk, L1_xattn_bk, L1_xattn_Wv, L1_xattn_bv), axis=-1)
    x = _layernorm(x + _L1_ffn_ref(x, L1_ffn_Wfc_s, L1_ffn_bfc_s, L1_ffn_Wproj_s, L1_ffn_bproj_s, L1_ffn_Wr, L1_ffn_Wfc, L1_ffn_bfc, L1_ffn_Wproj, L1_ffn_bproj), axis=-1)
    x = _layernorm(x + _L2_attn_ref(x, L2_attn_Wq, L2_attn_bq, L2_attn_Wk, L2_attn_bk, L2_attn_Wv, L2_attn_bv, L2_attn_Wp, L2_attn_bp), axis=-1)
    x = _layernorm(x + _L2_xattn_ref(x, ctx_512, L2_xattn_ln1_g, L2_xattn_ln1_b, L2_xattn_ln2_g, L2_xattn_ln2_b, L2_xattn_a1_wq, L2_xattn_a1_wk, L2_xattn_a1_wv, L2_xattn_a1_li1_w, L2_xattn_a1_li1_b, L2_xattn_a1_lnx_g, L2_xattn_a1_lnx_b, L2_xattn_a1_lny_g, L2_xattn_a1_lny_b, L2_xattn_a1_ln3_g, L2_xattn_a1_ln3_b, L2_xattn_a1_li2_w, L2_xattn_a1_li2_b, L2_xattn_a1_li3_w, L2_xattn_a1_li3_b, L2_xattn_a2_wq, L2_xattn_a2_wk, L2_xattn_a2_wv, L2_xattn_a2_li1_w, L2_xattn_a2_li1_b, L2_xattn_a2_lnx_g, L2_xattn_a2_lnx_b, L2_xattn_a2_lny_g, L2_xattn_a2_lny_b, L2_xattn_a2_ln3_g, L2_xattn_a2_ln3_b, L2_xattn_a2_li2_w, L2_xattn_a2_li2_b, L2_xattn_a2_li3_w, L2_xattn_a2_li3_b, 0), axis=-1)
    x = _layernorm(x + _L2_ffn_ref(x, L2_ffn_Wg, L2_ffn_We_gate, L2_ffn_We_up, L2_ffn_We_down, L2_ffn_Ws_gate, L2_ffn_Ws_up, L2_ffn_Ws_down, L2_ffn_Wsg), axis=-1)
    x = _layernorm(x + _L3_attn_ref(x, L3_attn_Wq, L3_attn_Wk, L3_attn_Wv, L3_attn_Wo, L3_attn_Wck, L3_attn_Wcv, L3_attn_Wg, L3_attn_bg), axis=-1)
    x = _layernorm(x + _L3_xattn_ref(x, ctx_512, L3_xattn_Wq, L3_xattn_Wkv, L3_xattn_Wo), axis=-1)
    x = _layernorm(x + _L3_ffn_ref(x, L3_ffn_CB, L3_ffn_SCB, L3_ffn_bias), axis=-1)
    return x

_drawn_inputs = setup_inputs


def setup_inputs(seed=0):
    import zlib

    import numpy as np

    out = dict(_drawn_inputs(seed))
    spreads = {'L0_attn_bq': (0.0, 0.1),
     'L0_attn_bk': (0.0, 0.1),
     'L0_attn_bv': (0.0, 0.1),
     'L0_attn_bo': (0.0, 0.1),
     'L0_attn_norm_weight': (1.0, 0.2),
     'L0_attn_norm_gate': (1.0, 0.2),
     'L0_xattn_bq': (0.0, 0.1),
     'L0_xattn_bk': (0.0, 2.0),
     'L0_xattn_bv': (0.0, 0.1),
     'L0_xattn_bo': (0.0, 0.1),
     'L1_attn_bo': (0.0, 0.1),
     'L1_xattn_bq': (0.0, 0.8),
     'L1_xattn_bk': (0.0, 2.0),
     'L1_xattn_bv': (0.0, 0.1),
     'L1_ffn_bfc_s': (0.0, 0.337),
     'L1_ffn_bproj_s': (0.0, 0.1),
     'L1_ffn_bfc': (0.0, 0.505),
     'L1_ffn_bproj': (0.0, 0.1),
     'L2_attn_bq': (0.0, 0.632),
     'L2_attn_bk': (0.0, 0.8),
     'L2_attn_bv': (0.0, 0.1),
     'L2_attn_bp': (0.0, 0.1),
     'L2_xattn_ln1_g': (1.0, 0.2),
     'L2_xattn_ln1_b': (0.0, 0.1),
     'L2_xattn_ln2_g': (1.0, 0.2),
     'L2_xattn_ln2_b': (0.0, 0.1),
     'L2_xattn_a1_li1_b': (0.0, 0.269),
     'L2_xattn_a1_lnx_g': (1.0, 0.6),
     'L2_xattn_a1_lnx_b': (0.0, 0.8),
     'L2_xattn_a1_lny_g': (1.0, 0.6),
     'L2_xattn_a1_lny_b': (0.0, 0.8),
     'L2_xattn_a1_ln3_g': (1.0, 0.6),
     'L2_xattn_a1_ln3_b': (0.0, 0.8),
     'L2_xattn_a1_li2_b': (0.0, 0.8),
     'L2_xattn_a1_li3_b': (0.0, 0.274),
     'L2_xattn_a2_li1_b': (0.0, 0.301),
     'L2_xattn_a2_lnx_g': (1.0, 0.6),
     'L2_xattn_a2_lnx_b': (0.0, 0.8),
     'L2_xattn_a2_lny_g': (1.0, 0.6),
     'L2_xattn_a2_lny_b': (0.0, 0.8),
     'L2_xattn_a2_ln3_g': (1.0, 0.6),
     'L2_xattn_a2_ln3_b': (0.0, 0.8),
     'L2_xattn_a2_li2_b': (0.0, 0.8),
     'L2_xattn_a2_li3_b': (0.0, 0.313),
     'L3_attn_bg': (0.0, 0.8)}
    factors = {'L1_xattn_Wq': 3.893,
     'L1_xattn_Wk': 3.527,
     'L2_xattn_a1_wq': 8.0,
     'L2_xattn_a1_wk': 8.0,
     'L2_xattn_a1_wv': 4.909,
     'L2_xattn_a1_li1_w': 4.933,
     'L2_xattn_a1_li2_w': 3.34,
     'L2_xattn_a1_li3_w': 3.062,
     'L2_xattn_a2_wq': 8.0,
     'L2_xattn_a2_wk': 8.0,
     'L2_xattn_a2_wv': 4.925,
     'L2_xattn_a2_li1_w': 4.865,
     'L2_xattn_a2_li2_w': 3.477,
     'L2_xattn_a2_li3_w': 3.231,
     'L2_ffn_Wg': 8.0,
     'L2_ffn_We_gate': 8.0,
     'L2_ffn_We_up': 8.0,
     'L2_ffn_We_down': 8.0,
     'L2_ffn_Ws_gate': 8.0,
     'L2_ffn_Ws_up': 8.0,
     'L2_ffn_Ws_down': 8.0,
     'L2_ffn_Wsg': 8.0,
     'L3_attn_Wq': 8.0,
     'L3_attn_Wk': 8.0,
     'L3_attn_Wv': 2.717,
     'L3_attn_Wo': 2.771,
     'L3_attn_Wck': 8.0,
     'L3_attn_Wcv': 8.0,
     'L3_attn_Wg': 37.608,
     'L3_ffn_bias': 8.0}
    for name, (base, spread) in spreads.items():
        noise = np.random.default_rng([zlib.crc32(name.encode()), seed]).standard_normal(out[name].shape)
        drawn = base * np.exp(spread * noise) if base else spread * noise
        out[name] = jnp.asarray(drawn.astype(out[name].dtype))
    for name, factor in factors.items():
        out[name] = (out[name] * factor).astype(out[name].dtype)
    return out
```

```python
from contextlib import ExitStack

import numpy as np

import concourse.bass as bass
from concourse import mybir

ALU = mybir.AluOpType
ACT = mybir.ActivationFunctionType
AX = mybir.AxisListType
F32 = mybir.dt.float32
BF16 = mybir.dt.bfloat16
I32 = mybir.dt.int32

SEQS, S, E, C = 64, 128, 128, 64
CTX = 77
HEADS = 16
LN_EPS = 1e-5
STAGES = ("relu_attn", "l0_xattn", "l0_ffn", "l1_attn", "l1_xattn", "l1_moe", "l2_attn", "l2_xattn",
          "l2_moe", "l3_attn", "l3_xattn", "l3_linear")


def tensors(ctx, nc, tag):
    def sb(name, shape, dt=F32):
        return ctx.enter_context(nc.sbuf_tensor(f"{tag}_{name}", shape, dt))

    def bank(name, shape, dt=F32):
        return ctx.enter_context(nc.psum_tensor(f"{tag}_{name}", shape, dt))

    def sems(names):
        return {n: ctx.enter_context(nc.semaphore(f"{tag}_{n}")) for n in names.split()}

    return sb, bank, sems


def clear(nc, sem):
    with nc.Block() as block:
        @block.gpsimd
        def _(pool):
            for s in sem.values():
                pool.sem_clear(s)


def over_slots(eng, slot, count):
    slot(0, 0)
    slot(1, 1)
    with eng.Fori(1, count // 2 - 1) as i:
        slot(i * 2, 0)
        slot(i * 2 + 1, 1)
    slot(count - 2, 0)
    slot(count - 1, 1)


def within(n, ahead, count):
    return not isinstance(n, int) or 0 <= n + ahead < count


def reach(eng, sem, value):
    if not isinstance(value, int) or value > 0:
        eng.wait_ge(sem, value)


def wait_alone(eng, sem, value, passed):
    reach(eng, sem, value)
    eng.sem_inc(passed, 1)


def load_all(sp, pairs, sem):
    for dst, src in pairs:
        sp.dma_start(dst, src).then_inc(sem, 16)


def copy_bcast(ap, n):
    return ap.unsqueeze(2).broadcast_to([ap.shape[0], ap.shape[1], n])


def head_attention(nc, d, keep, tag, head_dim, scale, *, cross=False, q_bias=False, v_bias=False,
                   out_bias=True, causal=False, future_only=False, low_rank=False, rope=False, src=None,
                   affine=None, dst="norm", count=None):
    count = SEQS if count is None else count
    keys = CTX if cross else S
    hd = HEADS * head_dim
    in_k = C if cross else E
    k_parts = 2 if low_rank or rope else 1
    q_parts = 2 if rope else 1
    rows = 12 if low_rank else head_dim
    x, ident = keep["x"], keep["ident"]
    src = x if src is None else src
    o_chunks = hd // E
    ctx_copy = "ctxn" in keep and cross and affine is not None
    with ExitStack() as ctx:
        sb, bank, sems = tensors(ctx, nc, tag)
        wq = [sb(f"wq{i}", [E, 4, E]) for i in range(q_parts)]
        wk = [sb(f"wk{i}", [in_k, 4, E]) for i in range(k_parts)]
        wv = sb("wv", [in_k, hd])
        wo = sb("wo", [E, o_chunks, E])
        bias = sb("bias", [S, E])
        loads = [(wv[:], d[tag + "_wv"]), (wo[:], d[tag + "_wo"])]
        loads += [(wq[i][:], d[f"{tag}_wq{i}"]) for i in range(q_parts)]
        loads += [(wk[i][:], d[f"{tag}_wk{i}"]) for i in range(k_parts)]
        if out_bias:
            loads += [(bias[:], d[tag + "_bo"])]
        if rope:
            rb = [[sb(f"rb{t}{i}", [E, 4]) for i in range(2)] for t in "qk"]
            tables = [[sb(f"{n}{t}", [E, S]) for n in ("cos", "sin")] for t in "qk"]
            rotated = [sb(f"rotated{t}", [E, 4, S]) for t in "qk"]
            terms = [[sb(f"term{t}{i}", [E, 4, S]) for i in range(2)] for t in "qk"]
            for t in range(2):
                loads += [(rb[t][i][:], d[f"{tag}_b{'qk'[t]}{i}"]) for i in range(2)]
                loads += [(tables[t][i][:], d[("cos", "sin")[i]]) for i in range(2)]
        elif q_bias:
            qb, kb = sb("qb", [E, 4]), sb("kb", [E, 4])
            qbs = sb("qbs", [E, 4])
            loads += [(qb[:], d[tag + "_bq"]), (kb[:], d[tag + "_bk"])]
        if v_bias:
            vb = sb("vb", [E, S])
            loads += [(vb[:], d[tag + "_bv"])]
        if affine is not None:
            aff = sb("aff", [E, 4])
            loads += [(aff[:], d[tag + "_aff"])]
        if causal:
            mask = sb("mask", [S, 4, S], BF16)
            mask_f = sb("mask_f", [S, S])
            loads += [(mask_f[:], d["causal"])]
        if low_rank:
            mask2 = sb("mask2", [S, 4, S], BF16)
        if future_only:
            future = sb("future", [S, S])
            loads += [(future[:], d["future"])]
        xin = [sb(f"xin{i}", [S, E]) for i in range(2)]
        xT = [sb(f"xT{i}", [E, S]) for i in range(2)]
        kin = [sb(f"kin{i}", [in_k, keys]) for i in range(2)] if (cross or affine is not None) else xT
        qT = [sb(f"qT{i}", [E, 4, S]) for i in range(2)]
        kT = [[sb(f"kT{j}_{i}", [E, 4, keys]) for i in range(2)] for j in range(2 if low_rank else 1)]
        v = [sb(f"v{i}", [keys, hd]) for i in range(2)]
        negmax = [sb(f"negmax{i}", [S, 4]) for i in range(2)]
        prob = [sb(f"prob{i}", [S, 4, keys]) for i in range(2)]
        sums = [sb(f"sums{i}", [S, HEADS]) for i in range(2)]
        inv = sb("inv", [S, HEADS])
        pT = [sb(f"pT{i}", [keys, 4, S]) for i in range(2)]
        o = sb("o", [S, hd])
        oT = sb("oT", [E, o_chunks, S])
        xb = [sb(f"xb{i}", [S, E]) for i in range(2)]
        r = [sb(f"r{i}", [S, E]) for i in range(2)]
        stats = sb("stats", [S, 6])
        mv = [sb(f"mv{i}", [S, 2]) for i in range(2)]
        rstd = [sb(f"rstd{i}", [S, 1]) for i in range(2)]
        if low_rank:
            a1 = [sb(f"a1{i}", [S, 4, S]) for i in range(2)]
            prod = [sb(f"prod{i}", [S, 4, S]) for i in range(2)]
        score = [bank(f"score{i}", [S, 4, S]) for i in range(2)]
        turned = [bank(f"turned{i}", [S, 4, S]) for i in range(2)]
        out_b = bank("out", [S, 512])
        q_b = bank("q", [E, 4, S])
        k_b = bank("k", [E, 4, S])
        misc = bank("misc", [S, 512])
        sem = sems("weights setup bias_ready xin_ready x_turned xT_copied ctx_loaded0 ctx_loaded1 ctx_copied q_ready q_copied k_ready "
                   "k_copied v_ready v_copied a1_ready a1_copied prod_ready scores_ready max_ready "
                   "probs_ready probs_turned pT_copied pv_done inv_ready o_ready o_turned oT_copied "
                   "roped y_ready xb_ready r_ready stats_ready mv_ready rstd_ready normed sum_stored var_ready")
        n_loads = 16 * len(loads)
        block = ctx.enter_context(nc.Block())

        @block.sync
        def _(sp):
            load_all(sp, loads, sem["weights"])
            if cross and not ctx_copy:
                def slot(n, p):
                    reach(sp, sem["v_ready"], n - 1)
                    sp.dma_start(kin[p][:], d["ctxT"][n]).then_inc(sem[f"ctx_loaded{p}"], 16)

                over_slots(sp, slot, count)

        @block.gpsimd
        def _(pool):
            pool.wait_ge(sem["weights"], n_loads)

            def stage_in(n, p):
                reach(pool, sem["x_turned"], n - 1)
                pool.tensor_copy(xin[p][:], src[:, n, :]).then_inc(sem["xin_ready"], 1)
                if ctx_copy:
                    reach(pool, sem["v_ready"], n - 1)
                    pool.tensor_copy(kin[p][:], keep["ctxn"][:, n, :]).then_inc(sem["ctx_copied"], 1)

            def root(n, p):
                pool.wait_ge(sem["var_ready"], n + 1)
                pool.tensor_tensor(rstd[p][:], rstd[p][:], keep["minus_half"][:], ALU.pow)\
                    .then_inc(sem["rstd_ready"], 1)

            def rope_sums(n, p):
                for t, out_t in enumerate((qT, kT[0])):
                    pool.wait_ge(sem["q_copied" if t == 0 else "k_copied"], (n + 1) * 2)
                    reach(pool, sem["scores_ready"], (n - 1) * 4)
                    pool.tensor_tensor(out_t[p][:], terms[t][0][:], terms[t][1][:], ALU.add)\
                        .then_inc(sem["roped"], 1)
                    pool.wait_ge(sem["roped"], n * 4 + 2 * t + 1)
                    pool.tensor_tensor(out_t[p][:], out_t[p][:], rotated[t][:], ALU.add)\
                        .then_inc(sem["roped"], 1)

            def slot(n, p):
                if rope and within(n, 1, count):
                    rope_sums(n + 1, 1 - p)
                if isinstance(n, int) and n == 0:
                    pool.wait_ge(sem["bias_ready"], 1)
                reach(pool, sem["r_ready"], n - 1)
                res = x if dst == "norm" else keep["b"]
                pool.tensor_tensor(xb[p][:], res[:, n, :], bias[:], ALU.add).then_inc(sem["xb_ready"], 1)
                if within(n, 2, count):
                    stage_in(n + 2, p)
                if within(n, -1, count):
                    root(n - 1, 1 - p)
                    if dst == "sum_and_norm":
                        wait_alone(pool, sem["r_ready"], n, keep["passed_pool"])
                        pool.tensor_tensor(keep["b"][:, n - 1, :], keep["b"][:, n - 1, :], r[1 - p][:], ALU.add)\
                            .then_inc(sem["sum_stored"], 1)

            stage_in(0, 0)
            stage_in(1, 1)
            if rope:
                rope_sums(0, 0)
            over_slots(pool, slot, count)
            root(count - 1, 1)
            if dst == "sum_and_norm":
                pool.tensor_tensor(keep["b"][:, count - 1, :], keep["b"][:, count - 1, :], r[1][:], ALU.add)\
                    .then_inc(sem["sum_stored"], 1)

        @block.tensor
        def _(pe):
            pe.wait_ge(sem["weights"], n_loads)
            pe.wait_ge(sem["setup"], 1)

            def turn_x(n, p):
                pe.wait_ge(sem["xin_ready"], n + 1)
                reach(pe, sem["r_ready"], n - 2)
                reach(pe, sem["v_copied"], n)
                pe.transpose(misc[:, 0:S], xin[p][:], ident[:]).then_inc(sem["x_turned"], 1)

            def project_q(n, p):
                pe.wait_ge(sem["xT_copied"], n + 1)
                for part in range(q_parts):
                    reach(pe, sem["q_copied"], n * q_parts + part)
                    for c in range(4):
                        mm = pe.matmul(q_b[:, c, :], wq[part][:, c, :], xT[p][:], start=True, stop=True)
                    mm.then_inc(sem["q_ready"], 1)

            def project_k(n, p):
                if cross:
                    if ctx_copy:
                        pe.wait_ge(sem["ctx_copied"], n + 1)
                    else:
                        pe.wait_ge(sem[f"ctx_loaded{p}"], (n - p) * 8 + 16)
                for part in range(k_parts):
                    reach(pe, sem["k_copied"], n * k_parts + part)
                    for c in range(4):
                        mm = pe.matmul(k_b[:, c, 0:keys], wk[part][:, c, :], kin[p][:], start=True, stop=True)
                    mm.then_inc(sem["k_ready"], 1)

            def project_v(n, p):
                reach(pe, sem["oT_copied"], n - 1)
                pe.wait_ge(sem["xT_copied"], n + 1)
                pe.matmul(misc[0:keys, 0:hd], kin[p][:], wv[:], start=True, stop=True).then_inc(sem["v_ready"], 1)

            def scores(n, p, c):
                u = n * 4 + c
                if c == 0 and rope:
                    pe.wait_ge(sem["roped"], (n + 1) * 4)
                elif c == 0:
                    pe.wait_ge(sem["q_copied"], n + 1)
                    pe.wait_ge(sem["k_copied"], (n + 1) * k_parts)
                if low_rank:
                    reach(pe, sem["a1_copied"], u)
                else:
                    reach(pe, sem["probs_ready"], u - 1)
                first = score[0] if low_rank else score[c % 2]
                for j in range(4):
                    mm = pe.matmul(first[:, j, 0:keys], qT[p][32 * c:32 * c + rows, j, :],
                                   kT[0][p][32 * c:32 * c + rows, j, :], start=(j == 0),
                                   stop=(j == 3 and not causal), skip_group_check=True)
                if causal:
                    mm = pe.matmul(first[:, :, :], keep["ident_bf"][:], mask[:], start=False, stop=True,
                                   skip_group_check=True)
                mm.then_inc(sem["a1_ready" if low_rank else "scores_ready"], 1)
                if low_rank:
                    reach(pe, sem["prod_ready"], u)
                    for j in range(4):
                        pe.matmul(score[1][:, j, :], qT[p][32 * c:32 * c + rows, j, :],
                                  kT[1][p][32 * c:32 * c + rows, j, :], start=(j == 0), stop=False,
                                  skip_group_check=True)
                    pe.matmul(score[1][:, :, :], keep["ident_bf"][:], mask2[:], start=False, stop=True,
                              skip_group_check=True).then_inc(sem["scores_ready"], 1)

            def turn_probs(n, p, c):
                u = n * 4 + c
                pe.wait_ge(sem["probs_ready"], u + 1)
                reach(pe, sem["pT_copied"], u - 1)
                for j in range(4):
                    mm = pe.transpose(turned[c % 2][0:keys, j, :], prob[c % 2][:, j, :], ident[:])
                mm.then_inc(sem["probs_turned"], 1)

            def weigh(n, p, c):
                u = n * 4 + c
                pe.wait_ge(sem["pT_copied"], u + 1)
                if c == 0:
                    pe.wait_ge(sem["v_copied"], n + 1)
                    reach(pe, sem["o_ready"], n)
                for j in range(4):
                    h = 4 * c + j
                    mm = pe.matmul(out_b[:, h * head_dim:(h + 1) * head_dim], pT[c % 2][:, j, :],
                                   v[p][:, h * head_dim:(h + 1) * head_dim], start=True, stop=True)
                mm.then_inc(sem["pv_done"], 1)

            def turn_o(n, p):
                pe.wait_ge(sem["o_ready"], n + 1)
                reach(pe, sem["r_ready"], n)
                pe.wait_ge(sem["xT_copied"], min(n + 3, count) if isinstance(n, int) else n + 3)
                for c in range(o_chunks):
                    mm = pe.transpose(misc[:, c * S:(c + 1) * S], o[:, c * E:(c + 1) * E], ident[:])
                mm.then_inc(sem["o_turned"], 1)

            def out_product(n, p):
                pe.wait_ge(sem["oT_copied"], n + 1)
                pe.wait_ge(sem["v_copied"], min(n + 3, count) if isinstance(n, int) else n + 3)
                for c in range(o_chunks):
                    mm = pe.matmul(misc[:, 0:E], oT[:, c, :], wo[:, c, :], start=(c == 0), stop=(c == o_chunks - 1))
                mm.then_inc(sem["y_ready"], 1)

            def slot(n, p):
                scores(n, p, 0)
                scores(n, p, 1)
                if within(n, 1, count):
                    project_q(n + 1, 1 - p)
                    project_k(n + 1, 1 - p)
                turn_probs(n, p, 0)
                scores(n, p, 2)
                turn_probs(n, p, 1)
                weigh(n, p, 0)
                scores(n, p, 3)
                if within(n, -1, count):
                    turn_o(n - 1, 1 - p)
                turn_probs(n, p, 2)
                weigh(n, p, 1)
                if within(n, 1, count):
                    project_v(n + 1, 1 - p)
                turn_probs(n, p, 3)
                weigh(n, p, 2)
                if within(n, -1, count):
                    out_product(n - 1, 1 - p)
                if within(n, 2, count):
                    turn_x(n + 2, p)
                weigh(n, p, 3)

            if v_bias:
                pe.matmul(misc[:, 0:E], vb[:], wo[:, 0, :], start=True, stop=True).then_inc(sem["y_ready"], 1)
                pe.wait_ge(sem["bias_ready"], 1)
            turn_x(0, 0)
            project_q(0, 0)
            project_k(0, 0)
            project_v(0, 0)
            turn_x(1, 1)
            over_slots(pe, slot, count)
            turn_o(count - 1, 1)
            out_product(count - 1, 1)

        y0 = 1 if v_bias else 0

        @block.scalar
        def _(act):
            act.wait_ge(sem["weights"], n_loads)

            def copy_xT(n, p):
                pe_count = n + 1
                act.wait_ge(sem["x_turned"], pe_count)
                reach(act, sem["v_ready"], n - 1)
                reach(act, sem["q_ready"], (n - 1) * q_parts)
                if affine is None:
                    act.activation(xT[p][:], misc[:, 0:S], ACT.Copy).then_inc(sem["xT_copied"], 1)
                else:
                    if not cross:
                        act.activation(kin[p][:], misc[:, 0:S], ACT.Identity, scale=aff[:, 2:3], bias=aff[:, 3:4])
                    act.activation(xT[p][:], misc[:, 0:S], ACT.Identity, scale=aff[:, 0:1], bias=aff[:, 1:2])\
                       .then_inc(sem["xT_copied"], 1)

            def copy_v(n, p):
                act.wait_ge(sem["v_ready"], n + 1)
                reach(act, sem["pv_done"], (n - 1) * 4)
                act.activation(v[p][:], misc[0:keys, 0:hd], ACT.Copy).then_inc(sem["v_copied"], 1)

            def copy_oT(n, p):
                act.wait_ge(sem["o_turned"], n + 1)
                reach(act, sem["y_ready"], n + y0)
                act.activation(oT[:], misc[:, 0:hd].rearrange("p (c s) -> p c s", c=o_chunks), ACT.Copy)\
                   .then_inc(sem["oT_copied"], 1)

            def copy_a1(n, p, c):
                u = n * 4 + c
                act.wait_ge(sem["a1_ready"], u + 1)
                reach(act, sem["prod_ready"], u - 1)
                act.activation(a1[c % 2][:], score[0][:], ACT.Copy, scale=scale).then_inc(sem["a1_copied"], 1)

            def exps(n, p, c):
                u = n * 4 + c
                act.wait_ge(sem["max_ready"], u + 1)
                reach(act, sem["probs_turned"], u - 1)
                if c == 0:
                    reach(act, sem["inv_ready"], n - 1)
                logits = prod[c % 2] if low_rank else score[c % 2]
                for j in range(4):
                    e = act.activation(prob[c % 2][:, j, :], logits[:, j, 0:keys], ACT.Exp,
                                       bias=negmax[c % 2][:, j:j + 1],
                                       accum_out=sums[p][:, 4 * c + j:4 * c + j + 1])
                e.then_inc(sem["probs_ready"], 1)

            def slot(n, p):
                if low_rank:
                    copy_a1(n, p, 0)
                    copy_a1(n, p, 1)
                exps(n, p, 0)
                exps(n, p, 1)
                if low_rank:
                    copy_a1(n, p, 2)
                exps(n, p, 2)
                if low_rank:
                    copy_a1(n, p, 3)
                if within(n, -1, count):
                    copy_oT(n - 1, 1 - p)
                exps(n, p, 3)
                if within(n, 1, count):
                    copy_v(n + 1, 1 - p)
                if within(n, 2, count):
                    copy_xT(n + 2, p)

            copy_xT(0, 0)
            copy_v(0, 0)
            copy_xT(1, 1)
            over_slots(act, slot, count)
            copy_oT(count - 1, 1)

        @block.vector
        def _(dve):
            dve.wait_ge(sem["weights"], n_loads)
            if causal:
                for j in range(4):
                    dve.tensor_copy(mask[:, j, :], mask_f[:])
                    if low_rank:
                        dve.tensor_scalar(mask2[:, j, :], mask_f[:], -1.0, None, ALU.mult)
            if rope:
                for i in range(2):
                    dve.tensor_scalar(tables[0][i][:], tables[0][i][:], scale, None, ALU.mult)
            elif q_bias:
                dve.tensor_scalar(qbs[:], qb[:], scale, None, ALU.mult)
            if not out_bias:
                dve.memset(bias[:], 0.0)
            dve.memset(stats[:], 0.0).then_inc(sem["setup"], 1)
            dve.wait_ge(sem["setup"], 1)
            if rope:
                for t in range(2):
                    for i, to in enumerate((rotated[t], terms[t][0])):
                        m = dve.tensor_tensor(to[:], copy_bcast(rb[t][i][:], S),
                                              tables[t][i][:].unsqueeze(1).broadcast_to([E, 4, S]), ALU.mult)
                m.then_inc(sem["setup"], 1)
                dve.wait_ge(sem["setup"], 2)
                for t in range(2):
                    m = dve.tensor_tensor(rotated[t][:], rotated[t][:], terms[t][0][:], ALU.add)
                m.then_inc(sem["setup"], 1)
                dve.wait_ge(sem["setup"], 3)
            if v_bias:
                dve.wait_ge(sem["y_ready"], 1)
                dve.tensor_tensor(bias[:], bias[:], misc[:, 0:E], ALU.add).then_inc(sem["bias_ready"], 1)
            else:
                dve.engine_nop().then_inc(sem["bias_ready"], 1)

            def rope_terms(n, t, bank, ready, copied):
                for part in range(2):
                    dve.wait_ge(sem[ready], n * 2 + part + 1)
                    reach(dve, sem["roped"], n * 4)
                    dve.tensor_tensor(terms[t][part][:], bank[:],
                                      tables[t][part][:].unsqueeze(1).broadcast_to([E, 4, S]), ALU.mult)\
                       .then_inc(sem[copied], 1)

            def copy_q(n, p):
                if rope:
                    rope_terms(n, 0, q_b, "q_ready", "q_copied")
                    return
                dve.wait_ge(sem["q_ready"], n + 1)
                reach(dve, sem["scores_ready"], (n - 1) * 4)
                if q_bias:
                    i = dve.scalar_tensor_tensor(out=qT[p][:], in0=q_b[:], scalar=scale, in1=copy_bcast(qbs[:], S),
                                                 op0=ALU.mult, op1=ALU.add)
                elif low_rank:
                    i = dve.tensor_copy(qT[p][:], q_b[:])
                else:
                    i = dve.tensor_scalar(qT[p][:], q_b[:], scale, None, ALU.mult)
                i.then_inc(sem["q_copied"], 1)

            def copy_k(n, p):
                if rope:
                    rope_terms(n, 1, k_b, "k_ready", "k_copied")
                    return
                for part in range(k_parts):
                    dve.wait_ge(sem["k_ready"], n * k_parts + part + 1)
                    reach(dve, sem["scores_ready"], (n - 1) * 4)
                    if q_bias:
                        i = dve.tensor_tensor(kT[part][p][:], k_b[:, :, 0:keys], copy_bcast(kb[:], keys), ALU.add)
                    else:
                        i = dve.tensor_copy(kT[part][p][:], k_b[:, :, 0:keys])
                    i.then_inc(sem["k_copied"], 1)

            def maxima(n, p, c):
                u = n * 4 + c
                dve.wait_ge(sem["scores_ready"], u + 1)
                logits = score[c % 2]
                if low_rank:
                    dve.wait_ge(sem["a1_copied"], u + 1)
                    reach(dve, sem["probs_ready"], u - 1)
                    dve.tensor_tensor(prod[c % 2][:], a1[c % 2][:], score[1][:], ALU.mult)\
                       .then_inc(sem["prod_ready"], 1)
                    dve.wait_ge(sem["prod_ready"], u + 1)
                    logits = prod[c % 2]
                reach(dve, sem["probs_ready"], u - 1)
                dve.tensor_reduce(negmax[c % 2][:], logits[:, :, 0:keys], AX.X, ALU.max, negate=True)\
                   .then_inc(sem["max_ready"], 1)

            def copy_pT(n, p, c):
                u = n * 4 + c
                dve.wait_ge(sem["probs_turned"], u + 1)
                reach(dve, sem["pv_done"], u - 1)
                if future_only:
                    i = dve.tensor_tensor(pT[c % 2][:], turned[c % 2][:],
                                          future[:].unsqueeze(1).broadcast_to([S, 4, S]), ALU.mult)
                else:
                    i = dve.tensor_copy(pT[c % 2][:], turned[c % 2][0:keys])
                i.then_inc(sem["pT_copied"], 1)

            def normalise(n, p):
                dve.wait_ge(sem["probs_ready"], (n + 1) * 4)
                reach(dve, sem["o_ready"], n)
                dve.reciprocal(inv[:], sums[p][:]).then_inc(sem["inv_ready"], 1)
                dve.wait_ge(sem["inv_ready"], n + 1)
                dve.wait_ge(sem["pv_done"], (n + 1) * 4)
                reach(dve, sem["o_turned"], n)
                dve.tensor_tensor(o[:].rearrange("p (h e) -> p h e", h=HEADS),
                                  out_b[:, 0:hd].rearrange("p (h e) -> p h e", h=HEADS),
                                  copy_bcast(inv[:], head_dim), ALU.mult).then_inc(sem["o_ready"], 1)

            def residual(n, p):
                dve.wait_ge(sem["y_ready"], n + 1 + y0)
                dve.wait_ge(sem["xb_ready"], n + 1)
                if dst == "sum_and_norm":
                    reach(dve, sem["sum_stored"], n - 1)
                reach(dve, sem["normed"], n - 1)
                dve.tensor_tensor(r[p][:], misc[:, 0:E], xb[p][:], ALU.add).then_inc(sem["r_ready"], 1)
                dve.wait_ge(sem["r_ready"], n + 1)
                dve.bn_stats(stats[:], r[p][:]).then_inc(sem["stats_ready"], 1)
                wait_alone(dve, sem["stats_ready"], n + 1, keep["passed"])
                dve.bn_aggr(mv[p][:], stats[:]).then_inc(sem["mv_ready"], 1)
                dve.wait_ge(sem["mv_ready"], n + 1)
                dve.tensor_scalar(rstd[p][:], mv[p][:, 1:2], LN_EPS, None, ALU.add).then_inc(sem["var_ready"], 1)

            def norm(n, p):
                dve.wait_ge(sem["rstd_ready"], n + 1)
                out = x if dst == "norm" else keep["z"]
                dve.tensor_scalar(out[:, n, :], r[p][:], mv[p][:, 0:1], rstd[p][:, 0:1], ALU.subtract, ALU.mult)\
                   .then_inc(sem["normed"], 1)

            def slot(n, p):
                if within(n, -1, count):
                    normalise(n - 1, 1 - p)
                maxima(n, p, 0)
                maxima(n, p, 1)
                if within(n, -2, count):
                    norm(n - 2, p)
                if within(n, 1, count):
                    copy_q(n + 1, 1 - p)
                    copy_k(n + 1, 1 - p)
                copy_pT(n, p, 0)
                maxima(n, p, 2)
                copy_pT(n, p, 1)
                maxima(n, p, 3)
                copy_pT(n, p, 2)
                copy_pT(n, p, 3)
                if within(n, -1, count):
                    residual(n - 1, 1 - p)

            copy_q(0, 0)
            copy_k(0, 0)
            over_slots(dve, slot, count)
            normalise(count - 1, 1)
            norm(count - 2, 0)
            residual(count - 1, 1)
            norm(count - 1, 1)

    clear(nc, sem)


def feed_forward(nc, d, keep, tag, kind, n_chunks, func, *, scale=1.0, ints=False, bias=False, out_bias=False,
                 experts=0, per_gate=1, gates=0, first_gated=0, shared_gate=False, gate_bias=False,
                 src=None, affine=False, dst="norm"):
    G, T = 4, 4 * S
    groups = SEQS // G
    glu, gated = kind == "glu", experts > 0
    routed = experts + (1 if shared_gate else 0)
    x, ident = keep["x"], keep["ident"]
    src = x if src is None else src
    J = n_chunks
    with ExitStack() as ctx:
        sb, bank, sems = tensors(ctx, nc, tag)
        wdt = I32 if ints else F32
        wu, wd = sb("wu", [E, J, E]), sb("wd", [E, J, E])
        mats = [("wu", wu), ("wd", wd)]
        if glu:
            wv = sb("wv", [E, J, E])
            mats.append(("wv", wv))
        loads, raw = [], []
        for n, t in mats:
            if ints:
                raw.append(sb(n + "_int", [E, J, E], I32))
                loads.append((raw[-1][:], d[f"{tag}_{n}"]))
            else:
                loads.append((t[:], d[f"{tag}_{n}"]))
        if bias:
            ub = sb("ub", [E, J])
            loads.append((ub[:], d[tag + "_bu"]))
        ob = sb("ob", [S, E])
        if out_bias:
            loads.append((ob[:], d[tag + "_bd"]))
        if affine:
            aff = sb("aff", [E, 2])
            loads.append((aff[:], d[tag + "_aff"]))
        if gated:
            wr = sb("wr", [E, routed])
            sel = sb("sel", [routed, gates, E])
            before = sb("before", [S, experts, experts])
            loads += [(wr[:], d[tag + "_wr"]), (sel[:], d[tag + "_sel"]), (before[:], d[tag + "_before"])]
            if gate_bias:
                gb = sb("gb", [experts, E])
                loads.append((gb[:], d[tag + "_gb"]))
            prob = sb("prob", [S, G, routed])
            top = sb("top", [S, G])
            more = sb("more", [S, G, experts, experts])
            same = sb("same", [S, G, experts, experts])
            rank = sb("rank", [S, G, experts])
            gate = sb("gate", [S, G, routed])
            gateT = [sb(f"gateT{i}", [routed, T]) for i in range(2)]
        xin = sb("xin", [S, G, E])
        xT = [sb(f"xT{i}", [E, T]) for i in range(2)]
        h = [sb(f"h{i}", [E, T]) for i in range(2)]
        hv = [sb(f"hv{i}", [E, T]) for i in range(2)] if glu else h
        hg = [sb(f"hg{i}", [E, T]) for i in range(2)] if gated else hv
        xb = sb("xb", [S, G, E])
        r = [sb(f"r{i}", [S, G, E]) for i in range(2)]
        stats = sb("stats", [S, G, 6])
        mv = [sb(f"mv{i}", [S, G, 2]) for i in range(2)]
        rstd = [sb(f"rstd{i}", [S, G]) for i in range(2)]
        x_b, v_b, y_b, r_b = bank("x", [E, T]), bank("v", [E, T]), bank("y", [S, G, E]), bank("r", [S, 512])
        u_b = [bank(f"u{i}", [E, T]) for i in range(2)]
        g_b = [bank(f"g{i}", [E, T]) for i in range(2)]
        sem = sems("weights setup xin_ready x_turned xT_copied up_ready act_done v_ready v_done hidden_ready "
                   "gate_spread down_done y_ready xb_ready xb_part r_ready stats_ready mv_ready var_ready rstd_ready "
                   "normed gate_sum routed route_step logits_shifted route_exp gates_ready gates_turned gateT_copied")
        n_loads = 16 * len(loads)
        hidden = "hidden_ready" if gated else "v_done" if glu else "act_done"
        block = ctx.enter_context(nc.Block())

        def gate_of(j):
            return (j - first_gated) // per_gate if gated and j >= first_gated else None

        def new_gate(j):
            return gate_of(j) is not None and (j - first_gated) % per_gate == 0

        @block.sync
        def _(sp):
            load_all(sp, loads, sem["weights"])

        @block.gpsimd
        def _(pool):
            pool.wait_ge(sem["weights"], n_loads)
            pool.wait_ge(sem["setup"], 1)

            def stage_in(g):
                reach(pool, sem["x_turned"], g)
                pool.tensor_copy(xin[:], src[:, bass.ds(g * G, G), :]).then_inc(sem["xin_ready"], 1)

            def residual_base(g):
                wait_alone(pool, sem["r_ready"], g, keep["passed_pool"])
                res = x if dst == "norm" else keep["b"]
                pool.tensor_tensor(xb[:], res[:, bass.ds(g * G, G), :], ob[:].unsqueeze(1).broadcast_to([S, G, E]),
                                   ALU.add).then_inc(sem["xb_part"], 1)
                if dst == "norm_with_x":
                    pool.wait_ge(sem["xb_part"], g + 1)
                    pool.tensor_tensor(xb[:], xb[:], x[:, bass.ds(g * G, G), :], ALU.add).then_inc(sem["xb_ready"], 1)

            def root(g, p):
                if dst != "store":
                    pool.wait_ge(sem["var_ready"], g + 1)
                    pool.tensor_tensor(rstd[p][:], rstd[p][:], keep["minus_half"][:, 0:1].broadcast_to([S, G]),
                                       ALU.pow).then_inc(sem["rstd_ready"], 1)

            def slot(g, p):
                if within(g, 1, groups):
                    stage_in(g + 1)
                if within(g, -1, groups):
                    root(g - 1, 1 - p)
                residual_base(g)

            stage_in(0)
            over_slots(pool, slot, groups)
            root(groups - 1, 1)

        @block.tensor
        def _(pe):
            pe.wait_ge(sem["weights"], n_loads)
            pe.wait_ge(sem["setup"], 1)

            def turn_x(g):
                pe.wait_ge(sem["xin_ready"], g + 1)
                reach(pe, sem["xT_copied"], g)
                for s in range(G):
                    mm = pe.transpose(x_b[:, s * S:(s + 1) * S], xin[:, s, :], ident[:])
                mm.then_inc(sem["x_turned"], 1)

            def route(g, p):
                pe.wait_ge(sem["xT_copied"], g + 1)
                reach(pe, sem["gateT_copied"], g)
                for s in range(G):
                    mm = pe.matmul(r_b[:, s * routed:(s + 1) * routed], xT[p][:, s * S:(s + 1) * S], wr[:],
                                   start=True, stop=True)
                mm.then_inc(sem["routed"], 1)

            def turn_gates(g):
                pe.wait_ge(sem["gates_ready"], g + 1)
                for s in range(G):
                    mm = pe.transpose(r_b[0:routed, s * S:(s + 1) * S], gate[:, s, :], ident[:])
                mm.then_inc(sem["gates_turned"], 1)

            def up(g, p, j):
                n = g * J + j
                if j == 0:
                    pe.wait_ge(sem["xT_copied"], g + 1)
                reach(pe, sem["act_done"], n - 1)
                pe.matmul(u_b[(p * J + j) % 2][:], wu[:, j, :], xT[p][:], start=True, stop=True).then_inc(sem["up_ready"], 1)
                if glu:
                    reach(pe, sem["v_done"], n)
                    pe.matmul(v_b[:], wv[:, j, :], xT[p][:], start=True, stop=True).then_inc(sem["v_ready"], 1)
                if new_gate(j):
                    k = gate_of(j)
                    if k == 0:
                        pe.wait_ge(sem["gateT_copied"], g + 1)
                    last = first_gated + (k - 1) * per_gate if k >= 2 else None
                    if last is not None:
                        pe.wait_ge(sem["hidden_ready"], g * J + last)
                    else:
                        reach(pe, sem["hidden_ready"], g * J)
                    pe.matmul(g_b[k % 2][:], sel[:, k, :], gateT[p][:], start=True, stop=True)\
                      .then_inc(sem["gate_spread"], 1)

            def down(g, p, j):
                n = g * J + j
                pe.wait_ge(sem[hidden], n + 1)
                if j == 0:
                    reach(pe, sem["r_ready"], g)
                    if gate_bias:
                        for s in range(G):
                            pe.matmul(y_b[:, s, :], gateT[p][0:experts, s * S:(s + 1) * S], gb[:],
                                      start=(s == 0), stop=False, skip_group_check=True)
                for s in range(G):
                    mm = pe.matmul(y_b[:, s, :], hg[(p * J + j) % 2][:, s * S:(s + 1) * S], wd[:, j, :],
                                   start=(j == 0 and s == 0 and not gate_bias), stop=(j == J - 1),
                                   skip_group_check=True)
                mm.then_inc(sem["down_done"], 1)

            def slot(g, p):
                for j in range(J):
                    up(g, p, j)
                    if j > 0:
                        down(g, p, j - 1)
                    elif within(g, -1, groups):
                        down(g - 1, 1 - p, J - 1)
                    if j == 1 and within(g, 1, groups):
                        turn_x(g + 1)
                    if gated and j == 3 and within(g, 1, groups):
                        route(g + 1, 1 - p)
                    if gated and j == J - 1 and within(g, 1, groups):
                        turn_gates(g + 1)

            turn_x(0)
            if gated:
                route(0, 0)
                turn_gates(0)
            over_slots(pe, slot, groups)
            down(groups - 1, 1, J - 1)

        @block.scalar
        def _(act):
            act.wait_ge(sem["weights"], n_loads)

            def copy_xT(g, p):
                act.wait_ge(sem["x_turned"], g + 1)
                reach(act, sem["up_ready"], (g - 1) * J)
                if glu:
                    reach(act, sem["v_ready"], (g - 1) * J)
                if affine:
                    i = act.activation(xT[p][:], x_b[:], ACT.Identity, scale=aff[:, 0:1], bias=aff[:, 1:2])
                else:
                    i = act.activation(xT[p][:], x_b[:], ACT.Copy)
                i.then_inc(sem["xT_copied"], 1)

            def route_exp(g):
                act.wait_ge(sem["logits_shifted"], g + 1)
                act.activation(prob[:], prob[:], ACT.Exp).then_inc(sem["route_exp"], 1)

            def copy_gateT(g, p):
                act.wait_ge(sem["gates_turned"], g + 1)
                reach(act, sem["down_done"], (g - 1) * J)
                act.activation(gateT[p][:], r_b[0:routed, :], ACT.Copy).then_inc(sem["gateT_copied"], 1)

            def activate(g, p, j):
                n = g * J + j
                act.wait_ge(sem["up_ready"], n + 1)
                reach(act, sem["v_done"] if glu else sem["hidden_ready"] if gated else sem["down_done"], n - 1)
                i = act.activation(h[(p * J + j) % 2][:], u_b[(p * J + j) % 2][:], func, scale=scale,
                                   **(dict(bias=ub[:, j:j + 1]) if bias else {}))
                i.then_inc(sem["act_done"], 1)

            def slot(g, p):
                for j in range(J):
                    activate(g, p, j)
                    if j == 1 and within(g, 1, groups):
                        copy_xT(g + 1, 1 - p)
                    if gated and j == 5 and within(g, 1, groups):
                        route_exp(g + 1)
                if gated and within(g, 1, groups):
                    copy_gateT(g + 1, 1 - p)

            copy_xT(0, 0)
            if gated:
                route_exp(0)
                copy_gateT(0, 0)
            over_slots(act, slot, groups)

        @block.vector
        def _(dve):
            dve.wait_ge(sem["weights"], n_loads)
            for (_, t), i in zip(mats, raw):
                dve.tensor_copy(t[:], i[:])
            if not out_bias:
                dve.memset(ob[:], 0.0)
            dve.memset(stats[:], 0.0).then_inc(sem["setup"], 1)

            STEPS = 10

            def chain(g, k, ins):
                ins.then_inc(sem["route_step"], 1)
                dve.wait_ge(sem["route_step"], g * STEPS + k)

            def per_n(ap):
                return ap.unsqueeze(2).broadcast_to([S, G, experts, experts])

            def per_m(ap):
                return ap.unsqueeze(3).broadcast_to([S, G, experts, experts])

            def route(g, part):
                pr = prob[:, :, 0:experts]
                if part == 0:
                    dve.wait_ge(sem["routed"], g + 1)
                    logits = r_b[:, 0:G * routed].rearrange("p (s e) -> p s e", s=G)
                    chain(g, 1, dve.tensor_reduce(top[:], logits[:, :, 0:experts], AX.X, ALU.max, negate=True))
                    if shared_gate:
                        dve.tensor_scalar(prob[:, :, experts:routed], logits[:, :, experts:routed], -1.0, None,
                                          ALU.mult)
                    dve.tensor_tensor(pr, logits[:, :, 0:experts], copy_bcast(top[:], experts), ALU.add)\
                       .then_inc(sem["logits_shifted"], 1)
                elif part == 1:
                    dve.wait_ge(sem["route_exp"], g + 1)
                    reach(dve, sem["gates_turned"], g)
                    chain(g, 2, dve.tensor_reduce(top[:], pr, AX.X, ALU.add))
                    chain(g, 3, dve.reciprocal(top[:], top[:]))
                    if shared_gate:
                        dve.tensor_scalar(gate[:, :, experts:routed], prob[:, :, experts:routed], 1.0, None, ALU.add)
                    chain(g, 4, dve.tensor_tensor(pr, pr, copy_bcast(top[:], experts), ALU.mult))
                    if shared_gate:
                        dve.reciprocal(gate[:, :, experts:routed], gate[:, :, experts:routed])
                elif part == 2:
                    dve.tensor_tensor(more[:], per_n(pr), per_m(pr), ALU.is_gt)
                    chain(g, 5, dve.tensor_tensor(same[:], per_n(pr), per_m(pr), ALU.is_equal))
                    chain(g, 6, dve.tensor_tensor(same[:], same[:], before[:].unsqueeze(1).broadcast_to(
                        [S, G, experts, experts]), ALU.mult))
                elif part == 3:
                    chain(g, 7, dve.tensor_tensor(more[:], more[:], same[:], ALU.add))
                    chain(g, 8, dve.tensor_reduce(rank[:], more[:], AX.X, ALU.add))
                else:
                    chain(g, 9, dve.scalar_tensor_tensor(out=rank[:], in0=rank[:], scalar=1.5, in1=pr,
                                                         op0=ALU.is_lt, op1=ALU.mult))
                    chain(g, 10, dve.tensor_reduce(top[:], rank[:], AX.X, ALU.add))
                    dve.reciprocal(top[:], top[:]).then_inc(sem["gate_sum"], 1)
                    dve.wait_ge(sem["gate_sum"], g + 1)
                    dve.tensor_tensor(gate[:, :, 0:experts], rank[:], copy_bcast(top[:], experts), ALU.mult)\
                       .then_inc(sem["gates_ready"], 1)

            def finish_hidden(g, p, j):
                n = g * J + j
                dve.wait_ge(sem["act_done"], n + 1)
                a = h[(p * J + j) % 2]
                if glu:
                    dve.wait_ge(sem["v_ready"], n + 1)
                    if gated:
                        i = dve.tensor_tensor(hv[(p * J + j) % 2][:], a[:], v_b[:], ALU.mult)
                    else:
                        reach(dve, sem["down_done"], n - 1)
                        i = dve.scalar_tensor_tensor(out=hv[(p * J + j) % 2][:], in0=v_b[:], scalar=scale, in1=a[:],
                                                     op0=ALU.mult, op1=ALU.mult)
                    i.then_inc(sem["v_done"], 1)
                    dve.wait_ge(sem["v_done"], n + 1)
                    a = hv[(p * J + j) % 2]
                if not gated:
                    return
                reach(dve, sem["down_done"], n - 1)
                k = gate_of(j)
                if k is None:
                    i = dve.tensor_copy(hg[(p * J + j) % 2][:], a[:])
                else:
                    if new_gate(j):
                        dve.wait_ge(sem["gate_spread"], g * gates + k + 1)
                    i = dve.tensor_tensor(hg[(p * J + j) % 2][:], a[:], g_b[k % 2][:], ALU.mult)
                i.then_inc(sem["hidden_ready"], 1)

            def residual(g, p):
                dve.wait_ge(sem["down_done"], (g + 1) * J)
                dve.wait_ge(sem["xb_ready" if dst == "norm_with_x" else "xb_part"], g + 1)
                if dst == "store":
                    dve.tensor_tensor(keep["b"][:, bass.ds(g * G, G), :], y_b[:], xb[:], ALU.add)\
                       .then_inc(sem["r_ready"], 1)
                    return
                if ints:
                    i = dve.scalar_tensor_tensor(out=r[p][:], in0=y_b[:], scalar=scale, in1=xb[:], op0=ALU.mult,
                                                 op1=ALU.add)
                else:
                    i = dve.tensor_tensor(r[p][:], y_b[:], xb[:], ALU.add)
                i.then_inc(sem["r_ready"], 1)
                dve.wait_ge(sem["r_ready"], g + 1)
                for s in range(G):
                    i = dve.bn_stats(stats[:, s, :], r[p][:, s, :])
                i.then_inc(sem["stats_ready"], 1)
                wait_alone(dve, sem["stats_ready"], g + 1, keep["passed"])
                for s in range(G):
                    i = dve.bn_aggr(mv[p][:, s, :], stats[:, s, :])
                i.then_inc(sem["mv_ready"], 1)
                dve.wait_ge(sem["mv_ready"], g + 1)
                dve.tensor_scalar(rstd[p][:], mv[p][:, :, 1], LN_EPS, None, ALU.add).then_inc(sem["var_ready"], 1)

            def norm(g, p):
                if dst == "store":
                    return
                dve.wait_ge(sem["rstd_ready"], g + 1)
                for s in range(G):
                    i = dve.tensor_scalar(x[:, g * G + s, :], r[p][:, s, :], mv[p][:, s, 0:1], rstd[p][:, s:s + 1],
                                          ALU.subtract, ALU.mult)
                i.then_inc(sem["normed"], 1)

            def slot(g, p):
                for j in range(J):
                    if glu or gated:
                        finish_hidden(g, p, j)
                    if j == 0 and within(g, -1, groups):
                        residual(g - 1, 1 - p)
                    if j == 2 and within(g, -1, groups):
                        norm(g - 1, 1 - p)
                    if gated and 4 <= j < 9 and within(g, 1, groups):
                        route(g + 1, j - 4)

            if gated:
                for part in range(5):
                    route(0, part)
            over_slots(dve, slot, groups)
            residual(groups - 1, 1)
            norm(groups - 1, 1)

    clear(nc, sem)


def renormalise(nc, d, keep, tag, src):
    G = 4
    groups = SEQS // G
    b, z = keep["b"], keep["z"]
    with ExitStack() as ctx:
        sb, _, sems = tensors(ctx, nc, tag)
        gain, shift = sb("gain", [S, E]), sb("shift", [S, E])
        loads = [(gain[:], d[tag + "_gain"]), (shift[:], d[tag + "_shift"])]
        scaled = [sb(f"scaled{i}", [S, G, E]) for i in range(2)]
        stats = sb("stats", [S, G, 6])
        mv = [[sb(f"mv{k}{i}", [S, G, 2]) for i in range(2)] for k in range(2)]
        rstd = [[sb(f"rstd{k}{i}", [S, G]) for i in range(2)] for k in range(2)]
        sem = sems("weights stats_ready mv_ready var0 var1 rstd0 rstd1 normed scaled stored z_stored")
        block = ctx.enter_context(nc.Block())

        @block.sync
        def _(sp):
            load_all(sp, loads, sem["weights"])

        @block.gpsimd
        def _(pool):
            def root(k, g, p):
                pool.wait_ge(sem[f"var{k}"], g + 1)
                pool.tensor_tensor(rstd[k][p][:], rstd[k][p][:], keep["minus_half"][:, 0:1].broadcast_to([S, G]),
                                   ALU.pow).then_inc(sem[f"rstd{k}"], 1)

            def slot(g, p):
                root(0, g, p)
                if within(g, -1, groups):
                    root(1, g - 1, 1 - p)

            over_slots(pool, slot, groups)
            root(1, groups - 1, 1)

        @block.vector
        def _(dve):
            dve.wait_ge(sem["weights"], 32)

            def moments(k, g, p, count):
                data = src if k == 0 else b
                if k == 1:
                    wait_alone(dve, sem["stored"], g + 1, keep["passed"])
                for s in range(G):
                    i = dve.bn_stats(stats[:, s, :], data[:, g * G + s, :])
                i.then_inc(sem["stats_ready"], 1)
                wait_alone(dve, sem["stats_ready"], count + 1, keep["passed"])
                for s in range(G):
                    i = dve.bn_aggr(mv[k][p][:, s, :], stats[:, s, :])
                i.then_inc(sem["mv_ready"], 1)
                dve.wait_ge(sem["mv_ready"], count + 1)
                dve.tensor_scalar(rstd[k][p][:], mv[k][p][:, :, 1], LN_EPS, None, ALU.add).then_inc(sem[f"var{k}"], 1)

            def scale_shift(g, p):
                dve.wait_ge(sem["rstd0"], g + 1)
                for s in range(G):
                    i = dve.tensor_scalar(scaled[p][:, s, :], src[:, g * G + s, :], mv[0][p][:, s, 0:1],
                                          rstd[0][p][:, s:s + 1], ALU.subtract, ALU.mult)
                i.then_inc(sem["normed"], 1)
                dve.wait_ge(sem["normed"], g + 1)
                dve.tensor_tensor(scaled[p][:], scaled[p][:], gain[:].unsqueeze(1).broadcast_to([S, G, E]), ALU.mult)\
                   .then_inc(sem["scaled"], 1)
                dve.wait_ge(sem["scaled"], g + 1)
                dve.tensor_tensor(b[:, bass.ds(g * G, G), :], scaled[p][:],
                                  shift[:].unsqueeze(1).broadcast_to([S, G, E]), ALU.add).then_inc(sem["stored"], 1)

            def store_z(g, p):
                dve.wait_ge(sem["rstd1"], g + 1)
                for s in range(G):
                    i = dve.tensor_scalar(z[:, g * G + s, :], b[:, g * G + s, :], mv[1][p][:, s, 0:1],
                                          rstd[1][p][:, s:s + 1], ALU.subtract, ALU.mult)
                i.then_inc(sem["z_stored"], 1)

            def slot(g, p):
                moments(0, g, p, g * 2 - (0 if isinstance(g, int) and g == 0 else 1))
                if within(g, -1, groups):
                    scale_shift(g - 1, 1 - p)
                    moments(1, g - 1, 1 - p, g * 2)
                if within(g, -2, groups):
                    store_z(g - 2, p)

            over_slots(dve, slot, groups)
            store_z(groups - 2, 0)
            scale_shift(groups - 1, 1)
            moments(1, groups - 1, 1, 2 * groups - 1)
            store_z(groups - 1, 1)

    clear(nc, sem)


def normalise_context(nc, d, keep, tag):
    G = 4
    groups = SEQS // G
    with ExitStack() as ctx:
        sb, bank, sems = tensors(ctx, nc, tag)
        c, sq = sb("c", [CTX, SEQS, C]), sb("sq", [CTX, SEQS, C])
        aff = sb("aff", [C, 2])
        mean, rstd = sb("mean", [CTX, SEQS]), sb("rstd", [CTX, SEQS])
        turned = [bank(f"turned{i}", [C, G, CTX]) for i in range(2)]
        sem = sems("loaded step var_ready rstd_ready normed turned stored")
        block = ctx.enter_context(nc.Block())

        @block.sync
        def _(sp):
            sp.dma_start(c[:], d["ctx"].rearrange("s t c -> t s c")).then_inc(sem["loaded"], 16)
            sp.dma_start(aff[:], d[tag + "_aff"]).then_inc(sem["loaded"], 16)

        @block.gpsimd
        def _(pool):
            pool.wait_ge(sem["var_ready"], 1)
            pool.tensor_tensor(rstd[:], rstd[:], keep["minus_half"][0:CTX, 0:1].broadcast_to([CTX, SEQS]), ALU.pow)\
                .then_inc(sem["rstd_ready"], 1)

        @block.vector
        def _(dve):
            def chain(k, ins):
                ins.then_inc(sem["step"], 1)
                dve.wait_ge(sem["step"], k)

            dve.wait_ge(sem["loaded"], 32)
            chain(1, dve.tensor_reduce(mean[:], c[:], AX.X, ALU.add))
            chain(2, dve.tensor_scalar(mean[:], mean[:], 1.0 / C, None, ALU.mult))
            chain(3, dve.tensor_tensor(c[:], c[:], copy_bcast(mean[:], C), ALU.subtract))
            chain(4, dve.tensor_tensor(sq[:], c[:], c[:], ALU.mult))
            chain(5, dve.tensor_reduce(rstd[:], sq[:], AX.X, ALU.add))
            dve.tensor_scalar(rstd[:], rstd[:], 1.0 / C, LN_EPS, ALU.mult, ALU.add).then_inc(sem["var_ready"], 1)
            dve.wait_ge(sem["rstd_ready"], 1)
            dve.tensor_tensor(c[:], c[:], copy_bcast(rstd[:], C), ALU.mult).then_inc(sem["normed"], 1)

        @block.tensor
        def _(pe):
            pe.wait_ge(sem["normed"], 1)
            for g in range(groups):
                if g >= 2:
                    pe.wait_ge(sem["stored"], g - 1)
                for s in range(G):
                    mm = pe.transpose(turned[g % 2][:, s, :], c[:, g * G + s, :], keep["ident"][0:CTX, 0:CTX])
                mm.then_inc(sem["turned"], 1)

        @block.scalar
        def _(act):
            act.wait_ge(sem["loaded"], 32)
            for g in range(groups):
                act.wait_ge(sem["turned"], g + 1)
                act.activation(keep["ctxn"][:, g * G:(g + 1) * G, :], turned[g % 2][:], ACT.Identity,
                               scale=aff[:, 0:1], bias=aff[:, 1:2]).then_inc(sem["stored"], 1)

    clear(nc, sem)


def relu_attention(nc, d, keep, tag):
    count, K, D = SEQS, 4, E // HEADS
    x, ident = keep["x"], keep["ident"]
    with ExitStack() as ctx:
        sb, bank, sems = tensors(ctx, nc, tag)
        w = {n: sb(n, [E, E]) for n in ("wq", "wk", "wv", "wo")}
        b = {n: sb(n, [S, E]) for n in ("bq", "bk", "bv", "bo", "weight", "gain")}
        rowsT = {n: sb(n, [E, K, S]) for n in ("keyT", "valueT")}
        loads = [(t[:], d[f"{tag}_{n}"]) for m in (w, b, rowsT) for n, t in m.items()]
        kk, vv = sb("k", [S, K, E]), sb("v", [S, K, E])
        half = sb("half", [S, 1])
        xin = [sb(f"xin{i}", [S, E]) for i in range(2)]
        xT = [sb(f"xT{i}", [E, S]) for i in range(2)]
        xb = [sb(f"xb{i}", [S, E]) for i in range(2)]
        q = sb("q", [S, E])
        prod = sb("prod", [S, K, E])
        logit = sb("logit", [S, K, HEADS])
        o = [sb(f"o{i}", [S, E]) for i in range(2)]
        sq = sb("sq", [S, E])
        ms = [sb(f"ms{i}", [S, 1]) for i in range(2)]
        gx = [sb(f"gx{i}", [S, E]) for i in range(2)]
        on = sb("on", [S, E])
        oT = sb("oT", [E, S])
        r = [sb(f"r{i}", [S, E]) for i in range(2)]
        stats = sb("stats", [S, 6])
        mv = [sb(f"mv{i}", [S, 2]) for i in range(2)]
        rstd = [sb(f"rstd{i}", [S, 1]) for i in range(2)]
        k_b, v_b = bank("k_b", [S, K, E]), bank("v_b", [S, K, E])
        x_b, q_b, t_b, y_b = (bank(n, [S, E]) for n in ("x_b", "q_b", "t_b", "y_b"))
        sem = sems("weights kv_ready setup xin_ready x_turned xT_copied q_ready xb_ready step meansq_ready rms_ready "
                   "gated sigmoid_ready on_ready on_turned oT_copied y_ready r_ready var_ready rstd_ready normed "
                   "gate_step res_step")
        n_loads = 16 * len(loads)
        STEPS = 8
        block = ctx.enter_context(nc.Block())

        @block.sync
        def _(sp):
            load_all(sp, loads, sem["weights"])

        @block.gpsimd
        def _(pool):
            pool.wait_ge(sem["weights"], n_loads)
            pool.wait_ge(sem["setup"], 1)

            def stage_in(n, p):
                reach(pool, sem["x_turned"], n - 1)
                pool.tensor_copy(xin[p][:], x[:, n, :]).then_inc(sem["xin_ready"], 1)

            def slot(n, p):
                pool.wait_ge(sem["meansq_ready"], n + 1)
                pool.tensor_tensor(ms[p][:], ms[p][:], half[:], ALU.pow).then_inc(sem["rms_ready"], 1)
                if within(n, 2, count):
                    stage_in(n + 2, p)
                if within(n, -1, count):
                    pool.wait_ge(sem["var_ready"], n)
                    pool.tensor_tensor(rstd[1 - p][:], rstd[1 - p][:], keep["minus_half"][:], ALU.pow)\
                        .then_inc(sem["rstd_ready"], 1)
                reach(pool, sem["r_ready"], n - 1)
                pool.tensor_tensor(xb[p][:], x[:, n, :], b["bo"][:], ALU.add).then_inc(sem["xb_ready"], 1)

            stage_in(0, 0)
            stage_in(1, 1)
            over_slots(pool, slot, count)
            pool.wait_ge(sem["var_ready"], count)
            pool.tensor_tensor(rstd[1][:], rstd[1][:], keep["minus_half"][:], ALU.pow).then_inc(sem["rstd_ready"], 1)

        @block.tensor
        def _(pe):
            pe.wait_ge(sem["weights"], n_loads)
            for s in range(K):
                pe.matmul(k_b[:, s, :], rowsT["keyT"][:, s, :], w["wk"][:], start=True, stop=True)
                mm = pe.matmul(v_b[:, s, :], rowsT["valueT"][:, s, :], w["wv"][:], start=True, stop=True)
            mm.then_inc(sem["kv_ready"], 1)

            def turn_x(n, p):
                pe.wait_ge(sem["xin_ready"], n + 1)
                reach(pe, sem["xT_copied"], n)
                pe.transpose(x_b[:], xin[p][:], ident[:]).then_inc(sem["x_turned"], 1)

            def queries(n, p):
                pe.wait_ge(sem["xT_copied"], n + 1)
                reach(pe, sem["step"], (n - 1) * STEPS + 1)
                pe.matmul(q_b[:], xT[p][:], w["wq"][:], start=True, stop=True).then_inc(sem["q_ready"], 1)

            def product(n):
                pe.wait_ge(sem["on_ready"], n + 1)
                reach(pe, sem["oT_copied"], n)
                pe.transpose(t_b[:], on[:], ident[:]).then_inc(sem["on_turned"], 1)
                pe.wait_ge(sem["oT_copied"], n + 1)
                reach(pe, sem["r_ready"], n)
                pe.matmul(y_b[:], oT[:], w["wo"][:], start=True, stop=True).then_inc(sem["y_ready"], 1)

            def slot(n, p):
                if within(n, 1, count):
                    turn_x(n + 1, 1 - p)
                    queries(n + 1, 1 - p)
                if within(n, -1, count):
                    product(n - 1)

            turn_x(0, 0)
            queries(0, 0)
            over_slots(pe, slot, count)
            product(count - 1)

        @block.scalar
        def _(act):
            def copy_xT(n, p):
                act.wait_ge(sem["x_turned"], n + 1)
                reach(act, sem["q_ready"], n - 1)
                act.activation(xT[p][:], x_b[:], ACT.Copy).then_inc(sem["xT_copied"], 1)

            def copy_oT(n):
                act.wait_ge(sem["on_turned"], n + 1)
                reach(act, sem["y_ready"], n)
                act.activation(oT[:], t_b[:], ACT.Copy).then_inc(sem["oT_copied"], 1)

            def slot(n, p):
                if within(n, 1, count):
                    copy_xT(n + 1, 1 - p)
                if within(n, -1, count):
                    copy_oT(n - 1)
                act.wait_ge(sem["gated"], n + 1)
                act.activation(gx[p][:], gx[p][:], ACT.Sigmoid).then_inc(sem["sigmoid_ready"], 1)

            copy_xT(0, 0)
            over_slots(act, slot, count)
            copy_oT(count - 1)

        @block.vector
        def _(dve):
            dve.wait_ge(sem["weights"], n_loads)
            dve.wait_ge(sem["kv_ready"], 1)
            dve.memset(half[:], 0.5)
            dve.tensor_tensor(kk[:], k_b[:], b["bk"][:].unsqueeze(1).broadcast_to([S, K, E]), ALU.add)
            dve.tensor_tensor(vv[:], v_b[:], b["bv"][:].unsqueeze(1).broadcast_to([S, K, E]), ALU.add)\
               .then_inc(sem["setup"], 1)
            dve.wait_ge(sem["setup"], 1)

            def chain(n, k, ins):
                ins.then_inc(sem["step"], 1)
                dve.wait_ge(sem["step"], n * STEPS + k)

            def attend(n, p):
                dve.wait_ge(sem["q_ready"], n + 1)
                chain(n, 1, dve.tensor_tensor(q[:], q_b[:], b["bq"][:], ALU.add))
                chain(n, 2, dve.scalar_tensor_tensor(out=prod[:], in0=kk[:], scalar=D ** -0.5,
                                                     in1=q[:].unsqueeze(1).broadcast_to([S, K, E]),
                                                     op0=ALU.mult, op1=ALU.mult))
                chain(n, 3, dve.tensor_reduce(logit[:], prod[:].rearrange("p k (h e) -> p k h e", h=HEADS),
                                              AX.X, ALU.add))
                chain(n, 4, dve.tensor_scalar(logit[:], logit[:], 0.0, None, ALU.max))
                chain(n, 5, dve.tensor_tensor(
                    prod[:].rearrange("p k (h e) -> p (k h) e", h=HEADS),
                    vv[:].rearrange("p k (h e) -> p (k h) e", h=HEADS),
                    copy_bcast(logit[:].rearrange("p k h -> p (k h)"), D), ALU.mult))
                reach(dve, sem["on_ready"], n - 1)
                chain(n, 6, dve.tensor_reduce(o[p][:], prod[:].rearrange("p k e -> p e k"), AX.X, ALU.add))
                dve.tensor_tensor(gx[p][:], o[p][:], b["gain"][:], ALU.mult).then_inc(sem["gated"], 1)
                chain(n, 7, dve.tensor_tensor(sq[:], o[p][:], o[p][:], ALU.mult))
                chain(n, 8, dve.tensor_reduce(ms[p][:], sq[:], AX.X, ALU.add))
                dve.tensor_scalar(ms[p][:], ms[p][:], 1.0 / E, None, ALU.mult).then_inc(sem["meansq_ready"], 1)

            def gated_norm(n, p):
                dve.wait_ge(sem["rms_ready"], n + 1)
                dve.wait_ge(sem["sigmoid_ready"], n + 1)
                gate_chain(n, 1, dve.tensor_scalar(ms[p][:], ms[p][:], 1e-8, None, ALU.add))
                gate_chain(n, 2, dve.reciprocal(ms[p][:], ms[p][:]))
                gate_chain(n, 3, dve.scalar_tensor_tensor(out=o[p][:], in0=o[p][:], scalar=ms[p][:, 0:1],
                                                          in1=b["weight"][:], op0=ALU.mult, op1=ALU.mult))
                reach(dve, sem["on_turned"], n)
                dve.tensor_tensor(on[:], o[p][:], gx[p][:], ALU.mult).then_inc(sem["on_ready"], 1)

            def gate_chain(n, k, ins):
                ins.then_inc(sem["gate_step"], 1)
                dve.wait_ge(sem["gate_step"], n * 3 + k)

            def residual(n, p):
                dve.wait_ge(sem["y_ready"], n + 1)
                dve.wait_ge(sem["xb_ready"], n + 1)
                dve.tensor_tensor(r[p][:], y_b[:], xb[p][:], ALU.add).then_inc(sem["r_ready"], 1)
                dve.wait_ge(sem["r_ready"], n + 1)
                res_chain(n, 1, dve.bn_stats(stats[:], r[p][:]))
                dve.sem_inc(keep["passed"], 1)
                res_chain(n, 2, dve.bn_aggr(mv[p][:], stats[:]))
                dve.tensor_scalar(rstd[p][:], mv[p][:, 1:2], LN_EPS, None, ALU.add).then_inc(sem["var_ready"], 1)

            def res_chain(n, k, ins):
                ins.then_inc(sem["res_step"], 1)
                dve.wait_ge(sem["res_step"], n * 2 + k)

            def norm(n, p):
                dve.wait_ge(sem["rstd_ready"], n + 1)
                dve.tensor_scalar(x[:, n, :], r[p][:], mv[p][:, 0:1], rstd[p][:, 0:1], ALU.subtract, ALU.mult)\
                   .then_inc(sem["normed"], 1)

            def slot(n, p):
                if within(n, -1, count):
                    gated_norm(n - 1, 1 - p)
                attend(n, p)
                if within(n, -2, count):
                    norm(n - 2, p)
                if within(n, -1, count):
                    residual(n - 1, 1 - p)

            over_slots(dve, slot, count)
            gated_norm(count - 1, 1)
            norm(count - 2, 0)
            residual(count - 1, 1)
            norm(count - 1, 1)

    clear(nc, sem)


def one_head_attention(nc, d, keep, tag):
    count = SEQS
    x, ident = keep["x"], keep["ident"]
    with ExitStack() as ctx:
        sb, bank, sems = tensors(ctx, nc, tag)
        wq, wk, wv = sb("wq", [E, E]), sb("wk", [C, E]), sb("wv", [C, E])
        qb, kb, vb = sb("qb", [E, 1]), sb("kb", [E, 1]), sb("vb", [S, E])
        loads = [(wq[:], d[tag + "_wq"]), (wk[:], d[tag + "_wk"]), (wv[:], d[tag + "_wv"]),
                 (qb[:], d[tag + "_bq"]), (kb[:], d[tag + "_bk"]), (vb[:], d[tag + "_bv"])]
        xin = [sb(f"xin{i}", [S, E]) for i in range(2)]
        cin = [sb(f"cin{i}", [C, CTX]) for i in range(2)]
        xb = [sb(f"xb{i}", [S, E]) for i in range(2)]
        xT = [sb(f"xT{i}", [E, S]) for i in range(2)]
        qT = [sb(f"qT{i}", [E, S]) for i in range(2)]
        kT = [sb(f"kT{i}", [E, CTX]) for i in range(2)]
        v = [sb(f"v{i}", [CTX, E]) for i in range(2)]
        negmax = [sb(f"negmax{i}", [S, 1]) for i in range(2)]
        prob = [sb(f"prob{i}", [S, CTX]) for i in range(2)]
        total = [sb(f"total{i}", [S, 1]) for i in range(2)]
        pT = [sb(f"pT{i}", [CTX, S]) for i in range(2)]
        r = [sb(f"r{i}", [S, E]) for i in range(2)]
        stats = sb("stats", [S, 6])
        mv = [sb(f"mv{i}", [S, 2]) for i in range(2)]
        rstd = [sb(f"rstd{i}", [S, 1]) for i in range(2)]
        x_b, q_b, k_b, v_b, s_b, t_b, o_b = (bank(n, [S, S]) for n in ("x", "q", "k", "v", "s", "t", "o"))
        sem = sems("weights xin_ready x_turned xT_copied ctx_loaded0 ctx_loaded1 q_ready q_copied k_ready k_copied "
                   "v_ready v_copied scores_ready max_ready probs_ready probs_turned pT_copied o_ready inv_ready "
                   "xb_ready r_ready step var_ready rstd_ready normed")
        n_loads = 16 * len(loads)
        block = ctx.enter_context(nc.Block())

        @block.sync
        def _(sp):
            load_all(sp, loads, sem["weights"])

            def slot(n, p):
                reach(sp, sem["v_ready"], n - 1)
                sp.dma_start(cin[p][:], d["ctxT"][n]).then_inc(sem[f"ctx_loaded{p}"], 16)

            over_slots(sp, slot, count)

        @block.gpsimd
        def _(pool):
            pool.wait_ge(sem["weights"], n_loads)

            def stage_in(n, p):
                reach(pool, sem["x_turned"], n - 1)
                pool.tensor_copy(xin[p][:], x[:, n, :]).then_inc(sem["xin_ready"], 1)

            def root(n, p):
                pool.wait_ge(sem["var_ready"], n + 1)
                pool.tensor_tensor(rstd[p][:], rstd[p][:], keep["minus_half"][:], ALU.pow)\
                    .then_inc(sem["rstd_ready"], 1)

            def slot(n, p):
                if within(n, 2, count):
                    stage_in(n + 2, p)
                reach(pool, sem["r_ready"], n - 1)
                pool.tensor_tensor(xb[p][:], x[:, n, :], vb[:], ALU.add).then_inc(sem["xb_ready"], 1)
                if within(n, -2, count):
                    root(n - 2, p)

            stage_in(0, 0)
            stage_in(1, 1)
            over_slots(pool, slot, count)
            root(count - 2, 0)
            root(count - 1, 1)

        @block.tensor
        def _(pe):
            pe.wait_ge(sem["weights"], n_loads)

            def turn_x(n, p):
                pe.wait_ge(sem["xin_ready"], n + 1)
                reach(pe, sem["xT_copied"], n)
                pe.transpose(x_b[:], xin[p][:], ident[:]).then_inc(sem["x_turned"], 1)

            def project(n, p):
                pe.wait_ge(sem["xT_copied"], n + 1)
                reach(pe, sem["q_copied"], n)
                pe.matmul(q_b[:], wq[:], xT[p][:], start=True, stop=True).then_inc(sem["q_ready"], 1)
                pe.wait_ge(sem[f"ctx_loaded{p}"], (n - p) * 8 + 16)
                reach(pe, sem["k_copied"], n)
                pe.matmul(k_b[:, 0:CTX], wk[:], cin[p][:], start=True, stop=True).then_inc(sem["k_ready"], 1)
                reach(pe, sem["v_copied"], n)
                pe.matmul(v_b[0:CTX, :], cin[p][:], wv[:], start=True, stop=True).then_inc(sem["v_ready"], 1)

            def score(n, p):
                pe.wait_ge(sem["q_copied"], n + 1)
                pe.wait_ge(sem["k_copied"], n + 1)
                reach(pe, sem["probs_ready"], n)
                pe.matmul(s_b[:, 0:CTX], qT[p][:], kT[p][:], start=True, stop=True).then_inc(sem["scores_ready"], 1)

            def turn_probs(n, p):
                pe.wait_ge(sem["probs_ready"], n + 1)
                reach(pe, sem["pT_copied"], n)
                pe.transpose(t_b[0:CTX, :], prob[p][:], ident[:]).then_inc(sem["probs_turned"], 1)

            def weigh(n, p):
                pe.wait_ge(sem["pT_copied"], n + 1)
                pe.wait_ge(sem["v_copied"], n + 1)
                reach(pe, sem["r_ready"], n)
                pe.matmul(o_b[:], pT[p][:], v[p][:], start=True, stop=True).then_inc(sem["o_ready"], 1)

            def slot(n, p):
                score(n, p)
                if within(n, 2, count):
                    turn_x(n + 2, p)
                if within(n, -1, count):
                    weigh(n - 1, 1 - p)
                if within(n, 1, count):
                    project(n + 1, 1 - p)
                turn_probs(n, p)

            turn_x(0, 0)
            project(0, 0)
            turn_x(1, 1)
            over_slots(pe, slot, count)
            weigh(count - 1, 1)

        @block.scalar
        def _(act):
            act.wait_ge(sem["weights"], n_loads)

            def copy_xT(n, p):
                act.wait_ge(sem["x_turned"], n + 1)
                reach(act, sem["q_ready"], n - 1)
                act.activation(xT[p][:], x_b[:], ACT.Copy).then_inc(sem["xT_copied"], 1)

            def copy_qkv(n, p):
                act.wait_ge(sem["q_ready"], n + 1)
                reach(act, sem["scores_ready"], n - 1)
                act.activation(qT[p][:], q_b[:], ACT.Identity, bias=qb[:, 0:1]).then_inc(sem["q_copied"], 1)
                act.wait_ge(sem["k_ready"], n + 1)
                act.activation(kT[p][:], k_b[:, 0:CTX], ACT.Identity, bias=kb[:, 0:1]).then_inc(sem["k_copied"], 1)
                act.wait_ge(sem["v_ready"], n + 1)
                reach(act, sem["o_ready"], n - 1)
                act.activation(v[p][:], v_b[0:CTX, :], ACT.Copy).then_inc(sem["v_copied"], 1)

            def slot(n, p):
                act.wait_ge(sem["max_ready"], n + 1)
                reach(act, sem["probs_turned"], n - 1)
                reach(act, sem["r_ready"], n - 1)
                act.activation(prob[p][:], s_b[:, 0:CTX], ACT.Exp, bias=negmax[p][:, 0:1],
                               accum_out=total[p][:, 0:1]).then_inc(sem["probs_ready"], 1)
                if within(n, 2, count):
                    copy_xT(n + 2, p)
                if within(n, 1, count):
                    copy_qkv(n + 1, 1 - p)

            copy_xT(0, 0)
            copy_qkv(0, 0)
            copy_xT(1, 1)
            over_slots(act, slot, count)

        @block.vector
        def _(dve):
            dve.wait_ge(sem["weights"], n_loads)

            def maximum(n, p):
                dve.wait_ge(sem["scores_ready"], n + 1)
                reach(dve, sem["probs_ready"], n - 1)
                dve.tensor_reduce(negmax[p][:], s_b[:, 0:CTX], AX.X, ALU.max, negate=True)\
                   .then_inc(sem["max_ready"], 1)

            def copy_pT(n, p):
                dve.wait_ge(sem["probs_turned"], n + 1)
                reach(dve, sem["o_ready"], n - 1)
                dve.tensor_copy(pT[p][:], t_b[0:CTX, :]).then_inc(sem["pT_copied"], 1)

            def residual(n, p):
                dve.wait_ge(sem["probs_ready"], n + 1)
                dve.reciprocal(total[p][:], total[p][:]).then_inc(sem["inv_ready"], 1)
                dve.wait_ge(sem["inv_ready"], n + 1)
                dve.wait_ge(sem["o_ready"], n + 1)
                dve.wait_ge(sem["xb_ready"], n + 1)
                dve.scalar_tensor_tensor(out=r[p][:], in0=o_b[:], scalar=total[p][:, 0:1], in1=xb[p][:],
                                         op0=ALU.mult, op1=ALU.add).then_inc(sem["r_ready"], 1)
                dve.wait_ge(sem["r_ready"], n + 1)
                dve.bn_stats(stats[:], r[p][:]).then_inc(sem["step"], 1)
                wait_alone(dve, sem["step"], n * 2 + 1, keep["passed"])
                dve.bn_aggr(mv[p][:], stats[:]).then_inc(sem["step"], 1)
                dve.wait_ge(sem["step"], n * 2 + 2)
                dve.tensor_scalar(rstd[p][:], mv[p][:, 1:2], LN_EPS, None, ALU.add).then_inc(sem["var_ready"], 1)

            def norm(n, p):
                dve.wait_ge(sem["rstd_ready"], n + 1)
                dve.tensor_scalar(x[:, n, :], r[p][:], mv[p][:, 0:1], rstd[p][:, 0:1], ALU.subtract, ALU.mult)\
                   .then_inc(sem["normed"], 1)

            def slot(n, p):
                maximum(n, p)
                if within(n, -2, count):
                    norm(n - 2, p)
                if within(n, -1, count):
                    residual(n - 1, 1 - p)
                copy_pT(n, p)

            over_slots(dve, slot, count)
            norm(count - 2, 0)
            residual(count - 1, 1)
            norm(count - 1, 1)

    clear(nc, sem)


def linear(nc, d, keep, tag):
    count = SEQS
    x, ident = keep["x"], keep["ident"]
    with ExitStack() as ctx:
        sb, bank, sems = tensors(ctx, nc, tag)
        w, factor, bias = sb("w", [E, E]), sb("factor", [S, E]), sb("bias", [S, E])
        loads = [(w[:], d[tag + "_w"]), (factor[:], d[tag + "_scale"]), (bias[:], d[tag + "_bias"])]
        xin = [sb(f"xin{i}", [S, E]) for i in range(2)]
        xb = [sb(f"xb{i}", [S, E]) for i in range(2)]
        xT = [sb(f"xT{i}", [E, S]) for i in range(2)]
        y = sb("y", [S, E])
        r = [sb(f"r{i}", [S, E]) for i in range(2)]
        stats = sb("stats", [S, 6])
        mv = [sb(f"mv{i}", [S, 2]) for i in range(2)]
        rstd = [sb(f"rstd{i}", [S, 1]) for i in range(2)]
        x_b = [bank(f"x{i}", [S, S]) for i in range(2)]
        y_b = [bank(f"y{i}", [S, S]) for i in range(2)]
        sem = sems("weights setup xin_ready x_turned xT_copied y_ready scaled xb_ready r_ready step var_ready "
                   "rstd_ready normed")
        block = ctx.enter_context(nc.Block())

        @block.sync
        def _(sp):
            load_all(sp, loads, sem["weights"])

        @block.gpsimd
        def _(pool):
            pool.wait_ge(sem["weights"], 48)

            def stage_in(n, p):
                reach(pool, sem["x_turned"], n - 1)
                pool.tensor_copy(xin[p][:], x[:, n, :]).then_inc(sem["xin_ready"], 1)

            def root(n, p):
                pool.wait_ge(sem["var_ready"], n + 1)
                pool.tensor_tensor(rstd[p][:], rstd[p][:], keep["minus_half"][:], ALU.pow)\
                    .then_inc(sem["rstd_ready"], 1)

            def slot(n, p):
                reach(pool, sem["r_ready"], n - 1)
                pool.tensor_tensor(xb[p][:], x[:, n, :], bias[:], ALU.add).then_inc(sem["xb_ready"], 1)
                if within(n, 2, count):
                    stage_in(n + 2, p)
                if within(n, -1, count):
                    root(n - 1, 1 - p)

            stage_in(0, 0)
            stage_in(1, 1)
            over_slots(pool, slot, count)
            root(count - 1, 1)

        @block.tensor
        def _(pe):
            pe.wait_ge(sem["weights"], 48)

            def turn_x(n, p):
                pe.wait_ge(sem["xin_ready"], n + 1)
                reach(pe, sem["xT_copied"], n - 1)
                pe.transpose(x_b[p][:], xin[p][:], ident[:]).then_inc(sem["x_turned"], 1)

            def slot(n, p):
                if within(n, 1, count):
                    turn_x(n + 1, 1 - p)
                pe.wait_ge(sem["xT_copied"], n + 1)
                reach(pe, sem["scaled"], n - 1)
                pe.matmul(y_b[p][:], xT[p][:], w[:], start=True, stop=True).then_inc(sem["y_ready"], 1)

            turn_x(0, 0)
            over_slots(pe, slot, count)

        @block.scalar
        def _(act):
            def slot(n, p):
                act.wait_ge(sem["x_turned"], n + 1)
                reach(act, sem["y_ready"], n - 1)
                act.activation(xT[p][:], x_b[p][:], ACT.Copy).then_inc(sem["xT_copied"], 1)

            over_slots(act, slot, count)

        @block.vector
        def _(dve):
            dve.wait_ge(sem["weights"], 48)
            dve.tensor_scalar(factor[:], factor[:], 1.0 / 127.0, None, ALU.mult).then_inc(sem["setup"], 1)
            dve.wait_ge(sem["setup"], 1)

            def residual(n, p):
                dve.wait_ge(sem["y_ready"], n + 1)
                dve.tensor_tensor(y[:], y_b[p][:], factor[:], ALU.mult).then_inc(sem["scaled"], 1)
                dve.wait_ge(sem["scaled"], n + 1)
                dve.wait_ge(sem["xb_ready"], n + 1)
                dve.tensor_tensor(r[p][:], y[:], xb[p][:], ALU.add).then_inc(sem["r_ready"], 1)
                dve.wait_ge(sem["r_ready"], n + 1)
                dve.bn_stats(stats[:], r[p][:]).then_inc(sem["step"], 1)
                wait_alone(dve, sem["step"], n * 2 + 1, keep["passed"])
                dve.bn_aggr(mv[p][:], stats[:]).then_inc(sem["step"], 1)
                dve.wait_ge(sem["step"], n * 2 + 2)
                dve.tensor_scalar(rstd[p][:], mv[p][:, 1:2], LN_EPS, None, ALU.add).then_inc(sem["var_ready"], 1)

            def norm(n, p):
                dve.wait_ge(sem["rstd_ready"], n + 1)
                dve.tensor_scalar(x[:, n, :], r[p][:], mv[p][:, 0:1], rstd[p][:, 0:1], ALU.subtract, ALU.mult)\
                   .then_inc(sem["normed"], 1)

            def slot(n, p):
                residual(n, p)
                if within(n, -1, count):
                    norm(n - 1, 1 - p)

            over_slots(dve, slot, count)
            norm(count - 1, 1)

    clear(nc, sem)


def compress_blocks(nc, d, keep, tag):
    G, T, B, N = 4, 4 * S, 16, 8
    groups = SEQS // G
    x, ident = keep["x"], keep["ident"]
    with ExitStack() as ctx:
        sb, bank, sems = tensors(ctx, nc, tag)
        w = {t: sb("w" + t, [E, E]) for t in "kv"}
        wc = {t: sb("wc" + t, [E, B, E]) for t in "kv"}
        loads = [(w[t][:], d[f"l3_attn_flat{t}"]) for t in "kv"]
        loads += [(wc[t][:], d[f"l3_attn_wc{t}"]) for t in "kv"]
        xin = sb("xin", [S, G, E])
        xT = sb("xT", [E, T])
        full = {t: [sb(f"{t}{i}", [E, T]) for i in range(2)] for t in "kv"}
        x_b = bank("x", [E, T])
        f_b = {t: bank("f" + t, [E, T]) for t in "kv"}
        c_b = {t: [bank(f"c{t}{i}", [E, G * N]) for i in range(2)] for t in "kv"}
        sem = sems("weights xin_ready x_turned xT_copied full_ready k_copied v_copied k_compressed v_compressed "
                   "k_stored v_stored")
        block = ctx.enter_context(nc.Block())

        @block.sync
        def _(sp):
            load_all(sp, loads, sem["weights"])

        @block.gpsimd
        def _(pool):
            def slot(g, p):
                reach(pool, sem["x_turned"], g)
                pool.tensor_copy(xin[:], x[:, bass.ds(g * G, G), :]).then_inc(sem["xin_ready"], 1)

            over_slots(pool, slot, groups)

        @block.tensor
        def _(pe):
            pe.wait_ge(sem["weights"], 64)

            def project(g):
                pe.wait_ge(sem["xin_ready"], g + 1)
                reach(pe, sem["xT_copied"], g)
                for s in range(G):
                    mm = pe.transpose(x_b[:, s * S:(s + 1) * S], xin[:, s, :], ident[:])
                mm.then_inc(sem["x_turned"], 1)
                pe.wait_ge(sem["xT_copied"], g + 1)
                for t in "kv":
                    reach(pe, sem[t + "_copied"], g)
                    pe.matmul(f_b[t][:], w[t][:], xT[:], start=True, stop=True).then_inc(sem["full_ready"], 1)

            def slot(g, p):
                if within(g, 1, groups):
                    project(g + 1)
                for t in "kv":
                    pe.wait_ge(sem[t + "_copied"], g + 1)
                    reach(pe, sem[t + "_stored"], g - 1)
                    for b in range(B):
                        mm = pe.matmul(c_b[t][p][:], wc[t][:, b, :],
                                       full[t][p][:].rearrange("p (n b) -> p b n", b=B)[:, b, :],
                                       start=(b == 0), stop=(b == B - 1))
                    mm.then_inc(sem[t + "_compressed"], 1)

            project(0)
            over_slots(pe, slot, groups)

        @block.scalar
        def _(act):
            def copies(g, p):
                act.wait_ge(sem["x_turned"], g + 1)
                reach(act, sem["full_ready"], g * 2)
                act.activation(xT[:], x_b[:], ACT.Copy).then_inc(sem["xT_copied"], 1)
                for i, t in enumerate("kv"):
                    act.wait_ge(sem["full_ready"], g * 2 + i + 1)
                    reach(act, sem[t + "_compressed"], g - 1)
                    act.activation(full[t][p][:], f_b[t][:], ACT.Copy).then_inc(sem[t + "_copied"], 1)

            def slot(g, p):
                if within(g, 1, groups):
                    copies(g + 1, 1 - p)

            copies(0, 0)
            over_slots(act, slot, groups)

        @block.vector
        def _(dve):
            def slot(g, p):
                for t in "kv":
                    dve.wait_ge(sem[t + "_compressed"], g + 1)
                    dve.tensor_copy(keep[t + "c"][:, bass.ds(g * G, G), :],
                                    c_b[t][p][:].rearrange("p (s n) -> p s n", s=G)).then_inc(sem[t + "_stored"], 1)

            over_slots(dve, slot, groups)

    clear(nc, sem)


def sparse_attention(nc, d, keep, tag):
    count, hd, N, D = SEQS, E, 8, 8
    x, ident = keep["x"], keep["ident"]
    with ExitStack() as ctx:
        sb, bank, sems = tensors(ctx, nc, tag)
        wq, wk = sb("wq", [E, 4, E]), sb("wk", [E, 4, E])
        wflat, wv, wo = sb("wflat", [E, E]), sb("wv", [E, E]), sb("wo", [E, E])
        wg, bg = sb("wg", [E, 3]), sb("bg", [S, 3])
        own = sb("own", [E, HEADS])
        ok, low = sb("ok", [S, N]), sb("low", [S, N])
        some = sb("some", [S, 1])
        before = sb("before", [S, N, N])
        m_f = {t: sb(t + "_f", [S, S]) for t in ("causal", "band")}
        blocks_f = sb("blocks_f", [S, 4, S])
        loads = [(wq[:], d["l3_attn_wq"]), (wk[:], d["l3_attn_wk"]), (wflat[:], d["l3_attn_flatq"]),
                 (wv[:], d["l3_attn_flatv"]), (wo[:], d["l3_attn_wo"]), (wg[:], d["l3_attn_wg"]),
                 (bg[:], d["l3_attn_bg"]), (own[:], d["own"]), (ok[:], d["block_ok"]), (low[:], d["block_low"]),
                 (some[:], d["block_some"]), (before[:], d["l1_moe_before"]), (m_f["causal"][:], d["causal"]),
                 (m_f["band"][:], d["band"]), (blocks_f[:], d["blocks"])]
        mask = {t: sb(t, [S, 4, S], BF16) for t in ("causal", "band")}
        blocks = sb("blocks", [S, 4, S], BF16)
        xin = [sb(f"xin{i}", [S, E]) for i in range(2)]
        xT = [sb(f"xT{i}", [E, S]) for i in range(2)]
        qT = [sb(f"qT{i}", [E, 4, S]) for i in range(2)]
        kT = [sb(f"kT{i}", [E, 4, S]) for i in range(2)]
        v = [sb(f"v{i}", [S, E]) for i in range(2)]
        qf = sb("qf", [E, S])
        kcd, vcd = sb("kcd", [E, HEADS, N]), sb("vcd", [E, HEADS, N])
        vcT = [sb(f"vcT{i}", [HEADS * N, E]) for i in range(2)]
        logit, e = sb("logit", [S, HEADS, N]), sb("e", [S, HEADS * N + 3])
        top, gtop = sb("top", [S, HEADS]), sb("gtop", [S, 1])
        more, same = sb("more", [S, HEADS, N, N]), sb("same", [S, HEADS, N, N])
        rank = sb("rank", [S, HEADS, N])
        closed, pc = sb("closed", [S, HEADS * N]), sb("pc", [S, HEADS, N])
        gate = [sb(f"gate{i}", [S, 3]) for i in range(2)]
        pcT = [sb(f"pcT{i}", [HEADS * N, S]) for i in range(2)]
        closedT = [sb(f"closedT{i}", [HEADS * N, S], BF16) for i in range(2)]
        negmax = [sb(f"negmax{i}", [S, 4]) for i in range(2)]
        prob = [[sb(f"prob{b}{i}", [S, 4, S]) for i in range(2)] for b in range(2)]
        sums = [sb(f"sums{i}", [S, 4, 2, 4]) for i in range(2)]
        wt = [sb(f"wt{i}", [S, 2, 4]) for i in range(2)]
        local = [sb(f"local{i}", [S, 4, S]) for i in range(2)]
        mix = [sb(f"mix{i}", [S, 4, S]) for i in range(2)]
        pT = [sb(f"pT{i}", [S, 4, S]) for i in range(2)]
        o, oT = sb("o", [S, hd]), sb("oT", [E, S])
        r = [sb(f"r{i}", [S, E]) for i in range(2)]
        stats = sb("stats", [S, 6])
        mv = [sb(f"mv{i}", [S, 2]) for i in range(2)]
        rstd = [sb(f"rstd{i}", [S, 1]) for i in range(2)]
        xb = [sb(f"xb{i}", [S, E]) for i in range(2)]
        score = [bank(f"score{i}", [S, 4, S]) for i in range(2)]
        turned = [bank(f"turned{i}", [S, 4, S]) for i in range(2)]
        out_b, qk_b = bank("out", [S, 512]), bank("qk", [E, 4, S])
        misc, comp = bank("misc", [S, 512]), bank("comp", [S, 512])
        sem = sems("weights setup xin_ready x_turned xT_copied q_ready q_copied k_ready k_copied qf_ready qf_copied "
                   "kcd_ready vcd_ready cs_ready e_ready e_exp v_ready v_copied comp_ready comp_turned comp_copied "
                   "scores_ready max_ready probs_ready wt_step wt_ready local_ready mix_ready probs_turned pT_copied "
                   "pv_done o_copied o_turned oT_copied y_ready xb_ready r_ready step comp_step var_ready rstd_ready "
                   "normed")
        n_loads = 16 * len(loads)
        block = ctx.enter_context(nc.Block())

        @block.sync
        def _(sp):
            load_all(sp, loads, sem["weights"])

        @block.gpsimd
        def _(pool):
            pool.wait_ge(sem["weights"], n_loads)

            def stage_in(n, p):
                reach(pool, sem["x_turned"], n - 1)
                pool.tensor_copy(xin[p][:], x[:, n, :]).then_inc(sem["xin_ready"], 1)

            def diagonal(n):
                for t, out_t, used in (("k", kcd, "cs_ready"), ("v", vcd, "v_ready")):
                    reach(pool, sem[used], n)
                    pool.tensor_tensor(out_t[:], keep[t + "c"][:, n, :].unsqueeze(1).broadcast_to([E, HEADS, N]),
                                       copy_bcast(own[:], N), ALU.mult).then_inc(sem[t + "cd_ready"], 1)

            def weigh_local(n, a):
                u = n * 4 + a
                pool.wait_ge(sem["wt_ready"], u + 1)
                reach(pool, sem["mix_ready"], u - 1)
                pool.tensor_tensor(local[a % 2][:], prob[1][a % 2][:], copy_bcast(wt[a % 2][:, 1, :], S), ALU.mult)\
                    .then_inc(sem["local_ready"], 1)

            def root(n, p):
                pool.wait_ge(sem["var_ready"], n + 1)
                pool.tensor_tensor(rstd[p][:], rstd[p][:], keep["minus_half"][:], ALU.pow)\
                    .then_inc(sem["rstd_ready"], 1)

            def slot(n, p):
                if within(n, 1, count):
                    diagonal(n + 1)
                weigh_local(n, 0)
                if within(n, 2, count):
                    stage_in(n + 2, p)
                weigh_local(n, 1)
                reach(pool, sem["r_ready"], n - 1)
                pool.tensor_copy(xb[p][:], x[:, n, :]).then_inc(sem["xb_ready"], 1)
                weigh_local(n, 2)
                weigh_local(n, 3)
                if within(n, -1, count):
                    root(n - 1, 1 - p)

            stage_in(0, 0)
            stage_in(1, 1)
            diagonal(0)
            over_slots(pool, slot, count)
            root(count - 1, 1)

        @block.tensor
        def _(pe):
            pe.wait_ge(sem["weights"], n_loads)
            pe.wait_ge(sem["setup"], 1)

            def turn_x(n, p):
                pe.wait_ge(sem["xin_ready"], n + 1)
                reach(pe, sem["r_ready"], n - 2)
                reach(pe, sem["v_copied"], n)
                pe.transpose(misc[:, 0:S], xin[p][:], ident[:]).then_inc(sem["x_turned"], 1)

            def flat_queries(n, p):
                pe.wait_ge(sem["xT_copied"], n + 1)
                reach(pe, sem["comp_copied"], n)
                pe.matmul(comp[:, 0:S], wflat[:], xT[p][:], start=True, stop=True).then_inc(sem["qf_ready"], 1)

            def queries(n, p):
                reach(pe, sem["k_copied"], n)
                for c in range(4):
                    mm = pe.matmul(qk_b[:, c, :], wq[:, c, :], xT[p][:], start=True, stop=True)
                mm.then_inc(sem["q_ready"], 1)

            def keys_of(n, p):
                pe.wait_ge(sem["q_copied"], n + 1)
                for c in range(4):
                    mm = pe.matmul(qk_b[:, c, :], wk[:, c, :], xT[p][:], start=True, stop=True)
                mm.then_inc(sem["k_ready"], 1)

            def block_scores(n):
                pe.wait_ge(sem["qf_copied"], n + 1)
                pe.wait_ge(sem["kcd_ready"], n + 1)
                pe.matmul(comp[:, 0:S], qf[:], kcd[:].rearrange("p h n -> p (h n)"), start=True, stop=True)
                pe.matmul(comp[:, S:S + 3], qf[:], wg[:], start=True, stop=True).then_inc(sem["cs_ready"], 1)

            def values_of(n, p):
                pe.wait_ge(sem["vcd_ready"], n + 1)
                pe.wait_ge(sem["xT_copied"], n + 1)
                pe.transpose(misc[:, S:2 * S], vcd[:].rearrange("p h n -> p (h n)"), ident[:])
                pe.matmul(misc[:, 0:E], xT[p][:], wv[:], start=True, stop=True).then_inc(sem["v_ready"], 1)

            def turn_comp(n):
                pe.wait_ge(sem["comp_ready"], n + 1)
                pe.transpose(comp[:, 0:S], pc[:].rearrange("p h n -> p (h n)"), ident[:])
                pe.transpose(comp[:, S:2 * S], closed[:], ident[:]).then_inc(sem["comp_turned"], 1)

            def scores(n, p, a, b):
                u = n * 8 + 2 * a + b
                if a == 0 and b == 0:
                    pe.wait_ge(sem["q_copied"], n + 1)
                    pe.wait_ge(sem["k_copied"], n + 1)
                    pe.wait_ge(sem["comp_copied"], n + 1)
                reach(pe, sem["probs_ready"], u - 1)
                rows = slice(32 * a, 32 * a + D)
                for j in range(4):
                    pe.matmul(score[b][:, j, :], qT[p][rows, j, :], kT[p][rows, j, :], start=(j == 0), stop=False,
                              skip_group_check=True)
                if b == 0:
                    rows = slice(32 * a, 32 * a + 32)
                    pe.matmul(score[b][:], closedT[p][rows, :], blocks[rows, :, :], start=False, stop=False,
                              skip_group_check=True)
                pe.matmul(score[b][:], keep["ident_bf"][:], mask["band" if b else "causal"][:], start=False,
                          stop=True, skip_group_check=True).then_inc(sem["scores_ready"], 1)

            def turn_probs(n, a):
                u = n * 4 + a
                pe.wait_ge(sem["mix_ready"], u + 1)
                reach(pe, sem["pT_copied"], u - 1)
                for j in range(4):
                    mm = pe.transpose(turned[a % 2][:, j, :], mix[a % 2][:, j, :], ident[:])
                mm.then_inc(sem["probs_turned"], 1)

            def weigh(n, p, a):
                u = n * 4 + a
                if a == 0:
                    pe.wait_ge(sem["v_copied"], n + 1)
                    reach(pe, sem["o_copied"], n)
                    pe.matmul(out_b[:, 0:hd], pcT[p][:], vcT[p][:], start=True, stop=False, skip_group_check=True)
                pe.wait_ge(sem["pT_copied"], u + 1)
                for j in range(4):
                    h = 4 * a + j
                    mm = pe.matmul(out_b[:, h * D:(h + 1) * D], pT[a % 2][:, j, :], v[p][:, h * D:(h + 1) * D],
                                   start=False, stop=True, skip_group_check=True)
                mm.then_inc(sem["pv_done"], 1)

            def turn_o(n):
                reach(pe, sem["r_ready"], n)
                pe.wait_ge(sem["o_copied"], n + 1)
                pe.wait_ge(sem["v_copied"], min(n + 3, count) if isinstance(n, int) else n + 3)
                pe.transpose(misc[:, 0:S], o[:], ident[:]).then_inc(sem["o_turned"], 1)

            def out_product(n):
                pe.wait_ge(sem["oT_copied"], n + 1)
                pe.matmul(misc[:, 0:E], oT[:], wo[:], start=True, stop=True).then_inc(sem["y_ready"], 1)

            def slot(n, p):
                nxt = within(n, 1, count)
                scores(n, p, 0, 0)
                scores(n, p, 0, 1)
                if nxt:
                    flat_queries(n + 1, 1 - p)
                    queries(n + 1, 1 - p)
                scores(n, p, 1, 0)
                scores(n, p, 1, 1)
                if nxt:
                    block_scores(n + 1)
                    keys_of(n + 1, 1 - p)
                turn_probs(n, 0)
                scores(n, p, 2, 0)
                scores(n, p, 2, 1)
                if nxt:
                    values_of(n + 1, 1 - p)
                turn_probs(n, 1)
                weigh(n, p, 0)
                scores(n, p, 3, 0)
                scores(n, p, 3, 1)
                if within(n, -1, count):
                    turn_o(n - 1)
                turn_probs(n, 2)
                weigh(n, p, 1)
                if within(n, -1, count):
                    out_product(n - 1)
                turn_probs(n, 3)
                weigh(n, p, 2)
                if within(n, 2, count):
                    turn_x(n + 2, p)
                if nxt:
                    turn_comp(n + 1)
                weigh(n, p, 3)

            turn_x(0, 0)
            flat_queries(0, 0)
            queries(0, 0)
            block_scores(0)
            keys_of(0, 0)
            values_of(0, 0)
            turn_comp(0)
            turn_x(1, 1)
            over_slots(pe, slot, count)
            turn_o(count - 1)
            out_product(count - 1)

        @block.scalar
        def _(act):
            def copy_xT(n, p):
                act.wait_ge(sem["x_turned"], n + 1)
                reach(act, sem["v_ready"], n - 1)
                act.activation(xT[p][:], misc[:, 0:S], ACT.Copy).then_inc(sem["xT_copied"], 1)

            def copy_qf(n):
                act.wait_ge(sem["qf_ready"], n + 1)
                reach(act, sem["cs_ready"], n)
                act.activation(qf[:], comp[:, 0:S], ACT.Copy).then_inc(sem["qf_copied"], 1)

            def block_exp(n):
                act.wait_ge(sem["e_ready"], n + 1)
                act.activation(e[:], e[:], ACT.Exp).then_inc(sem["e_exp"], 1)

            def copy_v(n, p):
                act.wait_ge(sem["v_ready"], n + 1)
                reach(act, sem["pv_done"], (n - 1) * 4)
                act.activation(v[p][:], misc[:, 0:E], ACT.Copy)
                act.activation(vcT[p][:], misc[:, S:2 * S], ACT.Copy).then_inc(sem["v_copied"], 1)

            def copy_comp(n, p):
                act.wait_ge(sem["comp_turned"], n + 1)
                reach(act, sem["pv_done"], (n - 1) * 4)
                act.activation(pcT[p][:], comp[:, 0:S], ACT.Copy)
                act.activation(closedT[p][:], comp[:, S:2 * S], ACT.Copy).then_inc(sem["comp_copied"], 1)

            def exps(n, p, a, b):
                u = n * 8 + 2 * a + b
                act.wait_ge(sem["max_ready"], u + 1)
                reach(act, sem["mix_ready"], n * 4 + a - 1)
                for j in range(4):
                    i = act.activation(prob[b][a % 2][:, j, :], score[b][:, j, :], ACT.Exp,
                                       bias=negmax[b][:, j:j + 1], accum_out=sums[p][:, a, b, j:j + 1])
                i.then_inc(sem["probs_ready"], 1)

            def copy_pT(n, a):
                u = n * 4 + a
                act.wait_ge(sem["probs_turned"], u + 1)
                reach(act, sem["pv_done"], u - 1)
                act.activation(pT[a % 2][:], turned[a % 2][:], ACT.Copy).then_inc(sem["pT_copied"], 1)

            def copy_o(n):
                act.wait_ge(sem["pv_done"], (n + 1) * 4)
                reach(act, sem["o_turned"], n)
                act.activation(o[:], out_b[:, 0:hd], ACT.Copy).then_inc(sem["o_copied"], 1)

            def copy_oT(n):
                act.wait_ge(sem["o_turned"], n + 1)
                reach(act, sem["y_ready"], n)
                act.activation(oT[:], misc[:, 0:S], ACT.Copy).then_inc(sem["oT_copied"], 1)

            def slot(n, p):
                nxt = within(n, 1, count)
                exps(n, p, 0, 0)
                if within(n, -1, count):
                    copy_o(n - 1)
                exps(n, p, 0, 1)
                if nxt:
                    copy_qf(n + 1)
                exps(n, p, 1, 0)
                exps(n, p, 1, 1)
                copy_pT(n, 0)
                exps(n, p, 2, 0)
                exps(n, p, 2, 1)
                if nxt:
                    block_exp(n + 1)
                    copy_v(n + 1, 1 - p)
                copy_pT(n, 1)
                exps(n, p, 3, 0)
                if within(n, -1, count):
                    copy_oT(n - 1)
                exps(n, p, 3, 1)
                copy_pT(n, 2)
                copy_pT(n, 3)
                if within(n, 2, count):
                    copy_xT(n + 2, p)
                if nxt:
                    copy_comp(n + 1, 1 - p)

            act.wait_ge(sem["weights"], n_loads)
            copy_xT(0, 0)
            copy_qf(0)
            block_exp(0)
            copy_v(0, 0)
            copy_comp(0, 0)
            copy_xT(1, 1)
            over_slots(act, slot, count)
            copy_o(count - 1)
            copy_oT(count - 1)

        @block.vector
        def _(dve):
            dve.wait_ge(sem["weights"], n_loads)
            for t in ("causal", "band"):
                dve.tensor_copy(mask[t][:], m_f[t][:].unsqueeze(1).broadcast_to([S, 4, S]))
            dve.tensor_copy(blocks[:], blocks_f[:]).then_inc(sem["setup"], 1)

            def copy_q(n, p):
                dve.wait_ge(sem["q_ready"], n + 1)
                reach(dve, sem["scores_ready"], (n - 1) * 8)
                dve.tensor_scalar(qT[p][:], qk_b[:], D ** -0.5, None, ALU.mult).then_inc(sem["q_copied"], 1)

            def copy_k(n, p):
                dve.wait_ge(sem["k_ready"], n + 1)
                reach(dve, sem["scores_ready"], (n - 1) * 8)
                dve.tensor_copy(kT[p][:], qk_b[:]).then_inc(sem["k_copied"], 1)

            STEPS = 16

            def chain(n, k, ins):
                ins.then_inc(sem["comp_step"], 1)
                dve.wait_ge(sem["comp_step"], n * STEPS + k)

            flat_e = e[:, 0:HEADS * N].rearrange("p (h n) -> p h n", h=HEADS)
            ge = e[:, HEADS * N:HEADS * N + 3]

            def per_head(ap):
                return ap.unsqueeze(1).broadcast_to([S, HEADS, N])

            def block_logits(n):
                dve.wait_ge(sem["cs_ready"], n + 1)
                cs = comp[:, 0:S].rearrange("p (h n) -> p h n", h=HEADS)
                chain(n, 1, dve.tensor_tensor(logit[:], cs, per_head(ok[:]), ALU.mult))
                chain(n, 2, dve.scalar_tensor_tensor(out=ge, in0=comp[:, S:S + 3], scalar=1.0 / HEADS, in1=bg[:],
                                                     op0=ALU.mult, op1=ALU.add))
                chain(n, 3, dve.tensor_tensor(logit[:], logit[:], per_head(low[:]), ALU.add))
                chain(n, 4, dve.tensor_reduce(gtop[:], ge, AX.X, ALU.max, negate=True))
                chain(n, 5, dve.tensor_reduce(top[:], logit[:], AX.X, ALU.max, negate=True))
                dve.tensor_scalar(ge, ge, gtop[:, 0:1], None, ALU.add)
                dve.tensor_tensor(flat_e, logit[:], copy_bcast(top[:], N), ALU.add).then_inc(sem["e_ready"], 1)

            def ranks(n, part):
                shape = [S, HEADS, N, N]
                if part == 0:
                    dve.tensor_tensor(more[:], logit[:].unsqueeze(2).broadcast_to(shape),
                                      logit[:].unsqueeze(3).broadcast_to(shape), ALU.is_gt)
                    chain(n, 6, dve.tensor_tensor(same[:], logit[:].unsqueeze(2).broadcast_to(shape),
                                                  logit[:].unsqueeze(3).broadcast_to(shape), ALU.is_equal))
                elif part == 1:
                    chain(n, 7, dve.tensor_tensor(same[:], same[:], before[:].unsqueeze(1).broadcast_to(shape),
                                                  ALU.mult))
                    chain(n, 8, dve.tensor_tensor(more[:], more[:], same[:], ALU.add))
                else:
                    chain(n, 9, dve.tensor_reduce(rank[:], more[:], AX.X, ALU.add))
                    reach(dve, sem["comp_turned"], n)
                    chain(n, 10, dve.tensor_scalar(closed[:], rank[:].rearrange("p h n -> p (h n)"), 3.5, -2.0 ** 60,
                                                   ALU.is_gt, ALU.mult))

            def block_probs(n, p):
                dve.wait_ge(sem["e_exp"], n + 1)
                chain(n, 11, dve.tensor_reduce(gtop[:], ge, AX.X, ALU.add))
                chain(n, 12, dve.reciprocal(gtop[:], gtop[:]))
                chain(n, 13, dve.tensor_scalar(gate[p][:], ge, gtop[:, 0:1], None, ALU.mult))
                chain(n, 14, dve.tensor_reduce(top[:], flat_e, AX.X, ALU.add))
                chain(n, 15, dve.reciprocal(top[:], top[:]))
                chain(n, 16, dve.tensor_scalar(top[:], top[:], gate[p][:, 0:1], some[:, 0:1], ALU.mult, ALU.mult))
                dve.tensor_tensor(pc[:], flat_e, copy_bcast(top[:], N), ALU.mult).then_inc(sem["comp_ready"], 1)

            def maxima(n, a, b):
                u = n * 8 + 2 * a + b
                dve.wait_ge(sem["scores_ready"], u + 1)
                reach(dve, sem["probs_ready"], u - 1)
                dve.tensor_reduce(negmax[b][:], score[b][:], AX.X, ALU.max, negate=True)\
                   .then_inc(sem["max_ready"], 1)

            def mixed(n, p, a):
                u = n * 4 + a
                dve.wait_ge(sem["probs_ready"], n * 8 + 2 * a + 2)
                reach(dve, sem["local_ready"], u - 1)
                w = wt[a % 2]
                dve.reciprocal(w[:], sums[p][:, a, :, :]).then_inc(sem["wt_step"], 1)
                dve.wait_ge(sem["wt_step"], u + 1)
                dve.tensor_tensor(w[:], w[:], copy_bcast(gate[p][:, 1:3], 4), ALU.mult).then_inc(sem["wt_ready"], 1)

            def mix_sum(n, p, a):
                u = n * 4 + a
                w = wt[a % 2]
                dve.wait_ge(sem["local_ready"], u + 1)
                reach(dve, sem["probs_turned"], u - 1)
                for j in range(4):
                    i = dve.scalar_tensor_tensor(out=mix[a % 2][:, j, :], in0=prob[0][a % 2][:, j, :],
                                                 scalar=w[:, 0, j:j + 1], in1=local[a % 2][:, j, :],
                                                 op0=ALU.mult, op1=ALU.add)
                i.then_inc(sem["mix_ready"], 1)

            def residual(n, p):
                dve.wait_ge(sem["y_ready"], n + 1)
                dve.wait_ge(sem["xb_ready"], n + 1)
                dve.tensor_tensor(r[p][:], misc[:, 0:E], xb[p][:], ALU.add).then_inc(sem["r_ready"], 1)
                dve.wait_ge(sem["r_ready"], n + 1)
                dve.bn_stats(stats[:], r[p][:]).then_inc(sem["step"], 1)
                wait_alone(dve, sem["step"], n * 2 + 1, keep["passed"])
                dve.bn_aggr(mv[p][:], stats[:]).then_inc(sem["step"], 1)
                dve.wait_ge(sem["step"], n * 2 + 2)
                dve.tensor_scalar(rstd[p][:], mv[p][:, 1:2], LN_EPS, None, ALU.add).then_inc(sem["var_ready"], 1)

            def norm(n, p):
                dve.wait_ge(sem["rstd_ready"], n + 1)
                dve.tensor_scalar(x[:, n, :], r[p][:], mv[p][:, 0:1], rstd[p][:, 0:1], ALU.subtract, ALU.mult)\
                   .then_inc(sem["normed"], 1)

            def slot(n, p):
                nxt = within(n, 1, count)
                maxima(n, 0, 0)
                maxima(n, 0, 1)
                if nxt:
                    copy_q(n + 1, 1 - p)
                maxima(n, 1, 0)
                mixed(n, p, 0)
                maxima(n, 1, 1)
                if within(n, -2, count):
                    norm(n - 2, p)
                if nxt:
                    block_logits(n + 1)
                    copy_k(n + 1, 1 - p)
                mix_sum(n, p, 0)
                maxima(n, 2, 0)
                mixed(n, p, 1)
                maxima(n, 2, 1)
                if nxt:
                    ranks(n + 1, 0)
                mix_sum(n, p, 1)
                maxima(n, 3, 0)
                mixed(n, p, 2)
                maxima(n, 3, 1)
                if nxt:
                    ranks(n + 1, 1)
                mix_sum(n, p, 2)
                mixed(n, p, 3)
                if nxt:
                    ranks(n + 1, 2)
                    block_probs(n + 1, 1 - p)
                mix_sum(n, p, 3)
                if within(n, -1, count):
                    residual(n - 1, 1 - p)

            copy_q(0, 0)
            block_logits(0)
            copy_k(0, 0)
            for part in range(3):
                ranks(0, part)
            block_probs(0, 0)
            over_slots(dve, slot, count)
            norm(count - 2, 0)
            residual(count - 1, 1)
            norm(count - 1, 1)

    clear(nc, sem)


def build(nc, d, out):
    with ExitStack() as ctx:
        sb, _, sems = tensors(ctx, nc, "keep")
        keep = {"x": sb("x", [S, SEQS, E]), "ident": sb("ident", [S, S]), "ident_bf": sb("ident_bf", [S, S], BF16),
                "minus_half": sb("minus_half", [S, 1])}
        sem = sems("loaded made stored passed passed_pool")
        keep.update(passed=sem["passed"], passed_pool=sem["passed_pool"])
        with nc.Block() as block:
            @block.sync
            def _(sp):
                sp.dma_start(keep["ident"][:], d["ident"]).then_inc(sem["loaded"], 16)
                sp.dma_start(keep["x"][:], d["x"].rearrange("s p e -> p s e")).then_inc(sem["loaded"], 16)

            @block.vector
            def _(dve):
                dve.memset(keep["minus_half"][:], -0.5).then_inc(sem["made"], 1)
                dve.wait_ge(sem["loaded"], 32)
                dve.tensor_copy(keep["ident_bf"][:], keep["ident"][:]).then_inc(sem["made"], 1)

        for stage in STAGES:
            if stage == "relu_attn":
                relu_attention(nc, d, keep, stage)
            elif stage == "l1_xattn":
                one_head_attention(nc, d, keep, stage)
            elif stage == "l3_attn":
                with ExitStack() as inner:
                    sb, _, _ = tensors(inner, nc, "l3")
                    with_blocks = dict(keep, kc=sb("kc", [E, SEQS, 8]), vc=sb("vc", [E, SEQS, 8]))
                    compress_blocks(nc, d, with_blocks, "l3_compress")
                    sparse_attention(nc, d, with_blocks, stage)
            elif stage == "l3_linear":
                linear(nc, d, keep, stage)
            elif stage == "l2_attn":
                head_attention(nc, d, keep, stage, 8, 8 ** -0.5, q_bias=True, v_bias=True, causal=True, rope=True)
            elif stage == "l2_xattn":
                l2_xattn(nc, d, keep)
            elif stage == "l0_xattn":
                head_attention(nc, d, keep, stage, 8, 8 ** -0.5, cross=True, q_bias=True, v_bias=True)
            elif stage == "l0_ffn":
                feed_forward(nc, d, keep, stage, "glu", 3, ACT.Silu, scale=1.0 / 127.0, ints=True)
            elif stage == "l1_moe":
                feed_forward(nc, d, keep, stage, "plain", 36, ACT.Gelu_apprx_tanh, bias=True, out_bias=True,
                             experts=8, per_gate=4, gates=8, first_gated=4, gate_bias=True)
            elif stage == "l2_moe":
                feed_forward(nc, d, keep, stage, "glu", 10, ACT.Silu, experts=16, gates=10, shared_gate=True)
            elif stage == "l1_attn":
                head_attention(nc, d, keep, stage, 8, 32 ** -0.5, causal=True, low_rank=True)
            elif stage == "l3_xattn":
                head_attention(nc, d, keep, stage, 8, 8 ** -0.5, cross=True, out_bias=False)

        with nc.Block() as block:
            @block.sync
            def _(sp):
                sp.dma_start(out.rearrange("s p e -> p s e"), keep["x"][:]).then_inc(sem["stored"], 16)
                sp.wait_ge(sem["stored"], 16)


def l2_xattn(nc, d, keep):
    with ExitStack() as ctx:
        sb, _, _ = tensors(ctx, nc, "l2x")
        keep = dict(keep, b=sb("b", [S, SEQS, E]), z=sb("z", [S, SEQS, E]))
        renormalise(nc, d, keep, "l2x_ln1", keep["x"])
        head_attention(nc, d, keep, "l2x_a1", 32, 32 ** -0.5, future_only=True, src=keep["z"], affine=True,
                       dst="sum_and_norm")
        feed_forward(nc, d, keep, "l2x_f1", "plain", 4, ACT.Gelu, bias=True, out_bias=True, src=keep["z"],
                     affine=True, dst="store")
        renormalise(nc, d, keep, "l2x_ln2", keep["b"])
        with ExitStack() as inner:
            sb, _, _ = tensors(inner, nc, "l2x")
            with_ctx = dict(keep, ctxn=sb("ctxn", [C, SEQS, CTX]))
            normalise_context(nc, d, with_ctx, "l2x_ctx")
            head_attention(nc, d, with_ctx, "l2x_a2", 32, 32 ** -0.5, cross=True, src=keep["z"], affine=True,
                           dst="sum_and_norm")
        feed_forward(nc, d, keep, "l2x_f2", "plain", 4, ACT.Gelu, bias=True, out_bias=True, src=keep["z"],
                     affine=True, dst="norm_with_x")


def layouts(i):
    f = np.float32

    def chunked(w, width=8, at=0, rows=None):
        w = np.asarray(w)
        out = np.zeros((w.shape[0], 4, 4, 32), w.dtype)
        out[:, :, :, at:at + width] = w.reshape(w.shape[0], 4, 4, width).transpose(0, 2, 1, 3)
        return out.reshape(w.shape[0], 4, 128)

    def chunked_bias(b):
        out = np.zeros((4, 4, 32), np.asarray(b).dtype)
        out[:, :, 0:8] = np.asarray(b).reshape(4, 4, 8).transpose(1, 0, 2)
        return np.ascontiguousarray(out.reshape(4, 128).T)

    def rows(b, n=128):
        b = np.asarray(b)
        return np.ascontiguousarray(np.broadcast_to(b.reshape(1, -1), (n, b.size)))

    def cols(b):
        b = np.asarray(b)
        return np.ascontiguousarray(np.broadcast_to(b.reshape(-1, 1), (b.size, 128)))

    def T(w):
        return np.ascontiguousarray(np.asarray(w).T)

    g = {}
    g["ident"] = np.eye(128, dtype=f)
    key = np.arange(128)
    big = np.float32(-2.0 ** 60)
    g["causal"] = np.where(key[None, :] > key[:, None], big, np.float32(0)).astype(f)
    g["future"] = (key[:, None] > key[None, :]).astype(f)
    g["x"] = np.asarray(i["x"])
    g["ctxT"] = np.ascontiguousarray(np.asarray(i["ctx_512"]).transpose(0, 2, 1))
    for n, p in (("l0_xattn", "L0_xattn_"),):
        g[n + "_wq0"] = chunked(i[p + "Wq"])
        g[n + "_wk0"] = chunked(i[p + "Wk"])
        g[n + "_wv"] = np.asarray(i[p + "Wv"])
        g[n + "_wo"] = np.asarray(i[p + "Wo"]).reshape(128, 1, 128)
        g[n + "_bq"] = chunked_bias(i[p + "bq"])
        g[n + "_bk"] = chunked_bias(i[p + "bk"])
        g[n + "_bv"] = cols(i[p + "bv"])
        g[n + "_bo"] = rows(i[p + "bo"])
    n, p = "l1_attn", "L1_attn_"
    g[n + "_wq0"] = chunked(T(i[p + "Wq2"]))
    g[n + "_wq0"].reshape(128, 4, 4, 32)[:, :, :, 8:12] = T(i[p + "Wq1"]).reshape(128, 4, 4, 4).transpose(0, 2, 1, 3)
    g[n + "_wk0"] = chunked(T(i[p + "Wk1"]), 4, 8)
    g[n + "_wk1"] = chunked(T(i[p + "Wk2"]))
    g[n + "_wv"], g[n + "_wo"] = T(i[p + "Wv"]), T(i[p + "Wo"]).reshape(128, 1, 128)
    g[n + "_bo"] = rows(i[p + "bo"])
    n, p = "l3_xattn", "L3_xattn_"
    g[n + "_wq0"] = chunked(T(i[p + "Wq"]))
    kv = T(i[p + "Wkv"])
    g[n + "_wk0"] = chunked(kv[:, 0:128])
    g[n + "_wv"] = np.ascontiguousarray(kv[:, 128:256])
    g[n + "_wo"] = T(i[p + "Wo"]).reshape(128, 1, 128)

    def chunks(w):
        return np.ascontiguousarray(w.reshape(w.shape[0], -1, 128))

    def stacked(w):
        return np.ascontiguousarray(w.reshape(-1, 128, w.shape[1]).transpose(1, 0, 2))

    n, p = "l0_ffn", "L0_ffn_"
    g[n + "_wu"], g[n + "_wv"] = chunks(T(i[p + "w_gate"])), chunks(T(i[p + "w_up"]))
    g[n + "_wd"] = stacked(T(i[p + "w_down"]))
    n, p = "l1_moe", "L1_ffn_"
    g[n + "_wu"] = chunks(np.concatenate([i[p + "Wfc_s"], *np.asarray(i[p + "Wfc"])], 1))
    g[n + "_bu"] = np.concatenate([i[p + "bfc_s"], np.asarray(i[p + "bfc"]).ravel()]).reshape(-1, 128).T
    g[n + "_wd"] = stacked(np.concatenate([i[p + "Wproj_s"], *np.asarray(i[p + "Wproj"])], 0))
    g[n + "_bd"], g[n + "_gb"], g[n + "_wr"] = rows(i[p + "bproj_s"]), i[p + "bproj"], i[p + "Wr"]
    g[n + "_sel"] = np.repeat(np.eye(8, dtype=f)[:, :, None], 128, 2)
    e = np.arange(8)
    g[n + "_before"] = np.tile((e[None, :] < e[:, None]).astype(f), (128, 1, 1))
    n, p = "l2_moe", "L2_ffn_"
    for t, w in (("_wu", "gate"), ("_wv", "up")):
        g[n + t] = chunks(T(np.concatenate([np.asarray(i[f"{p}We_{w}"]).reshape(1024, 128), i[f"{p}Ws_{w}"]], 0)))
    g[n + "_wd"] = stacked(np.concatenate([np.asarray(i[p + "We_down"]).transpose(0, 2, 1).reshape(1024, 128),
                                           T(i[p + "Ws_down"])], 0))
    g[n + "_wr"] = T(np.concatenate([i[p + "Wg"], i[p + "Wsg"]], 0))
    sel = np.zeros((17, 10, 128), f)
    for k in range(16):
        sel[k, k // 2, 64 * (k % 2):64 * (k % 2) + 64] = 1
    sel[16, 8:10] = 1
    g[n + "_sel"] = sel
    e = np.arange(16)
    g[n + "_before"] = np.tile((e[None, :] < e[:, None]).astype(f), (128, 1, 1))
    n, p = "relu_attn", "L0_attn_"
    for t in "qkvo":
        g[f"{n}_w{t}"], g[f"{n}_b{t}"] = T(i[f"{p}W{t}"]), rows(i[f"{p}b{t}"])
    g[n + "_weight"], g[n + "_gain"] = rows(i[p + "norm_weight"]), rows(i[p + "norm_gate"])
    for t in ("key", "value"):
        g[f"{n}_{t}T"] = T(np.asarray(i[p + t]).reshape(512, 128)).reshape(128, 4, 128)
    n, p = "l1_xattn", "L1_xattn_"
    for t in "qkv":
        g[f"{n}_w{t}"] = i[f"{p}W{t}"]
    g[n + "_bq"], g[n + "_bk"] = np.asarray(i[p + "bq"]).reshape(128, 1), np.asarray(i[p + "bk"]).reshape(128, 1)
    g[n + "_bv"] = rows(i[p + "bv"])
    n, p = "l3_linear", "L3_ffn_"
    g[n + "_w"], g[n + "_scale"], g[n + "_bias"] = T(i[p + "CB"]), rows(i[p + "SCB"]), rows(i[p + "bias"])
    n, p = "l2_attn", "L2_attn_"
    swap = np.arange(128) ^ 1
    for t in "qk":
        w, b = np.asarray(i[f"{p}W{t}"]), np.asarray(i[f"{p}b{t}"])
        g[f"{n}_w{t}0"], g[f"{n}_w{t}1"] = chunked(w), chunked(w[:, swap])
        g[f"{n}_b{t}0"], g[f"{n}_b{t}1"] = chunked_bias(b), chunked_bias(b[swap])
    freq = f(1.0) / f(10000.0) ** (np.arange(4, dtype=f) * f(2.0) / f(8))
    angle = np.arange(128, dtype=f)[None, :] * freq[:, None]
    pair = (np.arange(128) % 8) // 2
    g["cos"] = np.cos(angle)[pair].astype(f)
    g["sin"] = (np.sin(angle)[pair] * np.where(np.arange(128) % 2, f(1), f(-1))[:, None]).astype(f)
    g[n + "_wv"], g[n + "_wo"] = i[p + "Wv"], np.asarray(i[p + "Wp"]).reshape(128, 1, 128)
    g[n + "_bv"], g[n + "_bo"] = cols(i[p + "bv"]), rows(i[p + "bp"])
    g["ctx"] = i["ctx_512"]
    n, p = "l3_attn", "L3_attn_"
    g[n + "_wq"], g[n + "_wk"] = chunked(i[p + "Wq"]), chunked(i[p + "Wk"])
    for t in "qkv":
        g[f"{n}_flat{t}"] = i[f"{p}W{t}"]
    for t in "kv":
        w = np.asarray(i[f"{p}Wc{t}"]).reshape(16, 8, 8)
        wide = np.zeros((16, 8, 16, 16, 8), w.dtype)
        for h in range(16):
            wide[h, :, :, h, :] = w.transpose(1, 0, 2)
        g[f"{n}_wc{t}"] = wide.reshape(128, 16, 128)
    g[n + "_wo"] = i[p + "Wo"]
    g[n + "_wg"], g[n + "_bg"] = np.tile(np.asarray(i[p + "Wg"]), (16, 1)), rows(i[p + "bg"])
    g["own"] = np.repeat(np.eye(16, dtype=f), 8, 0)
    done = key[:, None] >= (np.arange(8)[None, :] + 1) * 16
    g["block_ok"] = np.where(done, f(1.0 / np.sqrt(8.0)), f(0))
    g["block_low"] = np.where(done, f(0), f(-1e9))
    g["block_some"] = done.any(1, keepdims=True).astype(f)
    back = key[:, None] - key[None, :]
    g["band"] = np.where((back >= 0) & (back <= 32), f(0), big).astype(f)
    row = np.arange(128)
    g["blocks"] = ((row[:, None, None] % 32 // 8 == np.arange(4)[None, :, None])
                   & (row[:, None, None] % 8 == key[None, None, :] // 16)).astype(f)
    for a, c in (("a1", 128), ("a2", 64)):
        n, p = "l2x_" + a, f"L2_xattn_{a}_"
        flat = {t: np.asarray(i[f"{p}w{t}"]).transpose(1, 0, 2).reshape(-1, 512) for t in "qkv"}
        g[n + "_wq0"], g[n + "_wk0"], g[n + "_wv"] = chunked(flat["q"], 32), chunked(flat["k"], 32), flat["v"]
        g[n + "_wo"], g[n + "_bo"] = stacked(np.asarray(i[p + "li1_w"])), rows(i[p + "li1_b"])
        aff = np.zeros((128, 4), f)
        aff[:, 0], aff[:, 1] = i[p + "lnx_g"], i[p + "lnx_b"]
        aff[0:c, 2], aff[0:c, 3] = i[p + "lny_g"], i[p + "lny_b"]
        g[n + "_aff"] = aff
        if a == "a2":
            g["l2x_ctx_aff"] = aff[0:64, 2:4]
        m = "l2x_f" + a[1]
        g[m + "_wu"], g[m + "_wd"] = chunks(np.asarray(i[p + "li2_w"])), stacked(np.asarray(i[p + "li3_w"]))
        g[m + "_bu"], g[m + "_bd"] = np.asarray(i[p + "li2_b"]).reshape(4, 128).T, rows(i[p + "li3_b"])
        g[m + "_aff"] = np.stack([i[p + "ln3_g"], i[p + "ln3_b"]], 1)
        g[f"l2x_ln{a[1]}_gain"] = rows(i[f"L2_xattn_ln{a[1]}_g"])
        g[f"l2x_ln{a[1]}_shift"] = rows(i[f"L2_xattn_ln{a[1]}_b"])
    return g


def kernel(**inputs):
    import concourse.bacc as bacc
    from concourse.bass_utils import run_bass_kernel_spmd as run

    nc = bacc.Bacc("TRN2", target_bir_lowering=False, num_devices=1)
    arrays = {f"in_{n}": np.ascontiguousarray(a) for n, a in layouts(inputs).items()}
    d = {n[3:]: nc.dram_tensor(n, a.shape, mybir.dt.from_np(a.dtype), kind="ExternalInput").ap()
         for n, a in arrays.items()}
    out = nc.dram_tensor("out", (SEQS, S, E), F32, kind="ExternalOutput").ap()
    build(nc, d, out)
    return run(nc, [arrays], core_ids=[0]).results[0]["out"]
```

```python
from contextlib import ExitStack

import numpy as np

import concourse.bass as bass
from concourse import mybir

ALU = mybir.AluOpType
ACT = mybir.ActivationFunctionType
AX = mybir.AxisListType
F32 = mybir.dt.float32
BF16 = mybir.dt.bfloat16
I32 = mybir.dt.int32

SEQS, S, E, C = 64, 128, 128, 64
CTX = 77
HEADS = 16
LN_EPS = 1e-5
STAGES = ("relu_attn", "l0_xattn", "l0_ffn", "l1_attn", "l1_xattn", "l1_moe", "l2_attn", "l2_xattn",
          "l2_moe", "l3_attn", "l3_xattn", "l3_linear")


def tensors(ctx, nc, tag):
    def sb(name, shape, dt=F32):
        return ctx.enter_context(nc.sbuf_tensor(f"{tag}_{name}", shape, dt))

    def bank(name, shape, dt=F32):
        return ctx.enter_context(nc.psum_tensor(f"{tag}_{name}", shape, dt))

    def sems(names):
        return {n: ctx.enter_context(nc.semaphore(f"{tag}_{n}")) for n in names.split()}

    return sb, bank, sems


def clear(nc, sem):
    with nc.Block() as block:
        @block.gpsimd
        def _(pool):
            for s in sem.values():
                pool.sem_clear(s)


def over_slots(eng, slot, count):
    slot(0, 0)
    slot(1, 1)
    with eng.Fori(1, count // 2 - 1) as i:
        slot(i * 2, 0)
        slot(i * 2 + 1, 1)
    slot(count - 2, 0)
    slot(count - 1, 1)


def within(n, ahead, count):
    return not isinstance(n, int) or 0 <= n + ahead < count


def reach(eng, sem, value):
    if not isinstance(value, int) or value > 0:
        eng.wait_ge(sem, value)


def wait_alone(eng, sem, value, passed):
    reach(eng, sem, value)
    eng.sem_inc(passed, 1)


def load_all(sp, pairs, sem):
    for dst, src in pairs:
        sp.dma_start(dst, src).then_inc(sem, 16)


def copy_bcast(ap, n):
    return ap.unsqueeze(2).broadcast_to([ap.shape[0], ap.shape[1], n])


def head_attention(nc, d, keep, tag, head_dim, scale, *, cross=False, q_bias=False, v_bias=False,
                   out_bias=True, causal=False, future_only=False, low_rank=False, rope=False, src=None,
                   affine=None, dst="norm", count=None):
    count = SEQS if count is None else count
    keys = CTX if cross else S
    hd = HEADS * head_dim
    in_k = C if cross else E
    k_parts = 2 if low_rank or rope else 1
    q_parts = 2 if rope else 1
    rows = 12 if low_rank else head_dim
    before, after = {0: [("q", 0)], 2: [("k", 0)]}, {}
    if low_rank:
        before, after = {0: [("q", 0)], 1: [("k", 1)]}, {0: [("k", 0)]}
    if rope:
        before, after = {0: [("q", 0), ("k", 0)]}, {0: [("q", 1), ("k", 1)]}
    first_parts = [part for c in range(4) for part in before.get(c, []) + after.get(c, [])]
    x, ident = keep["x"], keep["ident"]
    src = x if src is None else src
    o_chunks = hd // E
    ctx_copy = "ctxn" in keep and cross and affine is not None
    with ExitStack() as ctx:
        sb, bank, sems = tensors(ctx, nc, tag)
        wq = [sb(f"wq{i}", [E, 4, E]) for i in range(q_parts)]
        wk = [sb(f"wk{i}", [in_k, 4, E]) for i in range(k_parts)]
        wv = sb("wv", [in_k, hd])
        wo = sb("wo", [E, o_chunks, E])
        bias = sb("bias", [S, E])
        loads = [(wv[:], d[tag + "_wv"]), (wo[:], d[tag + "_wo"])]
        loads += [(wq[i][:], d[f"{tag}_wq{i}"]) for i in range(q_parts)]
        loads += [(wk[i][:], d[f"{tag}_wk{i}"]) for i in range(k_parts)]
        if out_bias:
            loads += [(bias[:], d[tag + "_bo"])]
        if rope:
            rb = [[sb(f"rb{t}{i}", [E, 4]) for i in range(2)] for t in "qk"]
            tables = [[sb(f"{n}{t}", [E, S]) for n in ("cos", "sin")] for t in "qk"]
            rotated = [sb(f"rotated{t}", [E, 4, S]) for t in "qk"]
            terms = [[sb(f"term{t}{i}", [E, 4, S]) for i in range(2)] for t in "qk"]
            for t in range(2):
                loads += [(rb[t][i][:], d[f"{tag}_b{'qk'[t]}{i}"]) for i in range(2)]
                loads += [(tables[t][i][:], d[("cos", "sin")[i]]) for i in range(2)]
        elif q_bias:
            qb, kb = sb("qb", [E, 4]), sb("kb", [E, 4])
            qbs = sb("qbs", [E, 4])
            loads += [(qb[:], d[tag + "_bq"]), (kb[:], d[tag + "_bk"])]
        if v_bias:
            vb = sb("vb", [E, S])
            loads += [(vb[:], d[tag + "_bv"])]
        if affine is not None:
            aff = sb("aff", [E, 4])
            loads += [(aff[:], d[tag + "_aff"])]
        if causal:
            mask = sb("mask", [S, 4, S], BF16)
            mask_f = sb("mask_f", [S, S])
            loads += [(mask_f[:], d["causal"])]
        if low_rank:
            mask2 = sb("mask2", [S, 4, S], BF16)
        if future_only:
            future = sb("future", [S, S])
            loads += [(future[:], d["future"])]
        xin = [sb(f"xin{i}", [S, E]) for i in range(2)]
        xT = [sb(f"xT{i}", [E, S]) for i in range(2)]
        kin = [sb(f"kin{i}", [in_k, keys]) for i in range(2)] if (cross or affine is not None) else xT
        qT = [sb(f"qT{i}", [E, 4, S]) for i in range(2)]
        kT = [[sb(f"kT{j}_{i}", [E, 4, keys]) for i in range(2)] for j in range(2 if low_rank else 1)]
        v = [sb(f"v{i}", [keys, hd]) for i in range(2)]
        negmax = [sb(f"negmax{i}", [S, 4]) for i in range(2)]
        prob = [sb(f"prob{i}", [S, 4, keys]) for i in range(2)]
        sums = [sb(f"sums{i}", [S, HEADS]) for i in range(2)]
        inv = sb("inv", [S, HEADS])
        pT = [sb(f"pT{i}", [keys, 4, S]) for i in range(2)]
        o = sb("o", [S, hd])
        oT = sb("oT", [E, o_chunks, S])
        xb = [sb(f"xb{i}", [S, E]) for i in range(2)]
        r = [sb(f"r{i}", [S, E]) for i in range(2)]
        stats = sb("stats", [S, 6])
        mv = [sb(f"mv{i}", [S, 2]) for i in range(2)]
        rstd = [sb(f"rstd{i}", [S, 1]) for i in range(2)]
        if low_rank:
            a1 = [sb(f"a1{i}", [S, 4, S]) for i in range(2)]
            prod = [sb(f"prod{i}", [S, 4, S]) for i in range(2)]
        score = [bank(f"score{i}", [S, 4, S]) for i in range(2)]
        turned = [bank(f"turned{i}", [S, 4, S]) for i in range(2)]
        out_b = bank("out", [S, 512])
        q_b = bank("q", [E, 4, S])
        k_b = bank("k", [E, 4, S])
        misc = bank("misc", [S, 512])
        sem = sems("weights setup bias_ready xin_ready x_turned xT_copied ctx_loaded0 ctx_loaded1 ctx_copied q_ready q_copied k_ready "
                   "k_copied v_ready v_copied a1_ready a1_copied prod_ready scores_ready max_ready "
                   "probs_ready probs_turned pT_copied pv_done inv_ready o_ready o_turned oT_copied "
                   "roped y_ready xb_ready r_ready stats_ready mv_ready rstd_ready normed sum_stored var_ready")
        n_loads = 16 * len(loads)
        block = ctx.enter_context(nc.Block())

        @block.sync
        def _(sp):
            load_all(sp, loads, sem["weights"])
            if cross and not ctx_copy:
                def slot(n, p):
                    reach(sp, sem["v_ready"], n - 1)
                    reach(sp, sem["k_ready"], (n - 1) * k_parts)
                    sp.dma_start(kin[p][:], d["ctxT"][n]).then_inc(sem[f"ctx_loaded{p}"], 16)

                over_slots(sp, slot, count)

        @block.gpsimd
        def _(pool):
            pool.wait_ge(sem["weights"], n_loads)

            def stage_in(n, p):
                reach(pool, sem["x_turned"], n - 1)
                pool.tensor_copy(xin[p][:], src[:, n, :]).then_inc(sem["xin_ready"], 1)
                if ctx_copy:
                    reach(pool, sem["v_ready"], n - 1)
                    reach(pool, sem["k_ready"], (n - 1) * k_parts)
                    pool.tensor_copy(kin[p][:], keep["ctxn"][:, n, :]).then_inc(sem["ctx_copied"], 1)

            def root(n, p):
                pool.wait_ge(sem["var_ready"], n + 1)
                pool.tensor_tensor(rstd[p][:], rstd[p][:], keep["minus_half"][:], ALU.pow)\
                    .then_inc(sem["rstd_ready"], 1)

            def rope_sums(n, p):
                for t, out_t in enumerate((qT, kT[0])):
                    pool.wait_ge(sem["q_copied" if t == 0 else "k_copied"], (n + 1) * 2)
                    reach(pool, sem["scores_ready"], (n - 1) * 4)
                    pool.tensor_tensor(out_t[p][:], terms[t][0][:], terms[t][1][:], ALU.add)\
                        .then_inc(sem["roped"], 1)
                    pool.wait_ge(sem["roped"], n * 4 + 2 * t + 1)
                    pool.tensor_tensor(out_t[p][:], out_t[p][:], rotated[t][:], ALU.add)\
                        .then_inc(sem["roped"], 1)

            def store_sum(n, p):
                wait_alone(pool, sem["r_ready"], n + 1, keep["passed_pool"])
                pool.tensor_tensor(keep["b"][:, n, :], keep["b"][:, n, :], r[p][:], ALU.add)\
                    .then_inc(sem["sum_stored"], 1)

            def slot(n, p):
                if within(n, 2, count):
                    stage_in(n + 2, p)
                if within(n, -2, count):
                    root(n - 2, p)
                    if dst == "sum_and_norm":
                        store_sum(n - 2, p)
                if rope and within(n, 1, count):
                    rope_sums(n + 1, 1 - p)
                if isinstance(n, int) and n == 0:
                    pool.wait_ge(sem["bias_ready"], 1)
                reach(pool, sem["r_ready"], n - 1)
                res = x if dst == "norm" else keep["b"]
                pool.tensor_tensor(xb[p][:], res[:, n, :], bias[:], ALU.add).then_inc(sem["xb_ready"], 1)

            stage_in(0, 0)
            stage_in(1, 1)
            if rope:
                rope_sums(0, 0)
            over_slots(pool, slot, count)
            for n in (count - 2, count - 1):
                root(n, n % 2)
                if dst == "sum_and_norm":
                    store_sum(n, n % 2)

        @block.tensor
        def _(pe):
            pe.wait_ge(sem["weights"], n_loads)
            pe.wait_ge(sem["setup"], 1)

            def turn_x(n, p):
                pe.wait_ge(sem["xin_ready"], n + 1)
                reach(pe, sem["r_ready"], n - 3)
                reach(pe, sem["v_copied"], n - 1)
                pe.transpose(misc[:, 0:S], xin[p][:], ident[:]).then_inc(sem["x_turned"], 1)

            def project(n, p, what, part):
                if what == "q":
                    dst_b, w, rhs, parts, width = q_b, wq[part], xT[p], q_parts, S
                else:
                    dst_b, w, rhs, parts, width = k_b, wk[part], kin[p], k_parts, keys
                if what == "q" or not cross:
                    pe.wait_ge(sem["xT_copied"], n + 1)
                elif ctx_copy:
                    pe.wait_ge(sem["ctx_copied"], n + 1)
                else:
                    pe.wait_ge(sem[f"ctx_loaded{p}"], (n - p) * 8 + 16)
                reach(pe, sem[what + "_copied"], n * parts + part)
                for c in range(4):
                    mm = pe.matmul(dst_b[:, c, 0:width], w[:, c, :], rhs[:], start=True, stop=True)
                mm.then_inc(sem[what + "_ready"], 1)

            def project_v(n, p):
                reach(pe, sem["r_ready"], n - 2)
                pe.wait_ge(sem["xT_copied"], min(n + 2, count) if isinstance(n, int) else n + 2)
                if cross and ctx_copy:
                    pe.wait_ge(sem["ctx_copied"], n + 1)
                elif cross:
                    pe.wait_ge(sem[f"ctx_loaded{p}"], (n - p) * 8 + 16)
                pe.matmul(misc[0:keys, 0:hd], kin[p][:], wv[:], start=True, stop=True).then_inc(sem["v_ready"], 1)

            def scores(n, p, c):
                u = n * 4 + c
                if c == 0 and rope:
                    pe.wait_ge(sem["roped"], (n + 1) * 4)
                elif c == 0:
                    pe.wait_ge(sem["q_copied"], n + 1)
                    pe.wait_ge(sem["k_copied"], (n + 1) * k_parts)
                if low_rank:
                    reach(pe, sem["a1_copied"], u)
                else:
                    reach(pe, sem["probs_ready"], u - 1)
                first = score[0] if low_rank else score[c % 2]
                for j in range(4):
                    mm = pe.matmul(first[:, j, 0:keys], qT[p][32 * c:32 * c + rows, j, :],
                                   kT[0][p][32 * c:32 * c + rows, j, :], start=(j == 0),
                                   stop=(j == 3 and not causal), skip_group_check=True)
                if causal:
                    mm = pe.matmul(first[:, :, :], keep["ident_bf"][:], mask[:], start=False, stop=True,
                                   skip_group_check=True)
                mm.then_inc(sem["a1_ready" if low_rank else "scores_ready"], 1)
                if low_rank:
                    reach(pe, sem["prod_ready"], u)
                    for j in range(4):
                        pe.matmul(score[1][:, j, :], qT[p][32 * c:32 * c + rows, j, :],
                                  kT[1][p][32 * c:32 * c + rows, j, :], start=(j == 0), stop=False,
                                  skip_group_check=True)
                    pe.matmul(score[1][:, :, :], keep["ident_bf"][:], mask2[:], start=False, stop=True,
                              skip_group_check=True).then_inc(sem["scores_ready"], 1)

            def turn_probs(n, p, c):
                u = n * 4 + c
                pe.wait_ge(sem["probs_ready"], u + 1)
                reach(pe, sem["pT_copied"], u - 1)
                for j in range(4):
                    mm = pe.transpose(turned[c % 2][0:keys, j, :], prob[c % 2][:, j, :], ident[:])
                mm.then_inc(sem["probs_turned"], 1)

            def weigh(n, p, c):
                u = n * 4 + c
                pe.wait_ge(sem["pT_copied"], u + 1)
                if c == 0:
                    pe.wait_ge(sem["v_copied"], n + 1)
                    reach(pe, sem["o_ready"], n)
                for j in range(4):
                    h = 4 * c + j
                    mm = pe.matmul(out_b[:, h * head_dim:(h + 1) * head_dim], pT[c % 2][:, j, :],
                                   v[p][:, h * head_dim:(h + 1) * head_dim], start=True, stop=True)
                mm.then_inc(sem["pv_done"], 1)

            def turn_o(n, p):
                pe.wait_ge(sem["o_ready"], n + 1)
                reach(pe, sem["r_ready"], n)
                pe.wait_ge(sem["v_copied"], min(n + 3, count) if isinstance(n, int) else n + 3)
                for c in range(o_chunks):
                    mm = pe.transpose(misc[:, c * S:(c + 1) * S], o[:, c * E:(c + 1) * E], ident[:])
                mm.then_inc(sem["o_turned"], 1)

            def out_product(n, p):
                pe.wait_ge(sem["oT_copied"], n + 1)
                for c in range(o_chunks):
                    mm = pe.matmul(misc[:, 0:E], oT[:, c, :], wo[:, c, :], start=(c == 0), stop=(c == o_chunks - 1))
                mm.then_inc(sem["y_ready"], 1)

            def step(n, p, c):
                nxt = within(n, 1, count)
                if c < 3:
                    scores(n, p, c + 1)
                elif nxt:
                    scores(n + 1, 1 - p, 0)
                if c == 0 and within(n, 2, count):
                    turn_x(n + 2, p)
                if c == 1 and nxt:
                    project_v(n + 1, 1 - p)
                for what, part in before.get(c, []) if nxt else []:
                    project(n + 1, 1 - p, what, part)
                if c == 2 and within(n, -1, count):
                    turn_o(n - 1, 1 - p)
                if c == 3 and within(n, -1, count):
                    out_product(n - 1, 1 - p)
                turn_probs(n, p, c)
                for what, part in after.get(c, []) if nxt else []:
                    project(n + 1, 1 - p, what, part)
                if c > 0:
                    weigh(n, p, c - 1)
                elif within(n, -1, count):
                    weigh(n - 1, 1 - p, 3)

            def slot(n, p):
                for c in range(4):
                    step(n, p, c)

            if v_bias:
                pe.matmul(misc[:, 0:E], vb[:], wo[:, 0, :], start=True, stop=True).then_inc(sem["y_ready"], 1)
                pe.wait_ge(sem["bias_ready"], 1)
            turn_x(0, 0)
            pe.wait_ge(sem["xT_copied"], 1)
            turn_x(1, 1)
            for what, part in first_parts:
                project(0, 0, what, part)
            project_v(0, 0)
            scores(0, 0, 0)
            over_slots(pe, slot, count)
            weigh(count - 1, 1, 3)
            turn_o(count - 1, 1)
            out_product(count - 1, 1)

        y0 = 1 if v_bias else 0

        @block.scalar
        def _(act):
            act.wait_ge(sem["weights"], n_loads)

            def copy_xT(n, p):
                pe_count = n + 1
                act.wait_ge(sem["x_turned"], pe_count)
                reach(act, sem["v_ready"], n - 1)
                reach(act, sem["q_ready"], (n - 1) * q_parts)
                if not cross:
                    reach(act, sem["k_ready"], (n - 1) * k_parts)
                if affine is None:
                    act.activation(xT[p][:], misc[:, 0:S], ACT.Copy).then_inc(sem["xT_copied"], 1)
                else:
                    if not cross:
                        act.activation(kin[p][:], misc[:, 0:S], ACT.Identity, scale=aff[:, 2:3], bias=aff[:, 3:4])
                    act.activation(xT[p][:], misc[:, 0:S], ACT.Identity, scale=aff[:, 0:1], bias=aff[:, 1:2])\
                       .then_inc(sem["xT_copied"], 1)

            def copy_v(n, p):
                act.wait_ge(sem["v_ready"], n + 1)
                reach(act, sem["pv_done"], (n - 1) * 4)
                act.activation(v[p][:], misc[0:keys, 0:hd], ACT.Copy).then_inc(sem["v_copied"], 1)

            def copy_oT(n, p):
                act.wait_ge(sem["o_turned"], n + 1)
                reach(act, sem["y_ready"], n + y0)
                act.activation(oT[:], misc[:, 0:hd].rearrange("p (c s) -> p c s", c=o_chunks), ACT.Copy)\
                   .then_inc(sem["oT_copied"], 1)

            def copy_a1(n, p, c):
                u = n * 4 + c
                act.wait_ge(sem["a1_ready"], u + 1)
                reach(act, sem["prod_ready"], u - 1)
                act.activation(a1[c % 2][:], score[0][:], ACT.Copy, scale=scale).then_inc(sem["a1_copied"], 1)

            def exps(n, p, c):
                u = n * 4 + c
                act.wait_ge(sem["max_ready"], u + 1)
                reach(act, sem["probs_turned"], u - 1)
                if c == 0:
                    reach(act, sem["inv_ready"], n - 1)
                logits = prod[c % 2] if low_rank else score[c % 2]
                for j in range(4):
                    e = act.activation(prob[c % 2][:, j, :], logits[:, j, 0:keys], ACT.Exp,
                                       bias=negmax[c % 2][:, j:j + 1],
                                       accum_out=sums[p][:, 4 * c + j:4 * c + j + 1])
                e.then_inc(sem["probs_ready"], 1)

            def next_unit(n, p, c):
                if c < 3:
                    return (n, p, c + 1)
                return (n + 1, 1 - p, 0) if within(n, 1, count) else None

            def slot(n, p):
                for c in range(4):
                    unit = next_unit(n, p, c)
                    if low_rank and unit:
                        copy_a1(*unit)
                    if c == 0 and within(n, 2, count):
                        copy_xT(n + 2, p)
                    if c == 1 and within(n, 1, count):
                        copy_v(n + 1, 1 - p)
                    if unit:
                        exps(*unit)
                    if c == 2 and within(n, -1, count):
                        copy_oT(n - 1, 1 - p)

            copy_xT(0, 0)
            copy_xT(1, 1)
            copy_v(0, 0)
            if low_rank:
                copy_a1(0, 0, 0)
            exps(0, 0, 0)
            over_slots(act, slot, count)
            copy_oT(count - 1, 1)

        @block.vector
        def _(dve):
            dve.wait_ge(sem["weights"], n_loads)
            if causal:
                for j in range(4):
                    dve.tensor_copy(mask[:, j, :], mask_f[:])
                    if low_rank:
                        dve.tensor_scalar(mask2[:, j, :], mask_f[:], -1.0, None, ALU.mult)
            if rope:
                for i in range(2):
                    dve.tensor_scalar(tables[0][i][:], tables[0][i][:], scale, None, ALU.mult)
            elif q_bias:
                dve.tensor_scalar(qbs[:], qb[:], scale, None, ALU.mult)
            if not out_bias:
                dve.memset(bias[:], 0.0)
            dve.memset(stats[:], 0.0).then_inc(sem["setup"], 1)
            dve.wait_ge(sem["setup"], 1)
            if rope:
                for t in range(2):
                    for i, to in enumerate((rotated[t], terms[t][0])):
                        m = dve.tensor_tensor(to[:], copy_bcast(rb[t][i][:], S),
                                              tables[t][i][:].unsqueeze(1).broadcast_to([E, 4, S]), ALU.mult)
                m.then_inc(sem["setup"], 1)
                dve.wait_ge(sem["setup"], 2)
                for t in range(2):
                    m = dve.tensor_tensor(rotated[t][:], rotated[t][:], terms[t][0][:], ALU.add)
                m.then_inc(sem["setup"], 1)
                dve.wait_ge(sem["setup"], 3)
            if v_bias:
                dve.wait_ge(sem["y_ready"], 1)
                dve.tensor_tensor(bias[:], bias[:], misc[:, 0:E], ALU.add).then_inc(sem["bias_ready"], 1)
            else:
                dve.engine_nop().then_inc(sem["bias_ready"], 1)

            def copy_part(n, p, what, part):
                parts, bank_in, width = (q_parts, q_b, S) if what == "q" else (k_parts, k_b, keys)
                dve.wait_ge(sem[what + "_ready"], n * parts + part + 1)
                if rope:
                    t = "qk".index(what)
                    reach(dve, sem["roped"], n * 4)
                    i = dve.tensor_tensor(terms[t][part][:], bank_in[:],
                                          tables[t][part][:].unsqueeze(1).broadcast_to([E, 4, S]), ALU.mult)
                else:
                    reach(dve, sem["scores_ready"], (n - 1) * 4)
                    out_t = qT[p] if what == "q" else kT[part][p]
                    if what == "q" and q_bias:
                        i = dve.scalar_tensor_tensor(out=out_t[:], in0=q_b[:], scalar=scale,
                                                     in1=copy_bcast(qbs[:], S), op0=ALU.mult, op1=ALU.add)
                    elif what == "q" and not low_rank:
                        i = dve.tensor_scalar(out_t[:], q_b[:], scale, None, ALU.mult)
                    elif q_bias:
                        i = dve.tensor_tensor(out_t[:], k_b[:, :, 0:width], copy_bcast(kb[:], width), ALU.add)
                    else:
                        i = dve.tensor_copy(out_t[:], bank_in[:, :, 0:width])
                i.then_inc(sem[what + "_copied"], 1)

            def maxima(n, p, c):
                u = n * 4 + c
                dve.wait_ge(sem["scores_ready"], u + 1)
                logits = score[c % 2]
                if low_rank:
                    dve.wait_ge(sem["a1_copied"], u + 1)
                    reach(dve, sem["probs_ready"], u - 1)
                    dve.tensor_tensor(prod[c % 2][:], a1[c % 2][:], score[1][:], ALU.mult)\
                       .then_inc(sem["prod_ready"], 1)
                    dve.wait_ge(sem["prod_ready"], u + 1)
                    logits = prod[c % 2]
                reach(dve, sem["probs_ready"], u - 1)
                dve.tensor_reduce(negmax[c % 2][:], logits[:, :, 0:keys], AX.X, ALU.max, negate=True)\
                   .then_inc(sem["max_ready"], 1)

            def copy_pT(n, p, c):
                u = n * 4 + c
                dve.wait_ge(sem["probs_turned"], u + 1)
                reach(dve, sem["pv_done"], u - 1)
                if future_only:
                    i = dve.tensor_tensor(pT[c % 2][:], turned[c % 2][:],
                                          future[:].unsqueeze(1).broadcast_to([S, 4, S]), ALU.mult)
                else:
                    i = dve.tensor_copy(pT[c % 2][:], turned[c % 2][0:keys])
                i.then_inc(sem["pT_copied"], 1)

            def normalise(n, p):
                dve.wait_ge(sem["probs_ready"], (n + 1) * 4)
                reach(dve, sem["o_ready"], n)
                dve.reciprocal(inv[:], sums[p][:]).then_inc(sem["inv_ready"], 1)
                dve.wait_ge(sem["inv_ready"], n + 1)
                dve.wait_ge(sem["pv_done"], (n + 1) * 4)
                reach(dve, sem["o_turned"], n)
                dve.tensor_tensor(o[:].rearrange("p (h e) -> p h e", h=HEADS),
                                  out_b[:, 0:hd].rearrange("p (h e) -> p h e", h=HEADS),
                                  copy_bcast(inv[:], head_dim), ALU.mult).then_inc(sem["o_ready"], 1)

            def residual(n, p):
                dve.wait_ge(sem["y_ready"], n + 1 + y0)
                dve.wait_ge(sem["xb_ready"], n + 1)
                if dst == "sum_and_norm":
                    reach(dve, sem["sum_stored"], n)
                reach(dve, sem["normed"], n)
                dve.tensor_tensor(r[p][:], misc[:, 0:E], xb[p][:], ALU.add).then_inc(sem["r_ready"], 1)

            def moments(n, p):
                dve.wait_ge(sem["r_ready"], n + 1)
                dve.bn_stats(stats[:], r[p][:]).then_inc(sem["stats_ready"], 1)
                wait_alone(dve, sem["stats_ready"], n + 1, keep["passed"])
                dve.bn_aggr(mv[p][:], stats[:]).then_inc(sem["mv_ready"], 1)
                dve.wait_ge(sem["mv_ready"], n + 1)
                dve.tensor_scalar(rstd[p][:], mv[p][:, 1:2], LN_EPS, None, ALU.add).then_inc(sem["var_ready"], 1)

            def norm(n, p):
                dve.wait_ge(sem["rstd_ready"], n + 1)
                out = x if dst == "norm" else keep["z"]
                dve.tensor_scalar(out[:, n, :], r[p][:], mv[p][:, 0:1], rstd[p][:, 0:1], ALU.subtract, ALU.mult)\
                   .then_inc(sem["normed"], 1)

            def slot(n, p):
                for c in range(4):
                    if c == 1 and within(n, -1, count):
                        normalise(n - 1, 1 - p)
                    if c < 3:
                        maxima(n, p, c + 1)
                    elif within(n, 1, count):
                        maxima(n + 1, 1 - p, 0)
                    if c == 1 and within(n, -2, count):
                        norm(n - 2, p)
                    for what, part in before.get(c, []) if within(n, 1, count) else []:
                        copy_part(n + 1, 1 - p, what, part)
                    if c == 3 and within(n, -1, count):
                        residual(n - 1, 1 - p)
                    copy_pT(n, p, c)
                    for what, part in after.get(c, []) if within(n, 1, count) else []:
                        copy_part(n + 1, 1 - p, what, part)
                    if c == 3 and within(n, -1, count):
                        moments(n - 1, 1 - p)

            for what, part in first_parts:
                copy_part(0, 0, what, part)
            maxima(0, 0, 0)
            over_slots(dve, slot, count)
            normalise(count - 1, 1)
            norm(count - 2, 0)
            residual(count - 1, 1)
            moments(count - 1, 1)
            norm(count - 1, 1)

    clear(nc, sem)


def softmax_attention(nc, d, keep, tag, head_dim, scale, *, cross=False, q_bias=False, v_bias=False,
                      out_bias=True, causal=False, future_only=False, rope=False, src=None, affine=None, dst="norm"):
    count = SEQS
    keys = CTX if cross else S
    hd = HEADS * head_dim
    chunks = hd // E
    narrow = head_dim == 8
    in_k = C if cross else E
    parts = 2 if rope else 1
    x, ident = keep["x"], keep["ident"]
    src = x if src is None else src
    ctx_copy = "ctxn" in keep and cross and affine is not None
    with ExitStack() as ctx:
        sb, bank, sems = tensors(ctx, nc, tag)
        wq = sb("wq", [E, parts * chunks, E])
        wk = sb("wk", [in_k, parts * chunks, E])
        wv = sb("wv", [in_k, hd])
        wo = sb("wo", [E, chunks, E])
        bias = sb("bias", [S, E])
        kmask = sb("kmask", [E, 4, 4])
        loads = [(wv[:], d[tag + "_wv"]), (wo[:], d[tag + "_wo"]), (wq[:], d[tag + "_wq"]), (wk[:], d[tag + "_wk"]),
                 (kmask[:], d["kmask8" if narrow else "kmask32"])]
        if narrow:
            vmask = sb("vmask", [S, 4, E])
            zeros = sb("zeros", [S, S], BF16)
            loads += [(vmask[:], d["vmask"])]
        if out_bias:
            loads += [(bias[:], d[tag + "_bo"])]
        if q_bias:
            qb, kb = sb("qb", [E, parts]), sb("kb", [E, parts])
            loads += [(qb[:], d[tag + "_bq"]), (kb[:], d[tag + "_bk"])]
        if rope:
            tables = [[sb(f"{n}{t}", [E, S]) for n in ("cos", "sin")] for t in "qk"]
            terms = [[sb(f"term{t}{i}", [E, S]) for i in range(2)] for t in "qk"]
            for t in range(2):
                loads += [(tables[t][i][:], d[("cos", "sin")[i]]) for i in range(2)]
        elif q_bias:
            qbs = sb("qbs", [E, parts])
        if v_bias:
            vb = sb("vb", [E, S])
            loads += [(vb[:], d[tag + "_bv"])]
        if affine is not None:
            aff = sb("aff", [E, 4])
            loads += [(aff[:], d[tag + "_aff"])]
        if causal:
            mask = sb("mask", [S, 4, S], BF16)
            mask_f = sb("mask_f", [S, S])
            loads += [(mask_f[:], d["causal"])]
        if future_only:
            future = sb("future", [S, S])
            loads += [(future[:], d["future"])]
        xin = [sb(f"xin{i}", [S, E]) for i in range(2)]
        xT = [sb(f"xT{i}", [E, S]) for i in range(2)]
        kin = [sb(f"kin{i}", [in_k, keys]) for i in range(2)] if (cross or affine is not None) else xT
        qT = [sb(f"qT{i}", [E, chunks, S]) for i in range(2)]
        kT = [sb(f"kT{i}", [E, chunks, keys]) for i in range(2)]
        kd = sb("kd", [E, 4, 4, keys])
        vd = [sb(f"vd{i}", [keys, 4, E]) for i in range(2)]
        negmax = [sb(f"negmax{i}", [S, 4]) for i in range(2)]
        prob = [sb(f"prob{i}", [S, 4, keys]) for i in range(2)]
        sums = [sb(f"sums{i}", [S, HEADS]) for i in range(2)]
        inv = sb("inv", [S, HEADS])
        invb = sb("invb", [S, hd])
        invT = sb("invT", [E, chunks, S])
        pT = [sb(f"pT{i}", [keys, 4, S]) for i in range(2)]
        oT = sb("oT", [E, chunks, S])
        xb = [sb(f"xb{i}", [S, E]) for i in range(2)]
        r = [sb(f"r{i}", [S, E]) for i in range(2)]
        stats = sb("stats", [S, 6])
        mv = [sb(f"mv{i}", [S, 2]) for i in range(2)]
        rstd = [sb(f"rstd{i}", [S, 1]) for i in range(2)]
        score = [bank(f"score{i}", [S, 4, S]) for i in range(2)]
        turned = [bank(f"turned{i}", [S, 4, S]) for i in range(2)]
        out_b = bank("out", [E, 4, S])
        q_b = bank("q", [E, 4, S])
        kv_b = bank("kv", [E, 4, S])
        misc = bank("misc", [S, 512])
        sem = sems("weights setup bias_ready xin_ready x_turned xT_copied ctx_loaded0 ctx_loaded1 ctx_copied q_ready "
                   "q_copied k_ready k_copied term_ready kd_ready last_kd_ready v_ready v_copied scores_ready max_ready "
                   "probs_ready probs_turned pT_copied pv_done inv_step inv_ready inv_turned invT_copied oT_ready "
                   "y_ready xb_ready r_ready stats_ready mv_ready rstd_ready normed sum_stored var_ready")
        n_loads = 16 * len(loads)
        y0 = 1 if v_bias else 0
        block = ctx.enter_context(nc.Block())

        def unit_after(n, p, c):
            if c < 3:
                return n, p, c + 1
            return (n + 1, 1 - p, 0) if within(n, 1, count) else None

        def at_most(value, ahead):
            return min(value + ahead, count) if isinstance(value, int) else value + ahead

        @block.sync
        def _(sp):
            load_all(sp, loads, sem["weights"])
            if cross and not ctx_copy:
                def slot(n, p):
                    reach(sp, sem["k_ready"], n - 1)
                    reach(sp, sem["v_ready"], n - 1)
                    sp.dma_start(kin[p][:], d["ctxT"][n]).then_inc(sem[f"ctx_loaded{p}"], 16)

                over_slots(sp, slot, count)

        @block.gpsimd
        def _(pool):
            pool.wait_ge(sem["weights"], n_loads)

            def stage_in(n, p):
                reach(pool, sem["x_turned"], n - 1)
                pool.tensor_copy(xin[p][:], src[:, n, :]).then_inc(sem["xin_ready"], 1)
                if ctx_copy:
                    reach(pool, sem["k_ready"], n - 1)
                    reach(pool, sem["v_ready"], n - 1)
                    pool.tensor_copy(kin[p][:], keep["ctxn"][:, n, :]).then_inc(sem["ctx_copied"], 1)

            def root(n, p):
                pool.wait_ge(sem["var_ready"], n + 1)
                pool.tensor_tensor(rstd[p][:], rstd[p][:], keep["minus_half"][:], ALU.pow)\
                    .then_inc(sem["rstd_ready"], 1)

            def store_sum(n, p):
                wait_alone(pool, sem["r_ready"], n + 1, keep["passed_pool"])
                pool.tensor_tensor(keep["b"][:, n, :], keep["b"][:, n, :], r[p][:], ALU.add)\
                    .then_inc(sem["sum_stored"], 1)

            def spread_last(n, p):
                pool.wait_ge(sem["k_copied"], n + 1)
                reach(pool, sem["scores_ready"], n * 4)
                pool.tensor_tensor(kd[:, 3, :, :],
                                   kT[p][:, 3 % chunks, :].unsqueeze(1).broadcast_to([E, 4, keys]),
                                   copy_bcast(kmask[:, 3, :], keys), ALU.mult).then_inc(sem["last_kd_ready"], 1)

            def slot(n, p):
                if within(n, 2, count):
                    stage_in(n + 2, p)
                if within(n, -2, count):
                    root(n - 2, p)
                    if dst == "sum_and_norm":
                        store_sum(n - 2, p)
                if isinstance(n, int) and n == 0:
                    pool.wait_ge(sem["bias_ready"], 1)
                reach(pool, sem["r_ready"], n - 1)
                res = x if dst == "norm" else keep["b"]
                pool.tensor_tensor(xb[p][:], res[:, n, :], bias[:], ALU.add).then_inc(sem["xb_ready"], 1)
                if within(n, 1, count):
                    spread_last(n + 1, 1 - p)

            stage_in(0, 0)
            stage_in(1, 1)
            spread_last(0, 0)
            over_slots(pool, slot, count)
            for n in (count - 2, count - 1):
                root(n, n % 2)
                if dst == "sum_and_norm":
                    store_sum(n, n % 2)

        @block.tensor
        def _(pe):
            pe.wait_ge(sem["weights"], n_loads)
            pe.wait_ge(sem["setup"], 1)

            def turn_x(n, p):
                pe.wait_ge(sem["xin_ready"], n + 1)
                reach(pe, sem["xT_copied"], n)
                reach(pe, sem["invT_copied"], n - 2)
                pe.transpose(misc[:, 0:S], xin[p][:], ident[:]).then_inc(sem["x_turned"], 1)

            def wait_context(n, p):
                if not cross:
                    pe.wait_ge(sem["xT_copied"], n + 1)
                elif ctx_copy:
                    pe.wait_ge(sem["ctx_copied"], n + 1)
                else:
                    pe.wait_ge(sem[f"ctx_loaded{p}"], (n - p) * 8 + 16)

            def project_q(n, p):
                pe.wait_ge(sem["xT_copied"], n + 1)
                reach(pe, sem["q_copied"], n)
                for c in range(parts * chunks):
                    mm = pe.matmul(q_b[:, c, :], wq[:, c, :], xT[p][:], start=True, stop=True)
                mm.then_inc(sem["q_ready"], 1)

            def project_k(n, p):
                wait_context(n, p)
                reach(pe, sem["v_copied"], n)
                for c in range(parts * chunks):
                    mm = pe.matmul(kv_b[:, c, 0:keys], wk[:, c, :], kin[p][:], start=True, stop=True)
                mm.then_inc(sem["k_ready"], 1)

            def project_v(n, p):
                wait_context(n, p)
                pe.wait_ge(sem["k_copied"], n + 1)
                pe.matmul(kv_b[0:keys].rearrange("p c s -> p (c s)")[:, 0:hd], kin[p][:], wv[:],
                          start=True, stop=True).then_inc(sem["v_ready"], 1)

            def scores(n, p, c):
                if c == 0:
                    pe.wait_ge(sem["q_copied"], n + 1)
                if c == 3:
                    pe.wait_ge(sem["last_kd_ready"], n + 1)
                else:
                    pe.wait_ge(sem["kd_ready"], n * 3 + c + 1)
                reach(pe, sem["probs_ready"], n * 4 + c - 1)
                mm = pe.matmul(score[c % 2][:, :, 0:keys], qT[p][:, c % chunks, :], kd[:, c, :, :],
                               start=True, stop=not causal, skip_group_check=True)
                if causal:
                    mm = pe.matmul(score[c % 2][:, :, :], keep["ident_bf"][:], mask[:], start=False, stop=True,
                                   skip_group_check=True)
                mm.then_inc(sem["scores_ready"], 1)

            def turn_probs(n, p, c):
                u = n * 4 + c
                pe.wait_ge(sem["probs_ready"], u + 1)
                reach(pe, sem["pT_copied"], u - 1)
                for j in range(4):
                    mm = pe.transpose(turned[c % 2][0:keys, j, :], prob[c % 2][:, j, :], ident[:])
                mm.then_inc(sem["probs_turned"], 1)

            def weigh(n, p, c):
                pe.wait_ge(sem["pT_copied"], n * 4 + c + 1)
                if c == 0:
                    pe.wait_ge(sem["v_copied"], n + 1)
                    reach(pe, sem["oT_ready"], n)
                    if narrow:
                        pe.matmul(out_b[:, 0, :], zeros[:], zeros[:], start=True, stop=False, skip_group_check=True)
                for j in range(4):
                    mm = pe.matmul(out_b[32 * j:32 * j + 32, 0 if narrow else c, :], vd[p][:, c, 32 * j:32 * j + 32],
                                   pT[c % 2][:, j, :], start=not narrow, stop=not narrow or c == 3,
                                   tile_position=(0, 32 * j), skip_group_check=True)
                mm.then_inc(sem["pv_done"], 1)

            def turn_inverse(n):
                pe.wait_ge(sem["inv_ready"], n + 1)
                reach(pe, sem["r_ready"], n)
                pe.wait_ge(sem["xT_copied"], at_most(n, 3))
                for c in range(chunks):
                    mm = pe.transpose(misc[:, c * S:(c + 1) * S], invb[:, c * E:(c + 1) * E], ident[:])
                mm.then_inc(sem["inv_turned"], 1)

            def out_product(n):
                pe.wait_ge(sem["oT_ready"], n + 1)
                pe.wait_ge(sem["xT_copied"], at_most(n, 4))
                pe.wait_ge(sem["invT_copied"], n + 1)
                for c in range(chunks):
                    mm = pe.matmul(misc[:, 0:E], oT[:, c, :], wo[:, c, :], start=(c == 0), stop=(c == chunks - 1))
                mm.then_inc(sem["y_ready"], 1)

            def step(n, p, c):
                unit, nxt = unit_after(n, p, c), within(n, 1, count)
                if unit:
                    scores(*unit)
                if c == 0 and within(n, 2, count):
                    turn_x(n + 2, p)
                if c == 0 and nxt:
                    project_q(n + 1, 1 - p)
                    project_k(n + 1, 1 - p)
                if c == 2 and nxt:
                    project_v(n + 1, 1 - p)
                if c == 2 and within(n, -1, count):
                    out_product(n - 1)
                turn_probs(n, p, c)
                if c == 3:
                    turn_inverse(n)
                if c > 0:
                    weigh(n, p, c - 1)
                elif within(n, -1, count):
                    weigh(n - 1, 1 - p, 3)

            def slot(n, p):
                for c in range(4):
                    step(n, p, c)

            if v_bias:
                pe.matmul(misc[:, 0:E], vb[:], wo[:, 0, :], start=True, stop=True).then_inc(sem["y_ready"], 1)
                pe.wait_ge(sem["bias_ready"], 1)
            turn_x(0, 0)
            turn_x(1, 1)
            project_q(0, 0)
            project_k(0, 0)
            project_v(0, 0)
            scores(0, 0, 0)
            over_slots(pe, slot, count)
            weigh(count - 1, 1, 3)
            out_product(count - 1)

        @block.scalar
        def _(act):
            act.wait_ge(sem["weights"], n_loads)
            act.wait_ge(sem["setup"], 1)

            def copy_xT(n, p):
                act.wait_ge(sem["x_turned"], n + 1)
                reach(act, sem["q_ready"], n - 1)
                if not cross:
                    reach(act, sem["k_ready"], n - 1)
                    reach(act, sem["v_ready"], n - 1)
                if affine is None:
                    act.activation(xT[p][:], misc[:, 0:S], ACT.Copy).then_inc(sem["xT_copied"], 1)
                else:
                    if not cross:
                        act.activation(kin[p][:], misc[:, 0:S], ACT.Identity, scale=aff[:, 2:3], bias=aff[:, 3:4])
                    act.activation(xT[p][:], misc[:, 0:S], ACT.Identity, scale=aff[:, 0:1], bias=aff[:, 1:2])\
                       .then_inc(sem["xT_copied"], 1)

            def copy_q(n, p):
                act.wait_ge(sem["q_ready"], n + 1)
                reach(act, sem["scores_ready"], (n - 1) * 4)
                if q_bias:
                    i = act.activation(qT[p][:], q_b[:, 0:chunks, :], ACT.Identity, scale=scale, bias=qbs[:, 0:1])
                else:
                    i = act.activation(qT[p][:], q_b[:, 0:chunks, :], ACT.Copy, scale=scale)
                i.then_inc(sem["q_copied"], 1)

            def copy_k(n, p):
                act.wait_ge(sem["k_ready"], n + 1)
                reach(act, sem["kd_ready"], (n - 1) * 3)
                reach(act, sem["last_kd_ready"], n - 1)
                if q_bias:
                    i = act.activation(kT[p][:], kv_b[:, 0:chunks, 0:keys], ACT.Identity, bias=kb[:, 0:1])
                else:
                    i = act.activation(kT[p][:], kv_b[:, 0:chunks, 0:keys], ACT.Copy)
                i.then_inc(sem["k_copied"], 1)

            def copy_v(n, p):
                act.wait_ge(sem["v_ready"], n + 1)
                reach(act, sem["pv_done"], (n - 1) * 4)
                act.activation(vd[p][:], kv_b[0:keys], ACT.Copy).then_inc(sem["v_copied"], 1)

            def copy_invT(n):
                act.wait_ge(sem["inv_turned"], n + 1)
                reach(act, sem["oT_ready"], n)
                act.activation(invT[:], misc[:, 0:hd].rearrange("p (c s) -> p c s", c=chunks), ACT.Copy)\
                   .then_inc(sem["invT_copied"], 1)

            def exps(n, p, c):
                u = n * 4 + c
                act.wait_ge(sem["max_ready"], u + 1)
                reach(act, sem["probs_turned"], u - 1)
                if c == 0:
                    reach(act, sem["inv_step"], n - 1)
                for j in range(4):
                    head = 4 * j + c if narrow else 4 * c + j
                    e = act.activation(prob[c % 2][:, j, :], score[c % 2][:, j, 0:keys], ACT.Exp,
                                       bias=negmax[c % 2][:, j:j + 1], accum_out=sums[p][:, head:head + 1])
                e.then_inc(sem["probs_ready"], 1)

            def slot(n, p):
                for c in range(4):
                    unit = unit_after(n, p, c)
                    if c == 0 and within(n, -1, count):
                        copy_invT(n - 1)
                    if c == 0 and within(n, 2, count):
                        copy_xT(n + 2, p)
                    if unit:
                        exps(*unit)
                    if c == 0 and within(n, 1, count) and not rope:
                        copy_q(n + 1, 1 - p)
                        copy_k(n + 1, 1 - p)
                    if c == 2 and within(n, 1, count) and not narrow:
                        copy_v(n + 1, 1 - p)

            copy_xT(0, 0)
            copy_xT(1, 1)
            if not rope:
                copy_q(0, 0)
                copy_k(0, 0)
            if not narrow:
                copy_v(0, 0)
            exps(0, 0, 0)
            over_slots(act, slot, count)
            copy_invT(count - 1)

        @block.vector
        def _(dve):
            dve.wait_ge(sem["weights"], n_loads)
            if causal:
                for j in range(4):
                    dve.tensor_copy(mask[:, j, :], mask_f[:])
            if narrow:
                dve.memset(zeros[:], 0.0)
            if rope:
                for i in range(2):
                    dve.tensor_scalar(tables[0][i][:], tables[0][i][:], scale, None, ALU.mult)
            elif q_bias:
                dve.tensor_scalar(qbs[:], qb[:], scale, None, ALU.mult)
            if not out_bias:
                dve.memset(bias[:], 0.0)
            dve.memset(stats[:], 0.0).then_inc(sem["setup"], 1)
            dve.wait_ge(sem["setup"], 1)
            if v_bias:
                dve.wait_ge(sem["y_ready"], 1)
                dve.tensor_tensor(bias[:], bias[:], misc[:, 0:E], ALU.add).then_inc(sem["bias_ready"], 1)
            else:
                dve.engine_nop().then_inc(sem["bias_ready"], 1)

            def rotate(n, p):
                for t, what, bank_in, b, out_t in ((0, "q", q_b, qb, qT[p]), (1, "k", kv_b, kb, kT[p])):
                    dve.wait_ge(sem[what + "_ready"], n + 1)
                    for part in range(2):
                        i = dve.scalar_tensor_tensor(out=terms[t][part][:], in0=bank_in[:, part, :],
                                                     scalar=b[:, part:part + 1], in1=tables[t][part][:],
                                                     op0=ALU.add, op1=ALU.mult)
                    i.then_inc(sem["term_ready"], 1)
                    dve.wait_ge(sem["term_ready"], n * 2 + t + 1)
                    reach(dve, sem["scores_ready"], (n - 1) * 4)
                    reach(dve, sem["last_kd_ready"], n - 1)
                    dve.tensor_tensor(out_t[:, 0, :], terms[t][0][:], terms[t][1][:], ALU.add)\
                       .then_inc(sem[what + "_copied"], 1)

            def spread(n, p, c):
                dve.wait_ge(sem["k_copied"], n + 1)
                reach(dve, sem["scores_ready"], (n - 1) * 4 + c + 1)
                dve.tensor_tensor(kd[:, c, :, :], kT[p][:, c % chunks, :].unsqueeze(1).broadcast_to([E, 4, keys]),
                                  copy_bcast(kmask[:, c, :], keys), ALU.mult).then_inc(sem["kd_ready"], 1)

            def spread_v(n, p):
                dve.wait_ge(sem["v_ready"], n + 1)
                reach(dve, sem["pv_done"], (n - 1) * 4)
                dve.tensor_tensor(vd[p][:], kv_b[0:keys, 0:1, :].broadcast_to([keys, 4, E]), vmask[0:keys],
                                  ALU.mult).then_inc(sem["v_copied"], 1)

            def maxima(n, p, c):
                u = n * 4 + c
                dve.wait_ge(sem["scores_ready"], u + 1)
                reach(dve, sem["probs_ready"], u - 1)
                dve.tensor_reduce(negmax[c % 2][:], score[c % 2][:, :, 0:keys], AX.X, ALU.max, negate=True)\
                   .then_inc(sem["max_ready"], 1)

            def copy_pT(n, p, c):
                u = n * 4 + c
                dve.wait_ge(sem["probs_turned"], u + 1)
                reach(dve, sem["pv_done"], u - 1)
                if future_only:
                    i = dve.tensor_tensor(pT[c % 2][:], turned[c % 2][:],
                                          future[:].unsqueeze(1).broadcast_to([S, 4, S]), ALU.mult)
                else:
                    i = dve.tensor_copy(pT[c % 2][:], turned[c % 2][0:keys])
                i.then_inc(sem["pT_copied"], 1)

            def inverse(n, p):
                dve.wait_ge(sem["probs_ready"], (n + 1) * 4)
                dve.reciprocal(inv[:], sums[p][:]).then_inc(sem["inv_step"], 1)
                dve.wait_ge(sem["inv_step"], n + 1)
                reach(dve, sem["inv_turned"], n)
                dve.tensor_copy(invb[:].rearrange("p (h e) -> p h e", h=HEADS), copy_bcast(inv[:], head_dim))\
                   .then_inc(sem["inv_ready"], 1)

            def scale_out(n):
                dve.wait_ge(sem["pv_done"], (n + 1) * 4)
                dve.wait_ge(sem["invT_copied"], n + 1)
                reach(dve, sem["y_ready"], n + y0)
                dve.tensor_tensor(oT[:], out_b[:, 0:chunks, :], invT[:], ALU.mult).then_inc(sem["oT_ready"], 1)

            def residual(n, p):
                dve.wait_ge(sem["y_ready"], n + 1 + y0)
                dve.wait_ge(sem["xb_ready"], n + 1)
                if dst == "sum_and_norm":
                    reach(dve, sem["sum_stored"], n)
                reach(dve, sem["normed"], n)
                dve.tensor_tensor(r[p][:], misc[:, 0:E], xb[p][:], ALU.add).then_inc(sem["r_ready"], 1)

            def moments(n, p):
                dve.wait_ge(sem["r_ready"], n + 1)
                dve.bn_stats(stats[:], r[p][:]).then_inc(sem["stats_ready"], 1)
                wait_alone(dve, sem["stats_ready"], n + 1, keep["passed"])
                dve.bn_aggr(mv[p][:], stats[:]).then_inc(sem["mv_ready"], 1)
                dve.wait_ge(sem["mv_ready"], n + 1)
                dve.tensor_scalar(rstd[p][:], mv[p][:, 1:2], LN_EPS, None, ALU.add).then_inc(sem["var_ready"], 1)

            def norm(n, p):
                dve.wait_ge(sem["rstd_ready"], n + 1)
                out = x if dst == "norm" else keep["z"]
                dve.tensor_scalar(out[:, n, :], r[p][:], mv[p][:, 0:1], rstd[p][:, 0:1], ALU.subtract, ALU.mult)\
                   .then_inc(sem["normed"], 1)

            def slot(n, p):
                nxt = within(n, 1, count)
                for c in range(4):
                    unit = unit_after(n, p, c)
                    if c == 1 and within(n, -1, count):
                        scale_out(n - 1)
                    if c == 3:
                        inverse(n, p)
                    if unit:
                        maxima(*unit)
                    if c == 0 and nxt and rope:
                        rotate(n + 1, 1 - p)
                    if c > 0 and nxt:
                        spread(n + 1, 1 - p, c - 1)
                    if c == 2 and nxt and narrow:
                        spread_v(n + 1, 1 - p)
                    if c == 1 and within(n, -2, count):
                        norm(n - 2, p)
                    if c == 3 and within(n, -1, count):
                        residual(n - 1, 1 - p)
                    copy_pT(n, p, c)
                    if c == 3 and within(n, -1, count):
                        moments(n - 1, 1 - p)

            if rope:
                rotate(0, 0)
            for c in range(3):
                spread(0, 0, c)
            if narrow:
                spread_v(0, 0)
            maxima(0, 0, 0)
            over_slots(dve, slot, count)
            scale_out(count - 1)
            norm(count - 2, 0)
            residual(count - 1, 1)
            moments(count - 1, 1)
            norm(count - 1, 1)

    clear(nc, sem)


def feed_forward(nc, d, keep, tag, kind, n_chunks, func, *, scale=1.0, ints=False, bias=False, out_bias=False,
                 experts=0, per_gate=1, gates=0, first_gated=0, shared_gate=False, gate_bias=False,
                 src=None, affine=False, dst="norm"):
    G, T = 4, 4 * S
    groups = SEQS // G
    glu, gated = kind == "glu", experts > 0
    routed = experts + (1 if shared_gate else 0)
    x, ident = keep["x"], keep["ident"]
    src = x if src is None else src
    J = n_chunks
    with ExitStack() as ctx:
        sb, bank, sems = tensors(ctx, nc, tag)
        wdt = I32 if ints else F32
        wu, wd = sb("wu", [E, J, E]), sb("wd", [E, J, E])
        mats = [("wu", wu), ("wd", wd)]
        if glu:
            wv = sb("wv", [E, J, E])
            mats.append(("wv", wv))
        loads, raw = [], []
        for n, t in mats:
            if ints:
                raw.append(sb(n + "_int", [E, J, E], I32))
                loads.append((raw[-1][:], d[f"{tag}_{n}"]))
            else:
                loads.append((t[:], d[f"{tag}_{n}"]))
        if bias:
            ub = sb("ub", [E, J])
            loads.append((ub[:], d[tag + "_bu"]))
        ob = sb("ob", [S, E])
        if out_bias:
            loads.append((ob[:], d[tag + "_bd"]))
        if affine:
            aff = sb("aff", [E, 2])
            loads.append((aff[:], d[tag + "_aff"]))
        if gated:
            wr = sb("wr", [E, routed])
            sel = sb("sel", [routed, gates, E])
            before = sb("before", [S, experts, experts])
            loads += [(wr[:], d[tag + "_wr"]), (sel[:], d[tag + "_sel"]), (before[:], d[tag + "_before"])]
            if gate_bias:
                gb = sb("gb", [experts, E])
                loads.append((gb[:], d[tag + "_gb"]))
            prob = sb("prob", [S, G, routed])
            top = sb("top", [S, G])
            more = sb("more", [S, G, experts, experts])
            same = sb("same", [S, G, experts, experts])
            rank = sb("rank", [S, G, experts])
            gate = sb("gate", [S, G, routed])
            gateT = [sb(f"gateT{i}", [routed, T]) for i in range(2)]
        xin = sb("xin", [S, G, E])
        xT = [sb(f"xT{i}", [E, T]) for i in range(2)]
        h = [sb(f"h{i}", [E, T]) for i in range(2)]
        hv = [sb(f"hv{i}", [E, T]) for i in range(2)] if glu else h
        hg = [sb(f"hg{i}", [E, T]) for i in range(2)] if gated else hv
        xb = sb("xb", [S, G, E])
        r = [sb(f"r{i}", [S, G, E]) for i in range(2)]
        stats = sb("stats", [S, G, 6])
        mv = [sb(f"mv{i}", [S, G, 2]) for i in range(2)]
        rstd = [sb(f"rstd{i}", [S, G]) for i in range(2)]
        x_b, v_b, y_b, r_b = bank("x", [E, T]), bank("v", [E, T]), bank("y", [S, G, E]), bank("r", [S, 512])
        u_b = [bank(f"u{i}", [E, T]) for i in range(2)]
        g_b = [bank(f"g{i}", [E, T]) for i in range(2)]
        sem = sems("weights setup xin_ready x_turned xT_copied up_ready act_done v_ready v_done hidden_ready "
                   "gate_spread down_done y_ready xb_ready xb_part r_ready stats_ready mv_ready var_ready rstd_ready "
                   "normed gate_sum routed route_step logits_shifted route_exp gates_ready gates_turned gateT_copied")
        n_loads = 16 * len(loads)
        hidden = "hidden_ready" if gated else "v_done" if glu else "act_done"
        block = ctx.enter_context(nc.Block())

        def gate_of(j):
            return (j - first_gated) // per_gate if gated and j >= first_gated else None

        def new_gate(j):
            return gate_of(j) is not None and (j - first_gated) % per_gate == 0

        @block.sync
        def _(sp):
            load_all(sp, loads, sem["weights"])

        @block.gpsimd
        def _(pool):
            pool.wait_ge(sem["weights"], n_loads)
            pool.wait_ge(sem["setup"], 1)

            def stage_in(g):
                reach(pool, sem["x_turned"], g)
                pool.tensor_copy(xin[:], src[:, bass.ds(g * G, G), :]).then_inc(sem["xin_ready"], 1)

            def residual_base(g):
                wait_alone(pool, sem["r_ready"], g, keep["passed_pool"])
                res = x if dst == "norm" else keep["b"]
                pool.tensor_tensor(xb[:], res[:, bass.ds(g * G, G), :], ob[:].unsqueeze(1).broadcast_to([S, G, E]),
                                   ALU.add).then_inc(sem["xb_part"], 1)
                if dst == "norm_with_x":
                    pool.wait_ge(sem["xb_part"], g + 1)
                    pool.tensor_tensor(xb[:], xb[:], x[:, bass.ds(g * G, G), :], ALU.add).then_inc(sem["xb_ready"], 1)

            def root(g, p):
                if dst != "store":
                    pool.wait_ge(sem["var_ready"], g + 1)
                    pool.tensor_tensor(rstd[p][:], rstd[p][:], keep["minus_half"][:, 0:1].broadcast_to([S, G]),
                                       ALU.pow).then_inc(sem["rstd_ready"], 1)

            def slot(g, p):
                if within(g, 1, groups):
                    stage_in(g + 1)
                if within(g, -1, groups):
                    root(g - 1, 1 - p)
                residual_base(g)

            stage_in(0)
            over_slots(pool, slot, groups)
            root(groups - 1, 1)

        @block.tensor
        def _(pe):
            pe.wait_ge(sem["weights"], n_loads)
            pe.wait_ge(sem["setup"], 1)

            def turn_x(g):
                pe.wait_ge(sem["xin_ready"], g + 1)
                reach(pe, sem["xT_copied"], g)
                for s in range(G):
                    mm = pe.transpose(x_b[:, s * S:(s + 1) * S], xin[:, s, :], ident[:])
                mm.then_inc(sem["x_turned"], 1)

            def route(g, p):
                pe.wait_ge(sem["xT_copied"], g + 1)
                reach(pe, sem["gateT_copied"], g)
                for s in range(G):
                    mm = pe.matmul(r_b[:, s * routed:(s + 1) * routed], xT[p][:, s * S:(s + 1) * S], wr[:],
                                   start=True, stop=True)
                mm.then_inc(sem["routed"], 1)

            def turn_gates(g):
                pe.wait_ge(sem["gates_ready"], g + 1)
                for s in range(G):
                    mm = pe.transpose(r_b[0:routed, s * S:(s + 1) * S], gate[:, s, :], ident[:])
                mm.then_inc(sem["gates_turned"], 1)

            def up(g, p, j):
                n = g * J + j
                if j == 0:
                    pe.wait_ge(sem["xT_copied"], g + 1)
                reach(pe, sem["act_done"], n - 1)
                pe.matmul(u_b[(p * J + j) % 2][:], wu[:, j, :], xT[p][:], start=True, stop=True).then_inc(sem["up_ready"], 1)
                if glu:
                    reach(pe, sem["v_done"], n)
                    pe.matmul(v_b[:], wv[:, j, :], xT[p][:], start=True, stop=True).then_inc(sem["v_ready"], 1)
                if new_gate(j):
                    k = gate_of(j)
                    if k == 0:
                        pe.wait_ge(sem["gateT_copied"], g + 1)
                    last = first_gated + (k - 1) * per_gate if k >= 2 else None
                    if last is not None:
                        pe.wait_ge(sem["hidden_ready"], g * J + last)
                    else:
                        reach(pe, sem["hidden_ready"], g * J)
                    pe.matmul(g_b[k % 2][:], sel[:, k, :], gateT[p][:], start=True, stop=True)\
                      .then_inc(sem["gate_spread"], 1)

            def down(g, p, j):
                n = g * J + j
                pe.wait_ge(sem[hidden], n + 1)
                if j == 0:
                    reach(pe, sem["r_ready"], g)
                    if gate_bias:
                        for s in range(G):
                            pe.matmul(y_b[:, s, :], gateT[p][0:experts, s * S:(s + 1) * S], gb[:],
                                      start=(s == 0), stop=False, skip_group_check=True)
                for s in range(G):
                    mm = pe.matmul(y_b[:, s, :], hg[(p * J + j) % 2][:, s * S:(s + 1) * S], wd[:, j, :],
                                   start=(j == 0 and s == 0 and not gate_bias), stop=(j == J - 1),
                                   skip_group_check=True)
                mm.then_inc(sem["down_done"], 1)

            def slot(g, p):
                for j in range(J):
                    up(g, p, j)
                    if j > 0:
                        down(g, p, j - 1)
                    elif within(g, -1, groups):
                        down(g - 1, 1 - p, J - 1)
                    if j == 1 and within(g, 1, groups):
                        turn_x(g + 1)
                    if gated and j == 3 and within(g, 1, groups):
                        route(g + 1, 1 - p)
                    if gated and j == J - 1 and within(g, 1, groups):
                        turn_gates(g + 1)

            turn_x(0)
            if gated:
                route(0, 0)
                turn_gates(0)
            over_slots(pe, slot, groups)
            down(groups - 1, 1, J - 1)

        @block.scalar
        def _(act):
            act.wait_ge(sem["weights"], n_loads)

            def copy_xT(g, p):
                act.wait_ge(sem["x_turned"], g + 1)
                reach(act, sem["up_ready"], (g - 1) * J)
                if glu:
                    reach(act, sem["v_ready"], (g - 1) * J)
                if affine:
                    i = act.activation(xT[p][:], x_b[:], ACT.Identity, scale=aff[:, 0:1], bias=aff[:, 1:2])
                else:
                    i = act.activation(xT[p][:], x_b[:], ACT.Copy)
                i.then_inc(sem["xT_copied"], 1)

            def route_exp(g):
                act.wait_ge(sem["logits_shifted"], g + 1)
                act.activation(prob[:], prob[:], ACT.Exp).then_inc(sem["route_exp"], 1)

            def copy_gateT(g, p):
                act.wait_ge(sem["gates_turned"], g + 1)
                reach(act, sem["down_done"], (g - 1) * J)
                act.activation(gateT[p][:], r_b[0:routed, :], ACT.Copy).then_inc(sem["gateT_copied"], 1)

            def activate(g, p, j):
                n = g * J + j
                act.wait_ge(sem["up_ready"], n + 1)
                reach(act, sem["v_done"] if glu else sem["hidden_ready"] if gated else sem["down_done"], n - 1)
                i = act.activation(h[(p * J + j) % 2][:], u_b[(p * J + j) % 2][:], func, scale=scale,
                                   **(dict(bias=ub[:, j:j + 1]) if bias else {}))
                i.then_inc(sem["act_done"], 1)

            def slot(g, p):
                for j in range(J):
                    activate(g, p, j)
                    if j == 1 and within(g, 1, groups):
                        copy_xT(g + 1, 1 - p)
                    if gated and j == 5 and within(g, 1, groups):
                        route_exp(g + 1)
                if gated and within(g, 1, groups):
                    copy_gateT(g + 1, 1 - p)

            copy_xT(0, 0)
            if gated:
                route_exp(0)
                copy_gateT(0, 0)
            over_slots(act, slot, groups)

        @block.vector
        def _(dve):
            dve.wait_ge(sem["weights"], n_loads)
            for (_, t), i in zip(mats, raw):
                dve.tensor_copy(t[:], i[:])
            if not out_bias:
                dve.memset(ob[:], 0.0)
            dve.memset(stats[:], 0.0).then_inc(sem["setup"], 1)

            STEPS = 10

            def chain(g, k, ins):
                ins.then_inc(sem["route_step"], 1)
                dve.wait_ge(sem["route_step"], g * STEPS + k)

            def per_n(ap):
                return ap.unsqueeze(2).broadcast_to([S, G, experts, experts])

            def per_m(ap):
                return ap.unsqueeze(3).broadcast_to([S, G, experts, experts])

            def route(g, part):
                pr = prob[:, :, 0:experts]
                if part == 0:
                    dve.wait_ge(sem["routed"], g + 1)
                    logits = r_b[:, 0:G * routed].rearrange("p (s e) -> p s e", s=G)
                    chain(g, 1, dve.tensor_reduce(top[:], logits[:, :, 0:experts], AX.X, ALU.max, negate=True))
                    if shared_gate:
                        dve.tensor_scalar(prob[:, :, experts:routed], logits[:, :, experts:routed], -1.0, None,
                                          ALU.mult)
                    dve.tensor_tensor(pr, logits[:, :, 0:experts], copy_bcast(top[:], experts), ALU.add)\
                       .then_inc(sem["logits_shifted"], 1)
                elif part == 1:
                    dve.wait_ge(sem["route_exp"], g + 1)
                    reach(dve, sem["gates_turned"], g)
                    chain(g, 2, dve.tensor_reduce(top[:], pr, AX.X, ALU.add))
                    chain(g, 3, dve.reciprocal(top[:], top[:]))
                    if shared_gate:
                        dve.tensor_scalar(gate[:, :, experts:routed], prob[:, :, experts:routed], 1.0, None, ALU.add)
                    chain(g, 4, dve.tensor_tensor(pr, pr, copy_bcast(top[:], experts), ALU.mult))
                    if shared_gate:
                        dve.reciprocal(gate[:, :, experts:routed], gate[:, :, experts:routed])
                elif part == 2:
                    dve.tensor_tensor(more[:], per_n(pr), per_m(pr), ALU.is_gt)
                    chain(g, 5, dve.tensor_tensor(same[:], per_n(pr), per_m(pr), ALU.is_equal))
                    chain(g, 6, dve.tensor_tensor(same[:], same[:], before[:].unsqueeze(1).broadcast_to(
                        [S, G, experts, experts]), ALU.mult))
                elif part == 3:
                    chain(g, 7, dve.tensor_tensor(more[:], more[:], same[:], ALU.add))
                    chain(g, 8, dve.tensor_reduce(rank[:], more[:], AX.X, ALU.add))
                else:
                    chain(g, 9, dve.scalar_tensor_tensor(out=rank[:], in0=rank[:], scalar=1.5, in1=pr,
                                                         op0=ALU.is_lt, op1=ALU.mult))
                    chain(g, 10, dve.tensor_reduce(top[:], rank[:], AX.X, ALU.add))
                    dve.reciprocal(top[:], top[:]).then_inc(sem["gate_sum"], 1)
                    dve.wait_ge(sem["gate_sum"], g + 1)
                    dve.tensor_tensor(gate[:, :, 0:experts], rank[:], copy_bcast(top[:], experts), ALU.mult)\
                       .then_inc(sem["gates_ready"], 1)

            def finish_hidden(g, p, j):
                n = g * J + j
                dve.wait_ge(sem["act_done"], n + 1)
                a = h[(p * J + j) % 2]
                if glu:
                    dve.wait_ge(sem["v_ready"], n + 1)
                    if gated:
                        i = dve.tensor_tensor(hv[(p * J + j) % 2][:], a[:], v_b[:], ALU.mult)
                    else:
                        reach(dve, sem["down_done"], n - 1)
                        i = dve.scalar_tensor_tensor(out=hv[(p * J + j) % 2][:], in0=v_b[:], scalar=scale, in1=a[:],
                                                     op0=ALU.mult, op1=ALU.mult)
                    i.then_inc(sem["v_done"], 1)
                    dve.wait_ge(sem["v_done"], n + 1)
                    a = hv[(p * J + j) % 2]
                if not gated:
                    return
                reach(dve, sem["down_done"], n - 1)
                k = gate_of(j)
                if k is None:
                    i = dve.tensor_copy(hg[(p * J + j) % 2][:], a[:])
                else:
                    if new_gate(j):
                        dve.wait_ge(sem["gate_spread"], g * gates + k + 1)
                    i = dve.tensor_tensor(hg[(p * J + j) % 2][:], a[:], g_b[k % 2][:], ALU.mult)
                i.then_inc(sem["hidden_ready"], 1)

            def residual(g, p):
                dve.wait_ge(sem["down_done"], (g + 1) * J)
                dve.wait_ge(sem["xb_ready" if dst == "norm_with_x" else "xb_part"], g + 1)
                if dst == "store":
                    dve.tensor_tensor(keep["b"][:, bass.ds(g * G, G), :], y_b[:], xb[:], ALU.add)\
                       .then_inc(sem["r_ready"], 1)
                    return
                if ints:
                    i = dve.scalar_tensor_tensor(out=r[p][:], in0=y_b[:], scalar=scale, in1=xb[:], op0=ALU.mult,
                                                 op1=ALU.add)
                else:
                    i = dve.tensor_tensor(r[p][:], y_b[:], xb[:], ALU.add)
                i.then_inc(sem["r_ready"], 1)
                dve.wait_ge(sem["r_ready"], g + 1)
                for s in range(G):
                    i = dve.bn_stats(stats[:, s, :], r[p][:, s, :])
                i.then_inc(sem["stats_ready"], 1)
                wait_alone(dve, sem["stats_ready"], g + 1, keep["passed"])
                for s in range(G):
                    i = dve.bn_aggr(mv[p][:, s, :], stats[:, s, :])
                i.then_inc(sem["mv_ready"], 1)
                dve.wait_ge(sem["mv_ready"], g + 1)
                dve.tensor_scalar(rstd[p][:], mv[p][:, :, 1], LN_EPS, None, ALU.add).then_inc(sem["var_ready"], 1)

            def norm(g, p):
                if dst == "store":
                    return
                dve.wait_ge(sem["rstd_ready"], g + 1)
                for s in range(G):
                    i = dve.tensor_scalar(x[:, g * G + s, :], r[p][:, s, :], mv[p][:, s, 0:1], rstd[p][:, s:s + 1],
                                          ALU.subtract, ALU.mult)
                i.then_inc(sem["normed"], 1)

            def slot(g, p):
                for j in range(J):
                    if glu or gated:
                        finish_hidden(g, p, j)
                    if j == 0 and within(g, -1, groups):
                        residual(g - 1, 1 - p)
                    if j == 2 and within(g, -1, groups):
                        norm(g - 1, 1 - p)
                    if gated and 4 <= j < 9 and within(g, 1, groups):
                        route(g + 1, j - 4)

            if gated:
                for part in range(5):
                    route(0, part)
            over_slots(dve, slot, groups)
            residual(groups - 1, 1)
            norm(groups - 1, 1)

    clear(nc, sem)


def renormalise(nc, d, keep, tag, src):
    G = 4
    groups = SEQS // G
    b, z = keep["b"], keep["z"]
    with ExitStack() as ctx:
        sb, _, sems = tensors(ctx, nc, tag)
        gain, shift = sb("gain", [S, E]), sb("shift", [S, E])
        loads = [(gain[:], d[tag + "_gain"]), (shift[:], d[tag + "_shift"])]
        scaled = [sb(f"scaled{i}", [S, G, E]) for i in range(2)]
        stats = sb("stats", [S, G, 6])
        mv = [[sb(f"mv{k}{i}", [S, G, 2]) for i in range(2)] for k in range(2)]
        rstd = [[sb(f"rstd{k}{i}", [S, G]) for i in range(2)] for k in range(2)]
        sem = sems("weights stats_ready mv_ready var0 var1 rstd0 rstd1 normed scaled stored z_stored")
        block = ctx.enter_context(nc.Block())

        @block.sync
        def _(sp):
            load_all(sp, loads, sem["weights"])

        @block.gpsimd
        def _(pool):
            def root(k, g, p):
                pool.wait_ge(sem[f"var{k}"], g + 1)
                pool.tensor_tensor(rstd[k][p][:], rstd[k][p][:], keep["minus_half"][:, 0:1].broadcast_to([S, G]),
                                   ALU.pow).then_inc(sem[f"rstd{k}"], 1)

            def slot(g, p):
                root(0, g, p)
                if within(g, -1, groups):
                    root(1, g - 1, 1 - p)

            over_slots(pool, slot, groups)
            root(1, groups - 1, 1)

        @block.vector
        def _(dve):
            dve.wait_ge(sem["weights"], 32)

            def moments(k, g, p, count):
                data = src if k == 0 else b
                if k == 1:
                    wait_alone(dve, sem["stored"], g + 1, keep["passed"])
                for s in range(G):
                    i = dve.bn_stats(stats[:, s, :], data[:, g * G + s, :])
                i.then_inc(sem["stats_ready"], 1)
                wait_alone(dve, sem["stats_ready"], count + 1, keep["passed"])
                for s in range(G):
                    i = dve.bn_aggr(mv[k][p][:, s, :], stats[:, s, :])
                i.then_inc(sem["mv_ready"], 1)
                dve.wait_ge(sem["mv_ready"], count + 1)
                dve.tensor_scalar(rstd[k][p][:], mv[k][p][:, :, 1], LN_EPS, None, ALU.add).then_inc(sem[f"var{k}"], 1)

            def scale_shift(g, p):
                dve.wait_ge(sem["rstd0"], g + 1)
                for s in range(G):
                    i = dve.tensor_scalar(scaled[p][:, s, :], src[:, g * G + s, :], mv[0][p][:, s, 0:1],
                                          rstd[0][p][:, s:s + 1], ALU.subtract, ALU.mult)
                i.then_inc(sem["normed"], 1)
                dve.wait_ge(sem["normed"], g + 1)
                dve.tensor_tensor(scaled[p][:], scaled[p][:], gain[:].unsqueeze(1).broadcast_to([S, G, E]), ALU.mult)\
                   .then_inc(sem["scaled"], 1)
                dve.wait_ge(sem["scaled"], g + 1)
                dve.tensor_tensor(b[:, bass.ds(g * G, G), :], scaled[p][:],
                                  shift[:].unsqueeze(1).broadcast_to([S, G, E]), ALU.add).then_inc(sem["stored"], 1)

            def store_z(g, p):
                dve.wait_ge(sem["rstd1"], g + 1)
                for s in range(G):
                    i = dve.tensor_scalar(z[:, g * G + s, :], b[:, g * G + s, :], mv[1][p][:, s, 0:1],
                                          rstd[1][p][:, s:s + 1], ALU.subtract, ALU.mult)
                i.then_inc(sem["z_stored"], 1)

            def slot(g, p):
                moments(0, g, p, g * 2 - (0 if isinstance(g, int) and g == 0 else 1))
                if within(g, -1, groups):
                    scale_shift(g - 1, 1 - p)
                    moments(1, g - 1, 1 - p, g * 2)
                if within(g, -2, groups):
                    store_z(g - 2, p)

            over_slots(dve, slot, groups)
            store_z(groups - 2, 0)
            scale_shift(groups - 1, 1)
            moments(1, groups - 1, 1, 2 * groups - 1)
            store_z(groups - 1, 1)

    clear(nc, sem)


def normalise_context(nc, d, keep, tag):
    G = 4
    groups = SEQS // G
    with ExitStack() as ctx:
        sb, bank, sems = tensors(ctx, nc, tag)
        c, sq = sb("c", [CTX, SEQS, C]), sb("sq", [CTX, SEQS, C])
        aff = sb("aff", [C, 2])
        mean, rstd = sb("mean", [CTX, SEQS]), sb("rstd", [CTX, SEQS])
        turned = [bank(f"turned{i}", [C, G, CTX]) for i in range(2)]
        sem = sems("loaded step var_ready rstd_ready normed turned stored")
        block = ctx.enter_context(nc.Block())

        @block.sync
        def _(sp):
            sp.dma_start(c[:], d["ctx"].rearrange("s t c -> t s c")).then_inc(sem["loaded"], 16)
            sp.dma_start(aff[:], d[tag + "_aff"]).then_inc(sem["loaded"], 16)

        @block.gpsimd
        def _(pool):
            pool.wait_ge(sem["var_ready"], 1)
            pool.tensor_tensor(rstd[:], rstd[:], keep["minus_half"][0:CTX, 0:1].broadcast_to([CTX, SEQS]), ALU.pow)\
                .then_inc(sem["rstd_ready"], 1)

        @block.vector
        def _(dve):
            def chain(k, ins):
                ins.then_inc(sem["step"], 1)
                dve.wait_ge(sem["step"], k)

            dve.wait_ge(sem["loaded"], 32)
            chain(1, dve.tensor_reduce(mean[:], c[:], AX.X, ALU.add))
            chain(2, dve.tensor_scalar(mean[:], mean[:], 1.0 / C, None, ALU.mult))
            chain(3, dve.tensor_tensor(c[:], c[:], copy_bcast(mean[:], C), ALU.subtract))
            chain(4, dve.tensor_tensor(sq[:], c[:], c[:], ALU.mult))
            chain(5, dve.tensor_reduce(rstd[:], sq[:], AX.X, ALU.add))
            dve.tensor_scalar(rstd[:], rstd[:], 1.0 / C, LN_EPS, ALU.mult, ALU.add).then_inc(sem["var_ready"], 1)
            dve.wait_ge(sem["rstd_ready"], 1)
            dve.tensor_tensor(c[:], c[:], copy_bcast(rstd[:], C), ALU.mult).then_inc(sem["normed"], 1)

        @block.tensor
        def _(pe):
            pe.wait_ge(sem["normed"], 1)
            for g in range(groups):
                if g >= 2:
                    pe.wait_ge(sem["stored"], g - 1)
                for s in range(G):
                    mm = pe.transpose(turned[g % 2][:, s, :], c[:, g * G + s, :], keep["ident"][0:CTX, 0:CTX])
                mm.then_inc(sem["turned"], 1)

        @block.scalar
        def _(act):
            act.wait_ge(sem["loaded"], 32)
            for g in range(groups):
                act.wait_ge(sem["turned"], g + 1)
                act.activation(keep["ctxn"][:, g * G:(g + 1) * G, :], turned[g % 2][:], ACT.Identity,
                               scale=aff[:, 0:1], bias=aff[:, 1:2]).then_inc(sem["stored"], 1)

    clear(nc, sem)


def relu_attention(nc, d, keep, tag):
    count, K, D = SEQS, 4, E // HEADS
    x, ident = keep["x"], keep["ident"]
    with ExitStack() as ctx:
        sb, bank, sems = tensors(ctx, nc, tag)
        w = {n: sb(n, [E, E]) for n in ("wq", "wk", "wv", "wo")}
        b = {n: sb(n, [S, E]) for n in ("bq", "bk", "bv", "bo", "weight", "gain")}
        rowsT = {n: sb(n, [E, K, S]) for n in ("keyT", "valueT")}
        loads = [(t[:], d[f"{tag}_{n}"]) for m in (w, b, rowsT) for n, t in m.items()]
        kk, vv = sb("k", [S, K, E]), sb("v", [S, K, E])
        half = sb("half", [S, 1])
        xin = [sb(f"xin{i}", [S, E]) for i in range(2)]
        xT = [sb(f"xT{i}", [E, S]) for i in range(2)]
        xb = [sb(f"xb{i}", [S, E]) for i in range(2)]
        q = sb("q", [S, E])
        prod = sb("prod", [S, K, E])
        logit = sb("logit", [S, K, HEADS])
        o = [sb(f"o{i}", [S, E]) for i in range(2)]
        sq = sb("sq", [S, E])
        ms = [sb(f"ms{i}", [S, 1]) for i in range(2)]
        gx = [sb(f"gx{i}", [S, E]) for i in range(2)]
        on = sb("on", [S, E])
        oT = sb("oT", [E, S])
        r = [sb(f"r{i}", [S, E]) for i in range(2)]
        stats = sb("stats", [S, 6])
        mv = [sb(f"mv{i}", [S, 2]) for i in range(2)]
        rstd = [sb(f"rstd{i}", [S, 1]) for i in range(2)]
        k_b, v_b = bank("k_b", [S, K, E]), bank("v_b", [S, K, E])
        x_b, q_b, t_b, y_b = (bank(n, [S, E]) for n in ("x_b", "q_b", "t_b", "y_b"))
        sem = sems("weights kv_ready setup xin_ready x_turned xT_copied q_ready xb_ready step meansq_ready rms_ready "
                   "gated sigmoid_ready on_ready on_turned oT_copied y_ready r_ready var_ready rstd_ready normed "
                   "gate_step res_step")
        n_loads = 16 * len(loads)
        STEPS = 8
        block = ctx.enter_context(nc.Block())

        @block.sync
        def _(sp):
            load_all(sp, loads, sem["weights"])

        @block.gpsimd
        def _(pool):
            pool.wait_ge(sem["weights"], n_loads)
            pool.wait_ge(sem["setup"], 1)

            def stage_in(n, p):
                reach(pool, sem["x_turned"], n - 1)
                pool.tensor_copy(xin[p][:], x[:, n, :]).then_inc(sem["xin_ready"], 1)

            def slot(n, p):
                pool.wait_ge(sem["meansq_ready"], n + 1)
                pool.tensor_tensor(ms[p][:], ms[p][:], half[:], ALU.pow).then_inc(sem["rms_ready"], 1)
                if within(n, 2, count):
                    stage_in(n + 2, p)
                if within(n, -1, count):
                    pool.wait_ge(sem["var_ready"], n)
                    pool.tensor_tensor(rstd[1 - p][:], rstd[1 - p][:], keep["minus_half"][:], ALU.pow)\
                        .then_inc(sem["rstd_ready"], 1)
                reach(pool, sem["r_ready"], n - 1)
                pool.tensor_tensor(xb[p][:], x[:, n, :], b["bo"][:], ALU.add).then_inc(sem["xb_ready"], 1)

            stage_in(0, 0)
            stage_in(1, 1)
            over_slots(pool, slot, count)
            pool.wait_ge(sem["var_ready"], count)
            pool.tensor_tensor(rstd[1][:], rstd[1][:], keep["minus_half"][:], ALU.pow).then_inc(sem["rstd_ready"], 1)

        @block.tensor
        def _(pe):
            pe.wait_ge(sem["weights"], n_loads)
            for s in range(K):
                pe.matmul(k_b[:, s, :], rowsT["keyT"][:, s, :], w["wk"][:], start=True, stop=True)
                mm = pe.matmul(v_b[:, s, :], rowsT["valueT"][:, s, :], w["wv"][:], start=True, stop=True)
            mm.then_inc(sem["kv_ready"], 1)

            def turn_x(n, p):
                pe.wait_ge(sem["xin_ready"], n + 1)
                reach(pe, sem["xT_copied"], n)
                pe.transpose(x_b[:], xin[p][:], ident[:]).then_inc(sem["x_turned"], 1)

            def queries(n, p):
                pe.wait_ge(sem["xT_copied"], n + 1)
                reach(pe, sem["step"], (n - 1) * STEPS + 1)
                pe.matmul(q_b[:], xT[p][:], w["wq"][:], start=True, stop=True).then_inc(sem["q_ready"], 1)

            def product(n):
                pe.wait_ge(sem["on_ready"], n + 1)
                reach(pe, sem["oT_copied"], n)
                pe.transpose(t_b[:], on[:], ident[:]).then_inc(sem["on_turned"], 1)
                pe.wait_ge(sem["oT_copied"], n + 1)
                reach(pe, sem["r_ready"], n)
                pe.matmul(y_b[:], oT[:], w["wo"][:], start=True, stop=True).then_inc(sem["y_ready"], 1)

            def slot(n, p):
                if within(n, 1, count):
                    turn_x(n + 1, 1 - p)
                    queries(n + 1, 1 - p)
                if within(n, -1, count):
                    product(n - 1)

            turn_x(0, 0)
            queries(0, 0)
            over_slots(pe, slot, count)
            product(count - 1)

        @block.scalar
        def _(act):
            def copy_xT(n, p):
                act.wait_ge(sem["x_turned"], n + 1)
                reach(act, sem["q_ready"], n - 1)
                act.activation(xT[p][:], x_b[:], ACT.Copy).then_inc(sem["xT_copied"], 1)

            def copy_oT(n):
                act.wait_ge(sem["on_turned"], n + 1)
                reach(act, sem["y_ready"], n)
                act.activation(oT[:], t_b[:], ACT.Copy).then_inc(sem["oT_copied"], 1)

            def slot(n, p):
                if within(n, 1, count):
                    copy_xT(n + 1, 1 - p)
                if within(n, -1, count):
                    copy_oT(n - 1)
                act.wait_ge(sem["gated"], n + 1)
                act.activation(gx[p][:], gx[p][:], ACT.Sigmoid).then_inc(sem["sigmoid_ready"], 1)

            copy_xT(0, 0)
            over_slots(act, slot, count)
            copy_oT(count - 1)

        @block.vector
        def _(dve):
            dve.wait_ge(sem["weights"], n_loads)
            dve.wait_ge(sem["kv_ready"], 1)
            dve.memset(half[:], 0.5)
            dve.tensor_tensor(kk[:], k_b[:], b["bk"][:].unsqueeze(1).broadcast_to([S, K, E]), ALU.add)
            dve.tensor_tensor(vv[:], v_b[:], b["bv"][:].unsqueeze(1).broadcast_to([S, K, E]), ALU.add)\
               .then_inc(sem["setup"], 1)
            dve.wait_ge(sem["setup"], 1)

            def chain(n, k, ins):
                ins.then_inc(sem["step"], 1)
                dve.wait_ge(sem["step"], n * STEPS + k)

            def attend(n, p):
                dve.wait_ge(sem["q_ready"], n + 1)
                chain(n, 1, dve.tensor_tensor(q[:], q_b[:], b["bq"][:], ALU.add))
                chain(n, 2, dve.scalar_tensor_tensor(out=prod[:], in0=kk[:], scalar=D ** -0.5,
                                                     in1=q[:].unsqueeze(1).broadcast_to([S, K, E]),
                                                     op0=ALU.mult, op1=ALU.mult))
                chain(n, 3, dve.tensor_reduce(logit[:], prod[:].rearrange("p k (h e) -> p k h e", h=HEADS),
                                              AX.X, ALU.add))
                chain(n, 4, dve.tensor_scalar(logit[:], logit[:], 0.0, None, ALU.max))
                chain(n, 5, dve.tensor_tensor(
                    prod[:].rearrange("p k (h e) -> p (k h) e", h=HEADS),
                    vv[:].rearrange("p k (h e) -> p (k h) e", h=HEADS),
                    copy_bcast(logit[:].rearrange("p k h -> p (k h)"), D), ALU.mult))
                reach(dve, sem["on_ready"], n - 1)
                chain(n, 6, dve.tensor_reduce(o[p][:], prod[:].rearrange("p k e -> p e k"), AX.X, ALU.add))
                dve.tensor_tensor(gx[p][:], o[p][:], b["gain"][:], ALU.mult).then_inc(sem["gated"], 1)
                chain(n, 7, dve.tensor_tensor(sq[:], o[p][:], o[p][:], ALU.mult))
                chain(n, 8, dve.tensor_reduce(ms[p][:], sq[:], AX.X, ALU.add))
                dve.tensor_scalar(ms[p][:], ms[p][:], 1.0 / E, None, ALU.mult).then_inc(sem["meansq_ready"], 1)

            def gated_norm(n, p):
                dve.wait_ge(sem["rms_ready"], n + 1)
                dve.wait_ge(sem["sigmoid_ready"], n + 1)
                gate_chain(n, 1, dve.tensor_scalar(ms[p][:], ms[p][:], 1e-8, None, ALU.add))
                gate_chain(n, 2, dve.reciprocal(ms[p][:], ms[p][:]))
                gate_chain(n, 3, dve.scalar_tensor_tensor(out=o[p][:], in0=o[p][:], scalar=ms[p][:, 0:1],
                                                          in1=b["weight"][:], op0=ALU.mult, op1=ALU.mult))
                reach(dve, sem["on_turned"], n)
                dve.tensor_tensor(on[:], o[p][:], gx[p][:], ALU.mult).then_inc(sem["on_ready"], 1)

            def gate_chain(n, k, ins):
                ins.then_inc(sem["gate_step"], 1)
                dve.wait_ge(sem["gate_step"], n * 3 + k)

            def residual(n, p):
                dve.wait_ge(sem["y_ready"], n + 1)
                dve.wait_ge(sem["xb_ready"], n + 1)
                dve.tensor_tensor(r[p][:], y_b[:], xb[p][:], ALU.add).then_inc(sem["r_ready"], 1)
                dve.wait_ge(sem["r_ready"], n + 1)
                res_chain(n, 1, dve.bn_stats(stats[:], r[p][:]))
                dve.sem_inc(keep["passed"], 1)
                res_chain(n, 2, dve.bn_aggr(mv[p][:], stats[:]))
                dve.tensor_scalar(rstd[p][:], mv[p][:, 1:2], LN_EPS, None, ALU.add).then_inc(sem["var_ready"], 1)

            def res_chain(n, k, ins):
                ins.then_inc(sem["res_step"], 1)
                dve.wait_ge(sem["res_step"], n * 2 + k)

            def norm(n, p):
                dve.wait_ge(sem["rstd_ready"], n + 1)
                dve.tensor_scalar(x[:, n, :], r[p][:], mv[p][:, 0:1], rstd[p][:, 0:1], ALU.subtract, ALU.mult)\
                   .then_inc(sem["normed"], 1)

            def slot(n, p):
                if within(n, -1, count):
                    gated_norm(n - 1, 1 - p)
                attend(n, p)
                if within(n, -2, count):
                    norm(n - 2, p)
                if within(n, -1, count):
                    residual(n - 1, 1 - p)

            over_slots(dve, slot, count)
            gated_norm(count - 1, 1)
            norm(count - 2, 0)
            residual(count - 1, 1)
            norm(count - 1, 1)

    clear(nc, sem)


def one_head_attention(nc, d, keep, tag):
    count = SEQS
    x, ident = keep["x"], keep["ident"]
    with ExitStack() as ctx:
        sb, bank, sems = tensors(ctx, nc, tag)
        wq, wk, wv = sb("wq", [E, E]), sb("wk", [C, E]), sb("wv", [C, E])
        qb, kb, vb = sb("qb", [E, 1]), sb("kb", [E, 1]), sb("vb", [S, E])
        loads = [(wq[:], d[tag + "_wq"]), (wk[:], d[tag + "_wk"]), (wv[:], d[tag + "_wv"]),
                 (qb[:], d[tag + "_bq"]), (kb[:], d[tag + "_bk"]), (vb[:], d[tag + "_bv"])]
        xin = [sb(f"xin{i}", [S, E]) for i in range(2)]
        cin = [sb(f"cin{i}", [C, CTX]) for i in range(2)]
        xb = [sb(f"xb{i}", [S, E]) for i in range(2)]
        xT = [sb(f"xT{i}", [E, S]) for i in range(2)]
        qT = [sb(f"qT{i}", [E, S]) for i in range(2)]
        kT = [sb(f"kT{i}", [E, CTX]) for i in range(2)]
        v = [sb(f"v{i}", [CTX, E]) for i in range(2)]
        negmax = [sb(f"negmax{i}", [S, 1]) for i in range(2)]
        prob = [sb(f"prob{i}", [S, CTX]) for i in range(2)]
        total = [sb(f"total{i}", [S, 1]) for i in range(2)]
        pT = [sb(f"pT{i}", [CTX, S]) for i in range(2)]
        r = [sb(f"r{i}", [S, E]) for i in range(2)]
        stats = sb("stats", [S, 6])
        mv = [sb(f"mv{i}", [S, 2]) for i in range(2)]
        rstd = [sb(f"rstd{i}", [S, 1]) for i in range(2)]
        x_b, q_b, k_b, v_b, s_b, t_b, o_b = (bank(n, [S, S]) for n in ("x", "q", "k", "v", "s", "t", "o"))
        sem = sems("weights xin_ready x_turned xT_copied ctx_loaded0 ctx_loaded1 q_ready q_copied k_ready k_copied "
                   "v_ready v_copied scores_ready max_ready probs_ready probs_turned pT_copied o_ready inv_ready "
                   "xb_ready r_ready step var_ready rstd_ready normed")
        n_loads = 16 * len(loads)
        block = ctx.enter_context(nc.Block())

        @block.sync
        def _(sp):
            load_all(sp, loads, sem["weights"])

            def slot(n, p):
                reach(sp, sem["v_ready"], n - 1)
                sp.dma_start(cin[p][:], d["ctxT"][n]).then_inc(sem[f"ctx_loaded{p}"], 16)

            over_slots(sp, slot, count)

        @block.gpsimd
        def _(pool):
            pool.wait_ge(sem["weights"], n_loads)

            def stage_in(n, p):
                reach(pool, sem["x_turned"], n - 1)
                pool.tensor_copy(xin[p][:], x[:, n, :]).then_inc(sem["xin_ready"], 1)

            def root(n, p):
                pool.wait_ge(sem["var_ready"], n + 1)
                pool.tensor_tensor(rstd[p][:], rstd[p][:], keep["minus_half"][:], ALU.pow)\
                    .then_inc(sem["rstd_ready"], 1)

            def slot(n, p):
                if within(n, 2, count):
                    stage_in(n + 2, p)
                reach(pool, sem["r_ready"], n - 1)
                pool.tensor_tensor(xb[p][:], x[:, n, :], vb[:], ALU.add).then_inc(sem["xb_ready"], 1)
                if within(n, -2, count):
                    root(n - 2, p)

            stage_in(0, 0)
            stage_in(1, 1)
            over_slots(pool, slot, count)
            root(count - 2, 0)
            root(count - 1, 1)

        @block.tensor
        def _(pe):
            pe.wait_ge(sem["weights"], n_loads)

            def turn_x(n, p):
                pe.wait_ge(sem["xin_ready"], n + 1)
                reach(pe, sem["xT_copied"], n)
                pe.transpose(x_b[:], xin[p][:], ident[:]).then_inc(sem["x_turned"], 1)

            def project(n, p):
                pe.wait_ge(sem["xT_copied"], n + 1)
                reach(pe, sem["q_copied"], n)
                pe.matmul(q_b[:], wq[:], xT[p][:], start=True, stop=True).then_inc(sem["q_ready"], 1)
                pe.wait_ge(sem[f"ctx_loaded{p}"], (n - p) * 8 + 16)
                reach(pe, sem["k_copied"], n)
                pe.matmul(k_b[:, 0:CTX], wk[:], cin[p][:], start=True, stop=True).then_inc(sem["k_ready"], 1)
                reach(pe, sem["v_copied"], n)
                pe.matmul(v_b[0:CTX, :], cin[p][:], wv[:], start=True, stop=True).then_inc(sem["v_ready"], 1)

            def score(n, p):
                pe.wait_ge(sem["q_copied"], n + 1)
                pe.wait_ge(sem["k_copied"], n + 1)
                reach(pe, sem["probs_ready"], n)
                pe.matmul(s_b[:, 0:CTX], qT[p][:], kT[p][:], start=True, stop=True).then_inc(sem["scores_ready"], 1)

            def turn_probs(n, p):
                pe.wait_ge(sem["probs_ready"], n + 1)
                reach(pe, sem["pT_copied"], n)
                pe.transpose(t_b[0:CTX, :], prob[p][:], ident[:]).then_inc(sem["probs_turned"], 1)

            def weigh(n, p):
                pe.wait_ge(sem["pT_copied"], n + 1)
                pe.wait_ge(sem["v_copied"], n + 1)
                reach(pe, sem["r_ready"], n)
                pe.matmul(o_b[:], pT[p][:], v[p][:], start=True, stop=True).then_inc(sem["o_ready"], 1)

            def slot(n, p):
                score(n, p)
                if within(n, 2, count):
                    turn_x(n + 2, p)
                if within(n, -1, count):
                    weigh(n - 1, 1 - p)
                if within(n, 1, count):
                    project(n + 1, 1 - p)
                turn_probs(n, p)

            turn_x(0, 0)
            project(0, 0)
            turn_x(1, 1)
            over_slots(pe, slot, count)
            weigh(count - 1, 1)

        @block.scalar
        def _(act):
            act.wait_ge(sem["weights"], n_loads)

            def copy_xT(n, p):
                act.wait_ge(sem["x_turned"], n + 1)
                reach(act, sem["q_ready"], n - 1)
                act.activation(xT[p][:], x_b[:], ACT.Copy).then_inc(sem["xT_copied"], 1)

            def copy_qkv(n, p):
                act.wait_ge(sem["q_ready"], n + 1)
                reach(act, sem["scores_ready"], n - 1)
                act.activation(qT[p][:], q_b[:], ACT.Identity, bias=qb[:, 0:1]).then_inc(sem["q_copied"], 1)
                act.wait_ge(sem["k_ready"], n + 1)
                act.activation(kT[p][:], k_b[:, 0:CTX], ACT.Identity, bias=kb[:, 0:1]).then_inc(sem["k_copied"], 1)
                act.wait_ge(sem["v_ready"], n + 1)
                reach(act, sem["o_ready"], n - 1)
                act.activation(v[p][:], v_b[0:CTX, :], ACT.Copy).then_inc(sem["v_copied"], 1)

            def slot(n, p):
                act.wait_ge(sem["max_ready"], n + 1)
                reach(act, sem["probs_turned"], n - 1)
                reach(act, sem["r_ready"], n - 1)
                act.activation(prob[p][:], s_b[:, 0:CTX], ACT.Exp, bias=negmax[p][:, 0:1],
                               accum_out=total[p][:, 0:1]).then_inc(sem["probs_ready"], 1)
                if within(n, 2, count):
                    copy_xT(n + 2, p)
                if within(n, 1, count):
                    copy_qkv(n + 1, 1 - p)

            copy_xT(0, 0)
            copy_qkv(0, 0)
            copy_xT(1, 1)
            over_slots(act, slot, count)

        @block.vector
        def _(dve):
            dve.wait_ge(sem["weights"], n_loads)

            def maximum(n, p):
                dve.wait_ge(sem["scores_ready"], n + 1)
                reach(dve, sem["probs_ready"], n - 1)
                dve.tensor_reduce(negmax[p][:], s_b[:, 0:CTX], AX.X, ALU.max, negate=True)\
                   .then_inc(sem["max_ready"], 1)

            def copy_pT(n, p):
                dve.wait_ge(sem["probs_turned"], n + 1)
                reach(dve, sem["o_ready"], n - 1)
                dve.tensor_copy(pT[p][:], t_b[0:CTX, :]).then_inc(sem["pT_copied"], 1)

            def residual(n, p):
                dve.wait_ge(sem["probs_ready"], n + 1)
                dve.reciprocal(total[p][:], total[p][:]).then_inc(sem["inv_ready"], 1)
                dve.wait_ge(sem["inv_ready"], n + 1)
                dve.wait_ge(sem["o_ready"], n + 1)
                dve.wait_ge(sem["xb_ready"], n + 1)
                dve.scalar_tensor_tensor(out=r[p][:], in0=o_b[:], scalar=total[p][:, 0:1], in1=xb[p][:],
                                         op0=ALU.mult, op1=ALU.add).then_inc(sem["r_ready"], 1)
                dve.wait_ge(sem["r_ready"], n + 1)
                dve.bn_stats(stats[:], r[p][:]).then_inc(sem["step"], 1)
                wait_alone(dve, sem["step"], n * 2 + 1, keep["passed"])
                dve.bn_aggr(mv[p][:], stats[:]).then_inc(sem["step"], 1)
                dve.wait_ge(sem["step"], n * 2 + 2)
                dve.tensor_scalar(rstd[p][:], mv[p][:, 1:2], LN_EPS, None, ALU.add).then_inc(sem["var_ready"], 1)

            def norm(n, p):
                dve.wait_ge(sem["rstd_ready"], n + 1)
                dve.tensor_scalar(x[:, n, :], r[p][:], mv[p][:, 0:1], rstd[p][:, 0:1], ALU.subtract, ALU.mult)\
                   .then_inc(sem["normed"], 1)

            def slot(n, p):
                maximum(n, p)
                if within(n, -2, count):
                    norm(n - 2, p)
                if within(n, -1, count):
                    residual(n - 1, 1 - p)
                copy_pT(n, p)

            over_slots(dve, slot, count)
            norm(count - 2, 0)
            residual(count - 1, 1)
            norm(count - 1, 1)

    clear(nc, sem)


def linear(nc, d, keep, tag):
    count = SEQS
    x, ident = keep["x"], keep["ident"]
    with ExitStack() as ctx:
        sb, bank, sems = tensors(ctx, nc, tag)
        w, factor, bias = sb("w", [E, E]), sb("factor", [S, E]), sb("bias", [S, E])
        loads = [(w[:], d[tag + "_w"]), (factor[:], d[tag + "_scale"]), (bias[:], d[tag + "_bias"])]
        xin = [sb(f"xin{i}", [S, E]) for i in range(2)]
        xb = [sb(f"xb{i}", [S, E]) for i in range(2)]
        xT = [sb(f"xT{i}", [E, S]) for i in range(2)]
        y = sb("y", [S, E])
        r = [sb(f"r{i}", [S, E]) for i in range(2)]
        stats = sb("stats", [S, 6])
        mv = [sb(f"mv{i}", [S, 2]) for i in range(2)]
        rstd = [sb(f"rstd{i}", [S, 1]) for i in range(2)]
        x_b = [bank(f"x{i}", [S, S]) for i in range(2)]
        y_b = [bank(f"y{i}", [S, S]) for i in range(2)]
        sem = sems("weights setup xin_ready x_turned xT_copied y_ready scaled xb_ready r_ready step var_ready "
                   "rstd_ready normed")
        block = ctx.enter_context(nc.Block())

        @block.sync
        def _(sp):
            load_all(sp, loads, sem["weights"])

        @block.gpsimd
        def _(pool):
            pool.wait_ge(sem["weights"], 48)

            def stage_in(n, p):
                reach(pool, sem["x_turned"], n - 1)
                pool.tensor_copy(xin[p][:], x[:, n, :]).then_inc(sem["xin_ready"], 1)

            def root(n, p):
                pool.wait_ge(sem["var_ready"], n + 1)
                pool.tensor_tensor(rstd[p][:], rstd[p][:], keep["minus_half"][:], ALU.pow)\
                    .then_inc(sem["rstd_ready"], 1)

            def slot(n, p):
                reach(pool, sem["r_ready"], n - 1)
                pool.tensor_tensor(xb[p][:], x[:, n, :], bias[:], ALU.add).then_inc(sem["xb_ready"], 1)
                if within(n, 2, count):
                    stage_in(n + 2, p)
                if within(n, -1, count):
                    root(n - 1, 1 - p)

            stage_in(0, 0)
            stage_in(1, 1)
            over_slots(pool, slot, count)
            root(count - 1, 1)

        @block.tensor
        def _(pe):
            pe.wait_ge(sem["weights"], 48)

            def turn_x(n, p):
                pe.wait_ge(sem["xin_ready"], n + 1)
                reach(pe, sem["xT_copied"], n - 1)
                pe.transpose(x_b[p][:], xin[p][:], ident[:]).then_inc(sem["x_turned"], 1)

            def slot(n, p):
                if within(n, 1, count):
                    turn_x(n + 1, 1 - p)
                pe.wait_ge(sem["xT_copied"], n + 1)
                reach(pe, sem["scaled"], n - 1)
                pe.matmul(y_b[p][:], xT[p][:], w[:], start=True, stop=True).then_inc(sem["y_ready"], 1)

            turn_x(0, 0)
            over_slots(pe, slot, count)

        @block.scalar
        def _(act):
            def slot(n, p):
                act.wait_ge(sem["x_turned"], n + 1)
                reach(act, sem["y_ready"], n - 1)
                act.activation(xT[p][:], x_b[p][:], ACT.Copy).then_inc(sem["xT_copied"], 1)

            over_slots(act, slot, count)

        @block.vector
        def _(dve):
            dve.wait_ge(sem["weights"], 48)
            dve.tensor_scalar(factor[:], factor[:], 1.0 / 127.0, None, ALU.mult).then_inc(sem["setup"], 1)
            dve.wait_ge(sem["setup"], 1)

            def residual(n, p):
                dve.wait_ge(sem["y_ready"], n + 1)
                dve.tensor_tensor(y[:], y_b[p][:], factor[:], ALU.mult).then_inc(sem["scaled"], 1)
                dve.wait_ge(sem["scaled"], n + 1)
                dve.wait_ge(sem["xb_ready"], n + 1)
                dve.tensor_tensor(r[p][:], y[:], xb[p][:], ALU.add).then_inc(sem["r_ready"], 1)
                dve.wait_ge(sem["r_ready"], n + 1)
                dve.bn_stats(stats[:], r[p][:]).then_inc(sem["step"], 1)
                wait_alone(dve, sem["step"], n * 2 + 1, keep["passed"])
                dve.bn_aggr(mv[p][:], stats[:]).then_inc(sem["step"], 1)
                dve.wait_ge(sem["step"], n * 2 + 2)
                dve.tensor_scalar(rstd[p][:], mv[p][:, 1:2], LN_EPS, None, ALU.add).then_inc(sem["var_ready"], 1)

            def norm(n, p):
                dve.wait_ge(sem["rstd_ready"], n + 1)
                dve.tensor_scalar(x[:, n, :], r[p][:], mv[p][:, 0:1], rstd[p][:, 0:1], ALU.subtract, ALU.mult)\
                   .then_inc(sem["normed"], 1)

            def slot(n, p):
                residual(n, p)
                if within(n, -1, count):
                    norm(n - 1, 1 - p)

            over_slots(dve, slot, count)
            norm(count - 1, 1)

    clear(nc, sem)


def compress_blocks(nc, d, keep, tag):
    G, T, B, N = 4, 4 * S, 16, 8
    groups = SEQS // G
    x, ident = keep["x"], keep["ident"]
    with ExitStack() as ctx:
        sb, bank, sems = tensors(ctx, nc, tag)
        w = {t: sb("w" + t, [E, E]) for t in "kv"}
        wc = {t: sb("wc" + t, [E, B, E]) for t in "kv"}
        loads = [(w[t][:], d[f"l3_attn_flat{t}"]) for t in "kv"]
        loads += [(wc[t][:], d[f"l3_attn_wc{t}"]) for t in "kv"]
        xin = sb("xin", [S, G, E])
        xT = sb("xT", [E, T])
        full = {t: [sb(f"{t}{i}", [E, T]) for i in range(2)] for t in "kv"}
        x_b = bank("x", [E, T])
        f_b = {t: bank("f" + t, [E, T]) for t in "kv"}
        c_b = {t: [bank(f"c{t}{i}", [E, G * N]) for i in range(2)] for t in "kv"}
        sem = sems("weights xin_ready x_turned xT_copied full_ready k_copied v_copied k_compressed v_compressed "
                   "k_stored v_stored")
        block = ctx.enter_context(nc.Block())

        @block.sync
        def _(sp):
            load_all(sp, loads, sem["weights"])

        @block.gpsimd
        def _(pool):
            def slot(g, p):
                reach(pool, sem["x_turned"], g)
                pool.tensor_copy(xin[:], x[:, bass.ds(g * G, G), :]).then_inc(sem["xin_ready"], 1)

            over_slots(pool, slot, groups)

        @block.tensor
        def _(pe):
            pe.wait_ge(sem["weights"], 64)

            def project(g):
                pe.wait_ge(sem["xin_ready"], g + 1)
                reach(pe, sem["xT_copied"], g)
                for s in range(G):
                    mm = pe.transpose(x_b[:, s * S:(s + 1) * S], xin[:, s, :], ident[:])
                mm.then_inc(sem["x_turned"], 1)
                pe.wait_ge(sem["xT_copied"], g + 1)
                for t in "kv":
                    reach(pe, sem[t + "_copied"], g)
                    pe.matmul(f_b[t][:], w[t][:], xT[:], start=True, stop=True).then_inc(sem["full_ready"], 1)

            def slot(g, p):
                if within(g, 1, groups):
                    project(g + 1)
                for t in "kv":
                    pe.wait_ge(sem[t + "_copied"], g + 1)
                    reach(pe, sem[t + "_stored"], g - 1)
                    for b in range(B):
                        mm = pe.matmul(c_b[t][p][:], wc[t][:, b, :],
                                       full[t][p][:].rearrange("p (n b) -> p b n", b=B)[:, b, :],
                                       start=(b == 0), stop=(b == B - 1))
                    mm.then_inc(sem[t + "_compressed"], 1)

            project(0)
            over_slots(pe, slot, groups)

        @block.scalar
        def _(act):
            def copies(g, p):
                act.wait_ge(sem["x_turned"], g + 1)
                reach(act, sem["full_ready"], g * 2)
                act.activation(xT[:], x_b[:], ACT.Copy).then_inc(sem["xT_copied"], 1)
                for i, t in enumerate("kv"):
                    act.wait_ge(sem["full_ready"], g * 2 + i + 1)
                    reach(act, sem[t + "_compressed"], g - 1)
                    act.activation(full[t][p][:], f_b[t][:], ACT.Copy).then_inc(sem[t + "_copied"], 1)

            def slot(g, p):
                if within(g, 1, groups):
                    copies(g + 1, 1 - p)

            copies(0, 0)
            over_slots(act, slot, groups)

        @block.vector
        def _(dve):
            def slot(g, p):
                for t in "kv":
                    dve.wait_ge(sem[t + "_compressed"], g + 1)
                    dve.tensor_copy(keep[t + "c"][:, bass.ds(g * G, G), :],
                                    c_b[t][p][:].rearrange("p (s n) -> p s n", s=G)).then_inc(sem[t + "_stored"], 1)

            over_slots(dve, slot, groups)

    clear(nc, sem)


def sparse_attention(nc, d, keep, tag):
    count, hd, N, D = SEQS, E, 8, 8
    x, ident = keep["x"], keep["ident"]
    with ExitStack() as ctx:
        sb, bank, sems = tensors(ctx, nc, tag)
        wq, wk = sb("wq", [E, 4, E]), sb("wk", [E, 4, E])
        wflat, wv, wo = sb("wflat", [E, E]), sb("wv", [E, E]), sb("wo", [E, E])
        wg, bg = sb("wg", [E, 3]), sb("bg", [S, 3])
        own = sb("own", [E, HEADS])
        ok, low = sb("ok", [S, N]), sb("low", [S, N])
        some = sb("some", [S, 1])
        before = sb("before", [S, N, N])
        m_f = {t: sb(t + "_f", [S, S]) for t in ("causal", "band")}
        blocks_f = sb("blocks_f", [S, 4, S])
        loads = [(wq[:], d["l3_attn_wq"]), (wk[:], d["l3_attn_wk"]), (wflat[:], d["l3_attn_flatq"]),
                 (wv[:], d["l3_attn_flatv"]), (wo[:], d["l3_attn_wo"]), (wg[:], d["l3_attn_wg"]),
                 (bg[:], d["l3_attn_bg"]), (own[:], d["own"]), (ok[:], d["block_ok"]), (low[:], d["block_low"]),
                 (some[:], d["block_some"]), (before[:], d["l1_moe_before"]), (m_f["causal"][:], d["causal"]),
                 (m_f["band"][:], d["band"]), (blocks_f[:], d["blocks"])]
        mask = {t: sb(t, [S, 4, S], BF16) for t in ("causal", "band")}
        blocks = sb("blocks", [S, 4, S], BF16)
        xin = [sb(f"xin{i}", [S, E]) for i in range(2)]
        xT = [sb(f"xT{i}", [E, S]) for i in range(2)]
        qT = [sb(f"qT{i}", [E, 4, S]) for i in range(2)]
        kT = [sb(f"kT{i}", [E, 4, S]) for i in range(2)]
        v = [sb(f"v{i}", [S, E]) for i in range(2)]
        qf = sb("qf", [E, S])
        kcd, vcd = sb("kcd", [E, HEADS, N]), sb("vcd", [E, HEADS, N])
        vcT = [sb(f"vcT{i}", [HEADS * N, E]) for i in range(2)]
        logit, e = sb("logit", [S, HEADS, N]), sb("e", [S, HEADS * N + 3])
        top, gtop = sb("top", [S, HEADS]), sb("gtop", [S, 1])
        more, same = sb("more", [S, HEADS, N, N]), sb("same", [S, HEADS, N, N])
        rank = sb("rank", [S, HEADS, N])
        closed, pc = sb("closed", [S, HEADS * N]), sb("pc", [S, HEADS, N])
        gate = [sb(f"gate{i}", [S, 3]) for i in range(2)]
        pcT = [sb(f"pcT{i}", [HEADS * N, S]) for i in range(2)]
        closedT = [sb(f"closedT{i}", [HEADS * N, S], BF16) for i in range(2)]
        negmax = [sb(f"negmax{i}", [S, 4]) for i in range(2)]
        prob = [[sb(f"prob{b}{i}", [S, 4, S]) for i in range(2)] for b in range(2)]
        sums = [sb(f"sums{i}", [S, 4, 2, 4]) for i in range(2)]
        wt = [sb(f"wt{i}", [S, 2, 4]) for i in range(2)]
        local = [sb(f"local{i}", [S, 4, S]) for i in range(2)]
        mix = [sb(f"mix{i}", [S, 4, S]) for i in range(2)]
        pT = [sb(f"pT{i}", [S, 4, S]) for i in range(2)]
        o, oT = sb("o", [S, hd]), sb("oT", [E, S])
        r = [sb(f"r{i}", [S, E]) for i in range(2)]
        stats = sb("stats", [S, 6])
        mv = [sb(f"mv{i}", [S, 2]) for i in range(2)]
        rstd = [sb(f"rstd{i}", [S, 1]) for i in range(2)]
        xb = [sb(f"xb{i}", [S, E]) for i in range(2)]
        score = [bank(f"score{i}", [S, 4, S]) for i in range(2)]
        turned = [bank(f"turned{i}", [S, 4, S]) for i in range(2)]
        out_b, qk_b = bank("out", [S, 512]), bank("qk", [E, 4, S])
        misc, comp = bank("misc", [S, 512]), bank("comp", [S, 512])
        sem = sems("weights setup xin_ready x_turned xT_copied q_ready q_copied k_ready k_copied qf_ready qf_copied "
                   "kcd_ready vcd_ready cs_ready e_ready e_exp v_ready v_copied comp_ready comp_turned comp_copied "
                   "scores_ready max_ready probs_ready wt_step wt_ready local_ready mix_ready probs_turned pT_copied "
                   "pv_done o_copied o_turned oT_copied y_ready xb_ready r_ready step comp_step var_ready rstd_ready "
                   "normed")
        n_loads = 16 * len(loads)
        block = ctx.enter_context(nc.Block())

        @block.sync
        def _(sp):
            load_all(sp, loads, sem["weights"])

        @block.gpsimd
        def _(pool):
            pool.wait_ge(sem["weights"], n_loads)

            def stage_in(n, p):
                reach(pool, sem["x_turned"], n - 1)
                pool.tensor_copy(xin[p][:], x[:, n, :]).then_inc(sem["xin_ready"], 1)

            def diagonal(n):
                for t, out_t, used in (("k", kcd, "cs_ready"), ("v", vcd, "v_ready")):
                    reach(pool, sem[used], n)
                    pool.tensor_tensor(out_t[:], keep[t + "c"][:, n, :].unsqueeze(1).broadcast_to([E, HEADS, N]),
                                       copy_bcast(own[:], N), ALU.mult).then_inc(sem[t + "cd_ready"], 1)

            def weigh_local(n, a):
                u = n * 4 + a
                pool.wait_ge(sem["wt_ready"], u + 1)
                reach(pool, sem["mix_ready"], u - 1)
                pool.tensor_tensor(local[a % 2][:], prob[1][a % 2][:], copy_bcast(wt[a % 2][:, 1, :], S), ALU.mult)\
                    .then_inc(sem["local_ready"], 1)

            def root(n, p):
                pool.wait_ge(sem["var_ready"], n + 1)
                pool.tensor_tensor(rstd[p][:], rstd[p][:], keep["minus_half"][:], ALU.pow)\
                    .then_inc(sem["rstd_ready"], 1)

            def slot(n, p):
                if within(n, 1, count):
                    diagonal(n + 1)
                weigh_local(n, 0)
                if within(n, 2, count):
                    stage_in(n + 2, p)
                weigh_local(n, 1)
                reach(pool, sem["r_ready"], n - 1)
                pool.tensor_copy(xb[p][:], x[:, n, :]).then_inc(sem["xb_ready"], 1)
                weigh_local(n, 2)
                weigh_local(n, 3)
                if within(n, -1, count):
                    root(n - 1, 1 - p)

            stage_in(0, 0)
            stage_in(1, 1)
            diagonal(0)
            over_slots(pool, slot, count)
            root(count - 1, 1)

        @block.tensor
        def _(pe):
            pe.wait_ge(sem["weights"], n_loads)
            pe.wait_ge(sem["setup"], 1)

            def turn_x(n, p):
                pe.wait_ge(sem["xin_ready"], n + 1)
                reach(pe, sem["r_ready"], n - 2)
                reach(pe, sem["v_copied"], n)
                pe.transpose(misc[:, 0:S], xin[p][:], ident[:]).then_inc(sem["x_turned"], 1)

            def flat_queries(n, p):
                pe.wait_ge(sem["xT_copied"], n + 1)
                reach(pe, sem["comp_copied"], n)
                pe.matmul(comp[:, 0:S], wflat[:], xT[p][:], start=True, stop=True).then_inc(sem["qf_ready"], 1)

            def queries(n, p):
                reach(pe, sem["k_copied"], n)
                for c in range(4):
                    mm = pe.matmul(qk_b[:, c, :], wq[:, c, :], xT[p][:], start=True, stop=True)
                mm.then_inc(sem["q_ready"], 1)

            def keys_of(n, p):
                pe.wait_ge(sem["q_copied"], n + 1)
                for c in range(4):
                    mm = pe.matmul(qk_b[:, c, :], wk[:, c, :], xT[p][:], start=True, stop=True)
                mm.then_inc(sem["k_ready"], 1)

            def block_scores(n):
                pe.wait_ge(sem["qf_copied"], n + 1)
                pe.wait_ge(sem["kcd_ready"], n + 1)
                pe.matmul(comp[:, 0:S], qf[:], kcd[:].rearrange("p h n -> p (h n)"), start=True, stop=True)
                pe.matmul(comp[:, S:S + 3], qf[:], wg[:], start=True, stop=True).then_inc(sem["cs_ready"], 1)

            def values_of(n, p):
                pe.wait_ge(sem["vcd_ready"], n + 1)
                pe.wait_ge(sem["xT_copied"], n + 1)
                pe.transpose(misc[:, S:2 * S], vcd[:].rearrange("p h n -> p (h n)"), ident[:])
                pe.matmul(misc[:, 0:E], xT[p][:], wv[:], start=True, stop=True).then_inc(sem["v_ready"], 1)

            def turn_comp(n):
                pe.wait_ge(sem["comp_ready"], n + 1)
                pe.transpose(comp[:, 0:S], pc[:].rearrange("p h n -> p (h n)"), ident[:])
                pe.transpose(comp[:, S:2 * S], closed[:], ident[:]).then_inc(sem["comp_turned"], 1)

            def scores(n, p, a, b):
                u = n * 8 + 2 * a + b
                if a == 0 and b == 0:
                    pe.wait_ge(sem["q_copied"], n + 1)
                    pe.wait_ge(sem["k_copied"], n + 1)
                    pe.wait_ge(sem["comp_copied"], n + 1)
                reach(pe, sem["probs_ready"], u - 1)
                rows = slice(32 * a, 32 * a + D)
                for j in range(4):
                    pe.matmul(score[b][:, j, :], qT[p][rows, j, :], kT[p][rows, j, :], start=(j == 0), stop=False,
                              skip_group_check=True)
                if b == 0:
                    rows = slice(32 * a, 32 * a + 32)
                    pe.matmul(score[b][:], closedT[p][rows, :], blocks[rows, :, :], start=False, stop=False,
                              skip_group_check=True)
                pe.matmul(score[b][:], keep["ident_bf"][:], mask["band" if b else "causal"][:], start=False,
                          stop=True, skip_group_check=True).then_inc(sem["scores_ready"], 1)

            def turn_probs(n, a):
                u = n * 4 + a
                pe.wait_ge(sem["mix_ready"], u + 1)
                reach(pe, sem["pT_copied"], u - 1)
                for j in range(4):
                    mm = pe.transpose(turned[a % 2][:, j, :], mix[a % 2][:, j, :], ident[:])
                mm.then_inc(sem["probs_turned"], 1)

            def weigh(n, p, a):
                u = n * 4 + a
                if a == 0:
                    pe.wait_ge(sem["v_copied"], n + 1)
                    reach(pe, sem["o_copied"], n)
                    pe.matmul(out_b[:, 0:hd], pcT[p][:], vcT[p][:], start=True, stop=False, skip_group_check=True)
                pe.wait_ge(sem["pT_copied"], u + 1)
                for j in range(4):
                    h = 4 * a + j
                    mm = pe.matmul(out_b[:, h * D:(h + 1) * D], pT[a % 2][:, j, :], v[p][:, h * D:(h + 1) * D],
                                   start=False, stop=True, skip_group_check=True)
                mm.then_inc(sem["pv_done"], 1)

            def turn_o(n):
                reach(pe, sem["r_ready"], n)
                pe.wait_ge(sem["o_copied"], n + 1)
                pe.wait_ge(sem["v_copied"], min(n + 3, count) if isinstance(n, int) else n + 3)
                pe.transpose(misc[:, 0:S], o[:], ident[:]).then_inc(sem["o_turned"], 1)

            def out_product(n):
                pe.wait_ge(sem["oT_copied"], n + 1)
                pe.matmul(misc[:, 0:E], oT[:], wo[:], start=True, stop=True).then_inc(sem["y_ready"], 1)

            def slot(n, p):
                nxt = within(n, 1, count)
                scores(n, p, 0, 0)
                scores(n, p, 0, 1)
                if nxt:
                    flat_queries(n + 1, 1 - p)
                    queries(n + 1, 1 - p)
                scores(n, p, 1, 0)
                scores(n, p, 1, 1)
                if nxt:
                    block_scores(n + 1)
                    keys_of(n + 1, 1 - p)
                turn_probs(n, 0)
                scores(n, p, 2, 0)
                scores(n, p, 2, 1)
                if nxt:
                    values_of(n + 1, 1 - p)
                turn_probs(n, 1)
                weigh(n, p, 0)
                scores(n, p, 3, 0)
                scores(n, p, 3, 1)
                if within(n, -1, count):
                    turn_o(n - 1)
                turn_probs(n, 2)
                weigh(n, p, 1)
                if within(n, -1, count):
                    out_product(n - 1)
                turn_probs(n, 3)
                weigh(n, p, 2)
                if within(n, 2, count):
                    turn_x(n + 2, p)
                if nxt:
                    turn_comp(n + 1)
                weigh(n, p, 3)

            turn_x(0, 0)
            flat_queries(0, 0)
            queries(0, 0)
            block_scores(0)
            keys_of(0, 0)
            values_of(0, 0)
            turn_comp(0)
            turn_x(1, 1)
            over_slots(pe, slot, count)
            turn_o(count - 1)
            out_product(count - 1)

        @block.scalar
        def _(act):
            def copy_xT(n, p):
                act.wait_ge(sem["x_turned"], n + 1)
                reach(act, sem["v_ready"], n - 1)
                act.activation(xT[p][:], misc[:, 0:S], ACT.Copy).then_inc(sem["xT_copied"], 1)

            def copy_qf(n):
                act.wait_ge(sem["qf_ready"], n + 1)
                reach(act, sem["cs_ready"], n)
                act.activation(qf[:], comp[:, 0:S], ACT.Copy).then_inc(sem["qf_copied"], 1)

            def block_exp(n):
                act.wait_ge(sem["e_ready"], n + 1)
                act.activation(e[:], e[:], ACT.Exp).then_inc(sem["e_exp"], 1)

            def copy_v(n, p):
                act.wait_ge(sem["v_ready"], n + 1)
                reach(act, sem["pv_done"], (n - 1) * 4)
                act.activation(v[p][:], misc[:, 0:E], ACT.Copy)
                act.activation(vcT[p][:], misc[:, S:2 * S], ACT.Copy).then_inc(sem["v_copied"], 1)

            def copy_comp(n, p):
                act.wait_ge(sem["comp_turned"], n + 1)
                reach(act, sem["pv_done"], (n - 1) * 4)
                act.activation(pcT[p][:], comp[:, 0:S], ACT.Copy)
                act.activation(closedT[p][:], comp[:, S:2 * S], ACT.Copy).then_inc(sem["comp_copied"], 1)

            def exps(n, p, a, b):
                u = n * 8 + 2 * a + b
                act.wait_ge(sem["max_ready"], u + 1)
                reach(act, sem["mix_ready"], n * 4 + a - 1)
                for j in range(4):
                    i = act.activation(prob[b][a % 2][:, j, :], score[b][:, j, :], ACT.Exp,
                                       bias=negmax[b][:, j:j + 1], accum_out=sums[p][:, a, b, j:j + 1])
                i.then_inc(sem["probs_ready"], 1)

            def copy_pT(n, a):
                u = n * 4 + a
                act.wait_ge(sem["probs_turned"], u + 1)
                reach(act, sem["pv_done"], u - 1)
                act.activation(pT[a % 2][:], turned[a % 2][:], ACT.Copy).then_inc(sem["pT_copied"], 1)

            def copy_o(n):
                act.wait_ge(sem["pv_done"], (n + 1) * 4)
                reach(act, sem["o_turned"], n)
                act.activation(o[:], out_b[:, 0:hd], ACT.Copy).then_inc(sem["o_copied"], 1)

            def copy_oT(n):
                act.wait_ge(sem["o_turned"], n + 1)
                reach(act, sem["y_ready"], n)
                act.activation(oT[:], misc[:, 0:S], ACT.Copy).then_inc(sem["oT_copied"], 1)

            def slot(n, p):
                nxt = within(n, 1, count)
                exps(n, p, 0, 0)
                if within(n, -1, count):
                    copy_o(n - 1)
                exps(n, p, 0, 1)
                if nxt:
                    copy_qf(n + 1)
                exps(n, p, 1, 0)
                exps(n, p, 1, 1)
                copy_pT(n, 0)
                exps(n, p, 2, 0)
                exps(n, p, 2, 1)
                if nxt:
                    block_exp(n + 1)
                    copy_v(n + 1, 1 - p)
                copy_pT(n, 1)
                exps(n, p, 3, 0)
                if within(n, -1, count):
                    copy_oT(n - 1)
                exps(n, p, 3, 1)
                copy_pT(n, 2)
                copy_pT(n, 3)
                if within(n, 2, count):
                    copy_xT(n + 2, p)
                if nxt:
                    copy_comp(n + 1, 1 - p)

            act.wait_ge(sem["weights"], n_loads)
            copy_xT(0, 0)
            copy_qf(0)
            block_exp(0)
            copy_v(0, 0)
            copy_comp(0, 0)
            copy_xT(1, 1)
            over_slots(act, slot, count)
            copy_o(count - 1)
            copy_oT(count - 1)

        @block.vector
        def _(dve):
            dve.wait_ge(sem["weights"], n_loads)
            for t in ("causal", "band"):
                dve.tensor_copy(mask[t][:], m_f[t][:].unsqueeze(1).broadcast_to([S, 4, S]))
            dve.tensor_copy(blocks[:], blocks_f[:]).then_inc(sem["setup"], 1)

            def copy_q(n, p):
                dve.wait_ge(sem["q_ready"], n + 1)
                reach(dve, sem["scores_ready"], (n - 1) * 8)
                dve.tensor_scalar(qT[p][:], qk_b[:], D ** -0.5, None, ALU.mult).then_inc(sem["q_copied"], 1)

            def copy_k(n, p):
                dve.wait_ge(sem["k_ready"], n + 1)
                reach(dve, sem["scores_ready"], (n - 1) * 8)
                dve.tensor_copy(kT[p][:], qk_b[:]).then_inc(sem["k_copied"], 1)

            STEPS = 16

            def chain(n, k, ins):
                ins.then_inc(sem["comp_step"], 1)
                dve.wait_ge(sem["comp_step"], n * STEPS + k)

            flat_e = e[:, 0:HEADS * N].rearrange("p (h n) -> p h n", h=HEADS)
            ge = e[:, HEADS * N:HEADS * N + 3]

            def per_head(ap):
                return ap.unsqueeze(1).broadcast_to([S, HEADS, N])

            def block_logits(n):
                dve.wait_ge(sem["cs_ready"], n + 1)
                cs = comp[:, 0:S].rearrange("p (h n) -> p h n", h=HEADS)
                chain(n, 1, dve.tensor_tensor(logit[:], cs, per_head(ok[:]), ALU.mult))
                chain(n, 2, dve.scalar_tensor_tensor(out=ge, in0=comp[:, S:S + 3], scalar=1.0 / HEADS, in1=bg[:],
                                                     op0=ALU.mult, op1=ALU.add))
                chain(n, 3, dve.tensor_tensor(logit[:], logit[:], per_head(low[:]), ALU.add))
                chain(n, 4, dve.tensor_reduce(gtop[:], ge, AX.X, ALU.max, negate=True))
                chain(n, 5, dve.tensor_reduce(top[:], logit[:], AX.X, ALU.max, negate=True))
                dve.tensor_scalar(ge, ge, gtop[:, 0:1], None, ALU.add)
                dve.tensor_tensor(flat_e, logit[:], copy_bcast(top[:], N), ALU.add).then_inc(sem["e_ready"], 1)

            def ranks(n, part):
                shape = [S, HEADS, N, N]
                if part == 0:
                    dve.tensor_tensor(more[:], logit[:].unsqueeze(2).broadcast_to(shape),
                                      logit[:].unsqueeze(3).broadcast_to(shape), ALU.is_gt)
                    chain(n, 6, dve.tensor_tensor(same[:], logit[:].unsqueeze(2).broadcast_to(shape),
                                                  logit[:].unsqueeze(3).broadcast_to(shape), ALU.is_equal))
                elif part == 1:
                    chain(n, 7, dve.tensor_tensor(same[:], same[:], before[:].unsqueeze(1).broadcast_to(shape),
                                                  ALU.mult))
                    chain(n, 8, dve.tensor_tensor(more[:], more[:], same[:], ALU.add))
                else:
                    chain(n, 9, dve.tensor_reduce(rank[:], more[:], AX.X, ALU.add))
                    reach(dve, sem["comp_turned"], n)
                    chain(n, 10, dve.tensor_scalar(closed[:], rank[:].rearrange("p h n -> p (h n)"), 3.5, -2.0 ** 60,
                                                   ALU.is_gt, ALU.mult))

            def block_probs(n, p):
                dve.wait_ge(sem["e_exp"], n + 1)
                chain(n, 11, dve.tensor_reduce(gtop[:], ge, AX.X, ALU.add))
                chain(n, 12, dve.reciprocal(gtop[:], gtop[:]))
                chain(n, 13, dve.tensor_scalar(gate[p][:], ge, gtop[:, 0:1], None, ALU.mult))
                chain(n, 14, dve.tensor_reduce(top[:], flat_e, AX.X, ALU.add))
                chain(n, 15, dve.reciprocal(top[:], top[:]))
                chain(n, 16, dve.tensor_scalar(top[:], top[:], gate[p][:, 0:1], some[:, 0:1], ALU.mult, ALU.mult))
                dve.tensor_tensor(pc[:], flat_e, copy_bcast(top[:], N), ALU.mult).then_inc(sem["comp_ready"], 1)

            def maxima(n, a, b):
                u = n * 8 + 2 * a + b
                dve.wait_ge(sem["scores_ready"], u + 1)
                reach(dve, sem["probs_ready"], u - 1)
                dve.tensor_reduce(negmax[b][:], score[b][:], AX.X, ALU.max, negate=True)\
                   .then_inc(sem["max_ready"], 1)

            def mixed(n, p, a):
                u = n * 4 + a
                dve.wait_ge(sem["probs_ready"], n * 8 + 2 * a + 2)
                reach(dve, sem["local_ready"], u - 1)
                w = wt[a % 2]
                dve.reciprocal(w[:], sums[p][:, a, :, :]).then_inc(sem["wt_step"], 1)
                dve.wait_ge(sem["wt_step"], u + 1)
                dve.tensor_tensor(w[:], w[:], copy_bcast(gate[p][:, 1:3], 4), ALU.mult).then_inc(sem["wt_ready"], 1)

            def mix_sum(n, p, a):
                u = n * 4 + a
                w = wt[a % 2]
                dve.wait_ge(sem["local_ready"], u + 1)
                reach(dve, sem["probs_turned"], u - 1)
                for j in range(4):
                    i = dve.scalar_tensor_tensor(out=mix[a % 2][:, j, :], in0=prob[0][a % 2][:, j, :],
                                                 scalar=w[:, 0, j:j + 1], in1=local[a % 2][:, j, :],
                                                 op0=ALU.mult, op1=ALU.add)
                i.then_inc(sem["mix_ready"], 1)

            def residual(n, p):
                dve.wait_ge(sem["y_ready"], n + 1)
                dve.wait_ge(sem["xb_ready"], n + 1)
                dve.tensor_tensor(r[p][:], misc[:, 0:E], xb[p][:], ALU.add).then_inc(sem["r_ready"], 1)
                dve.wait_ge(sem["r_ready"], n + 1)
                dve.bn_stats(stats[:], r[p][:]).then_inc(sem["step"], 1)
                wait_alone(dve, sem["step"], n * 2 + 1, keep["passed"])
                dve.bn_aggr(mv[p][:], stats[:]).then_inc(sem["step"], 1)
                dve.wait_ge(sem["step"], n * 2 + 2)
                dve.tensor_scalar(rstd[p][:], mv[p][:, 1:2], LN_EPS, None, ALU.add).then_inc(sem["var_ready"], 1)

            def norm(n, p):
                dve.wait_ge(sem["rstd_ready"], n + 1)
                dve.tensor_scalar(x[:, n, :], r[p][:], mv[p][:, 0:1], rstd[p][:, 0:1], ALU.subtract, ALU.mult)\
                   .then_inc(sem["normed"], 1)

            def slot(n, p):
                nxt = within(n, 1, count)
                maxima(n, 0, 0)
                maxima(n, 0, 1)
                if nxt:
                    copy_q(n + 1, 1 - p)
                maxima(n, 1, 0)
                mixed(n, p, 0)
                maxima(n, 1, 1)
                if within(n, -2, count):
                    norm(n - 2, p)
                if nxt:
                    block_logits(n + 1)
                    copy_k(n + 1, 1 - p)
                mix_sum(n, p, 0)
                maxima(n, 2, 0)
                mixed(n, p, 1)
                maxima(n, 2, 1)
                if nxt:
                    ranks(n + 1, 0)
                mix_sum(n, p, 1)
                maxima(n, 3, 0)
                mixed(n, p, 2)
                maxima(n, 3, 1)
                if nxt:
                    ranks(n + 1, 1)
                mix_sum(n, p, 2)
                mixed(n, p, 3)
                if nxt:
                    ranks(n + 1, 2)
                    block_probs(n + 1, 1 - p)
                mix_sum(n, p, 3)
                if within(n, -1, count):
                    residual(n - 1, 1 - p)

            copy_q(0, 0)
            block_logits(0)
            copy_k(0, 0)
            for part in range(3):
                ranks(0, part)
            block_probs(0, 0)
            over_slots(dve, slot, count)
            norm(count - 2, 0)
            residual(count - 1, 1)
            norm(count - 1, 1)

    clear(nc, sem)


def build(nc, d, out):
    with ExitStack() as ctx:
        sb, _, sems = tensors(ctx, nc, "keep")
        keep = {"x": sb("x", [S, SEQS, E]), "ident": sb("ident", [S, S]), "ident_bf": sb("ident_bf", [S, S], BF16),
                "minus_half": sb("minus_half", [S, 1])}
        sem = sems("loaded made stored passed passed_pool")
        keep.update(passed=sem["passed"], passed_pool=sem["passed_pool"])
        with nc.Block() as block:
            @block.sync
            def _(sp):
                sp.dma_start(keep["ident"][:], d["ident"]).then_inc(sem["loaded"], 16)
                sp.dma_start(keep["x"][:], d["x"].rearrange("s p e -> p s e")).then_inc(sem["loaded"], 16)

            @block.vector
            def _(dve):
                dve.memset(keep["minus_half"][:], -0.5).then_inc(sem["made"], 1)
                dve.wait_ge(sem["loaded"], 32)
                dve.tensor_copy(keep["ident_bf"][:], keep["ident"][:]).then_inc(sem["made"], 1)

        for stage in STAGES:
            if stage == "relu_attn":
                relu_attention(nc, d, keep, stage)
            elif stage == "l1_xattn":
                one_head_attention(nc, d, keep, stage)
            elif stage == "l3_attn":
                with ExitStack() as inner:
                    sb, _, _ = tensors(inner, nc, "l3")
                    with_blocks = dict(keep, kc=sb("kc", [E, SEQS, 8]), vc=sb("vc", [E, SEQS, 8]))
                    compress_blocks(nc, d, with_blocks, "l3_compress")
                    sparse_attention(nc, d, with_blocks, stage)
            elif stage == "l3_linear":
                linear(nc, d, keep, stage)
            elif stage == "l2_attn":
                softmax_attention(nc, d, keep, stage, 8, 8 ** -0.5, q_bias=True, v_bias=True, causal=True, rope=True)
            elif stage == "l2_xattn":
                l2_xattn(nc, d, keep)
            elif stage == "l0_xattn":
                softmax_attention(nc, d, keep, stage, 8, 8 ** -0.5, cross=True, q_bias=True, v_bias=True)
            elif stage == "l0_ffn":
                feed_forward(nc, d, keep, stage, "glu", 3, ACT.Silu, scale=1.0 / 127.0, ints=True)
            elif stage == "l1_moe":
                feed_forward(nc, d, keep, stage, "plain", 36, ACT.Gelu_apprx_tanh, bias=True, out_bias=True,
                             experts=8, per_gate=4, gates=8, first_gated=4, gate_bias=True)
            elif stage == "l2_moe":
                feed_forward(nc, d, keep, stage, "glu", 10, ACT.Silu, experts=16, gates=10, shared_gate=True)
            elif stage == "l1_attn":
                head_attention(nc, d, keep, stage, 8, 32 ** -0.5, causal=True, low_rank=True)
            elif stage == "l3_xattn":
                softmax_attention(nc, d, keep, stage, 8, 8 ** -0.5, cross=True, out_bias=False)

        with nc.Block() as block:
            @block.sync
            def _(sp):
                sp.dma_start(out.rearrange("s p e -> p s e"), keep["x"][:]).then_inc(sem["stored"], 16)
                sp.wait_ge(sem["stored"], 16)


def l2_xattn(nc, d, keep):
    with ExitStack() as ctx:
        sb, _, _ = tensors(ctx, nc, "l2x")
        keep = dict(keep, b=sb("b", [S, SEQS, E]), z=sb("z", [S, SEQS, E]))
        renormalise(nc, d, keep, "l2x_ln1", keep["x"])
        softmax_attention(nc, d, keep, "l2x_a1", 32, 32 ** -0.5, future_only=True, src=keep["z"], affine=True,
                          dst="sum_and_norm")
        feed_forward(nc, d, keep, "l2x_f1", "plain", 4, ACT.Gelu, bias=True, out_bias=True, src=keep["z"],
                     affine=True, dst="store")
        renormalise(nc, d, keep, "l2x_ln2", keep["b"])
        with ExitStack() as inner:
            sb, _, _ = tensors(inner, nc, "l2x")
            with_ctx = dict(keep, ctxn=sb("ctxn", [C, SEQS, CTX]))
            normalise_context(nc, d, with_ctx, "l2x_ctx")
            softmax_attention(nc, d, with_ctx, "l2x_a2", 32, 32 ** -0.5, cross=True, src=keep["z"], affine=True,
                              dst="sum_and_norm")
        feed_forward(nc, d, keep, "l2x_f2", "plain", 4, ACT.Gelu, bias=True, out_bias=True, src=keep["z"],
                     affine=True, dst="norm_with_x")


def layouts(i):
    f = np.float32

    def chunked(w, width=8, at=0, rows=None):
        w = np.asarray(w)
        out = np.zeros((w.shape[0], 4, 4, 32), w.dtype)
        out[:, :, :, at:at + width] = w.reshape(w.shape[0], 4, 4, width).transpose(0, 2, 1, 3)
        return out.reshape(w.shape[0], 4, 128)

    def chunked_bias(b):
        out = np.zeros((4, 4, 32), np.asarray(b).dtype)
        out[:, :, 0:8] = np.asarray(b).reshape(4, 4, 8).transpose(1, 0, 2)
        return np.ascontiguousarray(out.reshape(4, 128).T)

    def rows(b, n=128):
        b = np.asarray(b)
        return np.ascontiguousarray(np.broadcast_to(b.reshape(1, -1), (n, b.size)))

    def cols(b):
        b = np.asarray(b)
        return np.ascontiguousarray(np.broadcast_to(b.reshape(-1, 1), (b.size, 128)))

    def T(w):
        return np.ascontiguousarray(np.asarray(w).T)

    g = {}
    g["ident"] = np.eye(128, dtype=f)
    key = np.arange(128)
    big = np.float32(-2.0 ** 60)
    g["causal"] = np.where(key[None, :] > key[:, None], big, np.float32(0)).astype(f)
    g["future"] = (key[:, None] > key[None, :]).astype(f)
    row, unit, place = np.arange(128)[:, None, None], np.arange(4)[None, :, None], np.arange(4)[None, None, :]
    g["kmask8"] = (row // 8 == 4 * place + unit).astype(f)
    g["kmask32"] = (row // 32 == place + 0 * unit).astype(f)
    g["vmask"] = np.tile((np.arange(128)[None, :] // 8 % 4 == np.arange(4)[:, None]).astype(f), (128, 1, 1))
    g["x"] = np.asarray(i["x"])
    g["ctxT"] = np.ascontiguousarray(np.asarray(i["ctx_512"]).transpose(0, 2, 1))
    for n, p in (("l0_xattn", "L0_xattn_"),):
        g[n + "_wq"] = np.asarray(i[p + "Wq"]).reshape(128, 1, 128)
        g[n + "_wk"] = np.asarray(i[p + "Wk"]).reshape(64, 1, 128)
        g[n + "_wv"] = np.asarray(i[p + "Wv"])
        g[n + "_wo"] = np.asarray(i[p + "Wo"]).reshape(128, 1, 128)
        g[n + "_bq"] = np.asarray(i[p + "bq"]).reshape(128, 1)
        g[n + "_bk"] = np.asarray(i[p + "bk"]).reshape(128, 1)
        g[n + "_bv"] = cols(i[p + "bv"])
        g[n + "_bo"] = rows(i[p + "bo"])
    n, p = "l1_attn", "L1_attn_"
    g[n + "_wq0"] = chunked(T(i[p + "Wq2"]))
    g[n + "_wq0"].reshape(128, 4, 4, 32)[:, :, :, 8:12] = T(i[p + "Wq1"]).reshape(128, 4, 4, 4).transpose(0, 2, 1, 3)
    g[n + "_wk0"] = chunked(T(i[p + "Wk1"]), 4, 8)
    g[n + "_wk1"] = chunked(T(i[p + "Wk2"]))
    g[n + "_wv"], g[n + "_wo"] = T(i[p + "Wv"]), T(i[p + "Wo"]).reshape(128, 1, 128)
    g[n + "_bo"] = rows(i[p + "bo"])
    n, p = "l3_xattn", "L3_xattn_"
    g[n + "_wq"] = T(i[p + "Wq"]).reshape(128, 1, 128)
    kv = T(i[p + "Wkv"])
    g[n + "_wk"] = np.ascontiguousarray(kv[:, 0:128]).reshape(64, 1, 128)
    g[n + "_wv"] = np.ascontiguousarray(kv[:, 128:256])
    g[n + "_wo"] = T(i[p + "Wo"]).reshape(128, 1, 128)

    def chunks(w):
        return np.ascontiguousarray(w.reshape(w.shape[0], -1, 128))

    def stacked(w):
        return np.ascontiguousarray(w.reshape(-1, 128, w.shape[1]).transpose(1, 0, 2))

    n, p = "l0_ffn", "L0_ffn_"
    g[n + "_wu"], g[n + "_wv"] = chunks(T(i[p + "w_gate"])), chunks(T(i[p + "w_up"]))
    g[n + "_wd"] = stacked(T(i[p + "w_down"]))
    n, p = "l1_moe", "L1_ffn_"
    g[n + "_wu"] = chunks(np.concatenate([i[p + "Wfc_s"], *np.asarray(i[p + "Wfc"])], 1))
    g[n + "_bu"] = np.concatenate([i[p + "bfc_s"], np.asarray(i[p + "bfc"]).ravel()]).reshape(-1, 128).T
    g[n + "_wd"] = stacked(np.concatenate([i[p + "Wproj_s"], *np.asarray(i[p + "Wproj"])], 0))
    g[n + "_bd"], g[n + "_gb"], g[n + "_wr"] = rows(i[p + "bproj_s"]), i[p + "bproj"], i[p + "Wr"]
    g[n + "_sel"] = np.repeat(np.eye(8, dtype=f)[:, :, None], 128, 2)
    e = np.arange(8)
    g[n + "_before"] = np.tile((e[None, :] < e[:, None]).astype(f), (128, 1, 1))
    n, p = "l2_moe", "L2_ffn_"
    for t, w in (("_wu", "gate"), ("_wv", "up")):
        g[n + t] = chunks(T(np.concatenate([np.asarray(i[f"{p}We_{w}"]).reshape(1024, 128), i[f"{p}Ws_{w}"]], 0)))
    g[n + "_wd"] = stacked(np.concatenate([np.asarray(i[p + "We_down"]).transpose(0, 2, 1).reshape(1024, 128),
                                           T(i[p + "Ws_down"])], 0))
    g[n + "_wr"] = T(np.concatenate([i[p + "Wg"], i[p + "Wsg"]], 0))
    sel = np.zeros((17, 10, 128), f)
    for k in range(16):
        sel[k, k // 2, 64 * (k % 2):64 * (k % 2) + 64] = 1
    sel[16, 8:10] = 1
    g[n + "_sel"] = sel
    e = np.arange(16)
    g[n + "_before"] = np.tile((e[None, :] < e[:, None]).astype(f), (128, 1, 1))
    n, p = "relu_attn", "L0_attn_"
    for t in "qkvo":
        g[f"{n}_w{t}"], g[f"{n}_b{t}"] = T(i[f"{p}W{t}"]), rows(i[f"{p}b{t}"])
    g[n + "_weight"], g[n + "_gain"] = rows(i[p + "norm_weight"]), rows(i[p + "norm_gate"])
    for t in ("key", "value"):
        g[f"{n}_{t}T"] = T(np.asarray(i[p + t]).reshape(512, 128)).reshape(128, 4, 128)
    n, p = "l1_xattn", "L1_xattn_"
    for t in "qkv":
        g[f"{n}_w{t}"] = i[f"{p}W{t}"]
    g[n + "_bq"], g[n + "_bk"] = np.asarray(i[p + "bq"]).reshape(128, 1), np.asarray(i[p + "bk"]).reshape(128, 1)
    g[n + "_bv"] = rows(i[p + "bv"])
    n, p = "l3_linear", "L3_ffn_"
    g[n + "_w"], g[n + "_scale"], g[n + "_bias"] = T(i[p + "CB"]), rows(i[p + "SCB"]), rows(i[p + "bias"])
    n, p = "l2_attn", "L2_attn_"
    swap = np.arange(128) ^ 1
    for t in "qk":
        w, b = np.asarray(i[f"{p}W{t}"]), np.asarray(i[f"{p}b{t}"])
        g[f"{n}_w{t}"], g[f"{n}_b{t}"] = np.stack([w, w[:, swap]], 1), np.stack([b, b[swap]], 1)
    freq = f(1.0) / f(10000.0) ** (np.arange(4, dtype=f) * f(2.0) / f(8))
    angle = np.arange(128, dtype=f)[None, :] * freq[:, None]
    pair = (np.arange(128) % 8) // 2
    g["cos"] = np.cos(angle)[pair].astype(f)
    g["sin"] = (np.sin(angle)[pair] * np.where(np.arange(128) % 2, f(1), f(-1))[:, None]).astype(f)
    g[n + "_wv"], g[n + "_wo"] = i[p + "Wv"], np.asarray(i[p + "Wp"]).reshape(128, 1, 128)
    g[n + "_bv"], g[n + "_bo"] = cols(i[p + "bv"]), rows(i[p + "bp"])
    g["ctx"] = i["ctx_512"]
    n, p = "l3_attn", "L3_attn_"
    g[n + "_wq"], g[n + "_wk"] = chunked(i[p + "Wq"]), chunked(i[p + "Wk"])
    for t in "qkv":
        g[f"{n}_flat{t}"] = i[f"{p}W{t}"]
    for t in "kv":
        w = np.asarray(i[f"{p}Wc{t}"]).reshape(16, 8, 8)
        wide = np.zeros((16, 8, 16, 16, 8), w.dtype)
        for h in range(16):
            wide[h, :, :, h, :] = w.transpose(1, 0, 2)
        g[f"{n}_wc{t}"] = wide.reshape(128, 16, 128)
    g[n + "_wo"] = i[p + "Wo"]
    g[n + "_wg"], g[n + "_bg"] = np.tile(np.asarray(i[p + "Wg"]), (16, 1)), rows(i[p + "bg"])
    g["own"] = np.repeat(np.eye(16, dtype=f), 8, 0)
    done = key[:, None] >= (np.arange(8)[None, :] + 1) * 16
    g["block_ok"] = np.where(done, f(1.0 / np.sqrt(8.0)), f(0))
    g["block_low"] = np.where(done, f(0), f(-1e9))
    g["block_some"] = done.any(1, keepdims=True).astype(f)
    back = key[:, None] - key[None, :]
    g["band"] = np.where((back >= 0) & (back <= 32), f(0), big).astype(f)
    row = np.arange(128)
    g["blocks"] = ((row[:, None, None] % 32 // 8 == np.arange(4)[None, :, None])
                   & (row[:, None, None] % 8 == key[None, None, :] // 16)).astype(f)
    for a, c in (("a1", 128), ("a2", 64)):
        n, p = "l2x_" + a, f"L2_xattn_{a}_"
        flat = {t: np.asarray(i[f"{p}w{t}"]).transpose(1, 0, 2).reshape(-1, 512) for t in "qkv"}
        g[n + "_wq"], g[n + "_wk"], g[n + "_wv"] = chunks(flat["q"]), chunks(flat["k"]), flat["v"]
        g[n + "_wo"], g[n + "_bo"] = stacked(np.asarray(i[p + "li1_w"])), rows(i[p + "li1_b"])
        aff = np.zeros((128, 4), f)
        aff[:, 0], aff[:, 1] = i[p + "lnx_g"], i[p + "lnx_b"]
        aff[0:c, 2], aff[0:c, 3] = i[p + "lny_g"], i[p + "lny_b"]
        g[n + "_aff"] = aff
        if a == "a2":
            g["l2x_ctx_aff"] = aff[0:64, 2:4]
        m = "l2x_f" + a[1]
        g[m + "_wu"], g[m + "_wd"] = chunks(np.asarray(i[p + "li2_w"])), stacked(np.asarray(i[p + "li3_w"]))
        g[m + "_bu"], g[m + "_bd"] = np.asarray(i[p + "li2_b"]).reshape(4, 128).T, rows(i[p + "li3_b"])
        g[m + "_aff"] = np.stack([i[p + "ln3_g"], i[p + "ln3_b"]], 1)
        g[f"l2x_ln{a[1]}_gain"] = rows(i[f"L2_xattn_ln{a[1]}_g"])
        g[f"l2x_ln{a[1]}_shift"] = rows(i[f"L2_xattn_ln{a[1]}_b"])
    return g


def kernel(**inputs):
    import concourse.bacc as bacc
    from concourse.bass_utils import run_bass_kernel_spmd as run

    nc = bacc.Bacc("TRN2", target_bir_lowering=False, num_devices=1)
    arrays = {f"in_{n}": np.ascontiguousarray(a) for n, a in layouts(inputs).items()}
    d = {n[3:]: nc.dram_tensor(n, a.shape, mybir.dt.from_np(a.dtype), kind="ExternalInput").ap()
         for n, a in arrays.items()}
    out = nc.dram_tensor("out", (SEQS, S, E), F32, kind="ExternalOutput").ap()
    build(nc, d, out)
    return run(nc, [arrays], core_ids=[0]).results[0]["out"]
```

```python
from contextlib import ExitStack

import numpy as np

import concourse.bass as bass
from concourse import mybir

ALU = mybir.AluOpType
ACT = mybir.ActivationFunctionType
AX = mybir.AxisListType
F32 = mybir.dt.float32
BF16 = mybir.dt.bfloat16
I32 = mybir.dt.int32

SEQS, S, E, C = 64, 128, 128, 64
CTX = 77
HEADS = 16
LN_EPS = 1e-5
STAGES = ("relu_attn", "l0_xattn", "l0_ffn", "l1_attn", "l1_xattn", "l1_moe", "l2_attn", "l2_xattn",
          "l2_moe", "l3_attn", "l3_xattn", "l3_linear")


def tensors(ctx, nc, tag):
    def sb(name, shape, dt=F32):
        return ctx.enter_context(nc.sbuf_tensor(f"{tag}_{name}", shape, dt))

    def bank(name, shape, dt=F32):
        return ctx.enter_context(nc.psum_tensor(f"{tag}_{name}", shape, dt))

    def sems(names):
        return {n: ctx.enter_context(nc.semaphore(f"{tag}_{n}")) for n in names.split()}

    return sb, bank, sems


def clear(nc, sem):
    with nc.Block() as block:
        @block.gpsimd
        def _(pool):
            for s in sem.values():
                pool.sem_clear(s)


def over_slots(eng, slot, count):
    slot(0, 0)
    slot(1, 1)
    with eng.Fori(1, count // 2 - 1) as i:
        slot(i * 2, 0)
        slot(i * 2 + 1, 1)
    slot(count - 2, 0)
    slot(count - 1, 1)


def within(n, ahead, count):
    return not isinstance(n, int) or 0 <= n + ahead < count


def reach(eng, sem, value):
    if not isinstance(value, int) or value > 0:
        eng.wait_ge(sem, value)


def wait_alone(eng, sem, value, passed):
    reach(eng, sem, value)
    eng.sem_inc(passed, 1)


def load_all(sp, pairs, sem):
    for dst, src in pairs:
        sp.dma_start(dst, src).then_inc(sem, 16)


def copy_bcast(ap, n):
    return ap.unsqueeze(2).broadcast_to([ap.shape[0], ap.shape[1], n])


def softmax_attention(nc, d, keep, tag, head_dim, scale, *, cross=False, q_bias=False, v_bias=False,
                      out_bias=True, causal=False, future_only=False, rope=False, src=None, affine=None, dst="norm",
                      odd_on_act=False, low_rank=False):
    count = SEQS
    keys = CTX if cross else S
    hd = HEADS * head_dim
    chunks = hd // E
    narrow = head_dim == 8
    in_k = C if cross else E
    parts = 2 if rope or low_rank else 1
    factors = 2 if low_rank else 1
    kept = factors * chunks
    x, ident = keep["x"], keep["ident"]
    src = x if src is None else src
    ctx_copy = "ctxn" in keep and cross and affine is not None
    with ExitStack() as ctx:
        sb, bank, sems = tensors(ctx, nc, tag)
        wq = sb("wq", [E, parts * chunks, E])
        wk = sb("wk", [in_k, parts * chunks, E])
        wv = sb("wv", [in_k, hd])
        wo = sb("wo", [E, chunks, E])
        bias = sb("bias", [S, E])
        kmask = [sb(f"kmask{f}", [E, 4, 4]) for f in range(factors)]
        loads = [(wv[:], d[tag + "_wv"]), (wo[:], d[tag + "_wo"]), (wq[:], d[tag + "_wq"]), (wk[:], d[tag + "_wk"]),
                 (kmask[0][:], d["kmask8" if narrow else "kmask32"])]
        if low_rank:
            loads += [(kmask[1][:], d["kmask4"])]
            mask2 = sb("mask2", [S, 4, S], BF16)
            a1 = [sb(f"a1{i}", [S, 4, S]) for i in range(2)]
            prod = [sb(f"prod{i}", [S, 4, S]) for i in range(2)]
        if narrow:
            vmask = sb("vmask", [S, 4, E])
            zeros = sb("zeros", [S, S], BF16)
            loads += [(vmask[:], d["vmask"])]
        if out_bias:
            loads += [(bias[:], d[tag + "_bo"])]
        if q_bias:
            qb, kb = sb("qb", [E, parts]), sb("kb", [E, parts])
            loads += [(qb[:], d[tag + "_bq"]), (kb[:], d[tag + "_bk"])]
        if rope:
            tables = [[sb(f"{n}{t}", [E, S]) for n in ("cos", "sin")] for t in "qk"]
            terms = [[sb(f"term{t}{i}", [E, S]) for i in range(2)] for t in "qk"]
            for t in range(2):
                loads += [(tables[t][i][:], d[("cos", "sin")[i]]) for i in range(2)]
        elif q_bias:
            qbs = sb("qbs", [E, parts])
        if v_bias:
            vb = sb("vb", [E, S])
            loads += [(vb[:], d[tag + "_bv"])]
        if affine is not None:
            aff = sb("aff", [E, 4])
            loads += [(aff[:], d[tag + "_aff"])]
        if causal:
            mask = sb("mask", [S, 4, S], BF16)
            mask_f = sb("mask_f", [S, S])
            loads += [(mask_f[:], d["causal"])]
        if future_only:
            future = sb("future", [S, S])
            loads += [(future[:], d["future"])]
        xin = [sb(f"xin{i}", [S, E]) for i in range(2)]
        xT = [sb(f"xT{i}", [E, S]) for i in range(2)]
        kin = [sb(f"kin{i}", [in_k, keys]) for i in range(2)] if (cross or affine is not None) else xT
        qT = [sb(f"qT{i}", [E, kept, S]) for i in range(2)]
        kT = [sb(f"kT{i}", [E, kept, keys]) for i in range(2)]
        kd = [sb(f"kd{f}", [E, 4, 4, keys]) for f in range(factors)]
        vd = [sb(f"vd{i}", [keys, 4, E]) for i in range(2)]
        negmax = [sb(f"negmax{i}", [S, 4]) for i in range(2)]
        prob = [sb(f"prob{i}", [S, 4, keys]) for i in range(2)]
        sums = [sb(f"sums{i}", [S, HEADS]) for i in range(2)]
        inv = sb("inv", [S, HEADS])
        invb = sb("invb", [S, hd])
        invT = sb("invT", [E, chunks, S])
        pT = [sb(f"pT{i}", [keys, 4, S]) for i in range(2)]
        oT = sb("oT", [E, chunks, S])
        xb = [sb(f"xb{i}", [S, E]) for i in range(2)]
        r = [sb(f"r{i}", [S, E]) for i in range(2)]
        stats = sb("stats", [S, 6])
        mv = [sb(f"mv{i}", [S, 2]) for i in range(2)]
        rstd = [sb(f"rstd{i}", [S, 1]) for i in range(2)]
        score = [bank(f"score{i}", [S, 4, S]) for i in range(2)]
        turned = [bank(f"turned{i}", [S, 4, S]) for i in range(2)]
        out_b = bank("out", [E, 4, S])
        q_b = bank("q", [E, 4, S])
        kv_b = bank("kv", [E, 4, S])
        misc = bank("misc", [S, 512])
        sem = sems("weights setup bias_ready xin_ready x_turned xT_copied ctx_loaded0 ctx_loaded1 ctx_copied q_ready "
                   "q_copied k_ready k_copied term_ready kd_ready last_kd_ready v_ready v_copied a1_ready a1_copied "
                   "prod_ready scores_ready max_ready "
                   "probs_ready probs_turned pT_copied0 pT_copied1 pv_done inv_step inv_ready inv_turned invT_copied oT_ready "
                   "y_ready xb_ready r_ready stats_ready mv_ready rstd_ready normed sum_stored var_ready")
        n_loads = 16 * len(loads)
        y0 = 1 if v_bias else 0
        block = ctx.enter_context(nc.Block())

        def unit_after(n, p, c, by):
            if c + by < 4:
                return n, p, c + by
            return (n + 1, 1 - p, c + by - 4) if within(n, 1, count) else None

        def at_most(value, ahead):
            return min(value + ahead, count) if isinstance(value, int) else value + ahead

        @block.sync
        def _(sp):
            load_all(sp, loads, sem["weights"])
            if cross and not ctx_copy:
                def slot(n, p):
                    reach(sp, sem["k_ready"], n - 1)
                    reach(sp, sem["v_ready"], n - 1)
                    sp.dma_start(kin[p][:], d["ctxT"][n]).then_inc(sem[f"ctx_loaded{p}"], 16)

                over_slots(sp, slot, count)

        @block.gpsimd
        def _(pool):
            pool.wait_ge(sem["weights"], n_loads)

            def stage_in(n, p):
                reach(pool, sem["x_turned"], n - 1)
                pool.tensor_copy(xin[p][:], src[:, n, :]).then_inc(sem["xin_ready"], 1)
                if ctx_copy:
                    reach(pool, sem["k_ready"], n - 1)
                    reach(pool, sem["v_ready"], n - 1)
                    pool.tensor_copy(kin[p][:], keep["ctxn"][:, n, :]).then_inc(sem["ctx_copied"], 1)

            def root(n, p):
                pool.wait_ge(sem["var_ready"], n + 1)
                pool.tensor_tensor(rstd[p][:], rstd[p][:], keep["minus_half"][:], ALU.pow)\
                    .then_inc(sem["rstd_ready"], 1)

            def store_sum(n, p):
                wait_alone(pool, sem["r_ready"], n + 1, keep["passed_pool"])
                pool.tensor_tensor(keep["b"][:, n, :], keep["b"][:, n, :], r[p][:], ALU.add)\
                    .then_inc(sem["sum_stored"], 1)

            def spread_last(n, p):
                pool.wait_ge(sem["k_copied"], n + 1)
                reach(pool, sem["scores_ready"], n * 4)
                for f in range(factors):
                    i = pool.tensor_tensor(kd[f][:, 3, :, :],
                                           kT[p][:, f if low_rank else 3 % chunks, :].unsqueeze(1)
                                           .broadcast_to([E, 4, keys]),
                                           copy_bcast(kmask[f][:, 3, :], keys), ALU.mult)
                i.then_inc(sem["last_kd_ready"], 1)

            def slot(n, p):
                if within(n, 2, count):
                    stage_in(n + 2, p)
                if within(n, -2, count):
                    root(n - 2, p)
                    if dst == "sum_and_norm":
                        store_sum(n - 2, p)
                if isinstance(n, int) and n == 0:
                    pool.wait_ge(sem["bias_ready"], 1)
                reach(pool, sem["r_ready"], n - 1)
                res = x if dst == "norm" else keep["b"]
                pool.tensor_tensor(xb[p][:], res[:, n, :], bias[:], ALU.add).then_inc(sem["xb_ready"], 1)
                if within(n, 1, count):
                    spread_last(n + 1, 1 - p)

            stage_in(0, 0)
            stage_in(1, 1)
            spread_last(0, 0)
            over_slots(pool, slot, count)
            for n in (count - 2, count - 1):
                root(n, n % 2)
                if dst == "sum_and_norm":
                    store_sum(n, n % 2)

        @block.tensor
        def _(pe):
            pe.wait_ge(sem["weights"], n_loads)
            pe.wait_ge(sem["setup"], 1)

            def turn_x(n, p):
                pe.wait_ge(sem["xin_ready"], n + 1)
                reach(pe, sem["xT_copied"], n)
                reach(pe, sem["invT_copied"], n - 2)
                pe.transpose(misc[:, 0:S], xin[p][:], ident[:]).then_inc(sem["x_turned"], 1)

            def wait_context(n, p):
                if not cross:
                    pe.wait_ge(sem["xT_copied"], n + 1)
                elif ctx_copy:
                    pe.wait_ge(sem["ctx_copied"], n + 1)
                else:
                    pe.wait_ge(sem[f"ctx_loaded{p}"], (n - p) * 8 + 16)

            def project_q(n, p):
                pe.wait_ge(sem["xT_copied"], n + 1)
                reach(pe, sem["q_copied"], n)
                for c in range(parts * chunks):
                    mm = pe.matmul(q_b[:, c, :], wq[:, c, :], xT[p][:], start=True, stop=True)
                mm.then_inc(sem["q_ready"], 1)

            def project_k(n, p):
                wait_context(n, p)
                reach(pe, sem["v_copied"], n)
                for c in range(parts * chunks):
                    mm = pe.matmul(kv_b[:, c, 0:keys], wk[:, c, :], kin[p][:], start=True, stop=True)
                mm.then_inc(sem["k_ready"], 1)

            def project_v(n, p):
                wait_context(n, p)
                pe.wait_ge(sem["k_copied"], n + 1)
                pe.matmul(kv_b[0:keys].rearrange("p c s -> p (c s)")[:, 0:hd], kin[p][:], wv[:],
                          start=True, stop=True).then_inc(sem["v_ready"], 1)

            def scores(n, p, c):
                if c == 0:
                    pe.wait_ge(sem["q_copied"], n + 1)
                if c == 3:
                    pe.wait_ge(sem["last_kd_ready"], n + 1)
                else:
                    pe.wait_ge(sem["kd_ready"], n * 3 + c + 1)
                if low_rank:
                    reach(pe, sem["a1_copied"], n * 4 + c)
                    pe.matmul(score[0][:], qT[p][:, 1, :], kd[1][:, c, :, :], start=True, stop=False,
                              skip_group_check=True)
                    pe.matmul(score[0][:], keep["ident_bf"][:], mask[:], start=False, stop=True,
                              skip_group_check=True).then_inc(sem["a1_ready"], 1)
                    reach(pe, sem["prod_ready"], n * 4 + c)
                    pe.matmul(score[1][:], qT[p][:, 0, :], kd[0][:, c, :, :], start=True, stop=False,
                              skip_group_check=True)
                    pe.matmul(score[1][:], keep["ident_bf"][:], mask2[:], start=False, stop=True,
                              skip_group_check=True).then_inc(sem["scores_ready"], 1)
                    return
                reach(pe, sem["probs_ready"], n * 4 + c - 1)
                mm = pe.matmul(score[c % 2][:, :, 0:keys], qT[p][:, c % chunks, :], kd[0][:, c, :, :],
                               start=True, stop=not causal, skip_group_check=True)
                if causal:
                    mm = pe.matmul(score[c % 2][:, :, :], keep["ident_bf"][:], mask[:], start=False, stop=True,
                                   skip_group_check=True)
                mm.then_inc(sem["scores_ready"], 1)

            def turn_probs(n, p, c):
                u = n * 4 + c
                pe.wait_ge(sem["probs_ready"], u + 1)
                reach(pe, sem[f"pT_copied{c % 2}"], n * 2 + c // 2)
                for j in range(4):
                    mm = pe.transpose(turned[c % 2][0:keys, j, :], prob[c % 2][:, j, :], ident[:])
                mm.then_inc(sem["probs_turned"], 1)

            def weigh(n, p, c):
                pe.wait_ge(sem[f"pT_copied{c % 2}"], n * 2 + c // 2 + 1)
                if c == 0:
                    pe.wait_ge(sem["v_copied"], n + 1)
                    reach(pe, sem["oT_ready"], n)
                    if narrow:
                        pe.matmul(out_b[:, 0, :], zeros[:], zeros[:], start=True, stop=False, skip_group_check=True)
                for j in range(4):
                    mm = pe.matmul(out_b[32 * j:32 * j + 32, 0 if narrow else c, :], vd[p][:, c, 32 * j:32 * j + 32],
                                   pT[c % 2][:, j, :], start=not narrow, stop=not narrow or c == 3,
                                   tile_position=(0, 32 * j), skip_group_check=True)
                mm.then_inc(sem["pv_done"], 1)

            def turn_inverse(n):
                pe.wait_ge(sem["inv_ready"], n + 1)
                reach(pe, sem["r_ready"], n)
                pe.wait_ge(sem["xT_copied"], at_most(n, 3))
                for c in range(chunks):
                    mm = pe.transpose(misc[:, c * S:(c + 1) * S], invb[:, c * E:(c + 1) * E], ident[:])
                mm.then_inc(sem["inv_turned"], 1)

            def out_product(n):
                pe.wait_ge(sem["oT_ready"], n + 1)
                pe.wait_ge(sem["xT_copied"], at_most(n, 4))
                pe.wait_ge(sem["invT_copied"], n + 1)
                for c in range(chunks):
                    mm = pe.matmul(misc[:, 0:E], oT[:, c, :], wo[:, c, :], start=(c == 0), stop=(c == chunks - 1))
                mm.then_inc(sem["y_ready"], 1)

            def step(n, p, c):
                unit, nxt = unit_after(n, p, c, 2), within(n, 1, count)
                turn_probs(n, p, c)
                if unit:
                    scores(*unit)
                if c == 0 and within(n, 2, count):
                    turn_x(n + 2, p)
                if c == 3 and within(n, 2, count):
                    project_q(n + 2, p)
                    project_k(n + 2, p)
                if c == 2 and nxt:
                    project_v(n + 1, 1 - p)
                if c == 2 and within(n, -1, count):
                    out_product(n - 1)
                if c == 3:
                    turn_inverse(n)
                if c > 0:
                    weigh(n, p, c - 1)
                elif within(n, -1, count):
                    weigh(n - 1, 1 - p, 3)

            def slot(n, p):
                for c in range(4):
                    step(n, p, c)

            if v_bias:
                pe.matmul(misc[:, 0:E], vb[:], wo[:, 0, :], start=True, stop=True).then_inc(sem["y_ready"], 1)
                pe.wait_ge(sem["bias_ready"], 1)
            turn_x(0, 0)
            turn_x(1, 1)
            project_q(0, 0)
            project_k(0, 0)
            project_v(0, 0)
            project_q(1, 1)
            project_k(1, 1)
            scores(0, 0, 0)
            scores(0, 0, 1)
            over_slots(pe, slot, count)
            weigh(count - 1, 1, 3)
            out_product(count - 1)

        @block.scalar
        def _(act):
            act.wait_ge(sem["weights"], n_loads)
            act.wait_ge(sem["setup"], 1)

            def copy_xT(n, p):
                act.wait_ge(sem["x_turned"], n + 1)
                reach(act, sem["q_ready"], n - 1)
                if not cross:
                    reach(act, sem["k_ready"], n - 1)
                    reach(act, sem["v_ready"], n - 1)
                if affine is None:
                    act.activation(xT[p][:], misc[:, 0:S], ACT.Copy).then_inc(sem["xT_copied"], 1)
                else:
                    if not cross:
                        act.activation(kin[p][:], misc[:, 0:S], ACT.Identity, scale=aff[:, 2:3], bias=aff[:, 3:4])
                    act.activation(xT[p][:], misc[:, 0:S], ACT.Identity, scale=aff[:, 0:1], bias=aff[:, 1:2])\
                       .then_inc(sem["xT_copied"], 1)

            def copy_q(n, p):
                act.wait_ge(sem["q_ready"], n + 1)
                reach(act, sem["scores_ready"], (n - 1) * 4)
                if q_bias:
                    i = act.activation(qT[p][:], q_b[:, 0:chunks, :], ACT.Identity, scale=scale, bias=qbs[:, 0:1])
                else:
                    i = act.activation(qT[p][:], q_b[:, 0:kept, :], ACT.Copy, scale=1.0 if low_rank else scale)
                i.then_inc(sem["q_copied"], 1)

            def copy_k(n, p):
                act.wait_ge(sem["k_ready"], n + 1)
                reach(act, sem["kd_ready"], (n - 1) * 3)
                reach(act, sem["last_kd_ready"], n - 1)
                if q_bias:
                    i = act.activation(kT[p][:], kv_b[:, 0:chunks, 0:keys], ACT.Identity, bias=kb[:, 0:1])
                else:
                    i = act.activation(kT[p][:], kv_b[:, 0:kept, 0:keys], ACT.Copy)
                i.then_inc(sem["k_copied"], 1)

            def copy_v(n, p):
                act.wait_ge(sem["v_ready"], n + 1)
                reach(act, sem["pv_done"], (n - 1) * 4)
                act.activation(vd[p][:], kv_b[0:keys], ACT.Copy).then_inc(sem["v_copied"], 1)

            def copy_invT(n):
                act.wait_ge(sem["inv_turned"], n + 1)
                reach(act, sem["oT_ready"], n)
                act.activation(invT[:], misc[:, 0:hd].rearrange("p (c s) -> p c s", c=chunks), ACT.Copy)\
                   .then_inc(sem["invT_copied"], 1)

            def copy_a1(n, p, c):
                act.wait_ge(sem["a1_ready"], n * 4 + c + 1)
                reach(act, sem["prod_ready"], n * 4 + c - 1)
                act.activation(a1[c % 2][:], score[0][:], ACT.Copy, scale=scale).then_inc(sem["a1_copied"], 1)

            def exps(n, p, c):
                u = n * 4 + c
                act.wait_ge(sem["max_ready"], u + 1)
                reach(act, sem["probs_turned"], u - 1)
                if c == 0:
                    reach(act, sem["inv_step"], n - 1)
                logits = prod[c % 2] if low_rank else score[c % 2]
                for j in range(4):
                    head = 4 * j + c if narrow else 4 * c + j
                    e = act.activation(prob[c % 2][:, j, :], logits[:, j, 0:keys], ACT.Exp,
                                       bias=negmax[c % 2][:, j:j + 1], accum_out=sums[p][:, head:head + 1])
                e.then_inc(sem["probs_ready"], 1)

            def copy_pT(n, p, c):
                u = n * 4 + c
                act.wait_ge(sem["probs_turned"], u + 1)
                reach(act, sem["pv_done"], u - 1)
                act.activation(pT[1][:], turned[1][0:keys], ACT.Copy).then_inc(sem["pT_copied1"], 1)

            def slot(n, p):
                for c in range(4):
                    unit = unit_after(n, p, c, 1)
                    if c == 0 and within(n, -1, count):
                        copy_invT(n - 1)
                    if low_rank and unit_after(n, p, c, 2):
                        copy_a1(*unit_after(n, p, c, 2))
                    if unit:
                        exps(*unit)
                    if c % 2 == 1 and odd_on_act:
                        copy_pT(n, p, c)
                    if c == 0 and within(n, 2, count):
                        copy_xT(n + 2, p)
                    if c == 3 and within(n, 2, count) and not rope:
                        copy_q(n + 2, p)
                        copy_k(n + 2, p)
                    if c == 2 and within(n, 1, count) and not narrow:
                        copy_v(n + 1, 1 - p)

            copy_xT(0, 0)
            copy_xT(1, 1)
            if not rope:
                copy_q(0, 0)
                copy_k(0, 0)
            if not narrow:
                copy_v(0, 0)
            if not rope:
                copy_q(1, 1)
                copy_k(1, 1)
            if low_rank:
                copy_a1(0, 0, 0)
                copy_a1(0, 0, 1)
            exps(0, 0, 0)
            over_slots(act, slot, count)
            copy_invT(count - 1)

        @block.vector
        def _(dve):
            dve.wait_ge(sem["weights"], n_loads)
            if causal:
                for j in range(4):
                    dve.tensor_copy(mask[:, j, :], mask_f[:])
                    if low_rank:
                        dve.tensor_scalar(mask2[:, j, :], mask_f[:], -1.0, None, ALU.mult)
            if narrow:
                dve.memset(zeros[:], 0.0)
            if rope:
                for i in range(2):
                    dve.tensor_scalar(tables[0][i][:], tables[0][i][:], scale, None, ALU.mult)
            elif q_bias:
                dve.tensor_scalar(qbs[:], qb[:], scale, None, ALU.mult)
            if not out_bias:
                dve.memset(bias[:], 0.0)
            dve.memset(stats[:], 0.0).then_inc(sem["setup"], 1)
            dve.wait_ge(sem["setup"], 1)
            if v_bias:
                dve.wait_ge(sem["y_ready"], 1)
                dve.tensor_tensor(bias[:], bias[:], misc[:, 0:E], ALU.add).then_inc(sem["bias_ready"], 1)
            else:
                dve.engine_nop().then_inc(sem["bias_ready"], 1)

            def rotate(n, p):
                for t, what, bank_in, b, out_t in ((0, "q", q_b, qb, qT[p]), (1, "k", kv_b, kb, kT[p])):
                    dve.wait_ge(sem[what + "_ready"], n + 1)
                    for part in range(2):
                        i = dve.scalar_tensor_tensor(out=terms[t][part][:], in0=bank_in[:, part, :],
                                                     scalar=b[:, part:part + 1], in1=tables[t][part][:],
                                                     op0=ALU.add, op1=ALU.mult)
                    i.then_inc(sem["term_ready"], 1)
                    dve.wait_ge(sem["term_ready"], n * 2 + t + 1)
                    reach(dve, sem["scores_ready"], (n - 1) * 4)
                    reach(dve, sem["last_kd_ready"], n - 1)
                    dve.tensor_tensor(out_t[:, 0, :], terms[t][0][:], terms[t][1][:], ALU.add)\
                       .then_inc(sem[what + "_copied"], 1)

            def spread(n, p, c):
                dve.wait_ge(sem["k_copied"], n + 1)
                reach(dve, sem["scores_ready"], (n - 1) * 4 + c + 1)
                for f in range(factors):
                    i = dve.tensor_tensor(kd[f][:, c, :, :],
                                          kT[p][:, f if low_rank else c % chunks, :].unsqueeze(1)
                                          .broadcast_to([E, 4, keys]),
                                          copy_bcast(kmask[f][:, c, :], keys), ALU.mult)
                i.then_inc(sem["kd_ready"], 1)

            def spread_v(n, p):
                dve.wait_ge(sem["v_ready"], n + 1)
                reach(dve, sem["pv_done"], (n - 1) * 4)
                dve.tensor_tensor(vd[p][:], kv_b[0:keys, 0:1, :].broadcast_to([keys, 4, E]), vmask[0:keys],
                                  ALU.mult).then_inc(sem["v_copied"], 1)

            def maxima(n, p, c):
                u = n * 4 + c
                dve.wait_ge(sem["scores_ready"], u + 1)
                reach(dve, sem["probs_ready"], u - 1)
                logits = score[c % 2]
                if low_rank:
                    dve.wait_ge(sem["a1_copied"], u + 1)
                    logits = prod[c % 2]
                    dve.tensor_tensor(logits[:], a1[c % 2][:], score[1][:], ALU.mult).then_inc(sem["prod_ready"], 1)
                    dve.wait_ge(sem["prod_ready"], u + 1)
                dve.tensor_reduce(negmax[c % 2][:], logits[:, :, 0:keys], AX.X, ALU.max, negate=True)\
                   .then_inc(sem["max_ready"], 1)

            def copy_pT(n, p, c):
                u = n * 4 + c
                dve.wait_ge(sem["probs_turned"], u + 1)
                reach(dve, sem["pv_done"], u - 1)
                if future_only:
                    i = dve.tensor_tensor(pT[c % 2][:], turned[c % 2][:],
                                          future[:].unsqueeze(1).broadcast_to([S, 4, S]), ALU.mult)
                else:
                    i = dve.tensor_copy(pT[c % 2][:], turned[c % 2][0:keys])
                i.then_inc(sem[f"pT_copied{c % 2}"], 1)

            def inverse(n, p):
                dve.wait_ge(sem["probs_ready"], (n + 1) * 4)
                dve.reciprocal(inv[:], sums[p][:]).then_inc(sem["inv_step"], 1)
                dve.wait_ge(sem["inv_step"], n + 1)
                reach(dve, sem["inv_turned"], n)
                dve.tensor_copy(invb[:].rearrange("p (h e) -> p h e", h=HEADS), copy_bcast(inv[:], head_dim))\
                   .then_inc(sem["inv_ready"], 1)

            def scale_out(n):
                dve.wait_ge(sem["pv_done"], (n + 1) * 4)
                dve.wait_ge(sem["invT_copied"], n + 1)
                reach(dve, sem["y_ready"], n + y0)
                dve.tensor_tensor(oT[:], out_b[:, 0:chunks, :], invT[:], ALU.mult).then_inc(sem["oT_ready"], 1)

            def residual(n, p):
                dve.wait_ge(sem["y_ready"], n + 1 + y0)
                dve.wait_ge(sem["xb_ready"], n + 1)
                if dst == "sum_and_norm":
                    reach(dve, sem["sum_stored"], n)
                reach(dve, sem["normed"], n)
                dve.tensor_tensor(r[p][:], misc[:, 0:E], xb[p][:], ALU.add).then_inc(sem["r_ready"], 1)

            def moments(n, p):
                dve.wait_ge(sem["r_ready"], n + 1)
                dve.bn_stats(stats[:], r[p][:]).then_inc(sem["stats_ready"], 1)
                wait_alone(dve, sem["stats_ready"], n + 1, keep["passed"])
                dve.bn_aggr(mv[p][:], stats[:]).then_inc(sem["mv_ready"], 1)
                dve.wait_ge(sem["mv_ready"], n + 1)
                dve.tensor_scalar(rstd[p][:], mv[p][:, 1:2], LN_EPS, None, ALU.add).then_inc(sem["var_ready"], 1)

            def norm(n, p):
                dve.wait_ge(sem["rstd_ready"], n + 1)
                out = x if dst == "norm" else keep["z"]
                dve.tensor_scalar(out[:, n, :], r[p][:], mv[p][:, 0:1], rstd[p][:, 0:1], ALU.subtract, ALU.mult)\
                   .then_inc(sem["normed"], 1)

            def slot(n, p):
                nxt = within(n, 1, count)
                for c in range(4):
                    unit = unit_after(n, p, c, 2)
                    if c == 1 and within(n, -1, count):
                        scale_out(n - 1)
                    if c == 3 and within(n, -1, count):
                        residual(n - 1, 1 - p)
                    if c == 3:
                        inverse(n, p)
                    if c % 2 == 0 or not odd_on_act:
                        copy_pT(n, p, c)
                    if unit:
                        maxima(*unit)
                    if c < 3 and nxt:
                        spread(n + 1, 1 - p, c)
                    if c == 3 and within(n, 2, count) and rope:
                        rotate(n + 2, p)
                    if c == 2 and nxt and narrow:
                        spread_v(n + 1, 1 - p)
                    if c == 1 and within(n, -2, count):
                        norm(n - 2, p)
                    if c == 3 and within(n, -1, count):
                        moments(n - 1, 1 - p)

            if rope:
                rotate(0, 0)
            for c in range(3):
                spread(0, 0, c)
            if narrow:
                spread_v(0, 0)
            if rope:
                rotate(1, 1)
            maxima(0, 0, 0)
            maxima(0, 0, 1)
            over_slots(dve, slot, count)
            scale_out(count - 1)
            norm(count - 2, 0)
            residual(count - 1, 1)
            moments(count - 1, 1)
            norm(count - 1, 1)

    clear(nc, sem)


def feed_forward(nc, d, keep, tag, kind, n_chunks, func, *, scale=1.0, ints=False, bias=False, out_bias=False,
                 experts=0, per_gate=1, gates=0, first_gated=0, shared_gate=False, gate_bias=False,
                 src=None, affine=False, dst="norm"):
    G, T = 4, 4 * S
    groups = SEQS // G
    glu, gated = kind == "glu", experts > 0
    routed = experts + (1 if shared_gate else 0)
    x, ident = keep["x"], keep["ident"]
    src = x if src is None else src
    J = n_chunks
    with ExitStack() as ctx:
        sb, bank, sems = tensors(ctx, nc, tag)
        wdt = I32 if ints else F32
        wu, wd = sb("wu", [E, J, E]), sb("wd", [E, J, E])
        mats = [("wu", wu), ("wd", wd)]
        if glu:
            wv = sb("wv", [E, J, E])
            mats.append(("wv", wv))
        loads, raw = [], []
        for n, t in mats:
            if ints:
                raw.append(sb(n + "_int", [E, J, E], I32))
                loads.append((raw[-1][:], d[f"{tag}_{n}"]))
            else:
                loads.append((t[:], d[f"{tag}_{n}"]))
        if bias:
            ub = sb("ub", [E, J])
            loads.append((ub[:], d[tag + "_bu"]))
        ob = sb("ob", [S, E])
        if out_bias:
            loads.append((ob[:], d[tag + "_bd"]))
        if affine:
            aff = sb("aff", [E, 2])
            loads.append((aff[:], d[tag + "_aff"]))
        if gated:
            wr = sb("wr", [E, routed])
            R3 = 3 * routed
            sel_f, sel = sb("sel_f", [R3, gates, E]), sb("sel", [R3, gates, E], BF16)
            before = sb("before", [S, experts, experts])
            loads += [(wr[:], d[tag + "_wr"]), (sel_f[:], d[tag + "_sel"]), (before[:], d[tag + "_before"])]
            if gate_bias:
                gb = sb("gb", [R3, E])
                loads.append((gb[:], d[tag + "_gb"]))
            prob = sb("prob", [S, G, routed])
            top = sb("top", [S, G])
            more = sb("more", [S, G, experts, experts])
            same = sb("same", [S, G, experts, experts])
            rank = sb("rank", [S, G, experts])
            gate = sb("gate", [S, G, routed])
            parts = sb("parts", [S, G, 3, routed])
            rest = sb("rest", [S, G, routed])
            rounded = [sb(f"rounded{i}", [S, G, routed], BF16) for i in range(2)]
            gateT = [sb(f"gateT{i}", [R3, T], BF16) for i in range(2)]
            if gate_bias:
                gateT_f = [sb(f"gateT_f{i}", [R3, T]) for i in range(2)]
        xin = sb("xin", [S, G, E])
        xT = [sb(f"xT{i}", [E, T]) for i in range(2)]
        h = [sb(f"h{i}", [E, T]) for i in range(2)]
        hv = [sb(f"hv{i}", [E, T]) for i in range(2)] if glu else h
        hg = [sb(f"hg{i}", [E, T]) for i in range(2)] if gated else hv
        xb = sb("xb", [S, G, E])
        r = [sb(f"r{i}", [S, G, E]) for i in range(2)]
        stats = sb("stats", [S, G, 6])
        mv = [sb(f"mv{i}", [S, G, 2]) for i in range(2)]
        rstd = [sb(f"rstd{i}", [S, G]) for i in range(2)]
        x_b, v_b, y_b, r_b = bank("x", [E, T]), bank("v", [E, T]), bank("y", [S, G, E]), bank("r", [S, 512])
        u_b = [bank(f"u{i}", [E, T]) for i in range(2)]
        g_b = [bank(f"g{i}", [E, T]) for i in range(2)]
        sem = sems("weights setup xin_ready x_turned xT_copied up_ready act_done v_ready v_done hidden_ready "
                   "gate_spread down_done y_ready xb_ready xb_part r_ready stats_ready mv_ready var_ready rstd_ready "
                   "normed gate_sum routed route_step logits_shifted route_exp gate_parts gates_ready gates_turned gateT_copied")
        n_loads = 16 * len(loads)
        hidden = "hidden_ready" if gated else "v_done" if glu else "act_done"
        block = ctx.enter_context(nc.Block())

        def gate_of(j):
            return (j - first_gated) // per_gate if gated and j >= first_gated else None

        def new_gate(j):
            return gate_of(j) is not None and (j - first_gated) % per_gate == 0

        @block.sync
        def _(sp):
            load_all(sp, loads, sem["weights"])

        @block.gpsimd
        def _(pool):
            pool.wait_ge(sem["weights"], n_loads)
            pool.wait_ge(sem["setup"], 1)

            def stage_in(g):
                reach(pool, sem["x_turned"], g)
                pool.tensor_copy(xin[:], src[:, bass.ds(g * G, G), :]).then_inc(sem["xin_ready"], 1)

            def residual_base(g):
                wait_alone(pool, sem["r_ready"], g, keep["passed_pool"])
                res = x if dst == "norm" else keep["b"]
                pool.tensor_tensor(xb[:], res[:, bass.ds(g * G, G), :], ob[:].unsqueeze(1).broadcast_to([S, G, E]),
                                   ALU.add).then_inc(sem["xb_part"], 1)
                if dst == "norm_with_x":
                    pool.wait_ge(sem["xb_part"], g + 1)
                    pool.tensor_tensor(xb[:], xb[:], x[:, bass.ds(g * G, G), :], ALU.add).then_inc(sem["xb_ready"], 1)

            def root(g, p):
                if dst != "store":
                    pool.wait_ge(sem["var_ready"], g + 1)
                    pool.tensor_tensor(rstd[p][:], rstd[p][:], keep["minus_half"][:, 0:1].broadcast_to([S, G]),
                                       ALU.pow).then_inc(sem["rstd_ready"], 1)

            def slot(g, p):
                if within(g, 1, groups):
                    stage_in(g + 1)
                if within(g, -1, groups):
                    root(g - 1, 1 - p)
                residual_base(g)

            stage_in(0)
            over_slots(pool, slot, groups)
            root(groups - 1, 1)

        @block.tensor
        def _(pe):
            pe.wait_ge(sem["weights"], n_loads)
            pe.wait_ge(sem["setup"], 1)

            def turn_x(g):
                pe.wait_ge(sem["xin_ready"], g + 1)
                reach(pe, sem["xT_copied"], g)
                for s in range(G):
                    mm = pe.transpose(x_b[:, s * S:(s + 1) * S], xin[:, s, :], ident[:])
                mm.then_inc(sem["x_turned"], 1)

            def route(g, p):
                pe.wait_ge(sem["xT_copied"], g + 1)
                reach(pe, sem["gateT_copied"], g)
                for s in range(G):
                    mm = pe.matmul(r_b[:, s * routed:(s + 1) * routed], xT[p][:, s * S:(s + 1) * S], wr[:],
                                   start=True, stop=True)
                mm.then_inc(sem["routed"], 1)

            def turn_gates(g):
                wait_alone(pe, sem["gates_ready"], g + 1, keep["passed_pe"])
                for s in range(G):
                    mm = pe.transpose(r_b[0:R3, s * S:(s + 1) * S], parts[:, s].rearrange("p k e -> p (k e)"),
                                      ident[:])
                mm.then_inc(sem["gates_turned"], 1)

            def up(g, p, j):
                n = g * J + j
                if j == 0:
                    pe.wait_ge(sem["xT_copied"], g + 1)
                reach(pe, sem["act_done"], n - 1)
                pe.matmul(u_b[(p * J + j) % 2][:], wu[:, j, :], xT[p][:], start=True, stop=True).then_inc(sem["up_ready"], 1)
                if glu:
                    reach(pe, sem["v_done"], n)
                    pe.matmul(v_b[:], wv[:, j, :], xT[p][:], start=True, stop=True).then_inc(sem["v_ready"], 1)
                if new_gate(j):
                    k = gate_of(j)
                    if k == 0:
                        pe.wait_ge(sem["gateT_copied"], g + 1)
                    last = first_gated + (k - 1) * per_gate if k >= 2 else None
                    if last is not None:
                        pe.wait_ge(sem["hidden_ready"], g * J + last)
                    else:
                        reach(pe, sem["hidden_ready"], g * J)
                    pe.matmul(g_b[k % 2][:], sel[:, k, :], gateT[p][:], start=True, stop=True)\
                      .then_inc(sem["gate_spread"], 1)

            def down(g, p, j):
                n = g * J + j
                pe.wait_ge(sem[hidden], n + 1)
                if j == 0:
                    reach(pe, sem["r_ready"], g)
                    if gate_bias:
                        for s in range(G):
                            pe.matmul(y_b[:, s, :], gateT_f[p][:, s * S:(s + 1) * S], gb[:],
                                      start=(s == 0), stop=False, skip_group_check=True)
                for s in range(G):
                    mm = pe.matmul(y_b[:, s, :], hg[(p * J + j) % 2][:, s * S:(s + 1) * S], wd[:, j, :],
                                   start=(j == 0 and s == 0 and not gate_bias), stop=(j == J - 1),
                                   skip_group_check=True)
                mm.then_inc(sem["down_done"], 1)

            def slot(g, p):
                for j in range(J):
                    up(g, p, j)
                    if j > 0:
                        down(g, p, j - 1)
                    elif within(g, -1, groups):
                        down(g - 1, 1 - p, J - 1)
                    if j == 1 and within(g, 1, groups):
                        turn_x(g + 1)
                    if gated and j == 3 and within(g, 1, groups):
                        route(g + 1, 1 - p)
                    if gated and j == J - 1 and within(g, 1, groups):
                        turn_gates(g + 1)

            turn_x(0)
            if gated:
                route(0, 0)
                turn_gates(0)
            over_slots(pe, slot, groups)
            down(groups - 1, 1, J - 1)

        @block.scalar
        def _(act):
            act.wait_ge(sem["weights"], n_loads)

            def copy_xT(g, p):
                act.wait_ge(sem["x_turned"], g + 1)
                reach(act, sem["up_ready"], (g - 1) * J)
                if glu:
                    reach(act, sem["v_ready"], (g - 1) * J)
                if affine:
                    i = act.activation(xT[p][:], x_b[:], ACT.Identity, scale=aff[:, 0:1], bias=aff[:, 1:2])
                else:
                    i = act.activation(xT[p][:], x_b[:], ACT.Copy)
                i.then_inc(sem["xT_copied"], 1)

            def route_exp(g):
                act.wait_ge(sem["logits_shifted"], g + 1)
                act.activation(prob[:], prob[:], ACT.Exp).then_inc(sem["route_exp"], 1)

            def copy_gateT(g, p):
                act.wait_ge(sem["gates_turned"], g + 1)
                reach(act, sem["down_done"], (g - 1) * J)
                if gate_bias:
                    act.activation(gateT_f[p][:], r_b[0:R3, :], ACT.Copy)
                act.activation(gateT[p][:], r_b[0:R3, :], ACT.Copy).then_inc(sem["gateT_copied"], 1)

            def activate(g, p, j):
                n = g * J + j
                act.wait_ge(sem["up_ready"], n + 1)
                reach(act, sem["v_done"] if glu else sem["hidden_ready"] if gated else sem["down_done"], n - 1)
                i = act.activation(h[(p * J + j) % 2][:], u_b[(p * J + j) % 2][:], func, scale=scale,
                                   **(dict(bias=ub[:, j:j + 1]) if bias else {}))
                i.then_inc(sem["act_done"], 1)

            def slot(g, p):
                for j in range(J):
                    activate(g, p, j)
                    if j == 1 and within(g, 1, groups):
                        copy_xT(g + 1, 1 - p)
                    if gated and j == 5 and within(g, 1, groups):
                        route_exp(g + 1)
                if gated and within(g, 1, groups):
                    copy_gateT(g + 1, 1 - p)

            copy_xT(0, 0)
            if gated:
                route_exp(0)
                copy_gateT(0, 0)
            over_slots(act, slot, groups)

        @block.vector
        def _(dve):
            dve.wait_ge(sem["weights"], n_loads)
            for (_, t), i in zip(mats, raw):
                dve.tensor_copy(t[:], i[:])
            if gated:
                dve.tensor_copy(sel[:], sel_f[:])
            if not out_bias:
                dve.memset(ob[:], 0.0)
            dve.memset(stats[:], 0.0).then_inc(sem["setup"], 1)

            STEPS = 10

            def chain(g, k, ins):
                ins.then_inc(sem["route_step"], 1)
                dve.wait_ge(sem["route_step"], g * STEPS + k)

            def split(g, k, ins):
                ins.then_inc(sem["gate_parts"], 1)
                dve.wait_ge(sem["gate_parts"], g * 4 + k)

            def per_n(ap):
                return ap.unsqueeze(2).broadcast_to([S, G, experts, experts])

            def per_m(ap):
                return ap.unsqueeze(3).broadcast_to([S, G, experts, experts])

            def route(g, part):
                pr = prob[:, :, 0:experts]
                if part == 0:
                    dve.wait_ge(sem["routed"], g + 1)
                    logits = r_b[:, 0:G * routed].rearrange("p (s e) -> p s e", s=G)
                    chain(g, 1, dve.tensor_reduce(top[:], logits[:, :, 0:experts], AX.X, ALU.max, negate=True))
                    if shared_gate:
                        dve.tensor_scalar(prob[:, :, experts:routed], logits[:, :, experts:routed], -1.0, None,
                                          ALU.mult)
                    dve.tensor_tensor(pr, logits[:, :, 0:experts], copy_bcast(top[:], experts), ALU.add)\
                       .then_inc(sem["logits_shifted"], 1)
                elif part == 1:
                    dve.wait_ge(sem["route_exp"], g + 1)
                    chain(g, 2, dve.tensor_reduce(top[:], pr, AX.X, ALU.add))
                    chain(g, 3, dve.reciprocal(top[:], top[:]))
                    if shared_gate:
                        dve.tensor_scalar(gate[:, :, experts:routed], prob[:, :, experts:routed], 1.0, None, ALU.add)
                    chain(g, 4, dve.tensor_tensor(pr, pr, copy_bcast(top[:], experts), ALU.mult))
                    if shared_gate:
                        dve.reciprocal(gate[:, :, experts:routed], gate[:, :, experts:routed])
                elif part == 2:
                    dve.tensor_tensor(more[:], per_n(pr), per_m(pr), ALU.is_gt)
                    chain(g, 5, dve.tensor_tensor(same[:], per_n(pr), per_m(pr), ALU.is_equal))
                    chain(g, 6, dve.tensor_tensor(same[:], same[:], before[:].unsqueeze(1).broadcast_to(
                        [S, G, experts, experts]), ALU.mult))
                elif part == 3:
                    chain(g, 7, dve.tensor_tensor(more[:], more[:], same[:], ALU.add))
                    chain(g, 8, dve.tensor_reduce(rank[:], more[:], AX.X, ALU.add))
                else:
                    chain(g, 9, dve.scalar_tensor_tensor(out=rank[:], in0=rank[:], scalar=1.5, in1=pr,
                                                         op0=ALU.is_lt, op1=ALU.mult))
                    chain(g, 10, dve.tensor_reduce(top[:], rank[:], AX.X, ALU.add))
                    dve.reciprocal(top[:], top[:]).then_inc(sem["gate_sum"], 1)
                    dve.wait_ge(sem["gate_sum"], g + 1)
                    split(g, 1, dve.tensor_tensor(gate[:, :, 0:experts], rank[:], copy_bcast(top[:], experts),
                                                  ALU.mult))
                    reach(dve, sem["gates_turned"], g)
                    split(g, 2, dve.tensor_copy(rounded[0][:], gate[:]))
                    dve.tensor_copy(parts[:, :, 0, :], rounded[0][:])
                    split(g, 3, dve.tensor_tensor(rest[:], gate[:], rounded[0][:], ALU.subtract))
                    split(g, 4, dve.tensor_copy(rounded[1][:], rest[:]))
                    dve.tensor_copy(parts[:, :, 1, :], rounded[1][:])
                    dve.tensor_tensor(parts[:, :, 2, :], rest[:], rounded[1][:], ALU.subtract)\
                       .then_inc(sem["gates_ready"], 1)

            def finish_hidden(g, p, j):
                n = g * J + j
                dve.wait_ge(sem["act_done"], n + 1)
                a = h[(p * J + j) % 2]
                if glu:
                    dve.wait_ge(sem["v_ready"], n + 1)
                    if gated:
                        i = dve.tensor_tensor(hv[(p * J + j) % 2][:], a[:], v_b[:], ALU.mult)
                    else:
                        reach(dve, sem["down_done"], n - 1)
                        i = dve.scalar_tensor_tensor(out=hv[(p * J + j) % 2][:], in0=v_b[:], scalar=scale, in1=a[:],
                                                     op0=ALU.mult, op1=ALU.mult)
                    i.then_inc(sem["v_done"], 1)
                    dve.wait_ge(sem["v_done"], n + 1)
                    a = hv[(p * J + j) % 2]
                if not gated:
                    return
                reach(dve, sem["down_done"], n - 1)
                k = gate_of(j)
                if k is None:
                    i = dve.tensor_copy(hg[(p * J + j) % 2][:], a[:])
                else:
                    if new_gate(j):
                        dve.wait_ge(sem["gate_spread"], g * gates + k + 1)
                    i = dve.tensor_tensor(hg[(p * J + j) % 2][:], a[:], g_b[k % 2][:], ALU.mult)
                i.then_inc(sem["hidden_ready"], 1)

            def residual(g, p):
                dve.wait_ge(sem["down_done"], (g + 1) * J)
                dve.wait_ge(sem["xb_ready" if dst == "norm_with_x" else "xb_part"], g + 1)
                if dst == "store":
                    dve.tensor_tensor(keep["b"][:, bass.ds(g * G, G), :], y_b[:], xb[:], ALU.add)\
                       .then_inc(sem["r_ready"], 1)
                    return
                if ints:
                    i = dve.scalar_tensor_tensor(out=r[p][:], in0=y_b[:], scalar=scale, in1=xb[:], op0=ALU.mult,
                                                 op1=ALU.add)
                else:
                    i = dve.tensor_tensor(r[p][:], y_b[:], xb[:], ALU.add)
                i.then_inc(sem["r_ready"], 1)
                dve.wait_ge(sem["r_ready"], g + 1)
                for s in range(G):
                    i = dve.bn_stats(stats[:, s, :], r[p][:, s, :])
                i.then_inc(sem["stats_ready"], 1)
                wait_alone(dve, sem["stats_ready"], g + 1, keep["passed"])
                for s in range(G):
                    i = dve.bn_aggr(mv[p][:, s, :], stats[:, s, :])
                i.then_inc(sem["mv_ready"], 1)
                dve.wait_ge(sem["mv_ready"], g + 1)
                dve.tensor_scalar(rstd[p][:], mv[p][:, :, 1], LN_EPS, None, ALU.add).then_inc(sem["var_ready"], 1)

            def norm(g, p):
                if dst == "store":
                    return
                dve.wait_ge(sem["rstd_ready"], g + 1)
                for s in range(G):
                    i = dve.tensor_scalar(x[:, g * G + s, :], r[p][:, s, :], mv[p][:, s, 0:1], rstd[p][:, s:s + 1],
                                          ALU.subtract, ALU.mult)
                i.then_inc(sem["normed"], 1)

            def slot(g, p):
                for j in range(J):
                    if glu or gated:
                        finish_hidden(g, p, j)
                    if j == 0 and within(g, -1, groups):
                        residual(g - 1, 1 - p)
                    if j == 2 and within(g, -1, groups):
                        norm(g - 1, 1 - p)
                    if gated and 4 <= j < 9 and within(g, 1, groups):
                        route(g + 1, j - 4)

            if gated:
                for part in range(5):
                    route(0, part)
            over_slots(dve, slot, groups)
            residual(groups - 1, 1)
            norm(groups - 1, 1)

    clear(nc, sem)


def renormalise(nc, d, keep, tag, src):
    G = 4
    groups = SEQS // G
    b, z = keep["b"], keep["z"]
    with ExitStack() as ctx:
        sb, _, sems = tensors(ctx, nc, tag)
        gain, shift = sb("gain", [S, E]), sb("shift", [S, E])
        loads = [(gain[:], d[tag + "_gain"]), (shift[:], d[tag + "_shift"])]
        scaled = [sb(f"scaled{i}", [S, G, E]) for i in range(2)]
        stats = sb("stats", [S, G, 6])
        mv = [[sb(f"mv{k}{i}", [S, G, 2]) for i in range(2)] for k in range(2)]
        rstd = [[sb(f"rstd{k}{i}", [S, G]) for i in range(2)] for k in range(2)]
        sem = sems("weights stats_ready mv_ready var0 var1 rstd0 rstd1 normed scaled stored z_stored")
        block = ctx.enter_context(nc.Block())

        @block.sync
        def _(sp):
            load_all(sp, loads, sem["weights"])

        @block.gpsimd
        def _(pool):
            def root(k, g, p):
                pool.wait_ge(sem[f"var{k}"], g + 1)
                pool.tensor_tensor(rstd[k][p][:], rstd[k][p][:], keep["minus_half"][:, 0:1].broadcast_to([S, G]),
                                   ALU.pow).then_inc(sem[f"rstd{k}"], 1)

            def scale_shift(g, p):
                pool.wait_ge(sem["normed"], g + 1)
                pool.tensor_tensor(scaled[p][:], scaled[p][:], gain[:].unsqueeze(1).broadcast_to([S, G, E]), ALU.mult)\
                    .then_inc(sem["scaled"], 1)
                wait_alone(pool, sem["scaled"], g + 1, keep["passed_pool"])
                pool.tensor_tensor(b[:, bass.ds(g * G, G), :], scaled[p][:],
                                   shift[:].unsqueeze(1).broadcast_to([S, G, E]), ALU.add).then_inc(sem["stored"], 1)

            def slot(g, p):
                if within(g, -2, groups):
                    root(1, g - 2, p)
                if within(g, -1, groups):
                    scale_shift(g - 1, 1 - p)
                root(0, g, p)

            pool.wait_ge(sem["weights"], 32)
            over_slots(pool, slot, groups)
            root(1, groups - 2, 0)
            scale_shift(groups - 1, 1)
            root(1, groups - 1, 1)

        @block.vector
        def _(dve):
            dve.wait_ge(sem["weights"], 32)

            def moments(k, g, p, count):
                data = src if k == 0 else b
                if k == 1:
                    wait_alone(dve, sem["stored"], g + 1, keep["passed"])
                for s in range(G):
                    i = dve.bn_stats(stats[:, s, :], data[:, g * G + s, :])
                i.then_inc(sem["stats_ready"], 1)
                wait_alone(dve, sem["stats_ready"], count + 1, keep["passed"])
                for s in range(G):
                    i = dve.bn_aggr(mv[k][p][:, s, :], stats[:, s, :])
                i.then_inc(sem["mv_ready"], 1)
                dve.wait_ge(sem["mv_ready"], count + 1)
                dve.tensor_scalar(rstd[k][p][:], mv[k][p][:, :, 1], LN_EPS, None, ALU.add).then_inc(sem[f"var{k}"], 1)

            def normalise(g, p):
                dve.wait_ge(sem["rstd0"], g + 1)
                for s in range(G):
                    i = dve.tensor_scalar(scaled[p][:, s, :], src[:, g * G + s, :], mv[0][p][:, s, 0:1],
                                          rstd[0][p][:, s:s + 1], ALU.subtract, ALU.mult)
                i.then_inc(sem["normed"], 1)

            def store_z(g, p):
                dve.wait_ge(sem["rstd1"], g + 1)
                for s in range(G):
                    i = dve.tensor_scalar(z[:, g * G + s, :], b[:, g * G + s, :], mv[1][p][:, s, 0:1],
                                          rstd[1][p][:, s:s + 1], ALU.subtract, ALU.mult)
                i.then_inc(sem["z_stored"], 1)

            def slot(g, p):
                if within(g, -2, groups):
                    moments(1, g - 2, p, g * 2 - 2)
                if within(g, -1, groups):
                    normalise(g - 1, 1 - p)
                moments(0, g, p, 0 if isinstance(g, int) and g == 0 else g * 2 - 1)
                if within(g, -2, groups):
                    store_z(g - 2, p)

            over_slots(dve, slot, groups)
            moments(1, groups - 2, 0, 2 * groups - 2)
            normalise(groups - 1, 1)
            store_z(groups - 2, 0)
            moments(1, groups - 1, 1, 2 * groups - 1)
            store_z(groups - 1, 1)

    clear(nc, sem)


def normalise_context(nc, d, keep, tag):
    G = 4
    groups = SEQS // G
    with ExitStack() as ctx:
        sb, bank, sems = tensors(ctx, nc, tag)
        c, sq = sb("c", [CTX, SEQS, C]), sb("sq", [CTX, SEQS, C])
        aff = sb("aff", [C, 2])
        mean, rstd = sb("mean", [CTX, SEQS]), sb("rstd", [CTX, SEQS])
        turned = [bank(f"turned{i}", [C, G, CTX]) for i in range(2)]
        sem = sems("loaded step var_ready rstd_ready normed turned stored")
        block = ctx.enter_context(nc.Block())

        @block.sync
        def _(sp):
            sp.dma_start(c[:], d["ctx"].rearrange("s t c -> t s c")).then_inc(sem["loaded"], 16)
            sp.dma_start(aff[:], d[tag + "_aff"]).then_inc(sem["loaded"], 16)

        @block.gpsimd
        def _(pool):
            pool.wait_ge(sem["var_ready"], 1)
            pool.tensor_tensor(rstd[:], rstd[:], keep["minus_half"][0:CTX, 0:1].broadcast_to([CTX, SEQS]), ALU.pow)\
                .then_inc(sem["rstd_ready"], 1)

        @block.vector
        def _(dve):
            def chain(k, ins):
                ins.then_inc(sem["step"], 1)
                dve.wait_ge(sem["step"], k)

            dve.wait_ge(sem["loaded"], 32)
            chain(1, dve.tensor_reduce(mean[:], c[:], AX.X, ALU.add))
            chain(2, dve.tensor_scalar(mean[:], mean[:], 1.0 / C, None, ALU.mult))
            chain(3, dve.tensor_tensor(c[:], c[:], copy_bcast(mean[:], C), ALU.subtract))
            chain(4, dve.tensor_tensor(sq[:], c[:], c[:], ALU.mult))
            chain(5, dve.tensor_reduce(rstd[:], sq[:], AX.X, ALU.add))
            dve.tensor_scalar(rstd[:], rstd[:], 1.0 / C, LN_EPS, ALU.mult, ALU.add).then_inc(sem["var_ready"], 1)
            dve.wait_ge(sem["rstd_ready"], 1)
            dve.tensor_tensor(c[:], c[:], copy_bcast(rstd[:], C), ALU.mult).then_inc(sem["normed"], 1)

        @block.tensor
        def _(pe):
            pe.wait_ge(sem["normed"], 1)
            for g in range(groups):
                if g >= 2:
                    pe.wait_ge(sem["stored"], g - 1)
                for s in range(G):
                    mm = pe.transpose(turned[g % 2][:, s, :], c[:, g * G + s, :], keep["ident"][0:CTX, 0:CTX])
                mm.then_inc(sem["turned"], 1)

        @block.scalar
        def _(act):
            act.wait_ge(sem["loaded"], 32)
            for g in range(groups):
                act.wait_ge(sem["turned"], g + 1)
                act.activation(keep["ctxn"][:, g * G:(g + 1) * G, :], turned[g % 2][:], ACT.Identity,
                               scale=aff[:, 0:1], bias=aff[:, 1:2]).then_inc(sem["stored"], 1)

    clear(nc, sem)


def relu_attention(nc, d, keep, tag):
    G = 2
    count, K, D = SEQS // G, 4, E // HEADS
    x, ident = keep["x"], keep["ident"]
    with ExitStack() as ctx:
        sb, bank, sems = tensors(ctx, nc, tag)
        w = {n: sb(n, [E, E]) for n in ("wq", "wk", "wv", "wo")}
        b = {n: sb(n, [S, E]) for n in ("bq", "bk", "bv", "bo", "weight", "gain")}
        rowsT = {n: sb(n, [E, K, S]) for n in ("keyT", "valueT")}
        loads = [(t[:], d[f"{tag}_{n}"]) for m in (w, b, rowsT) for n, t in m.items()]
        kk, vv = sb("k", [S, K, E]), sb("v", [S, G, K, E])
        half = sb("half", [S, 1])
        xin = [sb(f"xin{i}", [S, G, E]) for i in range(2)]
        xT = [sb(f"xT{i}", [E, G, S]) for i in range(2)]
        xb = [sb(f"xb{i}", [S, G, E]) for i in range(2)]
        q = sb("q", [S, G, E])
        prod = [sb(f"prod{i}", [S, G, K, E]) for i in range(2)]
        logit = sb("logit", [S, G * K * HEADS])
        o = [sb(f"o{i}", [S, G, E]) for i in range(2)]
        sq = sb("sq", [S, G, E])
        ms = [sb(f"ms{i}", [S, G]) for i in range(2)]
        gx = [sb(f"gx{i}", [S, G, E]) for i in range(2)]
        on = sb("on", [S, G, E])
        oT = sb("oT", [E, G, S])
        r = [sb(f"r{i}", [S, G, E]) for i in range(2)]
        stats = sb("stats", [S, G, 6])
        mv = [sb(f"mv{i}", [S, G, 2]) for i in range(2)]
        rstd = [sb(f"rstd{i}", [S, G]) for i in range(2)]
        k_b, v_b = bank("k_b", [S, K, E]), bank("v_b", [S, K, E])
        x_b, q_b, t_b, y_b = (bank(n, [S, G, E]) for n in ("x_b", "q_b", "t_b", "y_b"))
        sem = sems("weights kv_ready setup xin_ready x_turned xT_copied q_ready xb_ready step meansq_ready rms_ready "
                   "gated sigmoid_ready on_ready on_turned oT_copied y_ready r_ready var_ready rstd_ready normed "
                   "gate_step res_step logits_ready weighted summed out_step")
        n_loads = 16 * len(loads)
        STEPS = 3
        block = ctx.enter_context(nc.Block())

        @block.sync
        def _(sp):
            load_all(sp, loads, sem["weights"])

        @block.gpsimd
        def _(pool):
            pool.wait_ge(sem["weights"], n_loads)
            pool.wait_ge(sem["setup"], 1)

            def stage_in(n, p):
                reach(pool, sem["x_turned"], n - 1)
                pool.tensor_copy(xin[p][:], x[:, bass.ds(n * G, G), :]).then_inc(sem["xin_ready"], 1)

            def slot(n, p):
                pool.wait_ge(sem["logits_ready"], n + 1)
                reach(pool, sem["summed"], n - 1)
                pool.tensor_tensor(prod[p][:].rearrange("p g k (h e) -> p (g k h) e", h=HEADS),
                                   vv[:].rearrange("p g k (h e) -> p (g k h) e", h=HEADS),
                                   copy_bcast(logit[:], D), ALU.mult).then_inc(sem["weighted"], 1)
                pool.wait_ge(sem["meansq_ready"], n + 1)
                pool.tensor_tensor(ms[p][:], ms[p][:], half[:].broadcast_to([S, G]), ALU.pow).then_inc(sem["rms_ready"], 1)
                if within(n, 2, count):
                    stage_in(n + 2, p)
                if within(n, -1, count):
                    pool.wait_ge(sem["var_ready"], n)
                    pool.tensor_tensor(rstd[1 - p][:], rstd[1 - p][:],
                                       keep["minus_half"][:].broadcast_to([S, G]), ALU.pow)\
                        .then_inc(sem["rstd_ready"], 1)
                wait_alone(pool, sem["r_ready"], n - 1, keep["passed_pool"])
                pool.tensor_tensor(xb[p][:], x[:, bass.ds(n * G, G), :], b["bo"][:].unsqueeze(1).broadcast_to([S, G, E]),
                                   ALU.add).then_inc(sem["xb_ready"], 1)

            stage_in(0, 0)
            stage_in(1, 1)
            over_slots(pool, slot, count)
            pool.wait_ge(sem["var_ready"], count)
            pool.tensor_tensor(rstd[1][:], rstd[1][:], keep["minus_half"][:].broadcast_to([S, G]), ALU.pow).then_inc(sem["rstd_ready"], 1)

        @block.tensor
        def _(pe):
            pe.wait_ge(sem["weights"], n_loads)
            for s in range(K):
                pe.matmul(k_b[:, s, :], rowsT["keyT"][:, s, :], w["wk"][:], start=True, stop=True)
                mm = pe.matmul(v_b[:, s, :], rowsT["valueT"][:, s, :], w["wv"][:], start=True, stop=True)
            mm.then_inc(sem["kv_ready"], 1)

            def turn_x(n, p):
                pe.wait_ge(sem["xin_ready"], n + 1)
                reach(pe, sem["xT_copied"], n)
                for s in range(G):
                    mm = pe.transpose(x_b[:, s, :], xin[p][:, s, :], ident[:])
                mm.then_inc(sem["x_turned"], 1)

            def queries(n, p):
                pe.wait_ge(sem["xT_copied"], n + 1)
                reach(pe, sem["step"], (n - 1) * STEPS + 1)
                for s in range(G):
                    mm = pe.matmul(q_b[:, s, :], xT[p][:, s, :], w["wq"][:], start=True, stop=True)
                mm.then_inc(sem["q_ready"], 1)

            def product(n):
                pe.wait_ge(sem["on_ready"], n + 1)
                reach(pe, sem["oT_copied"], n)
                for s in range(G):
                    mm = pe.transpose(t_b[:, s, :], on[:, s, :], ident[:])
                mm.then_inc(sem["on_turned"], 1)
                pe.wait_ge(sem["oT_copied"], n + 1)
                reach(pe, sem["r_ready"], n)
                for s in range(G):
                    mm = pe.matmul(y_b[:, s, :], oT[:, s, :], w["wo"][:], start=True, stop=True)
                mm.then_inc(sem["y_ready"], 1)

            def slot(n, p):
                if within(n, 1, count):
                    turn_x(n + 1, 1 - p)
                    queries(n + 1, 1 - p)
                if within(n, -1, count):
                    product(n - 1)

            turn_x(0, 0)
            queries(0, 0)
            over_slots(pe, slot, count)
            product(count - 1)

        @block.scalar
        def _(act):
            def copy_xT(n, p):
                act.wait_ge(sem["x_turned"], n + 1)
                reach(act, sem["q_ready"], n - 1)
                act.activation(xT[p][:], x_b[:], ACT.Copy).then_inc(sem["xT_copied"], 1)

            def copy_oT(n):
                act.wait_ge(sem["on_turned"], n + 1)
                reach(act, sem["y_ready"], n)
                act.activation(oT[:], t_b[:], ACT.Copy).then_inc(sem["oT_copied"], 1)

            def slot(n, p):
                if within(n, 1, count):
                    copy_xT(n + 1, 1 - p)
                if within(n, -1, count):
                    copy_oT(n - 1)
                act.wait_ge(sem["gated"], n + 1)
                act.activation(gx[p][:], gx[p][:], ACT.Sigmoid).then_inc(sem["sigmoid_ready"], 1)

            copy_xT(0, 0)
            over_slots(act, slot, count)
            copy_oT(count - 1)

        @block.vector
        def _(dve):
            dve.wait_ge(sem["weights"], n_loads)
            dve.wait_ge(sem["kv_ready"], 1)
            dve.memset(half[:], 0.5)
            dve.tensor_tensor(kk[:], k_b[:], b["bk"][:].unsqueeze(1).broadcast_to([S, K, E]), ALU.add)
            for s in range(G):
                i = dve.tensor_tensor(vv[:, s], v_b[:], b["bv"][:].unsqueeze(1).broadcast_to([S, K, E]), ALU.add)
            i.then_inc(sem["setup"], 1)
            dve.wait_ge(sem["setup"], 1)

            def chain(n, k, ins):
                ins.then_inc(sem["step"], 1)
                dve.wait_ge(sem["step"], n * STEPS + k)

            def attend(n, p):
                dve.wait_ge(sem["q_ready"], n + 1)
                chain(n, 1, dve.tensor_tensor(q[:], q_b[:], b["bq"][:].unsqueeze(1).broadcast_to([S, G, E]), ALU.add))
                for s in range(G):
                    i = dve.scalar_tensor_tensor(out=prod[p][:, s], in0=kk[:], scalar=D ** -0.5,
                                                 in1=q[:, s, :].unsqueeze(1).broadcast_to([S, K, E]),
                                                 op0=ALU.mult, op1=ALU.mult)
                chain(n, 2, i)
                reach(dve, sem["weighted"], n)
                chain(n, 3, dve.tensor_reduce(logit[:], prod[p][:].rearrange("p g k (h e) -> p (g k h) e", h=HEADS),
                                              AX.X, ALU.add))
                dve.tensor_scalar(logit[:], logit[:], 0.0, None, ALU.max).then_inc(sem["logits_ready"], 1)

            def outputs(n, p):
                dve.wait_ge(sem["weighted"], n + 1)
                reach(dve, sem["on_ready"], n - 1)
                dve.tensor_reduce(o[p][:], prod[p][:].rearrange("p g k e -> p g e k"), AX.X, ALU.add)\
                   .then_inc(sem["summed"], 1)
                dve.wait_ge(sem["summed"], n + 1)
                dve.tensor_tensor(gx[p][:], o[p][:], b["gain"][:].unsqueeze(1).broadcast_to([S, G, E]), ALU.mult)\
                   .then_inc(sem["gated"], 1)
                out_chain(n, 1, dve.tensor_tensor(sq[:], o[p][:], o[p][:], ALU.mult))
                out_chain(n, 2, dve.tensor_reduce(ms[p][:], sq[:], AX.X, ALU.add))
                dve.tensor_scalar(ms[p][:], ms[p][:], 1.0 / E, None, ALU.mult).then_inc(sem["meansq_ready"], 1)

            def out_chain(n, k, ins):
                ins.then_inc(sem["out_step"], 1)
                dve.wait_ge(sem["out_step"], n * 2 + k)

            def gated_norm(n, p):
                dve.wait_ge(sem["rms_ready"], n + 1)
                dve.wait_ge(sem["sigmoid_ready"], n + 1)
                gate_chain(n, 1, dve.tensor_scalar(ms[p][:], ms[p][:], 1e-8, None, ALU.add))
                gate_chain(n, 2, dve.reciprocal(ms[p][:], ms[p][:]))
                for s in range(G):
                    i = dve.scalar_tensor_tensor(out=o[p][:, s, :], in0=o[p][:, s, :], scalar=ms[p][:, s:s + 1],
                                                 in1=b["weight"][:], op0=ALU.mult, op1=ALU.mult)
                gate_chain(n, 3, i)
                reach(dve, sem["on_turned"], n)
                dve.tensor_tensor(on[:], o[p][:], gx[p][:], ALU.mult).then_inc(sem["on_ready"], 1)

            def gate_chain(n, k, ins):
                ins.then_inc(sem["gate_step"], 1)
                dve.wait_ge(sem["gate_step"], n * 3 + k)

            def residual(n, p):
                dve.wait_ge(sem["y_ready"], n + 1)
                dve.wait_ge(sem["xb_ready"], n + 1)
                dve.tensor_tensor(r[p][:], y_b[:], xb[p][:], ALU.add).then_inc(sem["r_ready"], 1)
                dve.wait_ge(sem["r_ready"], n + 1)
                for s in range(G):
                    i = dve.bn_stats(stats[:, s, :], r[p][:, s, :])
                res_chain(n, 1, i)
                dve.sem_inc(keep["passed"], 1)
                for s in range(G):
                    i = dve.bn_aggr(mv[p][:, s, :], stats[:, s, :])
                res_chain(n, 2, i)
                dve.tensor_scalar(rstd[p][:], mv[p][:, :, 1], LN_EPS, None, ALU.add).then_inc(sem["var_ready"], 1)

            def res_chain(n, k, ins):
                ins.then_inc(sem["res_step"], 1)
                dve.wait_ge(sem["res_step"], n * 2 + k)

            def norm(n, p):
                dve.wait_ge(sem["rstd_ready"], n + 1)
                for s in range(G):
                    i = dve.tensor_scalar(x[:, n * G + s, :], r[p][:, s, :], mv[p][:, s, 0:1], rstd[p][:, s:s + 1],
                                          ALU.subtract, ALU.mult)
                i.then_inc(sem["normed"], 1)

            def slot(n, p):
                attend(n, p)
                if within(n, -1, count):
                    gated_norm(n - 1, 1 - p)
                if within(n, -2, count):
                    norm(n - 2, p)
                outputs(n, p)
                if within(n, -1, count):
                    residual(n - 1, 1 - p)

            over_slots(dve, slot, count)
            gated_norm(count - 1, 1)
            norm(count - 2, 0)
            residual(count - 1, 1)
            norm(count - 1, 1)

    clear(nc, sem)


def one_head_attention(nc, d, keep, tag):
    count = SEQS
    x, ident = keep["x"], keep["ident"]
    with ExitStack() as ctx:
        sb, bank, sems = tensors(ctx, nc, tag)
        wq, wk, wv = sb("wq", [E, E]), sb("wk", [C, E]), sb("wv", [C, E])
        qb, kb, vb = sb("qb", [E, 1]), sb("kb", [E, 1]), sb("vb", [S, E])
        loads = [(wq[:], d[tag + "_wq"]), (wk[:], d[tag + "_wk"]), (wv[:], d[tag + "_wv"]),
                 (qb[:], d[tag + "_bq"]), (kb[:], d[tag + "_bk"]), (vb[:], d[tag + "_bv"])]
        xin = [sb(f"xin{i}", [S, E]) for i in range(2)]
        cin = [sb(f"cin{i}", [C, CTX]) for i in range(2)]
        xb = [sb(f"xb{i}", [S, E]) for i in range(2)]
        xT = [sb(f"xT{i}", [E, S]) for i in range(2)]
        qT = [sb(f"qT{i}", [E, S]) for i in range(2)]
        kT = [sb(f"kT{i}", [E, CTX]) for i in range(2)]
        v = [sb(f"v{i}", [CTX, E]) for i in range(2)]
        negmax = [sb(f"negmax{i}", [S, 1]) for i in range(2)]
        prob = [sb(f"prob{i}", [S, CTX]) for i in range(2)]
        total = [sb(f"total{i}", [S, 1]) for i in range(2)]
        pT = [sb(f"pT{i}", [CTX, S]) for i in range(2)]
        r = [sb(f"r{i}", [S, E]) for i in range(2)]
        stats = sb("stats", [S, 6])
        mv = [sb(f"mv{i}", [S, 2]) for i in range(2)]
        rstd = [sb(f"rstd{i}", [S, 1]) for i in range(2)]
        x_b, q_b, k_b, v_b, s_b, t_b, o_b = (bank(n, [S, S]) for n in ("x", "q", "k", "v", "s", "t", "o"))
        sem = sems("weights xin_ready x_turned xT_copied ctx_loaded0 ctx_loaded1 q_ready q_copied k_ready k_copied "
                   "v_ready v_copied scores_ready max_ready probs_ready probs_turned pT_copied o_ready inv_ready "
                   "xb_ready r_ready step var_ready rstd_ready normed")
        n_loads = 16 * len(loads)
        block = ctx.enter_context(nc.Block())

        @block.sync
        def _(sp):
            load_all(sp, loads, sem["weights"])

            def slot(n, p):
                reach(sp, sem["v_ready"], n - 1)
                sp.dma_start(cin[p][:], d["ctxT"][n]).then_inc(sem[f"ctx_loaded{p}"], 16)

            over_slots(sp, slot, count)

        @block.gpsimd
        def _(pool):
            pool.wait_ge(sem["weights"], n_loads)

            def stage_in(n, p):
                reach(pool, sem["x_turned"], n - 1)
                pool.tensor_copy(xin[p][:], x[:, n, :]).then_inc(sem["xin_ready"], 1)

            def root(n, p):
                pool.wait_ge(sem["var_ready"], n + 1)
                pool.tensor_tensor(rstd[p][:], rstd[p][:], keep["minus_half"][:], ALU.pow)\
                    .then_inc(sem["rstd_ready"], 1)

            def slot(n, p):
                if within(n, 2, count):
                    stage_in(n + 2, p)
                reach(pool, sem["r_ready"], n - 1)
                pool.tensor_tensor(xb[p][:], x[:, n, :], vb[:], ALU.add).then_inc(sem["xb_ready"], 1)
                if within(n, -2, count):
                    root(n - 2, p)

            stage_in(0, 0)
            stage_in(1, 1)
            over_slots(pool, slot, count)
            root(count - 2, 0)
            root(count - 1, 1)

        @block.tensor
        def _(pe):
            pe.wait_ge(sem["weights"], n_loads)

            def turn_x(n, p):
                pe.wait_ge(sem["xin_ready"], n + 1)
                reach(pe, sem["xT_copied"], n)
                pe.transpose(x_b[:], xin[p][:], ident[:]).then_inc(sem["x_turned"], 1)

            def project(n, p):
                pe.wait_ge(sem["xT_copied"], n + 1)
                reach(pe, sem["q_copied"], n)
                pe.matmul(q_b[:], wq[:], xT[p][:], start=True, stop=True).then_inc(sem["q_ready"], 1)
                pe.wait_ge(sem[f"ctx_loaded{p}"], (n - p) * 8 + 16)
                reach(pe, sem["k_copied"], n)
                pe.matmul(k_b[:, 0:CTX], wk[:], cin[p][:], start=True, stop=True).then_inc(sem["k_ready"], 1)
                reach(pe, sem["v_copied"], n)
                pe.matmul(v_b[0:CTX, :], cin[p][:], wv[:], start=True, stop=True).then_inc(sem["v_ready"], 1)

            def score(n, p):
                pe.wait_ge(sem["q_copied"], n + 1)
                pe.wait_ge(sem["k_copied"], n + 1)
                reach(pe, sem["probs_ready"], n)
                pe.matmul(s_b[:, 0:CTX], qT[p][:], kT[p][:], start=True, stop=True).then_inc(sem["scores_ready"], 1)

            def turn_probs(n, p):
                pe.wait_ge(sem["probs_ready"], n + 1)
                reach(pe, sem["pT_copied"], n)
                pe.transpose(t_b[0:CTX, :], prob[p][:], ident[:]).then_inc(sem["probs_turned"], 1)

            def weigh(n, p):
                pe.wait_ge(sem["pT_copied"], n + 1)
                pe.wait_ge(sem["v_copied"], n + 1)
                reach(pe, sem["r_ready"], n)
                pe.matmul(o_b[:], pT[p][:], v[p][:], start=True, stop=True).then_inc(sem["o_ready"], 1)

            def slot(n, p):
                score(n, p)
                if within(n, 2, count):
                    turn_x(n + 2, p)
                if within(n, -1, count):
                    weigh(n - 1, 1 - p)
                if within(n, 1, count):
                    project(n + 1, 1 - p)
                turn_probs(n, p)

            turn_x(0, 0)
            project(0, 0)
            turn_x(1, 1)
            over_slots(pe, slot, count)
            weigh(count - 1, 1)

        @block.scalar
        def _(act):
            act.wait_ge(sem["weights"], n_loads)

            def copy_xT(n, p):
                act.wait_ge(sem["x_turned"], n + 1)
                reach(act, sem["q_ready"], n - 1)
                act.activation(xT[p][:], x_b[:], ACT.Copy).then_inc(sem["xT_copied"], 1)

            def copy_qkv(n, p):
                act.wait_ge(sem["q_ready"], n + 1)
                reach(act, sem["scores_ready"], n - 1)
                act.activation(qT[p][:], q_b[:], ACT.Identity, bias=qb[:, 0:1]).then_inc(sem["q_copied"], 1)
                act.wait_ge(sem["k_ready"], n + 1)
                act.activation(kT[p][:], k_b[:, 0:CTX], ACT.Identity, bias=kb[:, 0:1]).then_inc(sem["k_copied"], 1)
                act.wait_ge(sem["v_ready"], n + 1)
                reach(act, sem["o_ready"], n - 1)
                act.activation(v[p][:], v_b[0:CTX, :], ACT.Copy).then_inc(sem["v_copied"], 1)

            def slot(n, p):
                act.wait_ge(sem["max_ready"], n + 1)
                reach(act, sem["probs_turned"], n - 1)
                reach(act, sem["r_ready"], n - 1)
                act.activation(prob[p][:], s_b[:, 0:CTX], ACT.Exp, bias=negmax[p][:, 0:1],
                               accum_out=total[p][:, 0:1]).then_inc(sem["probs_ready"], 1)
                if within(n, 2, count):
                    copy_xT(n + 2, p)
                if within(n, 1, count):
                    copy_qkv(n + 1, 1 - p)

            copy_xT(0, 0)
            copy_qkv(0, 0)
            copy_xT(1, 1)
            over_slots(act, slot, count)

        @block.vector
        def _(dve):
            dve.wait_ge(sem["weights"], n_loads)

            def maximum(n, p):
                dve.wait_ge(sem["scores_ready"], n + 1)
                reach(dve, sem["probs_ready"], n - 1)
                dve.tensor_reduce(negmax[p][:], s_b[:, 0:CTX], AX.X, ALU.max, negate=True)\
                   .then_inc(sem["max_ready"], 1)

            def copy_pT(n, p):
                dve.wait_ge(sem["probs_turned"], n + 1)
                reach(dve, sem["o_ready"], n - 1)
                dve.tensor_copy(pT[p][:], t_b[0:CTX, :]).then_inc(sem["pT_copied"], 1)

            def residual(n, p):
                dve.wait_ge(sem["probs_ready"], n + 1)
                dve.reciprocal(total[p][:], total[p][:]).then_inc(sem["inv_ready"], 1)
                dve.wait_ge(sem["inv_ready"], n + 1)
                dve.wait_ge(sem["o_ready"], n + 1)
                dve.wait_ge(sem["xb_ready"], n + 1)
                dve.scalar_tensor_tensor(out=r[p][:], in0=o_b[:], scalar=total[p][:, 0:1], in1=xb[p][:],
                                         op0=ALU.mult, op1=ALU.add).then_inc(sem["r_ready"], 1)
                dve.wait_ge(sem["r_ready"], n + 1)
                dve.bn_stats(stats[:], r[p][:]).then_inc(sem["step"], 1)
                wait_alone(dve, sem["step"], n * 2 + 1, keep["passed"])
                dve.bn_aggr(mv[p][:], stats[:]).then_inc(sem["step"], 1)
                dve.wait_ge(sem["step"], n * 2 + 2)
                dve.tensor_scalar(rstd[p][:], mv[p][:, 1:2], LN_EPS, None, ALU.add).then_inc(sem["var_ready"], 1)

            def norm(n, p):
                dve.wait_ge(sem["rstd_ready"], n + 1)
                dve.tensor_scalar(x[:, n, :], r[p][:], mv[p][:, 0:1], rstd[p][:, 0:1], ALU.subtract, ALU.mult)\
                   .then_inc(sem["normed"], 1)

            def slot(n, p):
                maximum(n, p)
                if within(n, -2, count):
                    norm(n - 2, p)
                if within(n, -1, count):
                    residual(n - 1, 1 - p)
                copy_pT(n, p)

            over_slots(dve, slot, count)
            norm(count - 2, 0)
            residual(count - 1, 1)
            norm(count - 1, 1)

    clear(nc, sem)


def linear(nc, d, keep, tag):
    count = SEQS
    x, ident = keep["x"], keep["ident"]
    with ExitStack() as ctx:
        sb, bank, sems = tensors(ctx, nc, tag)
        w, factor, bias = sb("w", [E, E]), sb("factor", [S, E]), sb("bias", [S, E])
        loads = [(w[:], d[tag + "_w"]), (factor[:], d[tag + "_scale"]), (bias[:], d[tag + "_bias"])]
        xin = [sb(f"xin{i}", [S, E]) for i in range(2)]
        xb = [sb(f"xb{i}", [S, E]) for i in range(2)]
        xT = [sb(f"xT{i}", [E, S]) for i in range(2)]
        y = sb("y", [S, E])
        r = [sb(f"r{i}", [S, E]) for i in range(2)]
        stats = sb("stats", [S, 6])
        mv = [sb(f"mv{i}", [S, 2]) for i in range(2)]
        rstd = [sb(f"rstd{i}", [S, 1]) for i in range(2)]
        x_b = [bank(f"x{i}", [S, S]) for i in range(2)]
        y_b = [bank(f"y{i}", [S, S]) for i in range(2)]
        sem = sems("weights setup xin_ready x_turned xT_copied y_ready scaled xb_ready r_ready step var_ready "
                   "rstd_ready normed")
        block = ctx.enter_context(nc.Block())

        @block.sync
        def _(sp):
            load_all(sp, loads, sem["weights"])

        @block.gpsimd
        def _(pool):
            pool.wait_ge(sem["weights"], 48)

            def stage_in(n, p):
                reach(pool, sem["x_turned"], n - 1)
                pool.tensor_copy(xin[p][:], x[:, n, :]).then_inc(sem["xin_ready"], 1)

            def root(n, p):
                pool.wait_ge(sem["var_ready"], n + 1)
                pool.tensor_tensor(rstd[p][:], rstd[p][:], keep["minus_half"][:], ALU.pow)\
                    .then_inc(sem["rstd_ready"], 1)

            def slot(n, p):
                reach(pool, sem["r_ready"], n - 1)
                pool.tensor_tensor(xb[p][:], x[:, n, :], bias[:], ALU.add).then_inc(sem["xb_ready"], 1)
                if within(n, 2, count):
                    stage_in(n + 2, p)
                if within(n, -1, count):
                    root(n - 1, 1 - p)

            stage_in(0, 0)
            stage_in(1, 1)
            over_slots(pool, slot, count)
            root(count - 1, 1)

        @block.tensor
        def _(pe):
            pe.wait_ge(sem["weights"], 48)

            def turn_x(n, p):
                pe.wait_ge(sem["xin_ready"], n + 1)
                reach(pe, sem["xT_copied"], n - 1)
                pe.transpose(x_b[p][:], xin[p][:], ident[:]).then_inc(sem["x_turned"], 1)

            def slot(n, p):
                if within(n, 1, count):
                    turn_x(n + 1, 1 - p)
                pe.wait_ge(sem["xT_copied"], n + 1)
                reach(pe, sem["scaled"], n - 1)
                pe.matmul(y_b[p][:], xT[p][:], w[:], start=True, stop=True).then_inc(sem["y_ready"], 1)

            turn_x(0, 0)
            over_slots(pe, slot, count)

        @block.scalar
        def _(act):
            def slot(n, p):
                act.wait_ge(sem["x_turned"], n + 1)
                reach(act, sem["y_ready"], n - 1)
                act.activation(xT[p][:], x_b[p][:], ACT.Copy).then_inc(sem["xT_copied"], 1)

            over_slots(act, slot, count)

        @block.vector
        def _(dve):
            dve.wait_ge(sem["weights"], 48)
            dve.tensor_scalar(factor[:], factor[:], 1.0 / 127.0, None, ALU.mult).then_inc(sem["setup"], 1)
            dve.wait_ge(sem["setup"], 1)

            def residual(n, p):
                dve.wait_ge(sem["y_ready"], n + 1)
                dve.tensor_tensor(y[:], y_b[p][:], factor[:], ALU.mult).then_inc(sem["scaled"], 1)
                dve.wait_ge(sem["scaled"], n + 1)
                dve.wait_ge(sem["xb_ready"], n + 1)
                dve.tensor_tensor(r[p][:], y[:], xb[p][:], ALU.add).then_inc(sem["r_ready"], 1)
                dve.wait_ge(sem["r_ready"], n + 1)
                dve.bn_stats(stats[:], r[p][:]).then_inc(sem["step"], 1)
                wait_alone(dve, sem["step"], n * 2 + 1, keep["passed"])
                dve.bn_aggr(mv[p][:], stats[:]).then_inc(sem["step"], 1)
                dve.wait_ge(sem["step"], n * 2 + 2)
                dve.tensor_scalar(rstd[p][:], mv[p][:, 1:2], LN_EPS, None, ALU.add).then_inc(sem["var_ready"], 1)

            def norm(n, p):
                dve.wait_ge(sem["rstd_ready"], n + 1)
                dve.tensor_scalar(x[:, n, :], r[p][:], mv[p][:, 0:1], rstd[p][:, 0:1], ALU.subtract, ALU.mult)\
                   .then_inc(sem["normed"], 1)

            def slot(n, p):
                residual(n, p)
                if within(n, -1, count):
                    norm(n - 1, 1 - p)

            over_slots(dve, slot, count)
            norm(count - 1, 1)

    clear(nc, sem)


def compress_blocks(nc, d, keep, tag):
    G, T, B, N = 4, 4 * S, 16, 8
    groups = SEQS // G
    x, ident = keep["x"], keep["ident"]
    with ExitStack() as ctx:
        sb, bank, sems = tensors(ctx, nc, tag)
        w = {t: sb("w" + t, [E, E]) for t in "kv"}
        wc = {t: sb("wc" + t, [E, B, E]) for t in "kv"}
        loads = [(w[t][:], d[f"l3_attn_flat{t}"]) for t in "kv"]
        loads += [(wc[t][:], d[f"l3_attn_wc{t}"]) for t in "kv"]
        xin = [sb(f"xin{i}", [S, G, E]) for i in range(2)]
        xT = [sb(f"xT{i}", [E, T]) for i in range(2)]
        full = {t: sb(t, [E, SEQS * S]) for t in "kv"}
        x_b = bank("x", [E, T])
        f_b = {t: bank("f" + t, [E, T]) for t in "kv"}
        c_b = {t: bank("c" + t, [E, SEQS * N]) for t in "kv"}
        sem = sems("weights xin_ready x_turned xT_copied full_ready k_copied v_copied k_compressed v_compressed "
                   "stored")
        block = ctx.enter_context(nc.Block())

        @block.sync
        def _(sp):
            load_all(sp, loads, sem["weights"])

        @block.gpsimd
        def _(pool):
            def slot(g, p):
                reach(pool, sem["x_turned"], g - 1)
                pool.tensor_copy(xin[p][:], x[:, bass.ds(g * G, G), :]).then_inc(sem["xin_ready"], 1)

            over_slots(pool, slot, groups)

        @block.tensor
        def _(pe):
            pe.wait_ge(sem["weights"], 64)

            def turn_x(g, p):
                pe.wait_ge(sem["xin_ready"], g + 1)
                reach(pe, sem["xT_copied"], g)
                for s in range(G):
                    mm = pe.transpose(x_b[:, s * S:(s + 1) * S], xin[p][:, s, :], ident[:])
                mm.then_inc(sem["x_turned"], 1)

            def slot(g, p):
                if within(g, 1, groups):
                    turn_x(g + 1, 1 - p)
                pe.wait_ge(sem["xT_copied"], g + 1)
                for t in "kv":
                    reach(pe, sem[t + "_copied"], g)
                    pe.matmul(f_b[t][:], w[t][:], xT[p][:], start=True, stop=True).then_inc(sem["full_ready"], 1)

            turn_x(0, 0)
            over_slots(pe, slot, groups)
            for t in "kv":
                pe.wait_ge(sem[t + "_copied"], groups)
                for b in range(B):
                    mm = pe.matmul(c_b[t][:], wc[t][:, b, :], full[t][:].rearrange("p (n b) -> p b n", b=B)[:, b, :],
                                   start=(b == 0), stop=(b == B - 1))
                mm.then_inc(sem[t + "_compressed"], 1)

        @block.scalar
        def _(act):
            def copy_xT(g, p):
                act.wait_ge(sem["x_turned"], g + 1)
                reach(act, sem["full_ready"], (g - 1) * 2)
                act.activation(xT[p][:], x_b[:], ACT.Copy).then_inc(sem["xT_copied"], 1)

            def slot(g, p):
                if within(g, 1, groups):
                    copy_xT(g + 1, 1 - p)
                act.wait_ge(sem["full_ready"], g * 2 + 1)
                act.activation(full["k"][:, bass.ds(g * T, T)], f_b["k"][:], ACT.Copy).then_inc(sem["k_copied"], 1)

            copy_xT(0, 0)
            over_slots(act, slot, groups)

        @block.vector
        def _(dve):
            def slot(g, p):
                dve.wait_ge(sem["full_ready"], g * 2 + 2)
                dve.tensor_copy(full["v"][:, bass.ds(g * T, T)], f_b["v"][:]).then_inc(sem["v_copied"], 1)

            over_slots(dve, slot, groups)
            for t in "kv":
                dve.wait_ge(sem[t + "_compressed"], 1)
                dve.tensor_copy(keep[t + "c"][:], c_b[t][:].rearrange("p (s n) -> p s n", s=SEQS))\
                   .then_inc(sem["stored"], 1)

    clear(nc, sem)


def sparse_attention(nc, d, keep, tag):
    count, N, D = SEQS, 8, 8
    x, ident = keep["x"], keep["ident"]
    with ExitStack() as ctx:
        sb, bank, sems = tensors(ctx, nc, tag)
        wqkv, wo = sb("wqkv", [E, 3, E]), sb("wo", [E, E])
        bg = sb("bg", [S, 3])
        own = sb("own", [E, HEADS])
        ok, low = sb("ok", [S, N]), sb("low", [S, N])
        some = sb("some", [S, 1])
        before = sb("before", [S, N, N])
        place = sb("place", [S, N])
        kmask, vmask = sb("kmask", [E, 4, 4]), sb("vmask", [S, 4, E])
        kcd = sb("kcd", [E, HEADS * N + 3])
        m_f = {t: sb(t + "_f", [S, S]) for t in ("causal", "band")}
        blocks_f = sb("blocks_f", [S, 4, 4 * S])
        loads = [(wo[:], d["l3_attn_wo"]), (kcd[:, HEADS * N:HEADS * N + 3], d["l3_attn_wg"]), (bg[:], d["l3_attn_bg"]),
                 (own[:], d["own"]), (ok[:], d["block_ok"]), (low[:], d["block_low"]), (some[:], d["block_some"]),
                 (before[:], d["l1_moe_before"]), (place[:], d["block_place"]), (m_f["causal"][:], d["causal"]),
                 (m_f["band"][:], d["band"]), (blocks_f[:], d["blocks"]), (kmask[:], d["kmask8"]),
                 (vmask[:], d["vmask"])]
        loads += [(wqkv[:, t, :], d["l3_attn_flat" + "qkv"[t]]) for t in range(3)]
        mask = {t: sb(t, [S, 4, S], BF16) for t in ("causal", "band")}
        blocks = sb("blocks", [S, 4, 4 * S], BF16)
        zeros = sb("zeros", [S, 2 * S], BF16)
        xin = [sb(f"xin{i}", [S, E]) for i in range(2)]
        xT = [sb(f"xT{i}", [E, S]) for i in range(2)]
        qk = [sb(f"qk{i}", [E, 2, S]) for i in range(2)]
        v = [sb(f"v{i}", [S, E]) for i in range(2)]
        kd = sb("kd", [E, 4, 4, S])
        vd = [sb(f"vd{i}", [S, 4, E]) for i in range(2)]
        vcd = sb("vcd", [E, HEADS, N])
        vcT = [sb(f"vcT{i}", [HEADS * N, E]) for i in range(2)]
        logit, e = sb("logit", [S, HEADS, N]), sb("e", [S, HEADS * N + 3])
        top, gtop = sb("top", [S, HEADS]), sb("gtop", [S, 1])
        more, later, pairs = (sb(name, [S, HEADS, N, N]) for name in ("more", "later", "pairs"))
        ahead = sb("ahead", [S, HEADS, N])
        closed, pc = sb("closed", [S, HEADS, N]), sb("pc", [S, HEADS, N])
        gate = [sb(f"gate{i}", [S, 3]) for i in range(2)]
        pcT = [sb(f"pcT{i}", [HEADS * N, S]) for i in range(2)]
        closedT = [sb(f"closedT{i}", [HEADS * N, S], BF16) for i in range(2)]
        negmax = [sb(f"negmax{i}", [S, 4]) for i in range(2)]
        prob = [sb(f"prob{i}", [S, 4, S]) for i in range(2)]
        sums = [sb(f"sums{i}", [S, 2, HEADS]) for i in range(2)]
        wt, wide = sb("wt", [S, 2, HEADS]), sb("wide", [S, 2, E])
        wT = sb("wT", [E, 2, S])
        pT = [sb(f"pT{i}", [S, 4, S]) for i in range(2)]
        scaled, oT = sb("scaled", [E, 2, S]), sb("oT", [E, S])
        r = [sb(f"r{i}", [S, E]) for i in range(2)]
        stats = sb("stats", [S, 6])
        mv = [sb(f"mv{i}", [S, 2]) for i in range(2)]
        rstd = [sb(f"rstd{i}", [S, 1]) for i in range(2)]
        xb = [sb(f"xb{i}", [S, E]) for i in range(2)]
        score = [bank(f"score{i}", [S, 4, S]) for i in range(2)]
        turned = [bank(f"turned{i}", [S, 4, S]) for i in range(2)]
        out_b, qkv_b = bank("out", [E, 4, S]), bank("qkv", [E, 4, S])
        misc, comp = bank("misc", [S, 512]), bank("comp", [S, 512])
        sem = sems("weights setup xin_ready x_turned xT_copied qkv_ready qk_copied v_copied kcd_ready vcd_ready "
                   "cs_ready logits_ready e_ready e_exp compared later_ready pairs_ready comp_ready comp_turned comp_copied "
                   "kd_ready vd_ready scores_ready max_ready probs_ready probs_turned pT_copied pv_done wt_step "
                   "wt_ready wt_turned wT_copied out_step oT_ready y_ready xb_ready r_ready step comp_step var_ready "
                   "rstd_ready normed")
        n_loads = 16 * len(loads)
        block = ctx.enter_context(nc.Block())

        def unit_after(n, p, w, by):
            if w + by < 8:
                return n, p, w + by
            return (n + 1, 1 - p, w + by - 8) if within(n, 1, count) else None

        def at_most(value, ahead_by):
            return min(value + ahead_by, count) if isinstance(value, int) else value + ahead_by

        @block.sync
        def _(sp):
            load_all(sp, loads, sem["weights"])

        @block.gpsimd
        def _(pool):
            pool.wait_ge(sem["weights"], n_loads)

            def stage_in(n, p):
                reach(pool, sem["x_turned"], n - 1)
                pool.tensor_copy(xin[p][:], x[:, n, :]).then_inc(sem["xin_ready"], 1)

            def diagonal(n, t):
                if t == "k":
                    out_t = kcd[:, 0:HEADS * N].rearrange("p (h n) -> p h n", h=HEADS)
                    reach(pool, sem["cs_ready"], n)
                else:
                    out_t = vcd[:]
                    reach(pool, sem["comp_turned"], n)
                pool.tensor_tensor(out_t, keep[t + "c"][:, n, :].unsqueeze(1).broadcast_to([E, HEADS, N]),
                                   copy_bcast(own[:], N), ALU.mult).then_inc(sem[t + "cd_ready"], 1)

            def compare(n):
                shape = [S, HEADS, N, N]
                pool.wait_ge(sem["compared"], n + 1)
                pool.tensor_tensor(later[:], more[:],
                                   before[:].rearrange("p a b -> p b a").unsqueeze(1).broadcast_to(shape),
                                   ALU.mult).then_inc(sem["later_ready"], 1)
                pool.wait_ge(sem["later_ready"], n + 1)
                reach(pool, sem["comp_ready"], n)
                pool.tensor_tensor(pairs[:], later[:], later[:].rearrange("p h a b -> p h b a"), ALU.subtract)\
                    .then_inc(sem["pairs_ready"], 1)

            def root(n, p):
                pool.wait_ge(sem["var_ready"], n + 1)
                pool.tensor_tensor(rstd[p][:], rstd[p][:], keep["minus_half"][:], ALU.pow)\
                    .then_inc(sem["rstd_ready"], 1)

            def slot(n, p):
                if within(n, 2, count):
                    stage_in(n + 2, p)
                if within(n, 1, count):
                    diagonal(n + 1, "v")
                    compare(n + 1)
                if within(n, 2, count):
                    diagonal(n + 2, "k")
                if within(n, -1, count):
                    root(n - 1, 1 - p)
                reach(pool, sem["r_ready"], n - 1)
                pool.tensor_copy(xb[p][:], x[:, n, :]).then_inc(sem["xb_ready"], 1)

            stage_in(0, 0)
            stage_in(1, 1)
            diagonal(0, "k")
            diagonal(0, "v")
            compare(0)
            diagonal(1, "k")
            over_slots(pool, slot, count)
            root(count - 1, 1)

        @block.tensor
        def _(pe):
            pe.wait_ge(sem["weights"], n_loads)
            pe.wait_ge(sem["setup"], 1)

            def turn_x(n, p):
                pe.wait_ge(sem["xin_ready"], n + 1)
                reach(pe, sem["xT_copied"], n)
                reach(pe, sem["r_ready"], n - 2)
                pe.transpose(misc[:, 0:S], xin[p][:], ident[:]).then_inc(sem["x_turned"], 1)

            def project(n, p):
                pe.wait_ge(sem["xT_copied"], n + 1)
                reach(pe, sem["v_copied"], n)
                for t in range(2):
                    pe.matmul(qkv_b[:, t, :], wqkv[:, t, :], xT[p][:], start=True, stop=True)
                pe.matmul(qkv_b[:, 2, :], xT[p][:], wqkv[:, 2, :], start=True, stop=True).then_inc(sem["qkv_ready"], 1)

            def block_scores(n, p):
                pe.wait_ge(sem["qk_copied"], n + 1)
                pe.wait_ge(sem["kcd_ready"], n + 1)
                reach(pe, sem["comp_copied"], n)
                pe.matmul(comp[:, 0:HEADS * N + 3], qk[p][:, 0, :], kcd[:], start=True, stop=True)\
                    .then_inc(sem["cs_ready"], 1)

            def turn_comp(n):
                pe.wait_ge(sem["vcd_ready"], n + 1)
                pe.wait_ge(sem["comp_ready"], n + 1)
                pe.transpose(comp[:, 0:S], pc[:].rearrange("p h n -> p (h n)"), ident[:])
                pe.transpose(comp[:, S:2 * S], closed[:].rearrange("p h n -> p (h n)"), ident[:])
                pe.transpose(comp[:, 2 * S:3 * S], vcd[:].rearrange("p h n -> p (h n)"), ident[:])\
                    .then_inc(sem["comp_turned"], 1)

            def scores(n, p, w):
                c, b = w // 2, w % 2
                if w == 0:
                    pe.wait_ge(sem["qk_copied"], n + 1)
                    pe.wait_ge(sem["comp_copied"], n + 1)
                if b == 0:
                    pe.wait_ge(sem["kd_ready"], n * 4 + c + 1)
                reach(pe, sem["probs_ready"], n * 8 + w - 1)
                pe.matmul(score[b][:], qk[p][:, 0, :], kd[:, c, :, :], start=True, stop=False, skip_group_check=True)
                if b == 0:
                    pe.matmul(score[b][:], closedT[p][:], blocks[:, c, :], start=False, stop=False,
                              skip_group_check=True)
                pe.matmul(score[b][:], keep["ident_bf"][:], mask["band" if b else "causal"][:], start=False,
                          stop=True, skip_group_check=True).then_inc(sem["scores_ready"], 1)

            def turn_probs(n, p, w):
                u = n * 8 + w
                pe.wait_ge(sem["probs_ready"], u + 1)
                reach(pe, sem["pT_copied"], u - 1)
                for j in range(4):
                    mm = pe.transpose(turned[w % 2][:, j, :], prob[w % 2][:, j, :], ident[:])
                mm.then_inc(sem["probs_turned"], 1)

            def weigh(n, p, w):
                c, b = w // 2, w % 2
                pe.wait_ge(sem["pT_copied"], n * 8 + w + 1)
                if w == 0:
                    pe.wait_ge(sem["vd_ready"], n + 1)
                    reach(pe, sem["out_step"], n * 2)
                    pe.matmul(out_b[:, 0:2, :], zeros[:, 0:S], zeros[:], start=True, stop=False,
                              skip_group_check=True)
                    pe.matmul(out_b[:, 2, :], vcT[p][:], pcT[p][:], start=True, stop=True, skip_group_check=True)
                for j in range(4):
                    mm = pe.matmul(out_b[32 * j:32 * j + 32, b, :], vd[p][:, c, 32 * j:32 * j + 32],
                                   pT[b][:, j, :], start=False, stop=c == 3, tile_position=(0, 32 * j),
                                   skip_group_check=True)
                mm.then_inc(sem["pv_done"], 1)

            def turn_weights(n):
                pe.wait_ge(sem["wt_ready"], n + 1)
                reach(pe, sem["r_ready"], n)
                pe.wait_ge(sem["xT_copied"], at_most(n, 3))
                for b in range(2):
                    mm = pe.transpose(misc[:, b * S:(b + 1) * S], wide[:, b, :], ident[:])
                mm.then_inc(sem["wt_turned"], 1)

            def out_product(n):
                pe.wait_ge(sem["wT_copied"], n + 1)
                pe.wait_ge(sem["oT_ready"], n + 1)
                pe.matmul(misc[:, 0:E], oT[:], wo[:], start=True, stop=True).then_inc(sem["y_ready"], 1)

            def step(n, p, w):
                unit, nxt, next2 = unit_after(n, p, w, 2), within(n, 1, count), within(n, 2, count)
                turn_probs(n, p, w)
                if unit:
                    scores(*unit)
                if w == 5 and nxt:
                    turn_comp(n + 1)
                if w == 3 and within(n, -1, count):
                    out_product(n - 1)
                if w == 4 and next2:
                    turn_x(n + 2, p)
                if w == 5 and next2:
                    project(n + 2, p)
                if w == 6 and next2:
                    block_scores(n + 2, p)
                if w == 7:
                    turn_weights(n)
                if w > 0:
                    weigh(n, p, w - 1)
                elif within(n, -1, count):
                    weigh(n - 1, 1 - p, 7)

            def slot(n, p):
                for w in range(8):
                    step(n, p, w)

            turn_x(0, 0)
            turn_x(1, 1)
            project(0, 0)
            block_scores(0, 0)
            project(1, 1)
            turn_comp(0)
            block_scores(1, 1)
            scores(0, 0, 0)
            scores(0, 0, 1)
            over_slots(pe, slot, count)
            weigh(count - 1, 1, 7)
            out_product(count - 1)

        @block.scalar
        def _(act):
            act.wait_ge(sem["weights"], n_loads)

            def copy_xT(n, p):
                act.wait_ge(sem["x_turned"], n + 1)
                reach(act, sem["qkv_ready"], n - 1)
                act.activation(xT[p][:], misc[:, 0:S], ACT.Copy).then_inc(sem["xT_copied"], 1)

            def copy_qkv(n, p):
                act.wait_ge(sem["qkv_ready"], n + 1)
                reach(act, sem["scores_ready"], (n - 1) * 8)
                reach(act, sem["kd_ready"], (n - 1) * 4)
                reach(act, sem["vd_ready"], n - 1)
                act.activation(qk[p][:], qkv_b[:, 0:2, :], ACT.Copy).then_inc(sem["qk_copied"], 1)
                act.activation(v[p][:], qkv_b[:, 2, :], ACT.Copy).then_inc(sem["v_copied"], 1)

            def block_exp(n):
                act.wait_ge(sem["e_ready"], n + 1)
                act.activation(e[:], e[:], ACT.Exp).then_inc(sem["e_exp"], 1)

            def copy_comp(n, p):
                act.wait_ge(sem["comp_turned"], n + 1)
                reach(act, sem["pv_done"], (n - 1) * 8)
                act.activation(closedT[p][:], comp[:, S:2 * S], ACT.Copy)
                act.activation(pcT[p][:], comp[:, 0:S], ACT.Copy)
                act.activation(vcT[p][:], comp[:, 2 * S:3 * S], ACT.Copy).then_inc(sem["comp_copied"], 1)

            def exps(n, p, w):
                u, c, b = n * 8 + w, w // 2, w % 2
                act.wait_ge(sem["max_ready"], u + 1)
                reach(act, sem["probs_turned"], u - 1)
                if w == 0:
                    reach(act, sem["wt_step"], n - 1)
                for j in range(4):
                    i = act.activation(prob[b][:, j, :], score[b][:, j, :], ACT.Exp, bias=negmax[b][:, j:j + 1],
                                       accum_out=sums[p][:, b, 4 * j + c:4 * j + c + 1])
                i.then_inc(sem["probs_ready"], 1)

            def copy_pT(n, p, w):
                u = n * 8 + w
                act.wait_ge(sem["probs_turned"], u + 1)
                reach(act, sem["pv_done"], u - 1)
                act.activation(pT[w % 2][:], turned[w % 2][:], ACT.Copy).then_inc(sem["pT_copied"], 1)

            def copy_wT(n):
                act.wait_ge(sem["wt_turned"], n + 1)
                reach(act, sem["oT_ready"], n)
                act.activation(wT[:], misc[:, 0:2 * S].rearrange("p (b s) -> p b s", b=2), ACT.Copy)\
                   .then_inc(sem["wT_copied"], 1)

            def slot(n, p):
                nxt, next2 = within(n, 1, count), within(n, 2, count)
                for w in range(8):
                    unit = unit_after(n, p, w, 1)
                    if w == 0 and within(n, -1, count):
                        copy_wT(n - 1)
                    if unit:
                        exps(*unit)
                    if w == 2 and nxt:
                        block_exp(n + 1)
                    if w == 5 and nxt:
                        copy_comp(n + 1, 1 - p)
                    copy_pT(n, p, w)
                    if w == 4 and next2:
                        copy_xT(n + 2, p)
                    if w == 5 and next2:
                        copy_qkv(n + 2, p)

            copy_xT(0, 0)
            copy_xT(1, 1)
            copy_qkv(0, 0)
            copy_qkv(1, 1)
            block_exp(0)
            copy_comp(0, 0)
            exps(0, 0, 0)
            over_slots(act, slot, count)
            copy_wT(count - 1)

        @block.vector
        def _(dve):
            dve.wait_ge(sem["weights"], n_loads)
            for t in ("causal", "band"):
                dve.tensor_copy(mask[t][:], m_f[t][:].unsqueeze(1).broadcast_to([S, 4, S]))
            dve.tensor_scalar(blocks[:], blocks_f[:], -2.0 ** 60, None, ALU.mult)
            dve.tensor_scalar(kmask[:], kmask[:], D ** -0.5, None, ALU.mult)
            dve.memset(zeros[:], 0.0).then_inc(sem["setup"], 1)
            dve.wait_ge(sem["setup"], 1)

            STEPS = 13

            def chain(n, k, ins):
                ins.then_inc(sem["comp_step"], 1)
                dve.wait_ge(sem["comp_step"], n * STEPS + k)

            flat_e = e[:, 0:HEADS * N].rearrange("p (h n) -> p h n", h=HEADS)
            ge = e[:, HEADS * N:HEADS * N + 3]

            def per_head(ap):
                return ap.unsqueeze(1).broadcast_to([S, HEADS, N])

            def block_logits(n):
                dve.wait_ge(sem["cs_ready"], n + 1)
                cs = comp[:, 0:S].rearrange("p (h n) -> p h n", h=HEADS)
                chain(n, 1, dve.tensor_tensor(logit[:], cs, per_head(ok[:]), ALU.mult))
                dve.tensor_tensor(logit[:], logit[:], per_head(low[:]), ALU.add).then_inc(sem["logits_ready"], 1)
                chain(n, 2, dve.scalar_tensor_tensor(out=ge, in0=comp[:, S:S + 3], scalar=1.0 / HEADS, in1=bg[:],
                                                     op0=ALU.mult, op1=ALU.add))

            def exponents(n):
                chain(n, 3, dve.tensor_reduce(gtop[:], ge, AX.X, ALU.max, negate=True))
                dve.wait_ge(sem["logits_ready"], n + 1)
                chain(n, 4, dve.tensor_reduce(top[:], logit[:], AX.X, ALU.max, negate=True))
                chain(n, 5, dve.tensor_scalar(ge, ge, gtop[:, 0:1], None, ALU.add))
                dve.tensor_tensor(flat_e, logit[:], copy_bcast(top[:], N), ALU.add).then_inc(sem["e_ready"], 1)

            def compare_blocks(n):
                dve.wait_ge(sem["logits_ready"], n + 1)
                reach(dve, sem["pairs_ready"], n)
                shape = [S, HEADS, N, N]
                dve.tensor_tensor(more[:], logit[:].unsqueeze(2).broadcast_to(shape),
                                  logit[:].unsqueeze(3).broadcast_to(shape), ALU.is_gt).then_inc(sem["compared"], 1)

            def block_probs(n, p):
                dve.wait_ge(sem["e_exp"], n + 1)
                reach(dve, sem["comp_turned"], n)
                chain(n, 6, dve.tensor_reduce(gtop[:], ge, AX.X, ALU.add))
                chain(n, 7, dve.reciprocal(gtop[:], gtop[:]))
                chain(n, 8, dve.tensor_scalar(gate[p][:], ge, gtop[:, 0:1], None, ALU.mult))
                chain(n, 9, dve.tensor_reduce(top[:], flat_e, AX.X, ALU.add))
                chain(n, 10, dve.reciprocal(top[:], top[:]))
                chain(n, 11, dve.tensor_scalar(top[:], top[:], gate[p][:, 0:1], some[:, 0:1], ALU.mult, ALU.mult))
                chain(n, 12, dve.tensor_tensor(pc[:], flat_e, copy_bcast(top[:], N), ALU.mult))

            def close_blocks(n):
                dve.wait_ge(sem["pairs_ready"], n + 1)
                chain(n, 13, dve.tensor_reduce(ahead[:], pairs[:], AX.X, ALU.add))
                dve.tensor_tensor(closed[:], ahead[:], per_head(place[:]), ALU.is_gt).then_inc(sem["comp_ready"], 1)

            def spread(n, p, c):
                dve.wait_ge(sem["qk_copied"], n + 1)
                reach(dve, sem["scores_ready"], (n - 1) * 8 + 2 * c + 2)
                dve.tensor_tensor(kd[:, c, :, :], qk[p][:, 1, :].unsqueeze(1).broadcast_to([E, 4, S]),
                                  copy_bcast(kmask[:, c, :], S), ALU.mult).then_inc(sem["kd_ready"], 1)

            def spread_v(n, p):
                dve.wait_ge(sem["v_copied"], n + 1)
                reach(dve, sem["pv_done"], (n - 1) * 8)
                dve.tensor_tensor(vd[p][:], v[p][:].unsqueeze(1).broadcast_to([S, 4, E]), vmask[:],
                                  ALU.mult).then_inc(sem["vd_ready"], 1)

            def maxima(n, p, w):
                u = n * 8 + w
                dve.wait_ge(sem["scores_ready"], u + 1)
                reach(dve, sem["probs_ready"], u - 1)
                dve.tensor_reduce(negmax[w % 2][:], score[w % 2][:], AX.X, ALU.max, negate=True)\
                   .then_inc(sem["max_ready"], 1)

            def weights(n, p):
                dve.wait_ge(sem["probs_ready"], (n + 1) * 8)
                dve.reciprocal(wt[:], sums[p][:]).then_inc(sem["wt_step"], 1)
                dve.wait_ge(sem["wt_step"], n + 1)
                reach(dve, sem["wt_turned"], n)
                for b in range(2):
                    i = dve.tensor_scalar(wide[:, b, :].rearrange("p (h e) -> p h e", h=HEADS),
                                          copy_bcast(wt[:, b, :], D), gate[p][:, 1 + b:2 + b], None, ALU.mult)
                i.then_inc(sem["wt_ready"], 1)

            def scale_out(n):
                dve.wait_ge(sem["pv_done"], (n + 1) * 8)
                dve.wait_ge(sem["wT_copied"], n + 1)
                dve.tensor_tensor(scaled[:], out_b[:, 0:2, :], wT[:], ALU.mult).then_inc(sem["out_step"], 1)
                dve.wait_ge(sem["out_step"], n * 2 + 1)
                dve.tensor_tensor(scaled[:, 0, :], scaled[:, 0, :], out_b[:, 2, :], ALU.add)\
                   .then_inc(sem["out_step"], 1)
                dve.wait_ge(sem["out_step"], n * 2 + 2)
                reach(dve, sem["y_ready"], n)
                dve.tensor_tensor(oT[:], scaled[:, 0, :], scaled[:, 1, :], ALU.add).then_inc(sem["oT_ready"], 1)

            def residual(n, p):
                dve.wait_ge(sem["y_ready"], n + 1)
                dve.wait_ge(sem["xb_ready"], n + 1)
                reach(dve, sem["normed"], n)
                dve.tensor_tensor(r[p][:], misc[:, 0:E], xb[p][:], ALU.add).then_inc(sem["r_ready"], 1)

            def moments(n, p):
                dve.wait_ge(sem["r_ready"], n + 1)
                dve.bn_stats(stats[:], r[p][:]).then_inc(sem["step"], 1)
                wait_alone(dve, sem["step"], n * 2 + 1, keep["passed"])
                dve.bn_aggr(mv[p][:], stats[:]).then_inc(sem["step"], 1)
                dve.wait_ge(sem["step"], n * 2 + 2)
                dve.tensor_scalar(rstd[p][:], mv[p][:, 1:2], LN_EPS, None, ALU.add).then_inc(sem["var_ready"], 1)

            def norm(n, p):
                dve.wait_ge(sem["rstd_ready"], n + 1)
                dve.tensor_scalar(x[:, n, :], r[p][:], mv[p][:, 0:1], rstd[p][:, 0:1], ALU.subtract, ALU.mult)\
                   .then_inc(sem["normed"], 1)

            def slot(n, p):
                nxt, last = within(n, 1, count), within(n, -1, count)
                for w in range(8):
                    unit = unit_after(n, p, w, 2)
                    if w == 1 and last:
                        scale_out(n - 1)
                    if w == 4 and last:
                        residual(n - 1, 1 - p)
                    if w == 7:
                        weights(n, p)
                    if unit:
                        maxima(*unit)
                    if w == 7 and within(n, 2, count):
                        block_logits(n + 2)
                        compare_blocks(n + 2)
                    if w == 1 and nxt:
                        exponents(n + 1)
                    if w in (1, 3, 5, 6) and nxt:
                        spread(n + 1, 1 - p, w // 2)
                    if w == 3 and nxt:
                        block_probs(n + 1, 1 - p)
                    if w == 2 and nxt:
                        spread_v(n + 1, 1 - p)
                    if w == 4 and nxt:
                        close_blocks(n + 1)
                    if w == 4 and last:
                        moments(n - 1, 1 - p)
                    if w == 7 and last:
                        norm(n - 1, 1 - p)

            block_logits(0)
            compare_blocks(0)
            exponents(0)
            block_probs(0, 0)
            close_blocks(0)
            for c in range(4):
                spread(0, 0, c)
            spread_v(0, 0)
            block_logits(1)
            compare_blocks(1)
            maxima(0, 0, 0)
            maxima(0, 0, 1)
            over_slots(dve, slot, count)
            scale_out(count - 1)
            residual(count - 1, 1)
            moments(count - 1, 1)
            norm(count - 1, 1)

    clear(nc, sem)


def build(nc, d, out):
    with ExitStack() as ctx:
        sb, _, sems = tensors(ctx, nc, "keep")
        keep = {"x": sb("x", [S, SEQS, E]), "ident": sb("ident", [S, S]), "ident_bf": sb("ident_bf", [S, S], BF16),
                "minus_half": sb("minus_half", [S, 1])}
        sem = sems("loaded made stored passed passed_pool passed_pe")
        keep.update(passed=sem["passed"], passed_pool=sem["passed_pool"], passed_pe=sem["passed_pe"])
        with nc.Block() as block:
            @block.sync
            def _(sp):
                sp.dma_start(keep["ident"][:], d["ident"]).then_inc(sem["loaded"], 16)
                sp.dma_start(keep["x"][:], d["x"].rearrange("s p e -> p s e")).then_inc(sem["loaded"], 16)

            @block.vector
            def _(dve):
                dve.memset(keep["minus_half"][:], -0.5).then_inc(sem["made"], 1)
                dve.wait_ge(sem["loaded"], 32)
                dve.tensor_copy(keep["ident_bf"][:], keep["ident"][:]).then_inc(sem["made"], 1)

        for stage in STAGES:
            if stage == "relu_attn":
                relu_attention(nc, d, keep, stage)
            elif stage == "l1_xattn":
                one_head_attention(nc, d, keep, stage)
            elif stage == "l3_attn":
                with ExitStack() as inner:
                    sb, _, _ = tensors(inner, nc, "l3")
                    with_blocks = dict(keep, kc=sb("kc", [E, SEQS, 8]), vc=sb("vc", [E, SEQS, 8]))
                    compress_blocks(nc, d, with_blocks, "l3_compress")
                    sparse_attention(nc, d, with_blocks, stage)
            elif stage == "l3_linear":
                linear(nc, d, keep, stage)
            elif stage == "l2_attn":
                softmax_attention(nc, d, keep, stage, 8, 8 ** -0.5, q_bias=True, v_bias=True, causal=True, rope=True,
                                  odd_on_act=True)
            elif stage == "l2_xattn":
                l2_xattn(nc, d, keep)
            elif stage == "l0_xattn":
                softmax_attention(nc, d, keep, stage, 8, 8 ** -0.5, cross=True, q_bias=True, v_bias=True,
                                  odd_on_act=True)
            elif stage == "l0_ffn":
                feed_forward(nc, d, keep, stage, "glu", 3, ACT.Silu, scale=1.0 / 127.0, ints=True)
            elif stage == "l1_moe":
                feed_forward(nc, d, keep, stage, "plain", 36, ACT.Gelu_apprx_tanh, bias=True, out_bias=True,
                             experts=8, per_gate=4, gates=8, first_gated=4, gate_bias=True)
            elif stage == "l2_moe":
                feed_forward(nc, d, keep, stage, "glu", 10, ACT.Silu, experts=16, gates=10, shared_gate=True)
            elif stage == "l1_attn":
                softmax_attention(nc, d, keep, stage, 8, 32 ** -0.5, causal=True, low_rank=True, odd_on_act=True)
            elif stage == "l3_xattn":
                softmax_attention(nc, d, keep, stage, 8, 8 ** -0.5, cross=True, out_bias=False, odd_on_act=True)

        with nc.Block() as block:
            @block.sync
            def _(sp):
                sp.dma_start(out.rearrange("s p e -> p s e"), keep["x"][:]).then_inc(sem["stored"], 16)
                sp.wait_ge(sem["stored"], 16)


def l2_xattn(nc, d, keep):
    with ExitStack() as ctx:
        sb, _, _ = tensors(ctx, nc, "l2x")
        keep = dict(keep, b=sb("b", [S, SEQS, E]), z=sb("z", [S, SEQS, E]))
        renormalise(nc, d, keep, "l2x_ln1", keep["x"])
        softmax_attention(nc, d, keep, "l2x_a1", 32, 32 ** -0.5, future_only=True, src=keep["z"], affine=True,
                          dst="sum_and_norm")
        feed_forward(nc, d, keep, "l2x_f1", "plain", 4, ACT.Gelu, bias=True, out_bias=True, src=keep["z"],
                     affine=True, dst="store")
        renormalise(nc, d, keep, "l2x_ln2", keep["b"])
        with ExitStack() as inner:
            sb, _, _ = tensors(inner, nc, "l2x")
            with_ctx = dict(keep, ctxn=sb("ctxn", [C, SEQS, CTX]))
            normalise_context(nc, d, with_ctx, "l2x_ctx")
            softmax_attention(nc, d, with_ctx, "l2x_a2", 32, 32 ** -0.5, cross=True, src=keep["z"], affine=True,
                              dst="sum_and_norm")
        feed_forward(nc, d, keep, "l2x_f2", "plain", 4, ACT.Gelu, bias=True, out_bias=True, src=keep["z"],
                     affine=True, dst="norm_with_x")


def layouts(i):
    f = np.float32

    def rows(b, n=128):
        b = np.asarray(b)
        return np.ascontiguousarray(np.broadcast_to(b.reshape(1, -1), (n, b.size)))

    def cols(b):
        b = np.asarray(b)
        return np.ascontiguousarray(np.broadcast_to(b.reshape(-1, 1), (b.size, 128)))

    def T(w):
        return np.ascontiguousarray(np.asarray(w).T)

    g = {}
    g["ident"] = np.eye(128, dtype=f)
    key = np.arange(128)
    big = np.float32(-2.0 ** 60)
    g["causal"] = np.where(key[None, :] > key[:, None], big, np.float32(0)).astype(f)
    g["future"] = (key[:, None] > key[None, :]).astype(f)
    row, unit, place = np.arange(128)[:, None, None], np.arange(4)[None, :, None], np.arange(4)[None, None, :]
    g["kmask8"] = (row // 8 == 4 * place + unit).astype(f)
    g["kmask4"] = ((row // 4 == 4 * place + unit) & (row < 64)).astype(f)
    g["kmask32"] = (row // 32 == place + 0 * unit).astype(f)
    g["vmask"] = np.tile((np.arange(128)[None, :] // 8 % 4 == np.arange(4)[:, None]).astype(f), (128, 1, 1))
    g["x"] = np.asarray(i["x"])
    g["ctxT"] = np.ascontiguousarray(np.asarray(i["ctx_512"]).transpose(0, 2, 1))
    for n, p in (("l0_xattn", "L0_xattn_"),):
        g[n + "_wq"] = np.asarray(i[p + "Wq"]).reshape(128, 1, 128)
        g[n + "_wk"] = np.asarray(i[p + "Wk"]).reshape(64, 1, 128)
        g[n + "_wv"] = np.asarray(i[p + "Wv"])
        g[n + "_wo"] = np.asarray(i[p + "Wo"]).reshape(128, 1, 128)
        g[n + "_bq"] = np.asarray(i[p + "bq"]).reshape(128, 1)
        g[n + "_bk"] = np.asarray(i[p + "bk"]).reshape(128, 1)
        g[n + "_bv"] = cols(i[p + "bv"])
        g[n + "_bo"] = rows(i[p + "bo"])
    n, p = "l1_attn", "L1_attn_"
    for t in "qk":
        w = np.zeros((128, 2, 128), f)
        w[:, 0, :], w[:, 1, 0:64] = T(i[f"{p}W{t}2"]), T(i[f"{p}W{t}1"])
        g[f"{n}_w{t}"] = w
    g[n + "_wv"], g[n + "_wo"] = T(i[p + "Wv"]), T(i[p + "Wo"]).reshape(128, 1, 128)
    g[n + "_bo"] = rows(i[p + "bo"])
    n, p = "l3_xattn", "L3_xattn_"
    g[n + "_wq"] = T(i[p + "Wq"]).reshape(128, 1, 128)
    kv = T(i[p + "Wkv"])
    g[n + "_wk"] = np.ascontiguousarray(kv[:, 0:128]).reshape(64, 1, 128)
    g[n + "_wv"] = np.ascontiguousarray(kv[:, 128:256])
    g[n + "_wo"] = T(i[p + "Wo"]).reshape(128, 1, 128)

    def chunks(w):
        return np.ascontiguousarray(w.reshape(w.shape[0], -1, 128))

    def stacked(w):
        return np.ascontiguousarray(w.reshape(-1, 128, w.shape[1]).transpose(1, 0, 2))

    n, p = "l0_ffn", "L0_ffn_"
    g[n + "_wu"], g[n + "_wv"] = chunks(T(i[p + "w_gate"])), chunks(T(i[p + "w_up"]))
    g[n + "_wd"] = stacked(T(i[p + "w_down"]))
    n, p = "l1_moe", "L1_ffn_"
    g[n + "_wu"] = chunks(np.concatenate([i[p + "Wfc_s"], *np.asarray(i[p + "Wfc"])], 1))
    g[n + "_bu"] = np.concatenate([i[p + "bfc_s"], np.asarray(i[p + "bfc"]).ravel()]).reshape(-1, 128).T
    g[n + "_wd"] = stacked(np.concatenate([i[p + "Wproj_s"], *np.asarray(i[p + "Wproj"])], 0))
    g[n + "_bd"], g[n + "_gb"], g[n + "_wr"] = rows(i[p + "bproj_s"]), np.tile(i[p + "bproj"], (3, 1)), i[p + "Wr"]
    g[n + "_sel"] = np.tile(np.repeat(np.eye(8, dtype=f)[:, :, None], 128, 2), (3, 1, 1))
    e = np.arange(8)
    g[n + "_before"] = np.tile((e[None, :] < e[:, None]).astype(f), (128, 1, 1))
    n, p = "l2_moe", "L2_ffn_"
    for t, w in (("_wu", "gate"), ("_wv", "up")):
        g[n + t] = chunks(T(np.concatenate([np.asarray(i[f"{p}We_{w}"]).reshape(1024, 128), i[f"{p}Ws_{w}"]], 0)))
    g[n + "_wd"] = stacked(np.concatenate([np.asarray(i[p + "We_down"]).transpose(0, 2, 1).reshape(1024, 128),
                                           T(i[p + "Ws_down"])], 0))
    g[n + "_wr"] = T(np.concatenate([i[p + "Wg"], i[p + "Wsg"]], 0))
    sel = np.zeros((17, 10, 128), f)
    for k in range(16):
        sel[k, k // 2, 64 * (k % 2):64 * (k % 2) + 64] = 1
    sel[16, 8:10] = 1
    g[n + "_sel"] = np.tile(sel, (3, 1, 1))
    e = np.arange(16)
    g[n + "_before"] = np.tile((e[None, :] < e[:, None]).astype(f), (128, 1, 1))
    n, p = "relu_attn", "L0_attn_"
    for t in "qkvo":
        g[f"{n}_w{t}"], g[f"{n}_b{t}"] = T(i[f"{p}W{t}"]), rows(i[f"{p}b{t}"])
    g[n + "_weight"], g[n + "_gain"] = rows(i[p + "norm_weight"]), rows(i[p + "norm_gate"])
    for t in ("key", "value"):
        g[f"{n}_{t}T"] = T(np.asarray(i[p + t]).reshape(512, 128)).reshape(128, 4, 128)
    n, p = "l1_xattn", "L1_xattn_"
    for t in "qkv":
        g[f"{n}_w{t}"] = i[f"{p}W{t}"]
    g[n + "_bq"], g[n + "_bk"] = np.asarray(i[p + "bq"]).reshape(128, 1), np.asarray(i[p + "bk"]).reshape(128, 1)
    g[n + "_bv"] = rows(i[p + "bv"])
    n, p = "l3_linear", "L3_ffn_"
    g[n + "_w"], g[n + "_scale"], g[n + "_bias"] = T(i[p + "CB"]), rows(i[p + "SCB"]), rows(i[p + "bias"])
    n, p = "l2_attn", "L2_attn_"
    swap = np.arange(128) ^ 1
    for t in "qk":
        w, b = np.asarray(i[f"{p}W{t}"]), np.asarray(i[f"{p}b{t}"])
        g[f"{n}_w{t}"], g[f"{n}_b{t}"] = np.stack([w, w[:, swap]], 1), np.stack([b, b[swap]], 1)
    freq = f(1.0) / f(10000.0) ** (np.arange(4, dtype=f) * f(2.0) / f(8))
    angle = np.arange(128, dtype=f)[None, :] * freq[:, None]
    pair = (np.arange(128) % 8) // 2
    g["cos"] = np.cos(angle)[pair].astype(f)
    g["sin"] = (np.sin(angle)[pair] * np.where(np.arange(128) % 2, f(1), f(-1))[:, None]).astype(f)
    g[n + "_wv"], g[n + "_wo"] = i[p + "Wv"], np.asarray(i[p + "Wp"]).reshape(128, 1, 128)
    g[n + "_bv"], g[n + "_bo"] = cols(i[p + "bv"]), rows(i[p + "bp"])
    g["ctx"] = i["ctx_512"]
    n, p = "l3_attn", "L3_attn_"
    for t in "qkv":
        g[f"{n}_flat{t}"] = i[f"{p}W{t}"]
    for t in "kv":
        w = np.asarray(i[f"{p}Wc{t}"]).reshape(16, 8, 8)
        wide = np.zeros((16, 8, 16, 16, 8), w.dtype)
        for h in range(16):
            wide[h, :, :, h, :] = w.transpose(1, 0, 2)
        g[f"{n}_wc{t}"] = wide.reshape(128, 16, 128)
    g[n + "_wo"] = i[p + "Wo"]
    g[n + "_wg"], g[n + "_bg"] = np.tile(np.asarray(i[p + "Wg"]), (16, 1)), rows(i[p + "bg"])
    g["own"] = np.repeat(np.eye(16, dtype=f), 8, 0)
    done = key[:, None] >= (np.arange(8)[None, :] + 1) * 16
    g["block_ok"] = np.where(done, f(1.0 / np.sqrt(8.0)), f(0))
    g["block_low"] = np.where(done, f(0), f(-1e9))
    g["block_some"] = done.any(1, keepdims=True).astype(f)
    back = key[:, None] - key[None, :]
    g["band"] = np.where((back >= 0) & (back <= 32), f(0), big).astype(f)
    head, block = np.arange(128) // 8, np.arange(128) % 8
    g["blocks"] = ((head[:, None, None, None] == 4 * np.arange(4)[None, None, :, None] + np.arange(4)[None, :, None, None])
                   & (block[:, None, None, None] == key[None, None, None, :] // 16)).astype(f).reshape(128, 4, 512)
    g["block_place"] = rows(f(3.5) - np.arange(8, dtype=f))
    for a, c in (("a1", 128), ("a2", 64)):
        n, p = "l2x_" + a, f"L2_xattn_{a}_"
        flat = {t: np.asarray(i[f"{p}w{t}"]).transpose(1, 0, 2).reshape(-1, 512) for t in "qkv"}
        g[n + "_wq"], g[n + "_wk"], g[n + "_wv"] = chunks(flat["q"]), chunks(flat["k"]), flat["v"]
        g[n + "_wo"], g[n + "_bo"] = stacked(np.asarray(i[p + "li1_w"])), rows(i[p + "li1_b"])
        aff = np.zeros((128, 4), f)
        aff[:, 0], aff[:, 1] = i[p + "lnx_g"], i[p + "lnx_b"]
        aff[0:c, 2], aff[0:c, 3] = i[p + "lny_g"], i[p + "lny_b"]
        g[n + "_aff"] = aff
        if a == "a2":
            g["l2x_ctx_aff"] = aff[0:64, 2:4]
        m = "l2x_f" + a[1]
        g[m + "_wu"], g[m + "_wd"] = chunks(np.asarray(i[p + "li2_w"])), stacked(np.asarray(i[p + "li3_w"]))
        g[m + "_bu"], g[m + "_bd"] = np.asarray(i[p + "li2_b"]).reshape(4, 128).T, rows(i[p + "li3_b"])
        g[m + "_aff"] = np.stack([i[p + "ln3_g"], i[p + "ln3_b"]], 1)
        g[f"l2x_ln{a[1]}_gain"] = rows(i[f"L2_xattn_ln{a[1]}_g"])
        g[f"l2x_ln{a[1]}_shift"] = rows(i[f"L2_xattn_ln{a[1]}_b"])
    return g


def kernel(**inputs):
    import concourse.bacc as bacc
    from concourse.bass_utils import run_bass_kernel_spmd as run

    nc = bacc.Bacc("TRN2", target_bir_lowering=False, num_devices=1)
    arrays = {f"in_{n}": np.ascontiguousarray(a) for n, a in layouts(inputs).items()}
    d = {n[3:]: nc.dram_tensor(n, a.shape, mybir.dt.from_np(a.dtype), kind="ExternalInput").ap()
         for n, a in arrays.items()}
    out = nc.dram_tensor("out", (SEQS, S, E), F32, kind="ExternalOutput").ap()
    build(nc, d, out)
    return run(nc, [arrays], core_ids=[0]).results[0]["out"]
```
